# Optimizing a Trainium2 kernel written in Bass

```python
import numpy as np
import jax
import jax.numpy as jnp

def _softmax(x, axis=-1):
    return jax.nn.softmax(x, axis=axis)

def _gelu(x):
    return jax.nn.gelu(x, approximate=True)

def _silu(x):
    return jax.nn.silu(x)

def _sigmoid(x):
    return jax.nn.sigmoid(x)

def _layernorm(x, axis=-1, eps=1e-05):
    m = jnp.mean(x, axis=axis, keepdims=True)
    v = jnp.var(x, axis=axis, keepdims=True)
    return (x - m) / jnp.sqrt(v + eps)

def _scatter_add(tgt, idx, src, axis=0):
    return tgt.at[idx].add(src)

def _segment_sum(src, seg, n):
    return jax.ops.segment_sum(src, seg, n)
kernel_name = 'mk_perceiver_d4_seqx_r4_c803b6'

def setup_inputs(seed: int=0):
    np.random.seed(seed)
    _w = jnp.asarray

    def _rec_inputs():
        import jax
        import jax.numpy as jnp
        _rk = jax.random.key(seed)
        x = 0.0002417 + 0.9998 * jax.random.normal(jax.random.fold_in(_rk, 1), (2, 256, 256), jnp.float32)
        _lenS = 256 - jax.random.randint(jax.random.fold_in(_rk, 7), (2,), 0, max(1, 256 // 4) + 1, jnp.int32)
        _lenS2 = 4096 - jax.random.randint(jax.random.fold_in(_rk, 8), (2,), 0, max(1, 4096 // 4) + 1, jnp.int32)
        _ctx_1024P = jax.random.normal(jax.random.fold_in(_rk, 11), (2, 16, 256), jnp.float32)
        _ctx_1024c = jax.random.dirichlet(jax.random.fold_in(_rk, 511), 0.3 * jnp.ones((16,), jnp.float32), (2, 4096))
        _ctx_1024t = jnp.einsum('bsk,bkd->bsd', _ctx_1024c, _ctx_1024P)
        _ctx_1024t = _ctx_1024t * jax.lax.rsqrt(jnp.mean(jnp.square(_ctx_1024t)) + 1e-12) * 0.953939
        ctx_1024 = 7.22013e-05 + 1.00017 * (_ctx_1024t + 0.3 * jax.random.normal(jax.random.fold_in(_rk, 611), (2, 4096, 256), jnp.float32))
        return (x, ctx_1024)
    x, ctx_1024 = _rec_inputs()

    def _L0_xattn_setup():
        import jax, jax.numpy as jnp
        import numpy as np
        D_MODEL = 256
        B, S = (4, 512)
        key = jax.random.key(seed)
        ks = jax.random.split(key, 10)
        s = 1.0 / np.sqrt(D_MODEL)
        return {'k': jax.random.normal(ks[0], (B, S, D_MODEL), jnp.float32), 'v': jax.random.normal(ks[1], (B, S, D_MODEL), jnp.float32), 'q': jax.random.normal(ks[2], (B, S, D_MODEL), jnp.float32), 'Wk': jax.random.normal(ks[3], (D_MODEL, D_MODEL), jnp.float32) * s, 'Wv': jax.random.normal(ks[4], (D_MODEL, D_MODEL), jnp.float32) * s, 'bv': jnp.zeros((D_MODEL,), jnp.float32), 'Wq': jax.random.normal(ks[5], (D_MODEL, D_MODEL), jnp.float32) * s, 'bq': jnp.zeros((D_MODEL,), jnp.float32), 'Wo': jax.random.normal(ks[6], (D_MODEL, D_MODEL), jnp.float32) * s, 'bo': jnp.zeros((D_MODEL,), jnp.float32)}
    _L0_xattn_all = _L0_xattn_setup()
    _L0_xattn_in = {k: v for k, v in _L0_xattn_all.items() if k in ('Wk', 'Wv', 'bv', 'Wq', 'bq', 'Wo', 'bo')}
    del _L0_xattn_all

    def _L0_attn_setup():
        import jax, jax.numpy as jnp
        import numpy as np
        import math
        HIDDEN = 256
        HEADS = 16
        HEAD_DIM = HIDDEN // HEADS
        MAX_POS = 512
        BATCH = 2
        SEQ = 512
        key = jax.random.key(seed)
        ks = jax.random.split(key, 8)
        s = 0.02
        return {'hidden_states': jax.random.normal(ks[0], (BATCH, SEQ, HIDDEN), jnp.float32), 'Wq': jax.random.normal(ks[1], (HIDDEN, HIDDEN), jnp.float32) * s, 'bq': jnp.zeros((HIDDEN,), jnp.float32), 'Wk': jax.random.normal(ks[2], (HIDDEN, HIDDEN), jnp.float32) * s, 'bk': jnp.zeros((HIDDEN,), jnp.float32), 'Wv': jax.random.normal(ks[3], (HIDDEN, HIDDEN), jnp.float32) * s, 'bv': jnp.zeros((HIDDEN,), jnp.float32), 'dist_emb': jax.random.normal(ks[4], (2 * MAX_POS - 1, HEAD_DIM), jnp.float32) * s}
    _L0_attn_all = _L0_attn_setup()
    _L0_attn_in = {k: v for k, v in _L0_attn_all.items() if k in ('Wq', 'bq', 'Wk', 'bk', 'Wv', 'bv', 'dist_emb')}
    del _L0_attn_all

    def _L0_ffn_setup():
        import jax, jax.numpy as jnp
        import numpy as np
        DIM = 256
        HID = 1024
        E = 8
        TOPK = 2
        ALPHA = 2.0
        B, T = (1, 512)
        DOWN_SCALE = 0.01
        key = jax.random.key(seed)
        ks = jax.random.split(key, 8)
        s = 1.0 / np.sqrt(DIM)
        sh = 1.0 / np.sqrt(HID)
        return {'x': jax.random.normal(ks[0], (B, T, DIM), jnp.float32), 'w_router': jax.random.uniform(ks[1], (DIM, E), jnp.float32, -s, s), 'w_up': jax.random.uniform(ks[2], (E - 1, DIM, HID), jnp.float32, -s, s), 'w_gate': jax.random.uniform(ks[3], (E - 1, DIM, HID), jnp.float32, -s, s), 'w_down': jax.random.normal(ks[4], (E - 1, HID, DIM), jnp.float32) * DOWN_SCALE, 'ws_up': jax.random.uniform(ks[5], (DIM, HID), jnp.float32, -s, s), 'ws_gate': jax.random.uniform(ks[6], (DIM, HID), jnp.float32, -s, s), 'ws_down': jax.random.normal(ks[7], (HID, DIM), jnp.float32) * DOWN_SCALE}
    _L0_ffn_all = _L0_ffn_setup()
    _L0_ffn_in = {k: v for k, v in _L0_ffn_all.items() if k in ('w_router', 'w_up', 'w_gate', 'w_down', 'ws_up', 'ws_gate', 'ws_down')}
    del _L0_ffn_all

    def _L1_xattn_setup():
        import jax, jax.numpy as jnp
        import numpy as np
        EPS = 1e-05

        def layer_norm(x, g, b):
            mu = jnp.mean(x, axis=-1, keepdims=True)
            var = jnp.var(x, axis=-1, keepdims=True)
            return (x - mu) * jax.lax.rsqrt(var + EPS) * g + b
        key = jax.random.key(seed)
        ks = jax.random.split(key, 8)
        dim, heads, dim_head = (256, 16, 64)
        inner = heads * dim_head
        b, n, m = (8, 1024, 64)
        s = dim ** (-0.5)
        return {'x': jax.random.normal(ks[0], (b, n, dim), jnp.float32), 'latents': jax.random.normal(ks[1], (b, m, dim), jnp.float32), 'ln_m_g': jnp.ones((dim,), jnp.float32), 'ln_m_b': jnp.zeros((dim,), jnp.float32), 'ln_l_g': jnp.ones((dim,), jnp.float32), 'ln_l_b': jnp.zeros((dim,), jnp.float32), 'Wq': jax.random.normal(ks[2], (dim, inner), jnp.float32) * s, 'Wkv': jax.random.normal(ks[3], (dim, 2 * inner), jnp.float32) * s, 'Wout': jax.random.normal(ks[4], (inner, dim), jnp.float32) * s}
    _L1_xattn_all = _L1_xattn_setup()
    _L1_xattn_in = {k: v for k, v in _L1_xattn_all.items() if k in ('ln_m_g', 'ln_m_b', 'ln_l_g', 'ln_l_b', 'Wq', 'Wkv', 'Wout')}
    del _L1_xattn_all

    def _L1_attn_setup():
        import jax, jax.numpy as jnp
        import numpy as np
        EPS = 1e-06
        key = jax.random.key(seed)
        ks = jax.random.split(key, 8)
        b, n, d, h = (2, 512, 256, 16)
        std = 0.02
        x = jax.random.normal(ks[0], (b, n, d), jnp.float32)
        Wq = jax.random.normal(ks[1], (d, d), jnp.float32) * std
        Wk = jax.random.normal(ks[2], (d, d), jnp.float32) * std
        Wv = jax.random.normal(ks[3], (d, d), jnp.float32) * std
        Wo = jax.random.normal(ks[4], (d, d), jnp.float32) * std
        Wbet = jax.random.normal(ks[5], (d, h), jnp.float32) * std
        Wf = jax.random.normal(ks[6], (d, h), jnp.float32) * std
        norm_w = jnp.ones((d,), jnp.float32)
        return {'x': x, 'Wq': Wq, 'Wk': Wk, 'Wv': Wv, 'Wo': Wo, 'Wbet': Wbet, 'Wf': Wf, 'norm_w': norm_w}
    _L1_attn_all = _L1_attn_setup()
    _L1_attn_in = {k: v for k, v in _L1_attn_all.items() if k in ('Wq', 'Wk', 'Wv', 'Wo', 'Wbet', 'Wf', 'norm_w')}
    del _L1_attn_all

    def _L1_ffn_setup():
        import jax, jax.numpy as jnp
        import numpy as np
        E = 8
        K = 2
        CF = 1.2
        D = 256
        F = 1024
        B, S = (4, 256)
        key = jax.random.key(seed)
        ks = jax.random.split(key, 4)

        def init(k, shape, fan_in):
            return jax.random.normal(k, shape, jnp.float32) * (1.0 / np.sqrt(fan_in))
        return {'x': jax.random.normal(ks[0], (B, S, D), jnp.float32), 'Wg': init(ks[1], (D, E), D), 'bg': jnp.zeros((E,), jnp.float32), 'W1': init(ks[2], (E, D, F), D), 'b1': jnp.zeros((E, F), jnp.float32), 'W2': init(ks[3], (E, F, D), F), 'b2': jnp.zeros((E, D), jnp.float32)}
    _L1_ffn_all = _L1_ffn_setup()
    _L1_ffn_in = {k: v for k, v in _L1_ffn_all.items() if k in ('Wg', 'bg', 'W1', 'b1', 'W2', 'b2')}
    del _L1_ffn_all

    def _L2_xattn_setup():
        import jax, jax.numpy as jnp
        import numpy as np
        D_MODEL = 256
        NUM_HEADS = 16
        D_HEAD = D_MODEL // NUM_HEADS
        B, LQ, LK = (4, 512, 512)
        key = jax.random.key(seed)
        ks = jax.random.split(key, 11)
        s = 1.0 / np.sqrt(D_MODEL)
        return {'query': jax.random.normal(ks[0], (B, LQ, D_MODEL), jnp.float32), 'key': jax.random.normal(ks[1], (B, LK, D_MODEL), jnp.float32), 'value': jax.random.normal(ks[2], (B, LK, D_MODEL), jnp.float32), 'Wq': jax.random.normal(ks[3], (D_MODEL, D_MODEL), jnp.float32) * s, 'bq': jax.random.normal(ks[4], (D_MODEL,), jnp.float32) * s, 'Wk': jax.random.normal(ks[5], (D_MODEL, D_MODEL), jnp.float32) * s, 'bk': jax.random.normal(ks[6], (D_MODEL,), jnp.float32) * s, 'Wv': jax.random.normal(ks[7], (D_MODEL, D_MODEL), jnp.float32) * s, 'bv': jax.random.normal(ks[8], (D_MODEL,), jnp.float32) * s, 'Wo': jax.random.normal(ks[9], (D_MODEL, D_MODEL), jnp.float32) * s, 'bo': jax.random.normal(ks[10], (D_MODEL,), jnp.float32) * s}
    _L2_xattn_all = _L2_xattn_setup()
    _L2_xattn_in = {k: v for k, v in _L2_xattn_all.items() if k in ('Wq', 'bq', 'Wk', 'bk', 'Wv', 'bv', 'Wo', 'bo')}
    del _L2_xattn_all

    def _L2_attn_setup():
        import jax, jax.numpy as jnp
        import numpy as np
        import math
        D_MODEL = 256
        NUM_HEADS = 16
        HEAD_DIM = D_MODEL // NUM_HEADS
        LN_EPS = 1e-05

        def _layer_norm(x, g, b):
            mu = jnp.mean(x, axis=-1, keepdims=True)
            var = jnp.mean(jnp.square(x - mu), axis=-1, keepdims=True)
            return (x - mu) * jax.lax.rsqrt(var + LN_EPS) * g + b

        def _rope_tables(seq_len, dim, dtype):
            inv_freq = 1.0 / 10000.0 ** (jnp.arange(0, dim, 2, dtype=jnp.float32) / dim)
            t = jnp.arange(seq_len, dtype=jnp.float32)
            freqs = t[:, None] * inv_freq[None, :]
            emb = jnp.concatenate([freqs, freqs], axis=-1)
            return (jnp.cos(emb).astype(dtype), jnp.sin(emb).astype(dtype))

        def _rotate_half(x):
            x1, x2 = jnp.split(x, 2, axis=-1)
            return jnp.concatenate([-x2, x1], axis=-1)
        key = jax.random.key(seed)
        ks = jax.random.split(key, 8)
        B, S, D = (2, 512, D_MODEL)
        s_in = 1.0 / math.sqrt(D)
        return {'x': jax.random.normal(ks[0], (B, S, D), jnp.float32), 'ln1_g': jnp.ones((D,), jnp.float32), 'ln1_b': jnp.zeros((D,), jnp.float32), 'Wqkv': jax.random.normal(ks[1], (D, 3 * D), jnp.float32) * s_in, 'bqkv': jnp.zeros((3 * D,), jnp.float32), 'Wo': jax.random.normal(ks[2], (D, D), jnp.float32) * s_in, 'bo': jnp.zeros((D,), jnp.float32), 'ln2_g': jnp.ones((D,), jnp.float32), 'ln2_b': jnp.zeros((D,), jnp.float32), 'W1': jax.random.normal(ks[3], (D, 4 * D), jnp.float32) * s_in, 'b1': jnp.zeros((4 * D,), jnp.float32), 'W2': jax.random.normal(ks[4], (4 * D, D), jnp.float32) / math.sqrt(4 * D), 'b2': jnp.zeros((D,), jnp.float32)}
    _L2_attn_all = _L2_attn_setup()
    _L2_attn_in = {k: v for k, v in _L2_attn_all.items() if k in ('ln1_g', 'ln1_b', 'Wqkv', 'bqkv', 'Wo', 'bo', 'ln2_g', 'ln2_b', 'W1', 'b1', 'W2', 'b2')}
    del _L2_attn_all

    def _L2_ffn_setup():
        import jax, jax.numpy as jnp
        import numpy as np
        import math
        B, S, H = (8, 1024, 256)
        E, I, K = (8, 512, 2)
        CAP_FACTOR = 1.0

        def _router(x, expert_embeddings):
            dot = jnp.einsum('bsh,eh->bse', x, expert_embeddings)
            n = dot.shape[0] * dot.shape[1]
            dot2 = dot.reshape(n, E)
            vals, idx = jax.lax.top_k(dot2, K)
            rows = jnp.arange(n)[:, None]
            masked = jnp.full_like(dot2, -jnp.inf).at[rows, idx].set(vals)
            return jax.nn.softmax(masked, axis=-1)
        key = jax.random.key(seed)
        k1, k2, k3, k4 = jax.random.split(key, 4)

        def kaiming(k, shape):
            bound = math.sqrt(3.0 / shape[-1])
            return jax.random.uniform(k, shape, jnp.float32, -bound, bound)
        x = jax.random.normal(k1, (B, S, H), jnp.float32)
        expert_embeddings = kaiming(k2, (E, H))
        first_linear = kaiming(k3, (E, I, H))
        second_linear = kaiming(k4, (E, H, I))
        return {'x': x, 'expert_embeddings': expert_embeddings, 'first_linear': first_linear, 'second_linear': second_linear}
    _L2_ffn_all = _L2_ffn_setup()
    _L2_ffn_in = {k: v for k, v in _L2_ffn_all.items() if k in ('expert_embeddings', 'first_linear', 'second_linear')}
    del _L2_ffn_all

    def _L3_xattn_setup():
        import jax, jax.numpy as jnp
        import numpy as np
        EMBED_DIM = 256
        NUM_HEADS = 16
        HEAD_DIM = EMBED_DIM // NUM_HEADS
        B, N, M = (4, 512, 512)

        def _split_heads(x):
            b, t, _ = x.shape
            return x.reshape(b, t, NUM_HEADS, HEAD_DIM).transpose(0, 2, 1, 3)
        key = jax.random.key(seed)
        ks = jax.random.split(key, 10)
        s = 1.0 / np.sqrt(EMBED_DIM)
        return {'query_modal': jax.random.normal(ks[0], (B, N, EMBED_DIM), jnp.float32), 'key_value_modal': jax.random.normal(ks[1], (B, M, EMBED_DIM), jnp.float32), 'Wq': jax.random.normal(ks[2], (EMBED_DIM, EMBED_DIM), jnp.float32) * s, 'bq': jnp.zeros((EMBED_DIM,), jnp.float32), 'Wk': jax.random.normal(ks[3], (EMBED_DIM, EMBED_DIM), jnp.float32) * s, 'bk': jnp.zeros((EMBED_DIM,), jnp.float32), 'Wv': jax.random.normal(ks[4], (EMBED_DIM, EMBED_DIM), jnp.float32) * s, 'bv': jnp.zeros((EMBED_DIM,), jnp.float32), 'Wo': jax.random.normal(ks[5], (EMBED_DIM, EMBED_DIM), jnp.float32) * s, 'bo': jnp.zeros((EMBED_DIM,), jnp.float32)}
    _L3_xattn_all = _L3_xattn_setup()
    _L3_xattn_in = {k: v for k, v in _L3_xattn_all.items() if k in ('Wq', 'bq', 'Wk', 'bk', 'Wv', 'bv', 'Wo', 'bo')}
    del _L3_xattn_all

    def _L3_attn_setup():
        import jax, jax.numpy as jnp
        import numpy as np
        B_, L_, DM, DIN, N_, K_, R_ = (1, 256, 256, 512, 16, 4, 64)
        key = jax.random.key(seed)
        ks = jax.random.split(key, 10)
        rn = lambda k, shape, s: jax.random.normal(k, shape, jnp.float32) * s
        dt_min, dt_max = (0.001, 0.1)
        u = jax.random.uniform(ks[6], (DIN,), jnp.float32)
        dt = jnp.exp(u * (np.log(dt_max) - np.log(dt_min)) + np.log(dt_min))
        b_dt = dt + jnp.log(-jnp.expm1(-dt))
        A_log = jnp.log(jnp.broadcast_to(jnp.arange(1, N_ + 1, dtype=jnp.float32), (DIN, N_)))
        return {'x': rn(ks[0], (B_, L_, DM), 1.0), 'W_in': rn(ks[1], (2 * DIN, DM), 0.02), 'conv_w': rn(ks[2], (DIN, K_), 0.1), 'conv_b': rn(ks[3], (DIN,), 0.02), 'W_x': rn(ks[4], (R_ + 2 * N_, DIN), 0.02), 'W_dt': rn(ks[5], (DIN, R_), R_ ** (-0.5)), 'b_dt': b_dt, 'A_log': A_log, 'D_param': jnp.ones((DIN,), jnp.float32), 'W_out': rn(ks[7], (DM, DIN), 0.02)}
    _L3_attn_all = _L3_attn_setup()
    _L3_attn_in = {k: v for k, v in _L3_attn_all.items() if k in ('W_in', 'conv_w', 'conv_b', 'W_x', 'W_dt', 'b_dt', 'A_log', 'D_param', 'W_out')}
    del _L3_attn_all

    def _L3_ffn_setup():
        import jax, jax.numpy as jnp
        import numpy as np
        B, S, D, H, E, K = (2, 256, 256, 128, 16, 4)
        HS = 2 * H

        def silu(z):
            return z * jax.nn.sigmoid(z)
        key = jax.random.key(seed)
        ks = jax.random.split(key, 8)
        sc = lambda fan_in: 1.0 / np.sqrt(fan_in)
        x = jax.random.normal(ks[0], (B, S, D), jnp.float32)
        gate_w = jax.random.normal(ks[1], (E, D), jnp.float32) * sc(D)
        ws_in = jax.random.normal(ks[2], (D, HS), jnp.float32) * sc(D)
        vs_in = jax.random.normal(ks[3], (D, HS), jnp.float32) * sc(D)
        ws_out = jax.random.normal(ks[4], (HS, D), jnp.float32) * sc(HS)
        e_win = jax.random.normal(ks[5], (E, D, H), jnp.float32) * sc(D)
        e_vin = jax.random.normal(ks[6], (E, D, H), jnp.float32) * sc(D)
        e_wout = jax.random.normal(ks[7], (E, H, D), jnp.float32) * sc(H)
        return {'x': x, 'gate_w': gate_w, 'ws_in': ws_in, 'vs_in': vs_in, 'ws_out': ws_out, 'e_win': e_win, 'e_vin': e_vin, 'e_wout': e_wout}
    _L3_ffn_all = _L3_ffn_setup()
    _L3_ffn_in = {k: v for k, v in _L3_ffn_all.items() if k in ('gate_w', 'ws_in', 'vs_in', 'ws_out', 'e_win', 'e_vin', 'e_wout')}
    del _L3_ffn_all
    return {'x': x, 'ctx_1024': ctx_1024, 'L0_xattn_Wk': _L0_xattn_in['Wk'], 'L0_xattn_Wv': _L0_xattn_in['Wv'], 'L0_xattn_bv': _L0_xattn_in['bv'], 'L0_xattn_Wq': _L0_xattn_in['Wq'], 'L0_xattn_bq': _L0_xattn_in['bq'], 'L0_xattn_Wo': _L0_xattn_in['Wo'], 'L0_xattn_bo': _L0_xattn_in['bo'], 'L0_attn_Wq': _L0_attn_in['Wq'], 'L0_attn_bq': _L0_attn_in['bq'], 'L0_attn_Wk': _L0_attn_in['Wk'], 'L0_attn_bk': _L0_attn_in['bk'], 'L0_attn_Wv': _L0_attn_in['Wv'], 'L0_attn_bv': _L0_attn_in['bv'], 'L0_attn_dist_emb': _L0_attn_in['dist_emb'], 'L0_ffn_w_router': _L0_ffn_in['w_router'], 'L0_ffn_w_up': _L0_ffn_in['w_up'], 'L0_ffn_w_gate': _L0_ffn_in['w_gate'], 'L0_ffn_w_down': _L0_ffn_in['w_down'], 'L0_ffn_ws_up': _L0_ffn_in['ws_up'], 'L0_ffn_ws_gate': _L0_ffn_in['ws_gate'], 'L0_ffn_ws_down': _L0_ffn_in['ws_down'], 'L1_xattn_ln_m_g': _L1_xattn_in['ln_m_g'], 'L1_xattn_ln_m_b': _L1_xattn_in['ln_m_b'], 'L1_xattn_ln_l_g': _L1_xattn_in['ln_l_g'], 'L1_xattn_ln_l_b': _L1_xattn_in['ln_l_b'], 'L1_xattn_Wq': _L1_xattn_in['Wq'], 'L1_xattn_Wkv': _L1_xattn_in['Wkv'], 'L1_xattn_Wout': _L1_xattn_in['Wout'], 'L1_attn_Wq': _L1_attn_in['Wq'], 'L1_attn_Wk': _L1_attn_in['Wk'], 'L1_attn_Wv': _L1_attn_in['Wv'], 'L1_attn_Wo': _L1_attn_in['Wo'], 'L1_attn_Wbet': _L1_attn_in['Wbet'], 'L1_attn_Wf': _L1_attn_in['Wf'], 'L1_attn_norm_w': _L1_attn_in['norm_w'], 'L1_ffn_Wg': _L1_ffn_in['Wg'], 'L1_ffn_bg': _L1_ffn_in['bg'], 'L1_ffn_W1': _L1_ffn_in['W1'], 'L1_ffn_b1': _L1_ffn_in['b1'], 'L1_ffn_W2': _L1_ffn_in['W2'], 'L1_ffn_b2': _L1_ffn_in['b2'], 'L2_xattn_Wq': _L2_xattn_in['Wq'], 'L2_xattn_bq': _L2_xattn_in['bq'], 'L2_xattn_Wk': _L2_xattn_in['Wk'], 'L2_xattn_bk': _L2_xattn_in['bk'], 'L2_xattn_Wv': _L2_xattn_in['Wv'], 'L2_xattn_bv': _L2_xattn_in['bv'], 'L2_xattn_Wo': _L2_xattn_in['Wo'], 'L2_xattn_bo': _L2_xattn_in['bo'], 'L2_attn_ln1_g': _L2_attn_in['ln1_g'], 'L2_attn_ln1_b': _L2_attn_in['ln1_b'], 'L2_attn_Wqkv': _L2_attn_in['Wqkv'], 'L2_attn_bqkv': _L2_attn_in['bqkv'], 'L2_attn_Wo': _L2_attn_in['Wo'], 'L2_attn_bo': _L2_attn_in['bo'], 'L2_attn_ln2_g': _L2_attn_in['ln2_g'], 'L2_attn_ln2_b': _L2_attn_in['ln2_b'], 'L2_attn_W1': _L2_attn_in['W1'], 'L2_attn_b1': _L2_attn_in['b1'], 'L2_attn_W2': _L2_attn_in['W2'], 'L2_attn_b2': _L2_attn_in['b2'], 'L2_ffn_expert_embeddings': _L2_ffn_in['expert_embeddings'], 'L2_ffn_first_linear': _L2_ffn_in['first_linear'], 'L2_ffn_second_linear': _L2_ffn_in['second_linear'], 'L3_xattn_Wq': _L3_xattn_in['Wq'], 'L3_xattn_bq': _L3_xattn_in['bq'], 'L3_xattn_Wk': _L3_xattn_in['Wk'], 'L3_xattn_bk': _L3_xattn_in['bk'], 'L3_xattn_Wv': _L3_xattn_in['Wv'], 'L3_xattn_bv': _L3_xattn_in['bv'], 'L3_xattn_Wo': _L3_xattn_in['Wo'], 'L3_xattn_bo': _L3_xattn_in['bo'], 'L3_attn_W_in': _L3_attn_in['W_in'], 'L3_attn_conv_w': _L3_attn_in['conv_w'], 'L3_attn_conv_b': _L3_attn_in['conv_b'], 'L3_attn_W_x': _L3_attn_in['W_x'], 'L3_attn_W_dt': _L3_attn_in['W_dt'], 'L3_attn_b_dt': _L3_attn_in['b_dt'], 'L3_attn_A_log': _L3_attn_in['A_log'], 'L3_attn_D_param': _L3_attn_in['D_param'], 'L3_attn_W_out': _L3_attn_in['W_out'], 'L3_ffn_gate_w': _L3_ffn_in['gate_w'], 'L3_ffn_ws_in': _L3_ffn_in['ws_in'], 'L3_ffn_vs_in': _L3_ffn_in['vs_in'], 'L3_ffn_ws_out': _L3_ffn_in['ws_out'], 'L3_ffn_e_win': _L3_ffn_in['e_win'], 'L3_ffn_e_vin': _L3_ffn_in['e_vin'], 'L3_ffn_e_wout': _L3_ffn_in['e_wout']}

def reference(x, ctx_1024, L0_xattn_Wk, L0_xattn_Wv, L0_xattn_bv, L0_xattn_Wq, L0_xattn_bq, L0_xattn_Wo, L0_xattn_bo, L0_attn_Wq, L0_attn_bq, L0_attn_Wk, L0_attn_bk, L0_attn_Wv, L0_attn_bv, L0_attn_dist_emb, L0_ffn_w_router, L0_ffn_w_up, L0_ffn_w_gate, L0_ffn_w_down, L0_ffn_ws_up, L0_ffn_ws_gate, L0_ffn_ws_down, L1_xattn_ln_m_g, L1_xattn_ln_m_b, L1_xattn_ln_l_g, L1_xattn_ln_l_b, L1_xattn_Wq, L1_xattn_Wkv, L1_xattn_Wout, L1_attn_Wq, L1_attn_Wk, L1_attn_Wv, L1_attn_Wo, L1_attn_Wbet, L1_attn_Wf, L1_attn_norm_w, L1_ffn_Wg, L1_ffn_bg, L1_ffn_W1, L1_ffn_b1, L1_ffn_W2, L1_ffn_b2, L2_xattn_Wq, L2_xattn_bq, L2_xattn_Wk, L2_xattn_bk, L2_xattn_Wv, L2_xattn_bv, L2_xattn_Wo, L2_xattn_bo, L2_attn_ln1_g, L2_attn_ln1_b, L2_attn_Wqkv, L2_attn_bqkv, L2_attn_Wo, L2_attn_bo, L2_attn_ln2_g, L2_attn_ln2_b, L2_attn_W1, L2_attn_b1, L2_attn_W2, L2_attn_b2, L2_ffn_expert_embeddings, L2_ffn_first_linear, L2_ffn_second_linear, L3_xattn_Wq, L3_xattn_bq, L3_xattn_Wk, L3_xattn_bk, L3_xattn_Wv, L3_xattn_bv, L3_xattn_Wo, L3_xattn_bo, L3_attn_W_in, L3_attn_conv_w, L3_attn_conv_b, L3_attn_W_x, L3_attn_W_dt, L3_attn_b_dt, L3_attn_A_log, L3_attn_D_param, L3_attn_W_out, L3_ffn_gate_w, L3_ffn_ws_in, L3_ffn_vs_in, L3_ffn_ws_out, L3_ffn_e_win, L3_ffn_e_vin, L3_ffn_e_wout):
    import jax
    import jax.numpy as jnp

    def _L0_xattn_ref(k, v, q, Wk, Wv, bv, Wq, bq, Wo, bo):
        import jax, jax.numpy as jnp
        import numpy as np
        D_MODEL = 256
        B, S = (4, 512)
        kp = jnp.einsum('bsd,ed->bse', k, Wk)
        vp = jnp.einsum('bsd,ed->bse', v, Wv) + bv
        qp = jnp.einsum('bsd,ed->bse', q, Wq) + bq
        scale = 1.0 / jnp.sqrt(jnp.float32(kp.shape[-1]))
        scores = jnp.einsum('bqd,bkd->bqk', qp, kp) * scale
        probs = jax.nn.softmax(scores, axis=-1)
        ctx = jnp.einsum('bqk,bkd->bqd', probs, vp)
        return jnp.einsum('bqd,ed->bqe', ctx, Wo) + bo

    def _L0_attn_ref(hidden_states, Wq, bq, Wk, bk, Wv, bv, dist_emb):
        import jax, jax.numpy as jnp
        import numpy as np
        import math
        HIDDEN = 256
        HEADS = 16
        HEAD_DIM = HIDDEN // HEADS
        MAX_POS = 512
        BATCH = 2
        SEQ = 512
        B, S, H = hidden_states.shape
        q = (hidden_states @ Wq.T + bq).reshape(B, S, HEADS, HEAD_DIM)
        k = (hidden_states @ Wk.T + bk).reshape(B, S, HEADS, HEAD_DIM)
        v = (hidden_states @ Wv.T + bv).reshape(B, S, HEADS, HEAD_DIM)
        scores = jnp.einsum('bqhd,bkhd->bhqk', q, k) / math.sqrt(HEAD_DIM)
        pos_q = jnp.arange(S)
        distance = pos_q[:, None] - pos_q[None, :]
        pos_emb = dist_emb[MAX_POS - 1 + distance]
        scores = scores + jnp.einsum('bqhd,qkd->bhqk', q, pos_emb)
        scores = scores + jnp.einsum('bkhd,qkd->bhqk', k, pos_emb)
        probs = jax.nn.softmax(scores, axis=-1)
        ctx = jnp.einsum('bhqk,bkhd->bqhd', probs, v)
        return ctx.reshape(B, S, H)

    def _L0_ffn_ref(x, w_router, w_up, w_gate, w_down, ws_up, ws_gate, ws_down):
        import jax, jax.numpy as jnp
        import numpy as np
        DIM = 256
        HID = 1024
        E = 8
        TOPK = 2
        ALPHA = 2.0
        B, T = (1, 512)
        DOWN_SCALE = 0.01
        logits = x @ w_router
        probs = jax.nn.softmax(logits.astype(jnp.float32), axis=-1).astype(logits.dtype)
        topk_vals, topk_idx = jax.lax.top_k(probs, TOPK)
        up = jnp.einsum('btd,edh->ebth', x, w_up)
        gate = jax.nn.silu(jnp.einsum('btd,edh->ebth', x, w_gate))
        exp_out = jnp.einsum('ebth,ehd->ebtd', up * gate, w_down)
        out = jnp.zeros_like(x)
        eids = jnp.arange(E - 1)
        for i in range(TOPK - 1):
            idx_i = topk_idx[..., i]
            sel = (idx_i[None, :, :] == eids[:, None, None]).astype(x.dtype)
            gathered = jnp.einsum('ebt,ebtd->btd', sel, exp_out)
            out = out + ALPHA * topk_vals[..., i:i + 1] * gathered
        shared = x @ ws_up * jax.nn.silu(x @ ws_gate) @ ws_down
        return out + shared

    def _L1_xattn_ref(x, latents, ln_m_g, ln_m_b, ln_l_g, ln_l_b, Wq, Wkv, Wout):
        import jax, jax.numpy as jnp
        import numpy as np
        EPS = 1e-05

        def layer_norm(x, g, b):
            mu = jnp.mean(x, axis=-1, keepdims=True)
            var = jnp.var(x, axis=-1, keepdims=True)
            return (x - mu) * jax.lax.rsqrt(var + EPS) * g + b
        heads, dim_head = (16, 64)
        scale = dim_head ** (-0.5)
        x = layer_norm(x, ln_m_g, ln_m_b)
        lat = layer_norm(latents, ln_l_g, ln_l_b)
        b, m, _ = lat.shape
        q = lat @ Wq
        kv_input = jnp.concatenate([x, lat], axis=1)
        kv = kv_input @ Wkv
        k, v = jnp.split(kv, 2, axis=-1)

        def split_heads(t):
            return t.reshape(t.shape[0], t.shape[1], heads, dim_head).transpose(0, 2, 1, 3)
        q, k, v = (split_heads(q), split_heads(k), split_heads(v))
        dots = jnp.einsum('bhid,bhjd->bhij', q, k) * scale
        attn = jax.nn.softmax(dots, axis=-1)
        out = jnp.einsum('bhij,bhjd->bhid', attn, v)
        out = out.transpose(0, 2, 1, 3).reshape(b, m, heads * dim_head)
        return out @ Wout

    def _L1_attn_ref(x, Wq, Wk, Wv, Wo, Wbet, Wf, norm_w):
        import jax, jax.numpy as jnp
        import numpy as np
        EPS = 1e-06
        b, n, d = x.shape
        h = Wbet.shape[1]
        hd = d // h
        q = jax.nn.silu(x @ Wq).reshape(b, n, h, hd)
        k = jax.nn.silu(x @ Wk).reshape(b, n, h, hd)
        k = k * jax.lax.rsqrt(jnp.sum(k * k, -1, keepdims=True) + 1e-12)
        v = (x @ Wv).reshape(b, n, h, hd)
        beta = 2.0 * jax.nn.sigmoid(x @ Wbet)
        a = jax.nn.sigmoid(x @ Wf)

        def step(S, inp):
            qt, kt, vt, at, bt = inp
            Sd = at[..., None, None] * S
            u = vt - jnp.einsum('bhk,bhkv->bhv', kt, Sd)
            Sn = Sd + bt[..., None, None] * kt[..., None] * u[:, :, None, :]
            o = jnp.einsum('bhk,bhkv->bhv', qt, Sn)
            return (Sn, o)
        tfirst = lambda z: jnp.moveaxis(z, 1, 0)
        S0 = jnp.zeros((b, h, hd, hd), x.dtype)
        _, o = jax.lax.scan(step, S0, (tfirst(q), tfirst(k), tfirst(v), tfirst(a), tfirst(beta)))
        o = jnp.moveaxis(o, 0, 1)
        o = o * jax.lax.rsqrt(jnp.mean(o * o, -1, keepdims=True) + EPS)
        o = o.reshape(b, n, d) * norm_w
        return o @ Wo

    def _L1_ffn_ref(x, Wg, bg, W1, b1, W2, b2):
        import jax, jax.numpy as jnp
        import numpy as np
        E = 8
        K = 2
        CF = 1.2
        D = 256
        F = 1024
        B, S = (4, 256)
        Bx, Sx, Dx = x.shape
        T = Bx * Sx
        xt = x.reshape(T, Dx)
        logits = xt @ Wg + bg
        probs = jax.nn.softmax(logits, axis=-1)
        gate_vals, exp_idx = jax.lax.top_k(probs, K)
        gate_vals = gate_vals / jnp.sum(gate_vals, axis=-1, keepdims=True)
        capacity = int(np.ceil(CF * T * K / E))
        eidx = exp_idx.T.reshape(-1)
        gv = gate_vals.T.reshape(-1)
        oh = jax.nn.one_hot(eidx, E, dtype=jnp.int32)
        pos = jnp.sum((jnp.cumsum(oh, axis=0) - oh) * oh, axis=-1)
        keep = pos < capacity
        pos_c = jnp.where(keep, pos, capacity)
        xk = jnp.tile(xt, (K, 1))
        buf = jnp.zeros((E, capacity + 1, Dx), x.dtype)
        buf = buf.at[eidx, pos_c].add(jnp.where(keep[:, None], xk, 0.0))
        buf = buf[:, :capacity]
        h = jax.nn.gelu(jnp.einsum('ecd,edf->ecf', buf, W1) + b1[:, None, :], approximate=True)
        ye = jnp.einsum('ecf,efd->ecd', h, W2) + b2[:, None, :]
        ye = jnp.concatenate([ye, jnp.zeros((E, 1, Dx), ye.dtype)], axis=1)
        gathered = ye[eidx, pos_c] * (gv * keep.astype(gv.dtype))[:, None]
        out = jnp.sum(gathered.reshape(K, T, Dx), axis=0)
        return out.reshape(Bx, Sx, Dx)

    def _L2_xattn_ref(query, key, value, Wq, bq, Wk, bk, Wv, bv, Wo, bo):
        import jax, jax.numpy as jnp
        import numpy as np
        D_MODEL = 256
        NUM_HEADS = 16
        D_HEAD = D_MODEL // NUM_HEADS
        B, LQ, LK = (4, 512, 512)
        b = query.shape[0]
        q = (query @ Wq.T + bq).reshape(b, -1, NUM_HEADS, D_HEAD)
        k = (key @ Wk.T + bk).reshape(b, -1, NUM_HEADS, D_HEAD)
        v = (value @ Wv.T + bv).reshape(b, -1, NUM_HEADS, D_HEAD)
        scale = 1.0 / np.sqrt(D_HEAD).astype(np.float32)
        attn = jnp.einsum('bqhd,bkhd->bhqk', q, k) * scale
        attn = jax.nn.softmax(attn, axis=-1)
        out = jnp.einsum('bhqk,bkhd->bqhd', attn, v).reshape(b, -1, D_MODEL)
        return out @ Wo.T + bo

    def _L2_attn_ref(x, ln1_g, ln1_b, Wqkv, bqkv, Wo, bo, ln2_g, ln2_b, W1, b1, W2, b2):
        import jax, jax.numpy as jnp
        import numpy as np
        import math
        D_MODEL = 256
        NUM_HEADS = 16
        HEAD_DIM = D_MODEL // NUM_HEADS
        LN_EPS = 1e-05

        def _layer_norm(x, g, b):
            mu = jnp.mean(x, axis=-1, keepdims=True)
            var = jnp.mean(jnp.square(x - mu), axis=-1, keepdims=True)
            return (x - mu) * jax.lax.rsqrt(var + LN_EPS) * g + b

        def _rope_tables(seq_len, dim, dtype):
            inv_freq = 1.0 / 10000.0 ** (jnp.arange(0, dim, 2, dtype=jnp.float32) / dim)
            t = jnp.arange(seq_len, dtype=jnp.float32)
            freqs = t[:, None] * inv_freq[None, :]
            emb = jnp.concatenate([freqs, freqs], axis=-1)
            return (jnp.cos(emb).astype(dtype), jnp.sin(emb).astype(dtype))

        def _rotate_half(x):
            x1, x2 = jnp.split(x, 2, axis=-1)
            return jnp.concatenate([-x2, x1], axis=-1)
        B, S, D = x.shape
        H, hd = (NUM_HEADS, HEAD_DIM)
        normed = _layer_norm(x, ln1_g, ln1_b)
        qkv = (normed @ Wqkv + bqkv).reshape(B, S, 3, H, hd)
        qkv = jnp.transpose(qkv, (2, 0, 3, 1, 4))
        q, k, v = (qkv[0], qkv[1], qkv[2])
        cos, sin = _rope_tables(S, hd, q.dtype)
        cos = cos[None, None, :, :]
        sin = sin[None, None, :, :]
        q = q * cos + _rotate_half(q) * sin
        k = k * cos + _rotate_half(k) * sin
        scores = jnp.einsum('bhqd,bhkd->bhqk', q, k) / math.sqrt(hd)
        causal = jnp.triu(jnp.ones((S, S), dtype=bool), k=1)
        scores = jnp.where(causal[None, None], -jnp.inf, scores)
        attn = jax.nn.softmax(scores, axis=-1)
        attn_out = jnp.einsum('bhqk,bhkd->bhqd', attn, v)
        attn_out = jnp.transpose(attn_out, (0, 2, 1, 3)).reshape(B, S, D)
        attn_out = attn_out @ Wo + bo
        x = x + attn_out
        h = _layer_norm(x, ln2_g, ln2_b)
        h = jax.nn.gelu(h @ W1 + b1, approximate=False) @ W2 + b2
        return x + h

    def _L2_ffn_ref(x, expert_embeddings, first_linear, second_linear):
        import jax, jax.numpy as jnp
        import numpy as np
        import math
        B, S, H = (8, 1024, 256)
        E, I, K = (8, 512, 2)
        CAP_FACTOR = 1.0

        def _router(x, expert_embeddings):
            dot = jnp.einsum('bsh,eh->bse', x, expert_embeddings)
            n = dot.shape[0] * dot.shape[1]
            dot2 = dot.reshape(n, E)
            vals, idx = jax.lax.top_k(dot2, K)
            rows = jnp.arange(n)[:, None]
            masked = jnp.full_like(dot2, -jnp.inf).at[rows, idx].set(vals)
            return jax.nn.softmax(masked, axis=-1)
        batch, seq, hidden = x.shape
        n_tokens = batch * seq
        expert_capacity = math.ceil(n_tokens / E * CAP_FACTOR)
        weights = _router(x, expert_embeddings)
        ones = (weights > 0).astype(weights.dtype)
        cap_ones = jnp.where(jnp.cumsum(ones, axis=0) <= expert_capacity, ones, 0.0)
        caw = weights * cap_ones
        vals, idx = jax.lax.top_k(caw.T, expert_capacity)
        index = idx.reshape(-1)
        x_flat = x.reshape(n_tokens, hidden)
        tokens = x_flat[index].reshape(E, expert_capacity, hidden)
        inter = jax.nn.relu(jnp.einsum('ech,eih->eci', tokens, first_linear))
        out = jnp.einsum('eci,ehi->ech', inter, second_linear)
        out = out * vals[:, :, None]
        final = jnp.zeros((n_tokens, hidden), x.dtype).at[index].add(out.reshape(-1, hidden))
        return final.reshape(x.shape)

    def _L3_xattn_ref(query_modal, key_value_modal, Wq, bq, Wk, bk, Wv, bv, Wo, bo):
        import jax, jax.numpy as jnp
        import numpy as np
        EMBED_DIM = 256
        NUM_HEADS = 16
        HEAD_DIM = EMBED_DIM // NUM_HEADS
        B, N, M = (4, 512, 512)

        def _split_heads(x):
            b, t, _ = x.shape
            return x.reshape(b, t, NUM_HEADS, HEAD_DIM).transpose(0, 2, 1, 3)
        q = _split_heads(query_modal @ Wq.T + bq)
        k = _split_heads(key_value_modal @ Wk.T + bk)
        v = _split_heads(key_value_modal @ Wv.T + bv)
        scale = HEAD_DIM ** (-0.5)
        scores = jnp.einsum('bhnd,bhmd->bhnm', q, k) * scale
        attn = jax.nn.softmax(scores, axis=-1)
        x = jnp.einsum('bhnm,bhmd->bhnd', attn, v)
        x = x.transpose(0, 2, 1, 3).reshape(query_modal.shape)
        return x @ Wo.T + bo

    def _L3_attn_ref(x, W_in, conv_w, conv_b, W_x, W_dt, b_dt, A_log, D_param, W_out):
        import jax, jax.numpy as jnp
        import numpy as np
        B_, L_, DM, DIN, N_, K_, R_ = (1, 256, 256, 512, 16, 4, 64)
        Din, K = conv_w.shape
        R = W_dt.shape[1]
        N = A_log.shape[1]
        xz = jnp.einsum('bld,ed->ble', x, W_in)
        xs, z = jnp.split(xz, 2, axis=-1)
        xt = jnp.transpose(xs, (0, 2, 1))
        xc = jax.lax.conv_general_dilated(xt, conv_w[:, None, :], (1,), [(K - 1, 0)], feature_group_count=Din)
        xc = jnp.transpose(xc, (0, 2, 1)) + conv_b
        xc = jax.nn.silu(xc)
        x_dbl = jnp.einsum('bld,ed->ble', xc, W_x)
        dt, Bm, Cm = jnp.split(x_dbl, [R, R + N], axis=-1)
        dt = jax.nn.softplus(jnp.einsum('blr,dr->bld', dt, W_dt) + b_dt)
        A = -jnp.exp(A_log)
        A_bar = jnp.exp(dt[..., None] * A)
        Bu = dt[..., None] * Bm[:, :, None, :] * xc[..., None]

        def comb(e1, e2):
            a1, b1 = e1
            a2, b2 = e2
            return (a2 * a1, a2 * b1 + b2)
        _, h_all = jax.lax.associative_scan(comb, (A_bar, Bu), axis=1)
        y = jnp.einsum('bldn,bln->bld', h_all, Cm) + D_param * xc
        y = y * jax.nn.silu(z)
        return jnp.einsum('bld,ed->ble', y, W_out)

    def _L3_ffn_ref(x, gate_w, ws_in, vs_in, ws_out, e_win, e_vin, e_wout):
        import jax, jax.numpy as jnp
        import numpy as np
        B, S, D, H, E, K = (2, 256, 256, 128, 16, 4)
        HS = 2 * H

        def silu(z):
            return z * jax.nn.sigmoid(z)
        b, s, d = x.shape
        T = b * s
        xf = x.reshape(T, d)
        g = jax.nn.sigmoid(xf @ gate_w.T)
        topv, topi = jax.lax.top_k(g, K)
        wn = topv / jnp.sum(topv, axis=-1, keepdims=True)
        combine = jnp.zeros_like(g).at[jnp.arange(T)[:, None], topi].add(wn)
        hin = jnp.einsum('td,edh->eth', xf, e_win)
        vin = jnp.einsum('td,edh->eth', xf, e_vin)
        h = silu(hin) * vin * combine.T[:, :, None]
        routed = jnp.einsum('eth,ehd->td', h, e_wout)
        shared = silu(xf @ ws_in) * (xf @ vs_in) @ ws_out
        return (shared + routed).reshape(b, s, d)
    x = x + _L0_xattn_ref(ctx_1024, ctx_1024, _layernorm(x, axis=-1), L0_xattn_Wk, L0_xattn_Wv, L0_xattn_bv, L0_xattn_Wq, L0_xattn_bq, L0_xattn_Wo, L0_xattn_bo)
    x = x + _L0_attn_ref(_layernorm(x, axis=-1), L0_attn_Wq, L0_attn_bq, L0_attn_Wk, L0_attn_bk, L0_attn_Wv, L0_attn_bv, L0_attn_dist_emb)
    x = x + _L0_ffn_ref(_layernorm(x, axis=-1), L0_ffn_w_router, L0_ffn_w_up, L0_ffn_w_gate, L0_ffn_w_down, L0_ffn_ws_up, L0_ffn_ws_gate, L0_ffn_ws_down)
    x = x + _L1_xattn_ref(ctx_1024, _layernorm(x, axis=-1), L1_xattn_ln_m_g, L1_xattn_ln_m_b, L1_xattn_ln_l_g, L1_xattn_ln_l_b, L1_xattn_Wq, L1_xattn_Wkv, L1_xattn_Wout)
    x = x + _L1_attn_ref(_layernorm(x, axis=-1), L1_attn_Wq, L1_attn_Wk, L1_attn_Wv, L1_attn_Wo, L1_attn_Wbet, L1_attn_Wf, L1_attn_norm_w)
    x = x + _L1_ffn_ref(_layernorm(x, axis=-1), L1_ffn_Wg, L1_ffn_bg, L1_ffn_W1, L1_ffn_b1, L1_ffn_W2, L1_ffn_b2)
    x = x + _L2_xattn_ref(_layernorm(x, axis=-1), ctx_1024, ctx_1024, L2_xattn_Wq, L2_xattn_bq, L2_xattn_Wk, L2_xattn_bk, L2_xattn_Wv, L2_xattn_bv, L2_xattn_Wo, L2_xattn_bo)
    x = x + _L2_attn_ref(_layernorm(x, axis=-1), L2_attn_ln1_g, L2_attn_ln1_b, L2_attn_Wqkv, L2_attn_bqkv, L2_attn_Wo, L2_attn_bo, L2_attn_ln2_g, L2_attn_ln2_b, L2_attn_W1, L2_attn_b1, L2_attn_W2, L2_attn_b2)
    x = x + _L2_ffn_ref(_layernorm(x, axis=-1), L2_ffn_expert_embeddings, L2_ffn_first_linear, L2_ffn_second_linear)
    x = x + _L3_xattn_ref(_layernorm(x, axis=-1), ctx_1024, L3_xattn_Wq, L3_xattn_bq, L3_xattn_Wk, L3_xattn_bk, L3_xattn_Wv, L3_xattn_bv, L3_xattn_Wo, L3_xattn_bo)
    x = x + _L3_attn_ref(_layernorm(x, axis=-1), L3_attn_W_in, L3_attn_conv_w, L3_attn_conv_b, L3_attn_W_x, L3_attn_W_dt, L3_attn_b_dt, L3_attn_A_log, L3_attn_D_param, L3_attn_W_out)
    x = x + _L3_ffn_ref(_layernorm(x, axis=-1), L3_ffn_gate_w, L3_ffn_ws_in, L3_ffn_vs_in, L3_ffn_ws_out, L3_ffn_e_win, L3_ffn_e_vin, L3_ffn_e_wout)
    return x

_drawn_inputs = setup_inputs


def setup_inputs(seed=0):
    import zlib

    import numpy as np

    out = dict(_drawn_inputs(seed))
    spreads = {'L0_xattn_bv': (0.0, 0.1),
     'L0_xattn_bq': (0.0, 0.1),
     'L0_xattn_bo': (0.0, 0.1),
     'L0_attn_bq': (0.0, 0.1),
     'L0_attn_bk': (0.0, 0.1),
     'L0_attn_bv': (0.0, 0.1),
     'L1_xattn_ln_m_g': (1.0, 0.2),
     'L1_xattn_ln_m_b': (0.0, 0.1),
     'L1_xattn_ln_l_g': (1.0, 0.2),
     'L1_xattn_ln_l_b': (0.0, 0.1),
     'L1_attn_norm_w': (1.0, 0.2),
     'L1_ffn_bg': (0.0, 0.1),
     'L1_ffn_b1': (0.0, 0.1),
     'L1_ffn_b2': (0.0, 0.1),
     'L2_attn_ln1_g': (1.0, 0.2),
     'L2_attn_ln1_b': (0.0, 0.1),
     'L2_attn_bqkv': (0.0, 0.1),
     'L2_attn_bo': (0.0, 0.1),
     'L2_attn_ln2_g': (1.0, 0.2),
     'L2_attn_ln2_b': (0.0, 0.1),
     'L2_attn_b1': (0.0, 0.1),
     'L2_attn_b2': (0.0, 0.1),
     'L3_xattn_bq': (0.0, 0.1),
     'L3_xattn_bk': (0.0, 0.1),
     'L3_xattn_bv': (0.0, 0.1),
     'L3_xattn_bo': (0.0, 0.1),
     'L3_attn_D_param': (1.0, 0.2)}
    factors = {}
    for name, (base, spread) in spreads.items():
        noise = np.random.default_rng([zlib.crc32(name.encode()), seed]).standard_normal(out[name].shape)
        drawn = base * np.exp(spread * noise) if base else spread * noise
        out[name] = jnp.asarray(drawn.astype(out[name].dtype))
    for name, factor in factors.items():
        out[name] = (out[name] * factor).astype(out[name].dtype)
    return out
```

```python
from contextlib import ExitStack, contextmanager

import numpy as np
import concourse.bass as bass
from concourse import mybir

ALU = mybir.AluOpType
ACT = mybir.ActivationFunctionType
F32 = mybir.dt.float32
BF16 = mybir.dt.bfloat16
U32 = mybir.dt.uint32
AX = mybir.AxisListType.X

P = 128
B = 2
S = 256
D = 256
KC = D // P
T = B * S
TT = T // P
QT = S // P
CTX = 4096
NH = 16


@contextmanager
def stage(nc, *names):
    with ExitStack() as held:
        sems = [held.enter_context(nc.semaphore(n)) for n in names]
        with nc.Block(no_gpsimd_drain=True) as block:
            yield (block, *sems)
        numbers = sorted(s.num for s in sems)
        starts = [n for n in numbers if n - 1 not in numbers]
        runs = [range(n, next(m for m in range(n, n + len(numbers) + 1) if m not in numbers)) for n in starts]
        for run in runs:
            nc.all_engine_barrier(sems_to_clear=run)


class Tensors:

    def __init__(self, nc):
        self.nc, self.held = nc, ExitStack()

    def __enter__(self):
        return self

    def __exit__(self, *said):
        return self.held.__exit__(*said)

    def sb(self, name, shape, dt=F32):
        return self.held.enter_context(self.nc.sbuf_tensor(name, shape, dt))

    def ps(self, name, shape, dt=F32):
        return self.held.enter_context(self.nc.psum_tensor(name, shape, dt))



def layer_norm(nc, k, src, dst, name, eps=1e-5):
    with Tensors(nc) as t, stage(nc, name + "_stats", name + "_var", name + "_std", name + "_rstd") as (
            block, stats_done, var_done, std_done, rstd_done):
        stats = t.sb(name + "_bn", [P, TT, 6])
        mv = t.sb(name + "_mv", [P, TT, 2])
        std = t.sb(name + "_sd", [P, TT])
        rstd = t.sb(name + "_rs", [P, TT])

        @block.vector
        def _(dve):
            for i in range(TT):
                nc.vector.bn_stats(stats[:, i, :], src[:, i, :]).then_inc(stats_done, 1)
            for i in range(TT):
                dve.wait_ge(stats_done, i + 1)
                nc.vector.bn_aggr(mv[:, i, :], stats[:, i, :]).then_inc(var_done, 1)
            dve.wait_ge(var_done, TT)
            nc.vector.tensor_scalar(std[:, :], mv[:, :, 1], eps, None, ALU.add).then_inc(var_done, 1)
            dve.wait_ge(std_done, 1)
            nc.vector.reciprocal(rstd[:, :], std[:, :]).then_inc(rstd_done, 1)
            dve.wait_ge(rstd_done, 1)
            for i in range(TT):
                nc.vector.tensor_scalar(dst[:, i, :], src[:, i, :], mv[:, i, 0:1], rstd[:, i:i + 1],
                                        ALU.subtract, ALU.mult)

        @block.scalar
        def _(act):
            act.wait_ge(var_done, TT + 1)
            nc.scalar.activation(std[:, :], std[:, :], ACT.Sqrt).then_inc(std_done, 1)


def transpose_tokens(nc, k, src, dst, name, chunks=KC, gain=None, shift=None):
    with Tensors(nc) as t, stage(nc, name + "_turned", name + "_copied") as (block, turned, copied):
        flip = t.ps(name + "_flip", [P, 2, T])
        loads = 32 * (gain is not None)
        if gain is not None:
            gb = t.sb(name + "_gb", [P, 2, chunks])

        @block.sync
        def _(sp):
            if gain is not None:
                sp.dma_start(gb[:, 0, :], gain).then_inc(copied, 16)
                sp.dma_start(gb[:, 1, :], shift).then_inc(copied, 16)

        @block.tensor
        def _(pe):
            for c in range(chunks):
                if c >= 2:
                    pe.wait_ge(copied, loads + c - 1)
                for i in range(TT):
                    m = nc.tensor.transpose(flip[:, c % 2, i * P:(i + 1) * P], src[:, i, c * P:(c + 1) * P],
                                            k.ident[:, :])
                m.then_inc(turned, 1)

        @block.scalar
        def _(act):
            if gain is not None:
                act.wait_ge(copied, loads)
            for c in range(chunks):
                act.wait_ge(turned, c + 1)
                if gain is not None:
                    nc.scalar.activation(dst[:, c, :], flip[:, c % 2, :], ACT.Identity, bias=gb[:, 1, c:c + 1],
                                         scale=gb[:, 0, c:c + 1]).then_inc(copied, 1)
                else:
                    nc.scalar.copy(dst[:, c, :], flip[:, c % 2, :]).then_inc(copied, 1)


def project_residual(nc, k, srcT, w, name, chunks=KC, bias=None, doubled=False):
    with Tensors(nc) as t, stage(nc, name + "_load", name + "_mm", name + "_sum") as (block, load, mm, summed):
        wt = t.sb(name + "_w", [P, chunks, D])
        br = t.sb(name + "_b", [P, D])
        out = t.ps(name + "_o", [P, TT, 512])

        @block.sync
        def _(sp):
            sp.dma_start(wt[:, :, :], w).then_inc(load, 16)
            if bias is not None:
                sp.dma_start(br[:, :], bias).then_inc(load, 16)

        @block.tensor
        def _(pe):
            pe.wait_ge(load, 32 if bias is not None else 16)
            for i in range(TT):
                for c in range(chunks):
                    m = nc.tensor.matmul(out[:, i, 0:D], srcT[:, c, i * P:(i + 1) * P], wt[:, c, :],
                                         start=(c == 0), stop=(c == chunks - 1))
                m.then_inc(mm, 1)

        @block.vector
        def _(dve):
            if bias is not None:
                dve.wait_ge(load, 32)
                for i in range(TT):
                    last = nc.vector.scalar_tensor_tensor(k.X[:, i, :], k.X[:, i, :], 2.0 if doubled else 1.0,
                                                          br[:, :], ALU.mult, ALU.add)
                last.then_inc(summed, 1)
                dve.wait_ge(summed, 1)
            for i in range(TT):
                dve.wait_ge(mm, i + 1)
                nc.vector.tensor_tensor(k.X[:, i, :], out[:, i, 0:D], k.X[:, i, :], ALU.add)



def context_attention_one_head(nc, k, d):
    KT = CTX // P
    STEPS = KT // 2
    SCALE = float(D) ** -0.5
    with Tensors(nc) as t:
        QK = t.sb("l0q_keys", [P, KC, T])
        OT = t.sb("l0_out", [P, KC, T])
        V = t.sb("l0_values", [P, TT, D])
        with Tensors(nc) as u, stage(nc, "l0q_load", "l0q_mm", "l0q_ev") as (block, load, mm, ev):
            wq = u.sb("l0_wq", [P, KC, D])
            wk = u.sb("l0_wk", [P, KC, D])
            bq = u.sb("l0_bq", [P, KC])
            qT = u.sb("l0_qT", [P, KC, T])
            ps = u.ps("l0_qps", [P, 2 * KC, T])

            @block.sync
            def _(sp):
                sp.dma_start(wq[:, :, :], d["L0x_wqT"]).then_inc(load, 16)
                sp.dma_start(wk[:, :, :], d["L0x_wk"]).then_inc(load, 16)
                sp.dma_start(bq[:, :], d["L0x_bq"]).then_inc(load, 16)

            @block.tensor
            def _(pe):
                pe.wait_ge(load, 48)
                for half, (w, src) in enumerate(((wq, k.NT), (wk, qT))):
                    if half:
                        pe.wait_ge(ev, KC)
                    for m in range(KC):
                        for c in range(KC):
                            i = nc.tensor.matmul(ps[:, KC * half + m, :], w[:, c, m * P:(m + 1) * P], src[:, c, :],
                                                 start=(c == 0), stop=(c == KC - 1))
                        i.then_inc(mm, 1)

            @block.scalar
            def _(act):
                act.wait_ge(load, 48)
                for m in range(KC):
                    act.wait_ge(mm, m + 1)
                    nc.scalar.activation(qT[:, m, :], ps[:, m, :], ACT.Identity, bias=bq[:, m:m + 1]).then_inc(ev, 1)
                for m in range(KC):
                    act.wait_ge(mm, KC + m + 1)
                    nc.scalar.copy(QK[:, m, :], ps[:, KC + m, :]).then_inc(ev, 1)

        with nc.Fori(0, B) as b:
            with Tensors(nc) as u, stage(nc, "l0_load", "l0_casts", "l0_peaks", "l0_peak_read", "l0_diag", "l0_scored",
                                         "l0_exps", "l0_averaged", "l0_normed") as (
                    block, load, casts, peaks, peak_read, diag, scored, exps, averaged, normed):
                NB = CTX // 512
                cT = u.sb("l0_cT", [P, KC, CTX])
                cTb = u.sb("l0_cTb", [P, KC, CTX], BF16)
                V1 = u.sb("l0_V1", [P, KT, D + 1])
                q = u.sb("l0_q", [P, KC, S])
                qb = u.sb("l0_qb", [P, KC, S], BF16)
                pk = u.sb("l0_pk", [P, QT, NB])
                mx = u.sb("l0_mx", [P, QT])
                dg = u.sb("l0_dg", [P, QT, P], BF16)
                pr = u.sb("l0_pr", [P, 2, 2, S])
                rec = u.sb("l0_rec", [P, QT])
                psm = u.ps("l0_psm", [P, 2, 512])
                pss = u.ps("l0_pss", [P, 2, 2, S])
                pso = u.ps("l0_pso", [P, QT, 512])

                @block.sync
                def _(sp):
                    sp.dma_start(cT[:, :, :], d["ctxT"][b]).then_inc(load, 16)
                    sp.dma_start(V1[:, :, 0:D], d["ctx_rows"][b]).then_inc(load, 16)

                @block.gpsimd
                def _(pool):
                    nc.gpsimd.tensor_copy(q[:, :, :], QK[:, :, bass.ds(b * S, S)]).then_inc(casts, 1)
                    nc.gpsimd.memset(V1[:, :, D:D + 1], 1.0).then_inc(casts, 1)
                    pool.wait_ge(casts, 2)
                    nc.gpsimd.tensor_copy(qb[:, :, :], q[:, :, :]).then_inc(casts, 1)

                @block.tensor
                def _(pe):
                    pe.wait_ge(casts, 3)
                    pe.wait_ge(load, 32)
                    for n in range(QT * NB):
                        qt, j = divmod(n, NB)
                        if qt == 0:
                            pe.wait_ge(exps, j + 1)
                        if n >= 2:
                            pe.wait_ge(peak_read, n - 1)
                        for c in range(KC):
                            m = nc.tensor.matmul(psm[:, n % 2, :], qb[:, c, qt * P:(qt + 1) * P],
                                                 cTb[:, c, j * 512:(j + 1) * 512], start=(c == 0), stop=(c == KC - 1))
                        m.then_inc(peaks, 1)
                    pe.wait_ge(diag, 1)
                    for s in range(STEPS + 1):
                        if s < STEPS:
                            if s >= 2:
                                pe.wait_ge(exps, NB + s - 1)
                            for qt in range(QT):
                                nc.tensor.matmul(pss[:, s % 2, :, qt * P:(qt + 1) * P], k.onesb[:, :],
                                                 dg[:, qt, :].unsqueeze(1).broadcast_to([P, 2, P]), start=(qt == 0), stop=False,
                                                 skip_group_check=True)
                            for h in range(2):
                                for c in range(KC):
                                    m = nc.tensor.matmul(pss[:, s % 2, h, :], cT[:, c, (2 * s + h) * P:(2 * s + h + 1) * P],
                                                         q[:, c, :], start=False, stop=(c == KC - 1), skip_group_check=True)
                            m.then_inc(scored, 1)
                        if s >= 1:
                            pe.wait_ge(exps, NB + s)
                            for h in range(2):
                                kt = 2 * (s - 1) + h
                                for qt in range(QT):
                                    m = nc.tensor.matmul(pso[:, qt, 0:D + 1], pr[:, (s - 1) % 2, h, qt * P:(qt + 1) * P],
                                                         V1[:, kt, :], start=(kt == 0), stop=(kt == KT - 1))
                            m.then_inc(averaged, 1)

                @block.vector
                def _(dve):
                    for n in range(QT * NB):
                        dve.wait_ge(peaks, n + 1)
                        nc.vector.reduce_max(pk[:, n // NB, n % NB:n % NB + 1], psm[:, n % 2, :], AX).then_inc(peak_read, 1)
                    dve.wait_ge(peak_read, QT * NB)
                    nc.vector.reduce_max(mx[:, :], pk[:, :, :], AX).then_inc(peak_read, 1)
                    dve.wait_ge(peak_read, QT * NB + 1)
                    for qt in range(QT):
                        m = nc.vector.tensor_scalar(dg[:, qt, :], k.ident[:, :], mx[:, qt:qt + 1], -1.0, ALU.mult, ALU.mult)
                    m.then_inc(diag, 1)
                    dve.wait_ge(averaged, STEPS)
                    nc.vector.reciprocal(rec[:, :], pso[:, :, D]).then_inc(normed, 1)
                    dve.wait_ge(normed, 1)
                    for qt in range(QT):
                        nc.vector.tensor_scalar(V[:, bass.ds(b * QT + qt, 1), :], pso[:, qt:qt + 1, 0:D], rec[:, qt:qt + 1], None,
                                                ALU.mult)

                @block.scalar
                def _(act):
                    act.wait_ge(load, 32)
                    for j in range(NB):
                        nc.scalar.copy(cTb[:, :, j * 512:(j + 1) * 512], cT[:, :, j * 512:(j + 1) * 512]).then_inc(exps, 1)
                    for s in range(STEPS):
                        act.wait_ge(scored, s + 1)
                        if s >= 2:
                            act.wait_ge(averaged, s - 1)
                        nc.scalar.activation(pr[:, s % 2, :, :], pss[:, s % 2, :, :], ACT.Exp, scale=SCALE).then_inc(exps, 1)

        transpose_tokens(nc, k, V, OT, "l0_avg")
        linear_T(nc, k, OT, QK, d["L0x_wvT"], "l0_v", bias=d["L0x_bv"])
        project_residual(nc, k, QK, d["L0x_woT"], "l0_o", bias=d["L0x_bo"])


def linear_T(nc, k, srcT, dstT, w, name, bias=None, out_chunks=KC, in_chunks=KC):
    with Tensors(nc) as t, stage(nc, name + "_load", name + "_mm", name + "_ev") as (block, load, mm, ev):
        wt = t.sb(name + "_w", [P, in_chunks, out_chunks * P])
        bt = t.sb(name + "_b", [P, out_chunks])
        ps = t.ps(name + "_ps", [P, 2, T])
        loads = 16 + 16 * (bias is not None)

        @block.sync
        def _(sp):
            sp.dma_start(wt[:, :, :], w).then_inc(load, 16)
            if bias is not None:
                sp.dma_start(bt[:, :], bias).then_inc(load, 16)

        @block.tensor
        def _(pe):
            pe.wait_ge(load, loads)
            for m in range(out_chunks):
                if m >= 2:
                    pe.wait_ge(ev, m - 1)
                for c in range(in_chunks):
                    i = nc.tensor.matmul(ps[:, m % 2, :], wt[:, c, m * P:(m + 1) * P], srcT[:, c, :],
                                         start=(c == 0), stop=(c == in_chunks - 1))
                i.then_inc(mm, 1)

        @block.scalar
        def _(act):
            act.wait_ge(load, loads)
            for m in range(out_chunks):
                act.wait_ge(mm, m + 1)
                if bias is not None:
                    nc.scalar.activation(dstT[:, m, :], ps[:, m % 2, :], ACT.Identity, bias=bt[:, m:m + 1]).then_inc(ev, 1)
                else:
                    nc.scalar.copy(dstT[:, m, :], ps[:, m % 2, :]).then_inc(ev, 1)


def layer0_cross(nc, k, d):
    layer_norm(nc, k, k.X, k.N, "n0")
    transpose_tokens(nc, k, k.N, k.NT, "t0")
    context_attention_one_head(nc, k, d)



HD16, HD64 = 16, 64


def context_attention(nc, k, d, pre, keysT, n_keys, hd, groups, out_tokens, biased):
    HPC = P // hd
    KT = n_keys // P
    SCALE = float(hd) ** -0.5
    G = 2 * P
    UH = min(HPC, 4)
    SK = 4 // UH
    STEPS = KT // SK
    UNITS = [(c, h) for c in range(KC) for h in range(0, HPC, UH)]
    NQ = [(j * 512, min(512, n_keys - j * 512)) for j in range((n_keys + 511) // 512)]
    NB = len(NQ)
    VW = hd + 1 if hd == HD16 else hd
    GH = G // hd
    VOFF = P // UH
    with nc.Fori(0, B) as b, nc.Fori(0, groups) as g, Tensors(nc) as t:
        KTf = t.sb(pre + "_KT", [P, KC, n_keys])
        KTb = t.sb(pre + "_KTb", [P, KC, n_keys], BF16)
        V = t.sb(pre + "_V", [P, KT, GH, VW])
        qz = t.sb(pre + "_qz", [P, KC, HPC, S])
        qzb = t.sb(pre + "_qzb", [P, KC, HPC, S], BF16)

        with Tensors(nc) as u, stage(nc, pre + "_wload", pre + "_kload0", pre + "_kload1", pre + "_k_mm", pre + "_k_ev", pre + "_k_cast", pre + "_v_mm",
                                     pre + "_v_ev", pre + "_q_mm", pre + "_q_ev", pre + "_ones") as (
                block, wload, kload0, kload1, k_mm, k_ev, k_cast, v_mm, v_ev, q_mm, q_ev, ones_set):
            src = u.sb(pre + "_src", [P, 2, KC, 512])
            w = u.sb(pre + "_w3", [P, 3, KC, G])
            bias = u.sb(pre + "_b2", [P, 2, KC])
            mask = u.sb(pre + "_mask", [P, HPC])
            nt = u.sb(pre + "_nt", [P, KC, S])
            kps = u.ps(pre + "_kps", [P, 3, 512])
            vps = u.ps(pre + "_vps", [P, 3, 512])
            qps = u.ps(pre + "_qps", [P, KC, 512])
            NV = KT // 2

            @block.sync
            def _(sp):
                sp.dma_start(w[:, :, :, :], d[pre + "_w3"][g]).then_inc(wload, 16)
                sp.dma_start(mask[:, :], d["mask%d" % hd]).then_inc(wload, 16)
                sp.dma_start(bias[:, :, :], d[pre + "_b2"][g]).then_inc(wload, 16)
                for j, (o, n) in enumerate(NQ):
                    if j >= 2:
                        sp.wait_ge(k_mm, KC * (j - 1))
                        sp.wait_ge(v_mm, 2 * (j - 1))
                    sp.dma_start(src[:, j % 2, :, 0:n], keysT[b][:, :, o:o + n]).then_inc((kload0, kload1)[j % 2], 16)

            @block.gpsimd
            def _(pool):
                nc.gpsimd.tensor_copy(nt[:, :, :], k.NTq[:, :, bass.ds(b * S, S)]).then_inc(ones_set, 1)
                if VW > hd:
                    nc.gpsimd.memset(V[:, :, :, hd:hd + 1], 1.0).then_inc(ones_set, 1)

                for j, (o, n) in enumerate(NQ):
                    for m in range(KC):
                        pool.wait_ge(k_ev, KC * j + m + 1)
                        nc.gpsimd.tensor_copy(KTb[:, m, o:o + n], KTf[:, m, o:o + n]).then_inc(k_cast, 1)

            @block.tensor
            def _(pe):
                pe.wait_ge(wload, 48)
                pe.wait_ge(ones_set, 1)
                for m in range(KC):
                    for c in range(KC):
                        i = nc.tensor.matmul(qps[:, m, 0:S], w[:, 0, c, m * P:(m + 1) * P], nt[:, c, :],
                                             start=(c == 0), stop=(c == KC - 1))
                    i.then_inc(q_mm, 1)
                kn = vn = 0
                for j, (o, n) in enumerate(NQ):
                    pe.wait_ge((kload0, kload1)[j % 2], 16 * (j // 2 + 1))
                    for m in range(KC):
                        if kn >= 3:
                            pe.wait_ge(k_ev, kn - 2)
                        for c in range(KC):
                            i = nc.tensor.matmul(kps[:, kn % 3, 0:n], w[:, 1, c, m * P:(m + 1) * P], src[:, j % 2, c, 0:n],
                                                 start=(c == 0), stop=(c == KC - 1))
                        i.then_inc(k_mm, 1)
                        kn += 1
                    for r in range(n // G):
                        if vn >= 3:
                            pe.wait_ge(v_ev, vn - 2)
                        for h in range(2):
                            for c in range(KC):
                                i = nc.tensor.matmul(vps[:, vn % 3, h * G:(h + 1) * G],
                                                     src[:, j % 2, c, (2 * r + h) * P:(2 * r + h + 1) * P], w[:, 2, c, :],
                                                     start=(c == 0), stop=(c == KC - 1))
                        i.then_inc(v_mm, 1)
                        vn += 1

            @block.scalar
            def _(act):
                act.wait_ge(wload, 48)
                kn = 0
                for j, (o, n) in enumerate(NQ):
                    for m in range(KC):
                        act.wait_ge(k_mm, kn + 1)
                        nc.scalar.activation(KTf[:, m, o:o + n], kps[:, kn % 3, 0:n], ACT.Identity,
                                             bias=bias[:, 1, m:m + 1]).then_inc(k_ev, 1)
                        kn += 1

            @block.vector
            def _(dve):
                dve.wait_ge(wload, 48)
                for m in range(KC):
                    dve.wait_ge(q_mm, m + 1)
                    for h in range(HPC):
                        nc.vector.tensor_scalar(qz[:, m, h, :], qps[:, m, 0:S], bias[:, 0, m:m + 1], mask[:, h:h + 1],
                                                ALU.add, ALU.mult).then_inc(q_ev, 1)
                dve.wait_ge(q_ev, KC * HPC)
                nc.vector.tensor_copy(qzb[:, :, :, :], qz[:, :, :, :])
                for r in range(NV):
                    dve.wait_ge(v_mm, r + 1)
                    nc.vector.tensor_copy(V[:, 2 * r:2 * r + 2, :, 0:hd],
                                          vps[:, r % 3, :].rearrange("p (t h e) -> p t h e", t=2, h=GH)).then_inc(v_ev, 1)

        with Tensors(nc) as u, stage(nc, pre + "_peaks", pre + "_peak_read", pre + "_diag", pre + "_scored", pre + "_exps",
                                     pre + "_averaged", pre + "_summed", pre + "_total", pre + "_o_copied", pre + "_turned", pre + "_normed",
                                     pre + "_chain", pre + "_bload") as (
                block, peaks, peak_read, diag, scored, exps, averaged, summed, total, o_copied, turned, normed, chain, bload):
            RING = 3
            pk = u.sb(pre + "_pk", [P, 2, UH * QT, NB])
            mx = u.sb(pre + "_mx", [P, 2, UH * QT])
            dg = u.sb(pre + "_dg", [P, 2, QT, UH, P], BF16)
            pr = u.sb(pre + "_pr", [P, RING, SK, UH, S])
            oc = u.sb(pre + "_oc", [P, 2, S])
            rec = u.sb(pre + "_rec", [P, QT, UH])
            tv = u.sb(pre + "_tv", [P, QT, UH, hd])
            bv = u.sb(pre + "_bv", [P, G])
            psm = u.ps(pre + "_psm", [P, 2, 512])
            pss = u.ps(pre + "_pss", [P, 2, 2, 512])
            pso = u.ps(pre + "_pso", [P, 1, 512])
            pst = u.ps(pre + "_pst", [P, 512])
            sums = hd != HD16
            if sums:
                acc = u.sb(pre + "_acc", [P, 2, SK, UH, S])
                psd = pst[:, 2 * P:2 * P + UH * QT]
            NP = UH * QT * NB
            PER = -(-NP // STEPS)

            @block.sync
            def _(sp):
                sp.dma_start(bv[:, :], d[pre + "_bv"][g]).then_inc(bload, 16)

            @block.tensor
            def _(pe):
                def peak_products(n, first, last):
                    c, h0 = UNITS[n]
                    for i in range(first, min(last, NP)):
                        hq, j = divmod(i, NB)
                        h, qt = divmod(hq, QT)
                        o, w_ = NQ[j]
                        if n * NP + i >= 2:
                            pe.wait_ge(peak_read, n * NP + i - 1)
                        nc.tensor.matmul(psm[:, i % 2, 0:w_], qzb[:, c, h0 + h, qt * P:(qt + 1) * P], KTb[:, c, o:o + w_],
                                         start=True, stop=True).then_inc(peaks, 1)

                def average(n, s):
                    c, h0 = UNITS[n]
                    pe.wait_ge(exps, n * STEPS + s + 1)
                    if s == 0 and n >= 1:
                        pe.wait_ge(o_copied, n)
                    for e in range(SK):
                        for h in range(UH):
                            kt = s * SK + e
                            m = nc.tensor.matmul(pso[VOFF * h:VOFF * h + VW, 0, 0:S], V[:, kt, c * HPC + h0 + h, :],
                                                 pr[:, (n * STEPS + s) % RING, e, h, :], start=(kt == 0), stop=(kt == KT - 1),
                                                 skip_group_check=True)
                    m.then_inc(averaged, 1)

                def finish(n):
                    if sums:
                        pe.wait_ge(total, n + 1)
                    pe.wait_ge(o_copied, n + 1)
                    if n >= 1:
                        pe.wait_ge(normed, n)
                    if sums:
                        for h in range(UH):
                            for qt in range(QT):
                                for e in range(SK):
                                    nc.tensor.matmul(psd[:, qt * UH + h:qt * UH + h + 1], acc[:, n % 2, e, h, qt * P:(qt + 1) * P],
                                                     k.ones[:, 0:1], start=(e == 0), stop=(e == SK - 1), skip_group_check=True)
                    for qt in range(QT):
                        m = nc.tensor.transpose(pst[:, qt * P:(qt + 1) * P], oc[:, n % 2, qt * P:(qt + 1) * P], k.ident[:, :])
                    m.then_inc(turned, 1)

                peak_products(0, 0, NP)
                for n, (c, h0) in enumerate(UNITS):
                    for s in range(STEPS):
                        a = n * STEPS + s
                        if s == 0:
                            pe.wait_ge(diag, n + 1)
                        if a >= 2:
                            pe.wait_ge(exps, a - 1)
                        for x in range(2):
                            e, h1 = (0, 2 * x) if UH == 4 else (x, 0)
                            bank = pss[:, a % 2, x, :].rearrange("p (h q) -> p h q", h=2)
                            for qt in range(QT):
                                nc.tensor.matmul(bank[:, :, qt * P:(qt + 1) * P], k.onesb[:, :], dg[:, n % 2, qt, h1:h1 + 2, :],
                                                 start=(qt == 0), stop=False, skip_group_check=True)
                            kt = s * SK + e
                            m = nc.tensor.matmul(bank, KTf[:, c, kt * P:(kt + 1) * P], qz[:, c, h0 + h1:h0 + h1 + 2, :],
                                                 start=False, stop=True, skip_group_check=True)
                        m.then_inc(scored, 1)
                        if s >= 1:
                            average(n, s - 1)
                        elif n >= 1:
                            average(n - 1, STEPS - 1)
                        if n + 1 < len(UNITS):
                            peak_products(n + 1, s * PER, (s + 1) * PER)
                        if s == 2 and n >= 1:
                            finish(n - 1)
                average(len(UNITS) - 1, STEPS - 1)
                finish(len(UNITS) - 1)

            @block.scalar
            def _(act):
                for n in range(len(UNITS)):
                    for s in range(STEPS):
                        a = n * STEPS + s
                        act.wait_ge(scored, a + 1)
                        if a >= RING:
                            act.wait_ge(averaged, a - RING + 1)
                            if sums:
                                act.wait_ge(summed, a - RING + 1)
                        nc.scalar.activation(pr[:, a % RING, :, :, :].rearrange("p e h q -> p (e h q)"),
                                             pss[:, a % 2, :, :].rearrange("p x q -> p (x q)"), ACT.Exp, scale=SCALE).then_inc(exps, 1)

            if sums:
                @block.gpsimd
                def _(pool):
                    for n in range(len(UNITS)):
                        for s in range(STEPS):
                            a = n * STEPS + s
                            if n >= 2 and s == 0:
                                pool.wait_ge(turned, n - 1)
                            pool.wait_ge(exps, a + 1)
                            if s:
                                pool.wait_ge(summed, a)
                                m = nc.gpsimd.tensor_tensor(acc[:, n % 2, :, :, :], acc[:, n % 2, :, :, :], pr[:, a % RING, :, :, :], ALU.add)
                            else:
                                m = nc.gpsimd.tensor_copy(acc[:, n % 2, :, :, :], pr[:, a % RING, :, :, :])
                            m.then_inc(summed, 1)
                        pool.wait_ge(summed, (n + 1) * STEPS)
                        nc.gpsimd.tensor_copy(acc[:, n % 2, 0:1, 0, 0:1], acc[:, n % 2, 0:1, 0, 0:1]).then_inc(total, 1)

            @block.vector
            def _(dve):
                links = [0]

                def link(i):
                    links[0] += 1
                    i.then_inc(chain, 1)
                    dve.wait_ge(chain, links[0])

                def read_peaks(n, first, last):
                    for i in range(first, min(last, NP)):
                        hq, j = divmod(i, NB)
                        dve.wait_ge(peaks, n * NP + i + 1)
                        m = nc.vector.reduce_max(pk[:, n % 2, hq, j:j + 1], psm[:, i % 2, 0:NQ[j][1]], AX)
                        m.then_inc(peak_read, 1)
                    if first < NP <= last:
                        dve.wait_ge(peak_read, (n + 1) * NP)
                        link(nc.vector.reduce_max(mx[:, n % 2, :], pk[:, n % 2, :, :], AX))
                        if n >= 2:
                            dve.wait_ge(scored, (n - 1) * STEPS)
                        for hq in range(UH * QT):
                            m = nc.vector.tensor_scalar(dg[:, n % 2, hq % QT, hq // QT, :], k.ident[:, :], mx[:, n % 2, hq:hq + 1], -1.0,
                                                        ALU.mult, ALU.mult)
                        m.then_inc(diag, 1)

                def copy_out(n):
                    dve.wait_ge(averaged, (n + 1) * STEPS)
                    if n >= 2:
                        dve.wait_ge(turned, n - 1)
                    for h in range(UH):
                        m = nc.vector.tensor_copy(oc[VOFF * h:VOFF * h + VW, n % 2, :], pso[VOFF * h:VOFF * h + VW, 0, 0:S])
                    m.then_inc(o_copied, 1)

                def normalize(n):
                    c, h0 = UNITS[n]
                    dve.wait_ge(turned, n + 1)
                    tiles = pst[:, 0:2 * P].rearrange("p (t h e) -> p t h e", t=QT, h=UH)
                    if sums:
                        link(nc.vector.reciprocal(rec[:, :, :], psd.rearrange("p (t h) -> p t h", t=QT)))
                    else:
                        link(nc.vector.reciprocal(rec[:, :, :], tiles[:, :, :, hd]))
                    m = nc.vector.tensor_tensor(tv[:, :, :, :], tiles[:, :, :, 0:hd],
                                                rec[:, :, :].unsqueeze(3).broadcast_to([P, QT, UH, hd]), ALU.mult)
                    m.then_inc(normed, 1)
                    dve.wait_ge(normed, n + 1)
                    f = c * P + h0 * hd
                    for qt in range(QT):
                        if biased:
                            i = nc.vector.tensor_tensor(out_tokens[:, bass.ds(b * QT + qt, 1), bass.ds(g * G + f, UH * hd)],
                                                        tv[:, qt:qt + 1, :, :].rearrange("p t h e -> p t (h e)"),
                                                        bv[:, f:f + UH * hd].unsqueeze(1), ALU.add)
                        else:
                            i = nc.vector.tensor_copy(out_tokens[:, bass.ds(b * QT + qt, 1), bass.ds(g * G + f, UH * hd)],
                                                      tv[:, qt:qt + 1, :, :].rearrange("p t h e -> p t (h e)"))
                    link(i)

                if VW < VOFF:
                    for x in range(2):
                        link(nc.vector.memset(oc[:, x, :], 0.0))
                dve.wait_ge(bload, 16)
                read_peaks(0, 0, NP)
                for n in range(len(UNITS)):
                    for s in range(STEPS):
                        if s == 1 and n >= 1:
                            copy_out(n - 1)
                        if n + 1 < len(UNITS):
                            read_peaks(n + 1, s * PER, (s + 1) * PER)
                        if s == 3 and n >= 1:
                            normalize(n - 1)
                copy_out(len(UNITS) - 1)
                normalize(len(UNITS) - 1)


def layer2_cross(nc, k, d):
    cross16(nc, k, d, "L2x")


def layer3_cross(nc, k, d):
    cross16(nc, k, d, "L3x")


def cross16(nc, k, d, pre):
    layer_norm(nc, k, k.X, k.N, pre + "n")
    transpose_tokens(nc, k, k.N, k.NT, pre + "t")
    k.NTq = k.NT
    with Tensors(nc) as t:
        O = t.sb(pre + "_O", [P, TT, D])
        OT = t.sb(pre + "_OT", [P, KC, T])
        context_attention(nc, k, d, pre, d["ctxT"], CTX, HD16, 1, O, True)
        transpose_tokens(nc, k, O, OT, pre + "o")
        project_residual(nc, k, OT, d[pre + "_woT"], pre + "p", bias=d[pre + "_bo"])


def cross_layouts(a, i, rows, cols, spread):
    for hd in (HD16, HD64):
        m = np.zeros((P, P // hd), np.float32)
        for h in range(P // hd):
            m[h * hd:(h + 1) * hd, h] = 1
        a["mask%d" % hd] = m
    for n, pre in (("L2_xattn_", "L2x"), ("L3_xattn_", "L3x")):
        a[pre + "_w3"] = np.stack([rows(i[n + w].T) for w in ("Wq", "Wk", "Wv")], 1)[None]
        a[pre + "_b2"] = np.stack([cols(i[n + w]) for w in ("bq", "bk")], 1)[None]
        a[pre + "_bv"] = spread(i[n + "bv"])[None]
        a[pre + "_woT"], a[pre + "_bo"] = rows(i[n + "Wo"].T), spread(i[n + "bo"])



def normed_context(nc, k, d, pre, dst, latents):
    R = 8
    with nc.Fori(0, B) as b, nc.Fori(0, CTX // (R * P)) as r:
        with Tensors(nc) as t, stage(nc, pre + "_load", pre + "_stat", pre + "_var", pre + "_std", pre + "_rstd", pre + "_norm", pre + "_turned",
                                     pre + "_copied", pre + "_stored") as (
                block, load, stat, var, std_done, rstd_done, norm, turned, copied, stored):
            x = t.sb(pre + "_x", [P, R, D])
            gb = t.sb(pre + "_gb", [P, 2, KC])
            st = t.sb(pre + "_st", [P, R, 6])
            mv = t.sb(pre + "_mv", [P, R, 2])
            sd = t.sb(pre + "_sd", [P, R])
            xT = t.sb(pre + "_xT", [P, KC, R * P])
            ps = t.ps(pre + "_ps", [P, 4, 512])

            @block.sync
            def _(sp):
                sp.dma_start(x[:, :, :], d["ctx_rows"][b][:, bass.ds(r * R, R), :]).then_inc(load, 16)
                sp.dma_start(gb[:, 0, :], d[pre + "_mg"]).then_inc(load, 16)
                sp.dma_start(gb[:, 1, :], d[pre + "_mb"]).then_inc(load, 16)
                sp.wait_ge(copied, R // 2)
                sp.dma_start(dst[b][:, :, bass.ds(r * R * P, R * P)], xT[:, :, :]).then_inc(stored, 16)
                sp.wait_ge(stored, 16)

            @block.vector
            def _(dve):
                dve.wait_ge(load, 48)
                for i in range(R):
                    nc.vector.bn_stats(st[:, i, :], x[:, i, :]).then_inc(stat, 1)
                for i in range(R):
                    dve.wait_ge(stat, i + 1)
                    nc.vector.bn_aggr(mv[:, i, :], st[:, i, :]).then_inc(var, 1)
                dve.wait_ge(var, R)
                nc.vector.tensor_scalar(sd[:, :], mv[:, :, 1], 1e-5, None, ALU.add).then_inc(var, 1)
                dve.wait_ge(std_done, 1)
                nc.vector.reciprocal(sd[:, :], sd[:, :]).then_inc(rstd_done, 1)
                dve.wait_ge(rstd_done, 1)
                for i in range(R):
                    nc.vector.tensor_scalar(x[:, i, :], x[:, i, :], mv[:, i, 0:1], sd[:, i:i + 1],
                                            ALU.subtract, ALU.mult).then_inc(norm, 1)

            @block.tensor
            def _(pe):
                for i in range(0, R, 2):
                    pe.wait_ge(norm, i + 2)
                    for c in range(KC):
                        for e in range(2):
                            m = nc.tensor.transpose(ps[:, i // 2, (c * 2 + e) * P:(c * 2 + e + 1) * P], x[:, i + e, c * P:(c + 1) * P],
                                                    k.ident[:, :])
                    m.then_inc(turned, 1)

            @block.scalar
            def _(act):
                act.wait_ge(var, R + 1)
                nc.scalar.activation(sd[:, :], sd[:, :], ACT.Sqrt).then_inc(std_done, 1)
                act.wait_ge(load, 48)
                for i in range(R // 2):
                    act.wait_ge(turned, i + 1)
                    for c in range(KC):
                        m = nc.scalar.activation(xT[:, c, i * 2 * P:(i + 1) * 2 * P], ps[:, i, c * 2 * P:(c + 1) * 2 * P],
                                                 ACT.Identity, bias=gb[:, 1, c:c + 1], scale=gb[:, 0, c:c + 1])
                    m.then_inc(copied, 1)
    with stage(nc, pre + "_lat_stored", pre + "_lat_unused") as (block, stored, _unused):
        @block.sync
        def _(sp):
            for b in range(B):
                sp.dma_start(dst[b][:, :, CTX:CTX + S], latents[:, :, b * S:(b + 1) * S]).then_inc(stored, 16)
            sp.wait_ge(stored, 16 * B)


def layer1_cross(nc, k, d):
    layer_norm(nc, k, k.X, k.N, "L1na")
    layer_norm(nc, k, k.N, k.N, "L1nb")
    transpose_tokens(nc, k, k.N, k.NT, "L1t", gain=d["L1x_lg"], shift=d["L1x_lb"])
    k.NTq = k.NT
    keysT = nc.dram_tensor("normed_context", (B, P, KC, CTX + S), F32, kind="Internal").ap()
    normed_context(nc, k, d, "L1c", keysT, k.NT)
    with Tensors(nc) as t:
        O = t.sb("L1x_O", [P, TT, NH * HD64])
        context_attention(nc, k, d, "L1x", keysT, CTX + S, HD64, 4, O, False)
        OT = t.sb("L1x_OT", [P, NH * HD64 // P, T])
        transpose_tokens(nc, k, O, OT, "L1o", chunks=NH * HD64 // P)
        project_residual(nc, k, OT, d["L1x_wo"], "L1p", chunks=NH * HD64 // P)


def cross64_layouts(a, i, rows, cols, spread):
    n = "L1_xattn_"
    a["L1c_mg"], a["L1c_mb"] = cols(i[n + "ln_m_g"]), cols(i[n + "ln_m_b"])
    a["L1x_lg"], a["L1x_lb"] = cols(i[n + "ln_l_g"]), cols(i[n + "ln_l_b"])
    inner = NH * HD64
    ws = (i[n + "Wq"], i[n + "Wkv"][:, :inner], i[n + "Wkv"][:, inner:])
    a["L1x_w3"] = np.stack([np.stack([rows(w[:, g * D:(g + 1) * D]) for w in ws], 1) for g in range(4)])
    a["L1x_b2"] = np.zeros((4, P, 2, KC), np.float32)
    a["L1x_bv"] = np.zeros((4, P, D), np.float32)
    a["L1x_wo"] = rows(i[n + "Wout"])



def experts(nc, k, pieces, name, n_experts, chunks, body, kind, weights, b1=None):
    gated = kind == "swiglu"
    NIN = 2 if gated else 1
    PW = 2 * (NIN * KC * P + D)
    PIECES = body * chunks // 2
    STEPS = body * chunks
    NR = 2
    with nc.Fori(0, n_experts // body) as it, Tensors(nc) as t:
        with stage(nc, *[name + f"_load{i}" for i in range(PIECES)], name + "_w", name + "_in", name + "_act", name + "_hid",
                   name + "_out", name + "_added") as (block, *sems):
            loads, (w_here, in_done, act_done, hid_done, out_done, added) = sems[:PIECES], sems[PIECES:]
            wt = t.sb(name + "_wt", [P, PIECES, PW])
            wi = t.sb(name + "_wi", [P, TT, body])
            g_act = t.sb(name + "_g", [P, 2, T])
            hT = t.sb(name + "_h", [P, 3, T])
            if b1 is not None:
                bt = t.sb(name + "_b1", [P, STEPS])
            pin = t.ps(name + "_pin", [P, NR, NIN, T])
            pout = t.ps(name + "_pout", [P, TT, 512])

            def w_in(s, part, c):
                p, half = divmod(s, 2)
                o = (part * KC + c) * 2 * P + half * P
                return wt[:, p, o:o + P]

            def w_out(s):
                p, half = divmod(s, 2)
                o = NIN * KC * 2 * P + half * D
                return wt[:, p, o:o + D]

            @block.sync
            def _(sp):
                if b1 is not None:
                    sp.dma_start(bt[:, :], b1[it]).then_inc(w_here, 16)
                for p in range(PIECES):
                    sp.dma_start(wt[:, p, :], pieces[it * PIECES + p]).then_inc(loads[p], 16)

            @block.gpsimd
            def _(pool):
                nc.gpsimd.tensor_copy(wi[:, :, :], weights[:, :, bass.ds(it * body, body)]).then_inc(w_here, 1)

            @block.tensor
            def _(pe):
                for s in range(STEPS + 1):
                    if s < STEPS:
                        if s % 2 == 0:
                            pe.wait_ge(loads[s // 2], 16)
                        if s >= NR:
                            pe.wait_ge(hid_done, s - NR + 1)
                        for part in range(NIN):
                            for c in range(KC):
                                m = nc.tensor.matmul(pin[:, s % NR, part, :], w_in(s, part, c), k.NT[:, c, :],
                                                     start=(c == 0), stop=(c == KC - 1))
                        m.then_inc(in_done, 1)
                    if s >= 1:
                        r = s - 1
                        pe.wait_ge(hid_done, r + 1)
                        e, j = divmod(r, chunks)
                        for i in range(TT):
                            if j == 0 and e >= 1:
                                pe.wait_ge(added, TT * (e - 1) + i + 1)
                            m = nc.tensor.matmul(pout[:, i, 0:D], hT[:, r % 3, i * P:(i + 1) * P], w_out(r),
                                                 start=(j == 0), stop=(j == chunks - 1))
                            m.then_inc(out_done, 1)

            @block.scalar
            def _(act):
                if b1 is not None:
                    act.wait_ge(w_here, 17)
                for s in range(STEPS):
                    act.wait_ge(in_done, s + 1)
                    if gated:
                        if s >= 2:
                            act.wait_ge(hid_done, s - 1)
                        nc.scalar.activation(g_act[:, s % 2, :], pin[:, s % NR, 1, :], ACT.Silu).then_inc(act_done, 1)
                    else:
                        if s >= 3:
                            act.wait_ge(out_done, TT * (s - 2))
                        if kind == "gelu":
                            nc.scalar.activation(hT[:, s % 3, :], pin[:, s % NR, 0, :], ACT.Gelu_apprx_tanh,
                                                 bias=bt[:, s:s + 1]).then_inc(hid_done, 1)
                        elif kind == "gelu_erf":
                            nc.scalar.activation(hT[:, s % 3, :], pin[:, s % NR, 0, :], ACT.Gelu,
                                                 bias=bt[:, s:s + 1]).then_inc(hid_done, 1)
                        else:
                            nc.scalar.activation(hT[:, s % 3, :], pin[:, s % NR, 0, :], ACT.Relu).then_inc(hid_done, 1)

            @block.vector
            def _(dve):
                dve.wait_ge(w_here, 17 if b1 is not None else 1)

                def add_expert(e):
                    for i in range(TT):
                        dve.wait_ge(out_done, TT * chunks * e + TT * (chunks - 1) + i + 1)
                        nc.vector.scalar_tensor_tensor(k.X[:, i, :], pout[:, i, 0:D], wi[:, i, e:e + 1], k.X[:, i, :],
                                                       ALU.mult, ALU.add).then_inc(added, 1)

                done = 0
                for s in range(STEPS):
                    if gated:
                        dve.wait_ge(act_done, s + 1)
                        if s >= 3:
                            dve.wait_ge(out_done, TT * (s - 2))
                        nc.vector.tensor_tensor(hT[:, s % 3, :], pin[:, s % NR, 0, :], g_act[:, s % 2, :], ALU.mult).then_inc(hid_done, 1)
                    if s >= 1 and s % chunks == 0:
                        if done:
                            dve.wait_ge(added, TT * done)
                        add_expert(done)
                        done += 1
                if done:
                    dve.wait_ge(added, TT * done)
                add_expert(done)


def route(nc, k, d, name, E, kind, W, capacity=0):
    K2 = kind in ("capacity_slots", "capacity_tokens")
    with Tensors(nc) as t, stage(nc, name + "_load", name + "_mm", name + "_chain", name + "_act", name + "_shifted", name + "_choices") as (
            block, load, mm, chain, act_done, shifted, choices):
        wr = t.sb(name + "_wr", [P, KC, E])
        tri = t.sb(name + "_tri", [P, P])
        bg = t.sb(name + "_bg", [P, E])
        lg = t.sb(name + "_lg", [P, TT, E])
        ex = t.sb(name + "_ex", [P, TT, E])
        m8 = t.sb(name + "_m8", [P, TT, 8])
        i8 = t.sb(name + "_i8", [P, TT, 8], U32)
        f8 = t.sb(name + "_f8", [P, TT, 8])
        sm = t.sb(name + "_sm", [P, TT])
        g1 = t.sb(name + "_g1", [P, TT, 2])
        oh = t.sb(name + "_oh", [P, TT, 4, E])
        kp = t.sb(name + "_kp", [P, TT, 2, E])
        ps = t.ps(name + "_ps", [P, TT, E])
        pc = t.ps(name + "_pc", [P, TT, 512])
        CW = 2 * E if kind == "capacity_slots" else E

        @block.sync
        def _(sp):
            sp.dma_start(wr[:, :, :], d[name + "_wr"]).then_inc(load, 16)
            if K2:
                sp.dma_start(tri[:, :], d["tri_below" if kind == "capacity_slots" else "tri_upto"]).then_inc(load, 16)
            if kind == "capacity_slots":
                sp.dma_start(bg[:, :], d[name + "_bg"]).then_inc(load, 16)

        LOADS = 16 * (1 + K2 + (kind == "capacity_slots"))

        @block.tensor
        def _(pe):
            pe.wait_ge(load, LOADS)
            for i in range(TT):
                for c in range(KC):
                    m = nc.tensor.matmul(ps[:, i, :], k.NT[:, c, i * P:(i + 1) * P], wr[:, c, :], start=(c == 0), stop=(c == KC - 1))
            m.then_inc(mm, 1)
            if K2:
                pe.wait_ge(choices, 1)

                def chosen(j):
                    slots = oh[:, j, 0:2, :] if kind == "capacity_slots" else oh[:, j, 2:3, :]
                    return slots.rearrange("p a e -> p (a e)")

                for i in range(TT):
                    terms = [(pc[:, i, 0:CW], tri, chosen(i))] + [(pc[:, i, 0:CW], k.ones, chosen(j)) for j in range(i)]
                    if kind == "capacity_slots":
                        terms += [(pc[:, i, E:2 * E], k.ones, oh[:, j, 0, :]) for j in range(TT)]
                    for n, (o, left, right) in enumerate(terms):
                        m = nc.tensor.matmul(o, left[:, :], right, start=(n == 0), stop=(n == len(terms) - 1), skip_group_check=True)
                m.then_inc(mm, 1)

        @block.scalar
        def _(act):
            if kind == "sigmoid_top4":
                act.wait_ge(mm, 1)
                nc.scalar.activation(lg[:, :, :], ps[:, :, :], ACT.Sigmoid).then_inc(act_done, 1)
            else:
                act.wait_ge(shifted, 1)
                nc.scalar.activation(ex[:, :, :], ex[:, :, :], ACT.Exp).then_inc(act_done, 1)

        @block.vector
        def _(dve):
            links = [0]

            def link(i):
                links[0] += 1
                i.then_inc(chain, 1)
                dve.wait_ge(chain, links[0])

            def one_hot(slot, i, j):
                return nc.vector.tensor_scalar(oh[:, i, slot, :], k.iota[:, 0:E], f8[:, i, j:j + 1], None, ALU.is_equal)

            dve.wait_ge(load, LOADS)
            dve.wait_ge(mm, 1)
            if kind == "sigmoid_top4":
                dve.wait_ge(act_done, 1)
            elif kind == "capacity_slots":
                link(nc.vector.tensor_tensor(lg[:, :, :], ps[:, :, :], bg[:, :].unsqueeze(1).broadcast_to([P, TT, E]), ALU.add))
            else:
                link(nc.vector.tensor_copy(lg[:, :, :], ps[:, :, :]))
            for i in range(TT):
                m = nc.vector.max(m8[:, i, :], lg[:, i, :])
            link(m)
            for i in range(TT):
                m = nc.vector.max_index(i8[:, i, :], m8[:, i, :], lg[:, i, :])
            link(m)
            link(nc.vector.tensor_copy(f8[:, :, :], i8[:, :, :]))
            if kind == "top1":
                for i in range(TT):
                    nc.vector.tensor_scalar(ex[:, i, :], lg[:, i, :], m8[:, i, 0:1], None, ALU.subtract)
                    m = one_hot(0, i, 0)
                m.then_inc(shifted, 1)
                dve.wait_ge(act_done, 1)
                link(nc.vector.reduce_sum(sm[:, :], ex[:, :, :], AX))
                link(nc.vector.reciprocal(sm[:, :], sm[:, :]))
                link(nc.vector.tensor_scalar(sm[:, :], sm[:, :], 2.0, None, ALU.mult))
                for i in range(TT):
                    m = nc.vector.tensor_scalar(W[:, i, 0:E], oh[:, i, 0, :], sm[:, i:i + 1], None, ALU.mult)
                link(m)
                nc.vector.memset(W[:, :, E - 1:E], 1.0)
            elif kind == "sigmoid_top4":
                link(nc.vector.reduce_sum(sm[:, :], m8[:, :, 0:4], AX))
                link(nc.vector.reciprocal(sm[:, :], sm[:, :]))
                for i in range(TT):
                    for j in range(4):
                        m = one_hot(j, i, j)
                link(m)
                link(nc.vector.tensor_tensor(kp[:, :, :, :], oh[:, :, 0:2, :], oh[:, :, 2:4, :], ALU.add))
                link(nc.vector.tensor_tensor(ex[:, :, :], kp[:, :, 0, :], kp[:, :, 1, :], ALU.add))
                for i in range(TT):
                    m = nc.vector.scalar_tensor_tensor(W[:, i, 0:E], lg[:, i, :], sm[:, i:i + 1], ex[:, i, :], ALU.mult, ALU.mult)
                nc.vector.memset(W[:, :, E:E + 2], 1.0)
            else:
                for i in range(TT):
                    nc.vector.tensor_scalar(ex[:, i, :], m8[:, i, :], m8[:, i, 0:1], None, ALU.subtract)
                    one_hot(0, i, 0)
                    m = one_hot(1, i, 1)
                m.then_inc(shifted, 1)
                if kind == "capacity_slots":
                    dve.wait_ge(shifted, 1)
                    nc.vector.tensor_copy(f8[:, :, 0:1], f8[:, :, 0:1]).then_inc(choices, 1)
                dve.wait_ge(act_done, 1)
                link(nc.vector.tensor_scalar(sm[:, :], ex[:, :, 1], 1.0, None, ALU.add))
                link(nc.vector.reciprocal(g1[:, :, 0], sm[:, :]))
                link(nc.vector.tensor_tensor(g1[:, :, 1], g1[:, :, 0], ex[:, :, 1], ALU.mult))
                if kind == "capacity_slots":
                    dve.wait_ge(mm, 2)
                    for i in range(TT):
                        m = nc.vector.tensor_scalar(kp[:, i, :, :].rearrange("p a e -> p (a e)"), pc[:, i, 0:2 * E], float(capacity), None,
                                                    ALU.is_lt)
                    link(m)
                    link(nc.vector.tensor_tensor(kp[:, :, :, :], kp[:, :, :, :], oh[:, :, 0:2, :], ALU.mult))
                else:
                    link(nc.vector.tensor_scalar(sm[:, :], g1[:, :, 1], 0.0, None, ALU.is_gt))
                    for i in range(TT):
                        m = nc.vector.scalar_tensor_tensor(oh[:, i, 2, :], oh[:, i, 1, :], sm[:, i:i + 1], oh[:, i, 0, :],
                                                           ALU.mult, ALU.add)
                    m.then_inc(choices, 1)
                    dve.wait_ge(mm, 2)
                    for i in range(TT):
                        m = nc.vector.tensor_scalar(ex[:, i, :], pc[:, i, 0:E], float(capacity), None, ALU.is_le)
                    link(m)
                    for a in range(2):
                        m = nc.vector.tensor_tensor(kp[:, :, a, :], ex[:, :, :], oh[:, :, a, :], ALU.mult)
                    link(m)
                for i in range(TT):
                    for a in range(2):
                        m = nc.vector.tensor_scalar(oh[:, i, 2 + a, :], kp[:, i, a, :], g1[:, i, a:a + 1], None, ALU.mult)
                link(m)
                nc.vector.tensor_tensor(W[:, :, 0:E], oh[:, :, 2, :], oh[:, :, 3, :], ALU.add)


def layer0_ff(nc, k, d):
    layer_norm(nc, k, k.X, k.N, "f0n")
    transpose_tokens(nc, k, k.N, k.NT, "f0t")
    with Tensors(nc) as t:
        W = t.sb("f0_W", [P, TT, 8])
        route(nc, k, d, "f0r", 8, "top1", W)
        experts(nc, k, d["f0_pieces"], "f0e", 8, 8, 2, "swiglu", W)


def layer1_ff(nc, k, d):
    layer_norm(nc, k, k.X, k.N, "f1n")
    transpose_tokens(nc, k, k.N, k.NT, "f1t")
    with Tensors(nc) as t:
        W = t.sb("f1_W", [P, TT, 8])
        route(nc, k, d, "f1r", 8, "capacity_slots", W, capacity=-(-12 * T * 2 // 80))
        weighted_bias(nc, k, d, W)
        experts(nc, k, d["f1_pieces"], "f1e", 8, 8, 2, "gelu", W, b1=d["f1_b1"])


def weighted_bias(nc, k, d, W):
    E = 8
    with Tensors(nc) as t, stage(nc, "wb_load", "wb_turned", "wb_copied", "wb_mm") as (block, load, turned, copied, mm):
        b2 = t.sb("wb_b2", [E, D])
        wT = t.sb("wb_wT", [E, T])
        pt = t.ps("wb_pt", [P, T])
        po = t.ps("wb_po", [P, TT, 512])

        @block.sync
        def _(sp):
            sp.dma_start(b2[:, :], d["f1_b2"]).then_inc(load, 16)

        @block.tensor
        def _(pe):
            for i in range(TT):
                m = nc.tensor.transpose(pt[0:E, i * P:(i + 1) * P], W[:, i, :], k.ident[:, :])
            m.then_inc(turned, 1)
            pe.wait_ge(load, 16)
            pe.wait_ge(copied, 1)
            for i in range(TT):
                nc.tensor.matmul(po[:, i, 0:D], wT[:, i * P:(i + 1) * P], b2[:, :], start=True, stop=True).then_inc(mm, 1)

        @block.scalar
        def _(act):
            act.wait_ge(turned, 1)
            nc.scalar.copy(wT[:, :], pt[0:E, :]).then_inc(copied, 1)

        @block.vector
        def _(dve):
            for i in range(TT):
                dve.wait_ge(mm, i + 1)
                nc.vector.tensor_tensor(k.X[:, i, :], po[:, i, 0:D], k.X[:, i, :], ALU.add)


def layer2_ff(nc, k, d):
    layer_norm(nc, k, k.X, k.N, "f2n")
    transpose_tokens(nc, k, k.N, k.NT, "f2t")
    with Tensors(nc) as t:
        W = t.sb("f2_W", [P, TT, 8])
        route(nc, k, d, "f2r", 8, "capacity_tokens", W, capacity=T // 8)
        experts(nc, k, d["f2_pieces"], "f2e", 8, 4, 4, "relu", W)


def layer3_ff(nc, k, d):
    layer_norm(nc, k, k.X, k.N, "f3n")
    transpose_tokens(nc, k, k.N, k.NT, "f3t")
    with Tensors(nc) as t:
        W = t.sb("f3_W", [P, TT, 18])
        route(nc, k, d, "f3r", 16, "sigmoid_top4", W)
        experts(nc, k, d["f3_pieces"], "f3e", 18, 1, 6, "swiglu", W)


def expert_layouts(a, i, rows, cols, spread):
    def pieces(ins, w_out):
        e, _, h = ins[0].shape
        n = e * h // (2 * P)
        parts = [w.transpose(1, 0, 2).reshape(KC, P, n, 2 * P).transpose(2, 1, 0, 3).reshape(n, P, -1) for w in ins]
        parts.append(w_out.reshape(n, 2, P, D).transpose(0, 2, 1, 3).reshape(n, P, -1))
        return np.ascontiguousarray(np.concatenate(parts, 2))

    def with_shared(w, s):
        return np.concatenate([w, s], 0)

    n = "L0_ffn_"
    a["f0r_wr"] = rows(i[n + "w_router"])
    a["f0_pieces"] = pieces([with_shared(i[n + "w_up"], i[n + "ws_up"][None]), with_shared(i[n + "w_gate"], i[n + "ws_gate"][None])],
                            with_shared(i[n + "w_down"], i[n + "ws_down"][None]))
    n = "L1_ffn_"
    a["f1r_wr"], a["f1r_bg"] = rows(i[n + "Wg"]), spread(i[n + "bg"])
    a["f1_pieces"] = pieces([i[n + "W1"]], i[n + "W2"])
    a["f1_b1"] = np.ascontiguousarray(i[n + "b1"].reshape(4, 16, P).transpose(0, 2, 1))
    a["f1_b2"] = i[n + "b2"]
    n = "L2_ffn_"
    a["f2r_wr"] = rows(i[n + "expert_embeddings"].T)
    a["f2_pieces"] = pieces([i[n + "first_linear"].transpose(0, 2, 1)], i[n + "second_linear"].transpose(0, 2, 1))
    n = "L3_ffn_"
    a["f3r_wr"] = rows(i[n + "gate_w"].T)

    def halves(w):
        return w.reshape(D, 2, P).transpose(1, 0, 2)

    a["f3_pieces"] = pieces([with_shared(i[n + "e_vin"], halves(i[n + "vs_in"])), with_shared(i[n + "e_win"], halves(i[n + "ws_in"]))],
                            with_shared(i[n + "e_wout"], i[n + "ws_out"].reshape(2, P, D)))
    one = np.ones((P, P), np.float32)
    a["tri_below"], a["tri_upto"] = np.triu(one, 1), np.triu(one)



def linear_tokens(nc, k, srcT, dst, w, name, bias, width=D, wide=D, chunks=KC, func=None):
    with Tensors(nc) as t, stage(nc, name + "_load", name + "_mm", name + "_ev") as (block, load, mm, ev):
        wt = t.sb(name + "_w", [P, chunks, width])
        bt = t.sb(name + "_b", [P, width])
        ps = t.ps(name + "_ps", [P, TT, 512])

        @block.sync
        def _(sp):
            sp.dma_start(wt[:, :, :], w).then_inc(load, 16)
            if bias is not None:
                sp.dma_start(bt[:, :], bias).then_inc(load, 16)

        @block.tensor
        def _(pe):
            pe.wait_ge(load, 16 * (1 + (bias is not None)))
            for i in range(TT):
                for c in range(chunks):
                    m = nc.tensor.matmul(ps[:, i, 0:width], srcT[:, c, i * P:(i + 1) * P], wt[:, c, :],
                                         start=(c == 0), stop=(c == chunks - 1))
                m.then_inc(mm, 1)

        @block.vector
        def _(dve):
            for i in range(TT):
                dve.wait_ge(mm, i + 1)
                if bias is not None:
                    nc.vector.tensor_tensor(dst[:, i, 0:width], ps[:, i, 0:width], bt[:, :], ALU.add)
                else:
                    nc.vector.tensor_copy(dst[:, i, 0:width], ps[:, i, 0:width])


def self_attention(nc, k, d, pre, qT, kT, V, O, relative):
    hd, HPC, RW = HD16, P // HD16, 3 * P
    Kz = None
    with nc.Fori(0, B) as b, nc.Fori(0, KC) as c, Tensors(nc) as t:
        qz = t.sb(pre + "_qz", [P, HPC, S])
        keys = t.sb(pre + "_keys", [P, S])
        vals = t.sb(pre + "_vals", [P, QT, P])
        mask = t.sb(pre + "_mask", [P, HPC])
        if relative:
            kz = t.sb(pre + "_kz", [P, HPC, S])
            scratch = k.rel_scratch
            with Tensors(nc) as u, stage(nc, pre + "_aload", pre + "_masked", pre + "_rel", pre + "_rel_dve", pre + "_rel_act", pre + "_rel_out") as (
                    block, aload, masked, rel, rel_dve, rel_act, rel_out):
                emb = u.sb(pre + "_emb", [P, 2, 512])
                rows = u.sb(pre + "_rows", [P, 4, 4, RW])
                ps = u.ps(pre + "_rps", [P, 4, 512])

                @block.sync
                def _(sp):
                    sp.dma_start(emb[:, :, :], d["rel_emb"]).then_inc(aload, 16)
                    sp.dma_start(mask[:, :], d["mask16"]).then_inc(aload, 16)
                    for h in range(HPC):
                        sp.wait_ge(rel_dve, 2 * (h + 1))
                        sp.wait_ge(rel_act, 2 * (h + 1))
                        if h >= 1:
                            sp.wait_ge(rel_out, 16 * h)
                        sp.dma_start(scratch[h].rearrange("x p w -> p x w"), rows[:, h % 4, :, :]).then_inc(rel_out, 16)
                    sp.wait_ge(rel_out, 16 * HPC)

                @block.vector
                def _(dve):
                    dve.wait_ge(aload, 32)
                    for src, dst in ((qT, qz), (kT, kz)):
                        for h in range(HPC):
                            nc.vector.tensor_scalar(dst[:, h:h + 1, :], src[:, bass.ds(c, 1), bass.ds(b * S, S)], mask[:, h:h + 1], None,
                                                    ALU.mult).then_inc(masked, 1)
                    for n in range(1, 4 * HPC, 2):
                        dve.wait_ge(rel, n + 1)
                        if n >= 16:
                            dve.wait_ge(rel_out, 16 * (n // 4 - 3))
                        nc.vector.tensor_copy(rows[:, n // 4 % 4, n % 4, :], ps[:, n % 4, 0:RW]).then_inc(rel_dve, 1)

                @block.scalar
                def _(act):
                    for n in range(0, 4 * HPC, 2):
                        act.wait_ge(rel, n + 1)
                        if n >= 16:
                            act.wait_ge(rel_out, 16 * (n // 4 - 3))
                        nc.scalar.copy(rows[:, n // 4 % 4, n % 4, :], ps[:, n % 4, 0:RW]).then_inc(rel_act, 1)

                @block.tensor
                def _(pe):
                    pe.wait_ge(masked, 2 * HPC)
                    for n in range(4 * HPC):
                        h, x = divmod(n, 4)
                        side, i = divmod(x, 2)
                        if n >= 4:
                            pe.wait_ge((rel_act, rel_dve)[n % 2], n // 2 - 1)
                        nc.tensor.matmul(ps[:, n % 4, 0:RW], (qz, kz)[side][:, h, i * P:(i + 1) * P],
                                         emb[:, side, P * (1 - i):P * (1 - i) + RW], start=True, stop=True).then_inc(rel, 1)

        with Tensors(nc) as u, stage(nc, pre + "_load", pre + "_add0", pre + "_add1", pre + "_ready", pre + "_scored", pre + "_sum", pre + "_peak",
                                     pre + "_exp", pre + "_turned", pre + "_pT", pre + "_av", pre + "_chain", pre + "_scaled", pre + "_static") as (
                block, load, add0, add1, ready, scored, summed, peak, expd, turned, pT_done, av, chain, scaled, static):
            NSL = 2
            sc = u.sb(pre + "_sc", [P, 2, QT, S])
            pr = u.sb(pre + "_pr", [P, 2, QT, S])
            pT = u.sb(pre + "_pT", [P, 2, QT, QT, P])
            mx = u.sb(pre + "_mx", [P, HPC, QT])
            nm = u.sb(pre + "_nm", [P, HPC, QT])
            sums = u.sb(pre + "_sums", [P, HPC, QT])
            rec = u.sb(pre + "_rec", [P, HPC, QT])
            add = u.sb(pre + "_add", [P, 2, 4, S])
            pss = u.ps(pre + "_pss", [P, 2, QT, S])
            pst = u.ps(pre + "_pst", [P, 2, QT, QT, P])
            pso = u.ps(pre + "_pso", [P, 2, 512])
            SC = 1.0 if relative else 0.25
            HEADS = range(HPC)

            @block.sync
            def _(sp):
                if not relative:
                    sp.dma_start(mask[:, :], d["mask16"]).then_inc(load, 16)
                    sp.dma_start(add[:, 0, 0:QT, :], d["causal"]).then_inc(load, 16)
                else:
                    for h in HEADS:
                        if h >= 2:
                            sp.wait_ge(summed, h - 1)
                            sp.wait_ge(scored, h - 1)
                        src = scratch[h]
                        skew = bass.AP(tensor=src.tensor, offset=src.offset + P - 1, ap=[[RW - 1, P], [P * RW, 4], [1, S]])
                        sp.dma_start(add[:, h % 2, :, :], skew).then_inc((add0, add1)[h % 2], 16)

            @block.gpsimd
            def _(pool):
                nc.gpsimd.tensor_copy(keys[:, :].unsqueeze(1), kT[:, bass.ds(c, 1), bass.ds(b * S, S)]).then_inc(static, 1)
                nc.gpsimd.tensor_copy(vals[:, :, :], V[:, bass.ds(b * QT, QT), bass.ds(c * P, P)]).then_inc(static, 1)
                if relative:
                    pool.wait_ge(static, 2)
                    nc.gpsimd.tensor_scalar(keys[:, :], keys[:, :], 0.25, None, ALU.mult).then_inc(static, 1)

            def added(eng, h):
                if relative:
                    eng.wait_ge((add0, add1)[h % 2], 16 * (h // 2 + 1))

            @block.tensor
            def _(pe):
                pe.wait_ge(static, 3 if relative else 2)
                if not relative:
                    pe.wait_ge(ready, HPC)

                def turn(h):
                    pe.wait_ge(expd, QT * (h + 1))
                    if h >= 2:
                        pe.wait_ge(pT_done, h - 1)
                    for kt in range(QT):
                        for qt in range(QT):
                            m = nc.tensor.transpose(pst[:, h % 2, kt, qt, :], pr[:, h % 2, qt, kt * P:(kt + 1) * P], k.ident[:, :])
                    m.then_inc(turned, 1)

                def average(h):
                    pe.wait_ge(pT_done, h + 1)
                    if h >= 2:
                        pe.wait_ge(scaled, QT * (h - 1))
                    for qt in range(QT):
                        for kt in range(QT):
                            m = nc.tensor.matmul(pso[:, h % 2, qt * hd:(qt + 1) * hd], pT[:, h % 2, kt, qt, :], vals[:, kt, h * hd:(h + 1) * hd],
                                                 start=(kt == 0), stop=(kt == QT - 1))
                    m.then_inc(av, 1)

                for h in range(HPC + 2):
                    if h < HPC:
                        added(pe, h)
                        if h >= 2:
                            pe.wait_ge(summed, h - 1)
                        for qt in range(QT):
                            m = nc.tensor.matmul(pss[:, h % 2, qt, :], qz[:, h, qt * P:(qt + 1) * P], keys[:, :], start=True, stop=not relative,
                                                 skip_group_check=True)
                            if relative:
                                for kt in range(QT):
                                    m = nc.tensor.matmul(pss[:, h % 2, qt, kt * P:(kt + 1) * P], add[:, h % 2, 2 + kt, qt * P:(qt + 1) * P],
                                                         k.ident[:, :], start=False, stop=(kt == QT - 1), skip_group_check=True)
                        m.then_inc(scored, 1)
                    if 1 <= h <= HPC:
                        turn(h - 1)
                    if h >= 2:
                        average(h - 2)

            @block.vector
            def _(dve):
                links = [0]

                def link(i):
                    links[0] += 1
                    i.then_inc(chain, 1)
                    dve.wait_ge(chain, links[0])

                if not relative:
                    dve.wait_ge(load, 32)
                    for h in HEADS:
                        nc.vector.tensor_scalar(qz[:, h:h + 1, :], qT[:, bass.ds(c, 1), bass.ds(b * S, S)], mask[:, h:h + 1], None,
                                                ALU.mult).then_inc(ready, 1)

                def normalize(h):
                    dve.wait_ge(av, h + 1)
                    link(nc.vector.reciprocal(rec[:, h, :], sums[:, h, :]))
                    for qt in range(QT):
                        nc.vector.tensor_scalar(O[:, bass.ds(b * QT + qt, 1), bass.ds(c * P + h * hd, hd)],
                                                pso[:, h % 2:h % 2 + 1, qt * hd:(qt + 1) * hd], rec[:, h, qt:qt + 1], None,
                                                ALU.mult).then_inc(scaled, 1)

                for h in range(HPC + 3):
                    if h < HPC:
                        dve.wait_ge(scored, h + 1)
                        added(dve, h)
                        if h >= 2:
                            dve.wait_ge(expd, QT * (h - 1))
                        m = nc.vector.tensor_tensor(sc[:, h % 2, :, :], pss[:, h % 2, :, :], add[:, h % 2 if relative else 0, 0:QT, :], ALU.add)
                        m.then_inc(summed, 1)
                        dve.wait_ge(summed, h + 1)
                        link(nc.vector.reduce_max(mx[:, h, :], sc[:, h % 2, :, :], AX))
                        nc.vector.tensor_scalar(nm[:, h, :], mx[:, h, :], -SC, None, ALU.mult).then_inc(peak, 1)
                    if h >= 3:
                        normalize(h - 3)

            @block.scalar
            def _(act):
                for h in range(HPC + 1):
                    if h < HPC:
                        act.wait_ge(peak, h + 1)
                        if h >= 2:
                            act.wait_ge(turned, h - 1)
                        for qt in range(QT):
                            nc.scalar.activation(pr[:, h % 2, qt, :], sc[:, h % 2, qt, :], ACT.Exp, bias=nm[:, h, qt:qt + 1], scale=SC,
                                                 accum_out=sums[:, h, qt:qt + 1]).then_inc(expd, 1)
                    if h >= 1:
                        act.wait_ge(turned, h)
                        if h >= 3:
                            act.wait_ge(av, h - 2)
                        nc.scalar.copy(pT[:, (h - 1) % 2, :, :, :], pst[:, (h - 1) % 2, :, :, :]).then_inc(pT_done, 1)


def layer0_self(nc, k, d):
    layer_norm(nc, k, k.X, k.N, "s0n")
    transpose_tokens(nc, k, k.N, k.NT, "s0t")
    k.rel_scratch = nc.dram_tensor("offset_rows", (P // HD16, 4, P, 3 * P), F32, kind="Internal").ap()
    with Tensors(nc) as t:
        qT = t.sb("s0_qT", [P, KC, T])
        kT = t.sb("s0_kT", [P, KC, T])
        V = t.sb("s0_V", [P, TT, D])
        O = t.sb("s0_O", [P, TT, D])
        linear_T(nc, k, k.NT, qT, d["s0_wq"], "s0q", bias=d["s0_bq"])
        linear_T(nc, k, k.NT, kT, d["s0_wk"], "s0k", bias=d["s0_bk"])
        linear_tokens(nc, k, k.NT, V, d["s0_wv"], "s0v", d["s0_bv"])
        self_attention(nc, k, d, "s0", qT, kT, V, O, True)
        add_to(nc, k.X, O, "s0a")


def add_to(nc, dst, src, name):
    with stage(nc, name + "_unused", name + "_unused1") as (block, _u, _v):
        @block.vector
        def _(dve):
            nc.vector.tensor_tensor(dst[:, :, :], dst[:, :, :], src[:, :, :], ALU.add)


def rotate(nc, k, d, xT, name):
    with Tensors(nc) as t, stage(nc, name + "_load", name + "_mm", name + "_a", name + "_b") as (block, load, mm, ca, cb):
        rot = t.sb(name + "_r", [P, P])
        tab = t.sb(name + "_tab", [P, 2, T])
        tmp = t.sb(name + "_tmp", [P, KC, T])
        ps = t.ps(name + "_ps", [P, KC, T])

        @block.sync
        def _(sp):
            sp.dma_start(rot[:, :], d["rope_swap"]).then_inc(load, 16)
            sp.dma_start(tab[:, :, :], d["rope_tables"]).then_inc(load, 16)

        @block.tensor
        def _(pe):
            pe.wait_ge(load, 32)
            for c in range(KC):
                nc.tensor.matmul(ps[:, c, :], rot[:, :], xT[:, c, :], start=True, stop=True).then_inc(mm, 1)

        @block.vector
        def _(dve):
            dve.wait_ge(load, 32)
            for c in range(KC):
                dve.wait_ge(mm, c + 1)
                nc.vector.tensor_tensor(tmp[:, c, :], ps[:, c, :], tab[:, 1, :], ALU.mult).then_inc(ca, 1)
                nc.vector.tensor_tensor(xT[:, c, :], xT[:, c, :], tab[:, 0, :], ALU.mult).then_inc(cb, 1)
            for c in range(KC):
                dve.wait_ge(ca, KC)
                dve.wait_ge(cb, KC)
                nc.vector.tensor_tensor(xT[:, c, :], xT[:, c, :], tmp[:, c, :], ALU.add)


def layer2_self(nc, k, d):
    with Tensors(nc) as t:
        X0 = t.sb("s2_X0", [P, TT, D])
        with stage(nc, "s2_keep", "s2_keep1") as (block, _u, _v):
            @block.vector
            def _(dve):
                nc.vector.tensor_copy(X0[:, :, :], k.X[:, :, :])
        layer_norm(nc, k, X0, k.X, "s2i")
        layer_norm(nc, k, k.X, k.N, "s2n")
        transpose_tokens(nc, k, k.N, k.NT, "s2t", gain=d["s2_g1"], shift=d["s2_h1"])
        with Tensors(nc) as u:
            qT = u.sb("s2_qT", [P, KC, T])
            kT = u.sb("s2_kT", [P, KC, T])
            V = u.sb("s2_V", [P, TT, D])
            O = u.sb("s2_O", [P, TT, D])
            OT = u.sb("s2_OT", [P, KC, T])
            linear_T(nc, k, k.NT, qT, d["s2_wq"], "s2q", bias=d["s2_bq"])
            linear_T(nc, k, k.NT, kT, d["s2_wk"], "s2k", bias=d["s2_bk"])
            linear_tokens(nc, k, k.NT, V, d["s2_wv"], "s2v", d["s2_bv"])
            rotate(nc, k, d, qT, "s2rq")
            rotate(nc, k, d, kT, "s2rk")
            self_attention(nc, k, d, "s2", qT, kT, V, O, False)
            transpose_tokens(nc, k, O, OT, "s2o")
            project_residual(nc, k, OT, d["s2_wo"], "s2p", bias=d["s2_bo"])
        layer_norm(nc, k, k.X, k.N, "s2m")
        transpose_tokens(nc, k, k.N, k.NT, "s2u", gain=d["s2_g2"], shift=d["s2_h2"])
        W = t.sb("s2_W", [P, TT, 1])
        b2 = t.sb("s2_b2", [P, D])
        with stage(nc, "s2_b2_load", "s2_b2_unused") as (block, load, _u):
            @block.sync
            def _(sp):
                sp.dma_start(b2[:, :], d["s2_b2"]).then_inc(load, 16)

            @block.vector
            def _(dve):
                nc.vector.memset(W[:, :, :], 1.0)
                dve.wait_ge(load, 16)
                nc.vector.tensor_tensor(X0[:, :, :], X0[:, :, :], b2[:, :].unsqueeze(1).broadcast_to([P, TT, D]), ALU.add)
        experts(nc, k, d["s2_pieces"], "s2e", 1, 8, 1, "gelu_erf", W, b1=d["s2_b1"])
        add_to(nc, k.X, X0, "s2a")


def self_layouts(a, i, rows, cols, spread):
    n = "L0_attn_"
    for w in "qk":
        a["s0_w" + w], a["s0_b" + w] = rows(i[n + "W" + w].T), cols(i[n + "b" + w])
    a["s0_wv"], a["s0_bv"] = rows(i[n + "Wv"].T), spread(i[n + "bv"])
    e = i[n + "dist_emb"]
    two = np.stack([e[255:767][::-1], e[256:768]])
    a["rel_emb"] = np.ascontiguousarray(np.tile(two.transpose(2, 0, 1), (P // HD16, 1, 1)))
    n = "L2_attn_"
    wqkv = i[n + "Wqkv"]
    bqkv = i[n + "bqkv"]
    a["s2_wq"], a["s2_wk"], a["s2_wv"] = (rows(wqkv[:, x * D:(x + 1) * D]) for x in range(3))
    a["s2_bq"], a["s2_bk"], a["s2_bv"] = cols(bqkv[:D]), cols(bqkv[D:2 * D]), spread(bqkv[2 * D:])
    for x in "12":
        a["s2_g" + x], a["s2_h" + x] = cols(i[n + f"ln{x}_g"]), cols(i[n + f"ln{x}_b"])
    a["s2_wo"], a["s2_bo"] = rows(i[n + "Wo"]), spread(i[n + "bo"])
    w1, w2 = i[n + "W1"], i[n + "W2"]
    parts = [w1.reshape(KC, P, 4, 2 * P).transpose(2, 1, 0, 3).reshape(4, P, -1), w2.reshape(4, 2, P, D).transpose(0, 2, 1, 3).reshape(4, P, -1)]
    a["s2_pieces"] = np.ascontiguousarray(np.concatenate(parts, 2))
    a["s2_b1"] = cols(i[n + "b1"])[None]
    a["s2_b2"] = spread(i[n + "b2"])
    q = np.arange(S)
    causal = np.where(q[None, :] > q[:, None], np.float32(-1e30), np.float32(0)).astype(np.float32)
    a["causal"] = np.ascontiguousarray(causal.reshape(QT, P, S).transpose(1, 0, 2))
    swap = np.zeros((P, P), np.float32)
    for f in range(P):
        h, r = divmod(f, HD16)
        if r < HD16 // 2:
            swap[h * HD16 + r + HD16 // 2, f] = -1
        else:
            swap[h * HD16 + r - HD16 // 2, f] = 1
    a["rope_swap"] = swap
    inv = (1.0 / 10000.0 ** (np.arange(0, HD16, 2, dtype=np.float32) / HD16)).astype(np.float32)
    fr = np.arange(S, dtype=np.float32)[:, None] * inv[None, :]
    emb = np.concatenate([fr, fr], -1).astype(np.float32)
    tab = np.stack([np.cos(emb), np.sin(emb)]).astype(np.float32).transpose(2, 0, 1)
    a["rope_tables"] = np.ascontiguousarray(np.tile(tab, (P // HD16, 1, B)))



VL = 4
VH = HD16 // VL
DELTA_STEPS = 64


def layer1_self(nc, k, d):
    layer_norm(nc, k, k.X, k.N, "dn")
    transpose_tokens(nc, k, k.N, k.NT, "dt")
    heads = nc.dram_tensor("delta_heads", (3, B, NH, S, HD16), F32, kind="Internal").ap()
    gates = nc.dram_tensor("delta_gates", (2, B, NH, S), F32, kind="Internal").ap()
    with Tensors(nc) as t:
        oA = t.sb("d_oA", [P, S, VL])
        state = t.sb("d_state", [P, VL, HD16])
        with Tensors(nc) as u, stage(nc, "d_load", "d_mm", "d_gmm", "d_silu", "d_sq", "d_root", "d_gate", "d_ready", "d_vready", "d_out") as (
                block, load, mm, gmm, silu, sq, root, gate, ready, vready, stored):
            w = u.sb("d_w", [P, 3, KC, D])
            wg = u.sb("d_wg", [P, KC, 2 * HD16])
            q = u.sb("d_q", [P, TT, D])
            kk = u.sb("d_k", [P, TT, D])
            v = u.sb("d_v", [P, TT, D])
            ss = u.sb("d_ss", [P, TT, D])
            nrm = u.sb("d_nrm", [P, TT, NH])
            g = u.sb("d_g", [2 * HD16, T])
            ps = u.ps("d_ps", [P, 3, 2, 512])
            pg = u.ps("d_pg", [2 * HD16, T])

            @block.sync
            def _(sp):
                sp.dma_start(w[:, :, :, :], d["d_w3"]).then_inc(load, 16)
                sp.dma_start(wg[:, :, :], d["d_wg"]).then_inc(load, 16)

                def store(n, src):
                    for b in range(B):
                        for i in range(QT):
                            sp.dma_start(heads[n, b][:, i * P:(i + 1) * P, :].rearrange("h p e -> p h e"),
                                         src[:, b * QT + i, :].rearrange("p (h e) -> p h e", h=NH)).then_inc(stored, 16)

                sp.wait_ge(gate, 2)
                for n in range(2):
                    sp.dma_start(gates[n].rearrange("b h s -> h b s"), g[n * NH:(n + 1) * NH, :].rearrange("h (b s) -> h b s", b=B)).then_inc(stored, 16)
                sp.wait_ge(vready, TT)
                store(2, v)
                sp.wait_ge(silu, 2 * TT)
                store(0, q)
                sp.wait_ge(ready, 1)
                store(1, kk)
                sp.wait_ge(stored, 16 * (2 + 3 * TT))

            @block.tensor
            def _(pe):
                pe.wait_ge(load, 32)
                for c in range(KC):
                    m = nc.tensor.matmul(pg[:, :], wg[:, c, :], k.NT[:, c, :], start=(c == 0), stop=(c == KC - 1))
                m.then_inc(gmm, 1)
                for i in range(TT):
                    if i >= 2:
                        pe.wait_ge(silu, 2 * (i - 1))
                        pe.wait_ge(vready, i - 1)
                    for n in range(3):
                        for c in range(KC):
                            m = nc.tensor.matmul(ps[:, n, i % 2, 0:D], k.NT[:, c, i * P:(i + 1) * P], w[:, n, c, :],
                                                 start=(c == 0), stop=(c == KC - 1))
                    m.then_inc(mm, 1)

            @block.scalar
            def _(act):
                act.wait_ge(gmm, 1)
                nc.scalar.activation(g[:, :], pg[:, :], ACT.Sigmoid).then_inc(gate, 1)
                for i in range(TT):
                    act.wait_ge(mm, i + 1)
                    nc.scalar.activation(q[:, i, :], ps[:, 0, i % 2, 0:D], ACT.Silu).then_inc(silu, 1)
                    nc.scalar.activation(kk[:, i, :], ps[:, 1, i % 2, 0:D], ACT.Silu).then_inc(silu, 1)
                act.wait_ge(sq, 3)
                nc.scalar.activation(nrm[:, :, :], nrm[:, :, :], ACT.Sqrt).then_inc(root, 1)

            @block.vector
            def _(dve):
                for i in range(TT):
                    dve.wait_ge(mm, i + 1)
                    nc.vector.tensor_copy(v[:, i, :], ps[:, 2, i % 2, 0:D]).then_inc(vready, 1)
                dve.wait_ge(gate, 1)
                nc.vector.tensor_scalar(g[:, :], g[:, :], k.twos[0:2 * NH, 0:1], None, ALU.mult).then_inc(gate, 1)
                dve.wait_ge(silu, 2 * TT)
                nc.vector.tensor_tensor(ss[:, :, :], kk[:, :, :], kk[:, :, :], ALU.mult).then_inc(sq, 1)
                dve.wait_ge(sq, 1)
                nc.vector.reduce_sum(nrm[:, :, :], ss[:, :, :].rearrange("p i (h e) -> p i h e", h=NH), AX).then_inc(sq, 1)
                dve.wait_ge(sq, 2)
                nc.vector.tensor_scalar(nrm[:, :, :], nrm[:, :, :], 1e-12, None, ALU.add).then_inc(sq, 1)
                dve.wait_ge(root, 1)
                nc.vector.reciprocal(nrm[:, :, :], nrm[:, :, :]).then_inc(root, 1)
                dve.wait_ge(root, 2)
                for i in range(TT):
                    m = nc.vector.tensor_tensor(kk[:, i, :].rearrange("p (h e) -> p h e", h=NH), kk[:, i, :].rearrange("p (h e) -> p h e", h=NH),
                                                nrm[:, i, :].unsqueeze(2).broadcast_to([P, NH, HD16]), ALU.mult)
                m.then_inc(ready, 1)

        with stage(nc, "d_zero", "d_zero1") as (block, _u, _v):
            @block.vector
            def _(dve):
                nc.vector.memset(state[:, :, :], 0.0)

        R = DELTA_STEPS
        SUB = 16
        with nc.Fori(0, S // R) as r, Tensors(nc) as u:
            with stage(nc, "e_load", "e_pre", "e_chain", "e_step", "e_prod", "e_out") as (block, load, pre_done, chain, stepped, prod, out):
                hv = u.sb("e_heads", [P, 3, R, HD16])
                ga = u.sb("e_gates", [P, 2, R])
                ab = u.sb("e_ab", [P, R])
                bv = u.sb("e_bv", [P, R, VL])
                ku = u.sb("e_ku", [P, 2, VL, HD16])
                us = u.sb("e_u", [P, 2, VL])
                H = u.sb("e_H", [P, R + 1, VL, HD16])
                pr = u.sb("e_pr", [P, 2, SUB, VL, HD16])
                vm = u.sb("e_vm", [P, VH])
                hp = NH * VH // VH

                @block.sync
                def _(sp):
                    for b in range(B):
                        rows = slice(b * NH * VH, (b + 1) * NH * VH)
                        for x in range(VH):
                            part = slice(b * NH * VH + x * NH, b * NH * VH + (x + 1) * NH)
                            for n in range(3):
                                sp.dma_start(hv[part, n, :, :], heads[n, b][:, bass.ds(r * R, R), :]).then_inc(load, 16)
                            for n in range(2):
                                sp.dma_start(ga[part, n, :], gates[n, b][:, bass.ds(r * R, R)]).then_inc(load, 16)
                    sp.dma_start(vm[:, :], d["d_fourth"]).then_inc(load, 16)

                @block.vector
                def _(dve):
                    links = [0]

                    def link(i):
                        links[0] += 1
                        i.then_inc(chain, 1)
                        dve.wait_ge(chain, links[0])

                    dve.wait_ge(load, 16 * (B * VH * 5 + 1))
                    link(nc.vector.scalar_tensor_tensor(ab[:, :], ga[:, 0, :], -1.0, ga[:, 1, :], ALU.mult, ALU.mult))
                    link(nc.vector.tensor_scalar(bv[:, :, :], hv[:, 2, :, 0:VL], vm[:, 0:1], None, ALU.mult))
                    for x in range(1, VH):
                        link(nc.vector.scalar_tensor_tensor(bv[:, :, :], hv[:, 2, :, x * VL:(x + 1) * VL], vm[:, x:x + 1], bv[:, :, :],
                                                            ALU.mult, ALU.add))
                    link(nc.vector.tensor_tensor(bv[:, :, :], bv[:, :, :], ga[:, 1, :].unsqueeze(2).broadcast_to([P, R, VL]), ALU.mult))
                    link(nc.vector.tensor_copy(H[:, 0, :, :], state[:, :, :]))
                    for s in range(R):
                        key = hv[:, 1, s, :].unsqueeze(1).broadcast_to([P, VL, HD16])
                        link(nc.vector.tensor_tensor(ku[:, 0, :, :], H[:, s, :, :], key, ALU.mult))
                        link(nc.vector.reduce_sum(us[:, 0, :], ku[:, 0, :, :], AX))
                        link(nc.vector.scalar_tensor_tensor(us[:, 1, :], us[:, 0, :], ab[:, s:s + 1], bv[:, s, :], ALU.mult, ALU.add))
                        link(nc.vector.tensor_tensor(ku[:, 1, :, :], key, us[:, 1, :].unsqueeze(2).broadcast_to([P, VL, HD16]), ALU.mult))
                        nc.vector.scalar_tensor_tensor(H[:, s + 1, :, :], H[:, s, :, :], ga[:, 0, s:s + 1], ku[:, 1, :, :],
                                                       ALU.mult, ALU.add).then_inc(stepped, 1)
                        dve.wait_ge(stepped, s + 1)
                    nc.vector.tensor_copy(state[:, :, :], H[:, R, :, :])
                    for n in range(R // SUB):
                        dve.wait_ge(prod, n + 1)
                        nc.vector.reduce_sum(oA[:, bass.ds(r * R + n * SUB, SUB), :], pr[:, n % 2, :, :, :], AX).then_inc(out, 1)

                @block.gpsimd
                def _(pool):
                    pool.wait_ge(load, 16 * (B * VH * 5 + 1))
                    for n in range(R // SUB):
                        pool.wait_ge(stepped, (n + 1) * SUB)
                        if n >= 2:
                            pool.wait_ge(out, n - 1)
                        qs = hv[:, 0, n * SUB:(n + 1) * SUB, :].unsqueeze(2).broadcast_to([P, SUB, VL, HD16])
                        nc.gpsimd.tensor_tensor(pr[:, n % 2, :, :, :], H[:, n * SUB + 1:(n + 1) * SUB + 1, :, :], qs, ALU.mult).then_inc(prod, 1)

        O = t.sb("d_O", [P, TT, D])
        with Tensors(nc) as u, stage(nc, "g_load", "g_turned", "g_copied", "g_chain", "g_root") as (block, load, turned, copied, chain, root):
            nw = u.sb("g_nw", [P, D])
            sqr = u.sb("g_sq", [P, TT, D])
            ms = u.sb("g_ms", [P, TT, NH])
            ps = u.ps("g_ps", [P, QT, VL, P])

            @block.sync
            def _(sp):
                sp.dma_start(nw[:, :], d["d_norm_w"]).then_inc(load, 16)

            @block.tensor
            def _(pe):
                for i in range(QT):
                    for x in range(VL):
                        m = nc.tensor.transpose(ps[:, i, x, :], oA[:, i * P:(i + 1) * P, x], k.ident[:, :])
                    m.then_inc(turned, 1)

            @block.vector
            def _(dve):
                links = [0]

                def link(i):
                    links[0] += 1
                    i.then_inc(chain, 1)
                    dve.wait_ge(chain, links[0])

                for i in range(QT):
                    dve.wait_ge(turned, i + 1)
                    for b in range(B):
                        for x in range(VL):
                            m = nc.vector.tensor_copy(O[:, b * QT + i, :].rearrange("p (h y x) -> p h y x", h=NH, y=VH)[:, :, :, x],
                                                      ps[:, i, x, b * NH * VH:(b + 1) * NH * VH].rearrange("p (y h) -> p h y", y=VH))
                link(m)
                link(nc.vector.tensor_tensor(sqr[:, :, :], O[:, :, :], O[:, :, :], ALU.mult))
                link(nc.vector.reduce_sum(ms[:, :, :], sqr[:, :, :].rearrange("p i (h e) -> p i h e", h=NH), AX))
                nc.vector.tensor_scalar(ms[:, :, :], ms[:, :, :], 1.0 / HD16, 1e-6, ALU.mult, ALU.add).then_inc(root, 1)
                dve.wait_ge(root, 2)
                link(nc.vector.reciprocal(ms[:, :, :], ms[:, :, :]))
                dve.wait_ge(load, 16)
                for i in range(TT):
                    o3 = O[:, i, :].rearrange("p (h e) -> p h e", h=NH)
                    link(nc.vector.tensor_tensor(o3, o3, ms[:, i, :].unsqueeze(2).broadcast_to([P, NH, HD16]), ALU.mult))
                    nc.vector.tensor_tensor(O[:, i, :], O[:, i, :], nw[:, :], ALU.mult)

            @block.scalar
            def _(act):
                act.wait_ge(root, 1)
                nc.scalar.activation(ms[:, :, :], ms[:, :, :], ACT.Sqrt).then_inc(root, 1)
        OT = t.sb("d_OT", [P, KC, T])
        transpose_tokens(nc, k, O, OT, "do")
        project_residual(nc, k, OT, d["d_wo"], "dp")



def layer3_self(nc, k, d):
    DI, NS, R, KW = 512, 16, 64, 4
    DC = DI // P
    XD = R + 2 * NS
    SEG = B * DC
    layer_norm(nc, k, k.X, k.N, "mn")
    transpose_tokens(nc, k, k.N, k.NT, "mt")
    with Tensors(nc) as t:
        xc = t.sb("m_xc", [P, DC, T])
        zs = t.sb("m_zs", [P, DC, T])
        dt = t.sb("m_dt", [P, DC, T])
        dbl = t.sb("m_dbl", [XD, T])
        A = t.sb("m_A", [P, DC, NS])
        par = t.sb("m_par", [P, DC, 3 + KW])
        with Tensors(nc) as u, stage(nc, "m_load", "m_mm", "m_ev", "m_zero", "m_conv", "m_xc_done") as (block, load, mm, ev, zero, conv, xc_done):
            w = u.sb("m_win", [P, KC, 2 * DI])
            xp = u.sb("m_xp", [P, DC, B, KW - 1 + S])
            cv = u.sb("m_cv", [P, 2, T])
            ps = u.ps("m_ps", [P, 2, T])

            @block.sync
            def _(sp):
                sp.dma_start(w[:, :, :], d["m_win"]).then_inc(load, 16)
                sp.dma_start(par[:, :, :], d["m_par"]).then_inc(load, 16)
                sp.dma_start(A[:, :, :], d["m_A_log"]).then_inc(load, 16)

            @block.tensor
            def _(pe):
                pe.wait_ge(load, 48)
                for m in range(2 * DC):
                    if m >= 2:
                        pe.wait_ge(ev, m - 1)
                    for c in range(KC):
                        i = nc.tensor.matmul(ps[:, m % 2, :], w[:, c, m * P:(m + 1) * P], k.NT[:, c, :], start=(c == 0), stop=(c == KC - 1))
                    i.then_inc(mm, 1)

            @block.scalar
            def _(act):
                for m in range(2 * DC):
                    act.wait_ge(mm, m + 1)
                    if m < DC:
                        nc.scalar.copy(xp[:, m, :, KW - 1:KW - 1 + S], ps[:, m % 2, :].rearrange("p (b s) -> p b s", b=B)).then_inc(ev, 1)
                    else:
                        nc.scalar.activation(zs[:, m - DC, :], ps[:, m % 2, :], ACT.Silu).then_inc(ev, 1)
                for m in range(DC):
                    act.wait_ge(conv, KW * (m + 1))
                    nc.scalar.activation(xc[:, m, :], cv[:, m % 2, :], ACT.Silu, bias=par[:, m, 0:1]).then_inc(xc_done, 1)
                act.wait_ge(load, 48)
                nc.scalar.activation(A[:, :, :], A[:, :, :], ACT.Exp)

            @block.vector
            def _(dve):
                nc.vector.memset(xp[:, :, :, 0:KW - 1], 0.0).then_inc(zero, 1)
                dve.wait_ge(zero, 1)
                dve.wait_ge(load, 48)
                for m in range(DC):
                    dve.wait_ge(ev, m + 1)
                    if m >= 2:
                        dve.wait_ge(xc_done, m - 1)
                    o = cv[:, m % 2, :].rearrange("p (b s) -> p b s", b=B)
                    for j in range(KW):
                        tap = par[:, m, 3 + j:4 + j]
                        if j == 0:
                            i = nc.vector.tensor_scalar(o, xp[:, m, :, 0:S], tap, None, ALU.mult)
                        else:
                            i = nc.vector.scalar_tensor_tensor(o, xp[:, m, :, j:j + S], tap, o, ALU.mult, ALU.add)
                        i.then_inc(conv, 1)
                        dve.wait_ge(conv, KW * m + j + 1)

        with Tensors(nc) as u, stage(nc, "n_load", "n_mm", "n_ev", "n_dmm", "n_pre", "n_exp", "n_chain") as (block, load, mm, ev, dmm, pre, expd, chain):
            wx = u.sb("n_wx", [P, DC, XD])
            wdt = u.sb("n_wdt", [R, DI])
            e = u.sb("n_e", [P, DC, T])
            w1 = u.sb("n_w1", [P, DC, T])
            ln = u.sb("n_ln", [P, DC, T])
            is1 = u.sb("n_is1", [P, DC, T])
            px = u.ps("n_px", [XD, T])
            pd = u.ps("n_pd", [P, DC, T])

            @block.sync
            def _(sp):
                sp.dma_start(wx[:, :, :], d["m_wx"]).then_inc(load, 16)
                sp.dma_start(wdt[:, :], d["m_wdt"]).then_inc(load, 16)

            @block.tensor
            def _(pe):
                pe.wait_ge(load, 32)
                for c in range(DC):
                    m = nc.tensor.matmul(px[:, :], wx[:, c, :], xc[:, c, :], start=(c == 0), stop=(c == DC - 1))
                m.then_inc(mm, 1)
                pe.wait_ge(ev, 1)
                for c in range(DC):
                    nc.tensor.matmul(pd[:, c, :], wdt[:, c * P:(c + 1) * P], dbl[0:R, :], start=True, stop=True).then_inc(dmm, 1)

            @block.scalar
            def _(act):
                act.wait_ge(mm, 1)
                nc.scalar.copy(dbl[:, :], px[:, :]).then_inc(ev, 1)
                act.wait_ge(pre, 2)
                nc.scalar.activation(e[:, :, :], e[:, :, :], ACT.Exp, scale=-1.0).then_inc(expd, 1)
                act.wait_ge(pre, 3)
                nc.scalar.activation(ln[:, :, :], w1[:, :, :], ACT.Ln).then_inc(expd, 1)

            @block.vector
            def _(dve):
                links = [0]

                def link(i):
                    links[0] += 1
                    i.then_inc(chain, 1)
                    dve.wait_ge(chain, links[0])

                for c in range(DC):
                    dve.wait_ge(dmm, c + 1)
                    i = nc.vector.tensor_scalar(dt[:, c, :], pd[:, c, :], par[:, c, 1:2], None, ALU.add)
                link(i)
                nc.vector.scalar_tensor_tensor(e[:, :, :], dt[:, :, :], -1.0, dt[:, :, :], ALU.mult, ALU.max).then_inc(pre, 1)
                dve.wait_ge(pre, 1)
                nc.vector.tensor_scalar(dt[:, :, :], dt[:, :, :], 0.0, None, ALU.max).then_inc(pre, 1)
                dve.wait_ge(expd, 1)
                nc.vector.tensor_scalar(w1[:, :, :], e[:, :, :], 1.0, None, ALU.add).then_inc(pre, 1)
                dve.wait_ge(pre, 3)
                link(nc.vector.tensor_scalar(is1[:, :, :], w1[:, :, :], 1.0, None, ALU.is_equal))
                dve.wait_ge(expd, 2)
                link(nc.vector.tensor_tensor(ln[:, :, :], ln[:, :, :], is1[:, :, :], ALU.add))
                link(nc.vector.scalar_tensor_tensor(w1[:, :, :], w1[:, :, :], 1.0, is1[:, :, :], ALU.subtract, ALU.add))
                link(nc.vector.reciprocal(w1[:, :, :], w1[:, :, :]))
                link(nc.vector.tensor_tensor(ln[:, :, :], ln[:, :, :], e[:, :, :], ALU.mult))
                link(nc.vector.tensor_tensor(ln[:, :, :], ln[:, :, :], w1[:, :, :], ALU.mult))
                link(nc.vector.tensor_tensor(dt[:, :, :], dt[:, :, :], ln[:, :, :], ALU.add))
                nc.vector.tensor_scalar(A[:, :, :], A[:, :, :], -1.0, None, ALU.mult)

        y = t.sb("m_y", [P, DC, T])
        with Tensors(nc) as u, stage(nc, "o_dx", "o_rows", "o_crow", "o_abar", "o_seg", "o_bu", "o_scan", "o_prod", "o_sum", "o_chain") as (
                block, dx_done, rows_done, crow, abar, seg, bu_done, scan, prod, summed, chain):
            dx = u.sb("o_dxs", [P, DC, T])
            ab = u.sb("o_ab", [P, 2, DC, T])
            bu = u.sb("o_bus", [P, DC, T])
            h = u.sb("o_h", [P, 2, DC, T])
            cr = u.sb("o_cr", [P, 2, T])
            pr = u.sb("o_pr", [P, 2, DC, T])
            pb = u.ps("o_pb", [P, 2, 2, T])
            py = u.ps("o_py", [P, DC, T])

            @block.tensor
            def _(pe):
                for n in range(NS + 1):
                    if n < NS:
                        if n >= 2:
                            pe.wait_ge(bu_done, n - 1)
                            pe.wait_ge(crow, n - 1)
                        for x in range(2):
                            r = R + NS * x + n
                            m = nc.tensor.matmul(pb[:, n % 2, x, :], k.ident[0:XD, r:r + 1].broadcast_to([XD, P]), dbl[:, :], start=True, stop=True)
                        m.then_inc(rows_done, 1)
                    if n >= 1:
                        pe.wait_ge(prod, n)
                        for c in range(DC):
                            m = nc.tensor.matmul(py[:, c, :], k.ident[:, :], pr[:, (n - 1) % 2, c, :], start=(n == 1), stop=(n == NS))
                        m.then_inc(summed, 1)

            @block.scalar
            def _(act):
                for n in range(NS):
                    if n >= 2:
                        act.wait_ge(scan, n - 1)
                    for c in range(DC):
                        m = nc.scalar.activation(ab[:, n % 2, c, :], dt[:, c, :], ACT.Exp, scale=A[:, c, n:n + 1])
                    m.then_inc(abar, 1)
                    act.wait_ge(rows_done, n + 1)
                    if n >= 2:
                        act.wait_ge(prod, n - 1)
                    nc.scalar.copy(cr[:, n % 2, :], pb[:, n % 2, 1, :]).then_inc(crow, 1)

            @block.gpsimd
            def _(pool):
                for n in range(NS + 1):
                    if n < NS:
                        pool.wait_ge(abar, n + 1)
                        nc.gpsimd.memset(ab[:, n % 2, :, :].rearrange("p c (b s) -> p (c b) s", b=B)[:, :, 0:1], 0.0).then_inc(seg, 1)
                    if n >= 1:
                        j = n - 1
                        pool.wait_ge(scan, j + 1)
                        pool.wait_ge(crow, j + 1)
                        if j >= 2:
                            pool.wait_ge(summed, j - 1)
                        nc.gpsimd.tensor_tensor(pr[:, j % 2, :, :], h[:, j % 2, :, :], cr[:, j % 2, :].unsqueeze(1).broadcast_to([P, DC, T]),
                                                ALU.mult).then_inc(prod, 1)

            @block.vector
            def _(dve):
                nc.vector.tensor_tensor(dx[:, :, :], dt[:, :, :], xc[:, :, :], ALU.mult).then_inc(dx_done, 1)
                dve.wait_ge(dx_done, 1)
                for n in range(NS):
                    dve.wait_ge(rows_done, n + 1)
                    if n >= 1:
                        dve.wait_ge(scan, n)
                    nc.vector.tensor_tensor(bu[:, :, :], dx[:, :, :], pb[:, n % 2, 0, :].unsqueeze(1).broadcast_to([P, DC, T]),
                                            ALU.mult).then_inc(bu_done, 1)
                    dve.wait_ge(bu_done, n + 1)
                    dve.wait_ge(seg, n + 1)
                    if n >= 2:
                        dve.wait_ge(prod, n - 1)
                    flat = "p c s -> p (c s)"
                    nc.vector.tensor_tensor_scan(h[:, n % 2, :, :].rearrange(flat), ab[:, n % 2, :, :].rearrange(flat), bu[:, :, :].rearrange(flat),
                                                 0.0, ALU.mult, ALU.add).then_inc(scan, 1)
                for c in range(DC):
                    nc.vector.tensor_scalar(y[:, c, :], xc[:, c, :], par[:, c, 2:3], None, ALU.mult).then_inc(chain, 1)
                dve.wait_ge(chain, DC)
                dve.wait_ge(summed, NS)
                nc.vector.tensor_tensor(y[:, :, :], py[:, :, :], y[:, :, :], ALU.add).then_inc(chain, 1)
                dve.wait_ge(chain, DC + 1)
                nc.vector.tensor_tensor(y[:, :, :], y[:, :, :], zs[:, :, :], ALU.mult)
        project_residual(nc, k, y, d["m_wout"], "mp", chunks=DC)


def scan_layouts(a, i, rows, cols, spread):
    n = "L1_attn_"
    a["d_w3"] = np.ascontiguousarray(np.stack([rows(i[n + w]) for w in ("Wq", "Wk", "Wv")], 1))
    a["d_wg"] = rows(np.concatenate([i[n + "Wf"], i[n + "Wbet"]], 1))
    a["d_norm_w"] = spread(i[n + "norm_w"])
    a["d_wo"] = rows(i[n + "Wo"])
    fourth = np.zeros((P, VH), np.float32)
    for p in range(P):
        fourth[p, p % (NH * VH) // NH] = 1
    a["d_fourth"] = fourth
    two = np.ones((P, 1), np.float32)
    two[NH:2 * NH] = 2
    a["twos"] = two
    n = "L3_attn_"
    a["m_win"] = rows(i[n + "W_in"].T)

    def lane(v):
        return np.ascontiguousarray(v.reshape(4, P, -1).transpose(1, 0, 2))

    a["m_par"] = np.concatenate([lane(i[n + "conv_b"]), lane(i[n + "b_dt"]), lane(i[n + "D_param"]), lane(i[n + "conv_w"])], 2)
    a["m_A_log"] = lane(i[n + "A_log"])
    a["m_wx"], a["m_wdt"], a["m_wout"] = rows(i[n + "W_x"].T), np.ascontiguousarray(i[n + "W_dt"].T), rows(i[n + "W_out"].T)



class Kernel:
    pass


def program(nc, d, out):
    k = Kernel()
    with Tensors(nc) as t:
        k.X = t.sb("X", [P, TT, D])
        k.N = t.sb("N", [P, TT, D])
        k.NT = t.sb("NT", [P, KC, T])
        k.ident = t.sb("ident", [P, P])
        k.onesb = t.sb("ones_bf16", [P, P], BF16)
        k.ones = t.sb("ones_f32", [P, P])
        k.iota = t.sb("iota16", [P, NH])
        k.twos = t.sb("twos", [P, 1])
        with stage(nc, "x_load", "unused") as (block, load, _unused):
            @block.sync
            def _(sp):
                sp.dma_start(k.X[:, :, :], d["x"]).then_inc(load, 16)
                sp.dma_start(k.ident[:, :], d["ident"]).then_inc(load, 16)
                sp.dma_start(k.iota[:, :], d["iota16"]).then_inc(load, 16)
                sp.dma_start(k.twos[:, :], d["twos"]).then_inc(load, 16)
                sp.wait_ge(load, 64)

            @block.gpsimd
            def _(pool):
                nc.gpsimd.memset(k.onesb[:, :], 1.0)
                nc.gpsimd.memset(k.ones[:, :], 1.0)

        for layer in (layer0_cross, layer0_self, layer0_ff, layer1_cross, layer1_self, layer1_ff,
                      layer2_cross, layer2_self, layer2_ff, layer3_cross, layer3_self, layer3_ff):
            layer(nc, k, d)

        with stage(nc, "stored", "unused2") as (block, stored, _unused):
            @block.sync
            def _(sp):
                sp.dma_start(out.rearrange("b (i p) f -> p (b i) f", p=P), k.X[:, :, :]).then_inc(stored, 16)
                sp.wait_ge(stored, 16)


def layouts(inp):
    def rows(w):
        return np.ascontiguousarray(np.asarray(w).reshape(-1, P, np.asarray(w).shape[-1]).transpose(1, 0, 2))

    def cols(v):
        return np.ascontiguousarray(np.asarray(v).reshape(-1, P).T)

    def spread(v):
        return np.ascontiguousarray(np.broadcast_to(np.asarray(v).reshape(1, -1), (P, np.asarray(v).size)))

    i = {n: np.asarray(a) for n, a in inp.items()}
    a = {}
    a["x"] = rows(i["x"].reshape(T, D))
    ctx = i["ctx_1024"]
    a["ctxT"] = np.stack([rows(np.ascontiguousarray(ctx[b].T)) for b in range(B)])
    a["ctx_rows"] = np.stack([rows(ctx[b]) for b in range(B)])
    a["ident"] = np.eye(P, dtype=np.float32)
    a["iota16"] = np.ascontiguousarray(np.broadcast_to(np.arange(NH, dtype=np.float32), (P, NH)))
    a["L0x_wqT"], a["L0x_wk"] = rows(i["L0_xattn_Wq"].T), rows(i["L0_xattn_Wk"])
    a["L0x_bq"] = cols(i["L0_xattn_bq"])
    a["L0x_wvT"], a["L0x_bv"] = rows(i["L0_xattn_Wv"].T), cols(i["L0_xattn_bv"])
    a["L0x_woT"], a["L0x_bo"] = rows(i["L0_xattn_Wo"].T), spread(i["L0_xattn_bo"])
    for more in (cross_layouts, cross64_layouts, expert_layouts, self_layouts, scan_layouts):
        more(a, i, rows, cols, spread)
    return a


def kernel(**inputs):
    import concourse.bacc as bacc
    from concourse.bass_utils import run_bass_kernel_spmd

    nc = bacc.Bacc("TRN2", target_bir_lowering=False, num_devices=1)
    arrays = {"in_" + n: a for n, a in layouts(inputs).items()}
    d = {n[3:]: nc.dram_tensor(n, a.shape, mybir.dt.from_np(a.dtype), kind="ExternalInput").ap() for n, a in arrays.items()}
    out = nc.dram_tensor("out", (B, S, D), F32, kind="ExternalOutput").ap()
    program(nc, d, out)
    r = run_bass_kernel_spmd(nc, [arrays], core_ids=[0])
    return r.results[0]["out"]
```

```python
from contextlib import ExitStack, contextmanager

import numpy as np
import concourse.bass as bass
from concourse import mybir

ALU = mybir.AluOpType
ACT = mybir.ActivationFunctionType
F32 = mybir.dt.float32
BF16 = mybir.dt.bfloat16
U32 = mybir.dt.uint32
AX = mybir.AxisListType.X

P = 128
B = 2
S = 256
D = 256
KC = D // P
T = B * S
TT = T // P
QT = S // P
CTX = 4096
NH = 16


@contextmanager
def stage(nc, *names):
    with ExitStack() as held:
        sems = [held.enter_context(nc.semaphore(n)) for n in names]
        with nc.Block(no_gpsimd_drain=True) as block:
            yield (block, *sems)
        numbers = sorted(s.num for s in sems)
        starts = [n for n in numbers if n - 1 not in numbers]
        runs = [range(n, next(m for m in range(n, n + len(numbers) + 1) if m not in numbers)) for n in starts]
        for run in runs:
            nc.all_engine_barrier(sems_to_clear=run)


class Tensors:

    def __init__(self, nc):
        self.nc, self.held = nc, ExitStack()

    def __enter__(self):
        return self

    def __exit__(self, *said):
        return self.held.__exit__(*said)

    def sb(self, name, shape, dt=F32):
        return self.held.enter_context(self.nc.sbuf_tensor(name, shape, dt))

    def ps(self, name, shape, dt=F32):
        return self.held.enter_context(self.nc.psum_tensor(name, shape, dt))



def layer_norm(nc, k, src, dst, name, eps=1e-5):
    with Tensors(nc) as t, stage(nc, name + "_stats", name + "_var", name + "_std", name + "_rstd") as (
            block, stats_done, var_done, std_done, rstd_done):
        stats = t.sb(name + "_bn", [P, TT, 6])
        mv = t.sb(name + "_mv", [P, TT, 2])
        std = t.sb(name + "_sd", [P, TT])
        rstd = t.sb(name + "_rs", [P, TT])

        @block.vector
        def _(dve):
            for i in range(TT):
                nc.vector.bn_stats(stats[:, i, :], src[:, i, :]).then_inc(stats_done, 1)
            for i in range(TT):
                dve.wait_ge(stats_done, i + 1)
                nc.vector.bn_aggr(mv[:, i, :], stats[:, i, :]).then_inc(var_done, 1)
            dve.wait_ge(var_done, TT)
            nc.vector.tensor_scalar(std[:, :], mv[:, :, 1], eps, None, ALU.add).then_inc(var_done, 1)
            dve.wait_ge(std_done, 1)
            nc.vector.reciprocal(rstd[:, :], std[:, :]).then_inc(rstd_done, 1)
            dve.wait_ge(rstd_done, 1)
            for i in range(TT):
                nc.vector.tensor_scalar(dst[:, i, :], src[:, i, :], mv[:, i, 0:1], rstd[:, i:i + 1],
                                        ALU.subtract, ALU.mult)

        @block.scalar
        def _(act):
            act.wait_ge(var_done, TT + 1)
            nc.scalar.activation(std[:, :], std[:, :], ACT.Sqrt).then_inc(std_done, 1)


def transpose_tokens(nc, k, src, dst, name, chunks=KC, gain=None, shift=None):
    with Tensors(nc) as t, stage(nc, name + "_turned", name + "_copied") as (block, turned, copied):
        flip = t.ps(name + "_flip", [P, 2, T])
        loads = 32 * (gain is not None)
        if gain is not None:
            gb = t.sb(name + "_gb", [P, 2, chunks])

        @block.sync
        def _(sp):
            if gain is not None:
                sp.dma_start(gb[:, 0, :], gain).then_inc(copied, 16)
                sp.dma_start(gb[:, 1, :], shift).then_inc(copied, 16)

        @block.tensor
        def _(pe):
            for c in range(chunks):
                if c >= 2:
                    pe.wait_ge(copied, loads + c - 1)
                for i in range(TT):
                    m = nc.tensor.transpose(flip[:, c % 2, i * P:(i + 1) * P], src[:, i, c * P:(c + 1) * P],
                                            k.ident[:, :])
                m.then_inc(turned, 1)

        @block.scalar
        def _(act):
            if gain is not None:
                act.wait_ge(copied, loads)
            for c in range(chunks):
                act.wait_ge(turned, c + 1)
                if gain is not None:
                    nc.scalar.activation(dst[:, c, :], flip[:, c % 2, :], ACT.Identity, bias=gb[:, 1, c:c + 1],
                                         scale=gb[:, 0, c:c + 1]).then_inc(copied, 1)
                else:
                    nc.scalar.copy(dst[:, c, :], flip[:, c % 2, :]).then_inc(copied, 1)


def project_residual(nc, k, srcT, w, name, chunks=KC, bias=None, doubled=False):
    with Tensors(nc) as t, stage(nc, name + "_load", name + "_mm", name + "_sum") as (block, load, mm, summed):
        wt = t.sb(name + "_w", [P, chunks, D])
        br = t.sb(name + "_b", [P, D])
        out = t.ps(name + "_o", [P, TT, 512])

        @block.sync
        def _(sp):
            sp.dma_start(wt[:, :, :], w).then_inc(load, 16)
            if bias is not None:
                sp.dma_start(br[:, :], bias).then_inc(load, 16)

        @block.tensor
        def _(pe):
            pe.wait_ge(load, 32 if bias is not None else 16)
            for i in range(TT):
                for c in range(chunks):
                    m = nc.tensor.matmul(out[:, i, 0:D], srcT[:, c, i * P:(i + 1) * P], wt[:, c, :],
                                         start=(c == 0), stop=(c == chunks - 1))
                m.then_inc(mm, 1)

        @block.vector
        def _(dve):
            if bias is not None:
                dve.wait_ge(load, 32)
                for i in range(TT):
                    last = nc.vector.scalar_tensor_tensor(k.X[:, i, :], k.X[:, i, :], 2.0 if doubled else 1.0,
                                                          br[:, :], ALU.mult, ALU.add)
                last.then_inc(summed, 1)
                dve.wait_ge(summed, 1)
            for i in range(TT):
                dve.wait_ge(mm, i + 1)
                nc.vector.tensor_tensor(k.X[:, i, :], out[:, i, 0:D], k.X[:, i, :], ALU.add)



def context_attention_one_head(nc, k, d):
    KT = CTX // P
    STEPS = KT // 2
    SCALE = float(D) ** -0.5
    with Tensors(nc) as t:
        QK = t.sb("l0q_keys", [P, KC, T])
        OT = t.sb("l0_out", [P, KC, T])
        V = t.sb("l0_values", [P, TT, D])
        with Tensors(nc) as u, stage(nc, "l0q_load", "l0q_mm", "l0q_ev") as (block, load, mm, ev):
            wq = u.sb("l0_wq", [P, KC, D])
            wk = u.sb("l0_wk", [P, KC, D])
            bq = u.sb("l0_bq", [P, KC])
            qT = u.sb("l0_qT", [P, KC, T])
            ps = u.ps("l0_qps", [P, 2 * KC, T])

            @block.sync
            def _(sp):
                sp.dma_start(wq[:, :, :], d["L0x_wqT"]).then_inc(load, 16)
                sp.dma_start(wk[:, :, :], d["L0x_wk"]).then_inc(load, 16)
                sp.dma_start(bq[:, :], d["L0x_bq"]).then_inc(load, 16)

            @block.tensor
            def _(pe):
                pe.wait_ge(load, 48)
                for half, (w, src) in enumerate(((wq, k.NT), (wk, qT))):
                    if half:
                        pe.wait_ge(ev, KC)
                    for m in range(KC):
                        for c in range(KC):
                            i = nc.tensor.matmul(ps[:, KC * half + m, :], w[:, c, m * P:(m + 1) * P], src[:, c, :],
                                                 start=(c == 0), stop=(c == KC - 1))
                        i.then_inc(mm, 1)

            @block.scalar
            def _(act):
                act.wait_ge(load, 48)
                for m in range(KC):
                    act.wait_ge(mm, m + 1)
                    nc.scalar.activation(qT[:, m, :], ps[:, m, :], ACT.Identity, bias=bq[:, m:m + 1]).then_inc(ev, 1)
                for m in range(KC):
                    act.wait_ge(mm, KC + m + 1)
                    nc.scalar.copy(QK[:, m, :], ps[:, KC + m, :]).then_inc(ev, 1)

        with nc.Fori(0, B) as b:
            with Tensors(nc) as u, stage(nc, "l0_load0", "l0_load1", "l0_load2", "l0_load3", "l0_rows_load", "l0_casts", "l0_peaks", "l0_peak_read", "l0_diag", "l0_scored",
                                         "l0_exps", "l0_averaged", "l0_normed") as (
                    block, load0, load1, load2, load3, rows_load, casts, peaks, peak_read, diag, scored, exps, averaged, normed):
                NB = CTX // 512
                loads = (load0, load1, load2, load3)
                cT = u.sb("l0_cT", [P, KC, CTX])
                cTb = u.sb("l0_cTb", [P, KC, CTX], BF16)
                V1 = u.sb("l0_V1", [P, KT, D + 1])
                q = u.sb("l0_q", [P, KC, S])
                qb = u.sb("l0_qb", [P, KC, S], BF16)
                pk = u.sb("l0_pk", [P, QT, NB])
                mx = u.sb("l0_mx", [P, QT])
                dg = u.sb("l0_dg", [P, QT, P], BF16)
                pr = u.sb("l0_pr", [P, 2, 2, S])
                rec = u.sb("l0_rec", [P, QT])
                psm = u.ps("l0_psm", [P, 2, 512])
                pss = u.ps("l0_pss", [P, 2, 2, S])
                pso = u.ps("l0_pso", [P, QT, 512])

                @block.sync
                def _(sp):
                    for x, load in enumerate(loads):
                        span = slice(x * CTX // 4, (x + 1) * CTX // 4)
                        sp.dma_start(cT[:, :, span], d["ctxT"][b][:, :, span]).then_inc(load, 16)
                    sp.dma_start(V1[:, :, 0:D], d["ctx_rows"][b]).then_inc(rows_load, 16)

                @block.gpsimd
                def _(pool):
                    nc.gpsimd.tensor_copy(q[:, :, :], QK[:, :, bass.ds(b * S, S)]).then_inc(casts, 1)
                    nc.gpsimd.memset(V1[:, :, D:D + 1], 1.0).then_inc(casts, 1)
                    pool.wait_ge(casts, 2)
                    nc.gpsimd.tensor_copy(qb[:, :, :], q[:, :, :]).then_inc(casts, 1)

                @block.tensor
                def _(pe):
                    pe.wait_ge(casts, 3)
                    for n in range(QT * NB):
                        j, qt = divmod(n, QT)
                        if qt == 0:
                            pe.wait_ge(exps, j + 1)
                        if n >= 2:
                            pe.wait_ge(peak_read, n - 1)
                        for c in range(KC):
                            m = nc.tensor.matmul(psm[:, n % 2, :], qb[:, c, qt * P:(qt + 1) * P],
                                                 cTb[:, c, j * 512:(j + 1) * 512], start=(c == 0), stop=(c == KC - 1))
                        m.then_inc(peaks, 1)
                    pe.wait_ge(diag, 1)
                    for s in range(STEPS + 1):
                        if s < STEPS:
                            if s >= 2:
                                pe.wait_ge(exps, NB + s - 1)
                            for qt in range(QT):
                                nc.tensor.matmul(pss[:, s % 2, :, qt * P:(qt + 1) * P], k.onesb[:, :],
                                                 dg[:, qt, :].unsqueeze(1).broadcast_to([P, 2, P]), start=(qt == 0), stop=False,
                                                 skip_group_check=True)
                            for h in range(2):
                                for c in range(KC):
                                    m = nc.tensor.matmul(pss[:, s % 2, h, :], cT[:, c, (2 * s + h) * P:(2 * s + h + 1) * P],
                                                         q[:, c, :], start=False, stop=(c == KC - 1), skip_group_check=True)
                            m.then_inc(scored, 1)
                        if s >= 1:
                            pe.wait_ge(exps, NB + s)
                            if s == 1:
                                pe.wait_ge(rows_load, 16)
                            for h in range(2):
                                kt = 2 * (s - 1) + h
                                for qt in range(QT):
                                    m = nc.tensor.matmul(pso[:, qt, 0:D + 1], pr[:, (s - 1) % 2, h, qt * P:(qt + 1) * P],
                                                         V1[:, kt, :], start=(kt == 0), stop=(kt == KT - 1))
                            m.then_inc(averaged, 1)

                @block.vector
                def _(dve):
                    for n in range(QT * NB):
                        dve.wait_ge(peaks, n + 1)
                        nc.vector.reduce_max(pk[:, n % QT, n // QT:n // QT + 1], psm[:, n % 2, :], AX).then_inc(peak_read, 1)
                    dve.wait_ge(peak_read, QT * NB)
                    nc.vector.reduce_max(mx[:, :], pk[:, :, :], AX).then_inc(peak_read, 1)
                    dve.wait_ge(peak_read, QT * NB + 1)
                    for qt in range(QT):
                        m = nc.vector.tensor_scalar(dg[:, qt, :], k.ident[:, :], mx[:, qt:qt + 1], -1.0, ALU.mult, ALU.mult)
                    m.then_inc(diag, 1)
                    dve.wait_ge(averaged, STEPS)
                    nc.vector.reciprocal(rec[:, :], pso[:, :, D]).then_inc(normed, 1)
                    dve.wait_ge(normed, 1)
                    for qt in range(QT):
                        nc.vector.tensor_scalar(V[:, bass.ds(b * QT + qt, 1), :], pso[:, qt:qt + 1, 0:D], rec[:, qt:qt + 1], None,
                                                ALU.mult)

                @block.scalar
                def _(act):
                    for j in range(NB):
                        act.wait_ge(loads[j // (NB // 4)], 16)
                        nc.scalar.copy(cTb[:, :, j * 512:(j + 1) * 512], cT[:, :, j * 512:(j + 1) * 512]).then_inc(exps, 1)
                    for s in range(STEPS):
                        act.wait_ge(scored, s + 1)
                        if s >= 2:
                            act.wait_ge(averaged, s - 1)
                        nc.scalar.activation(pr[:, s % 2, :, :], pss[:, s % 2, :, :], ACT.Exp, scale=SCALE).then_inc(exps, 1)

        transpose_tokens(nc, k, V, OT, "l0_avg")
        linear_T(nc, k, OT, QK, d["L0x_wvT"], "l0_v", bias=d["L0x_bv"])
        project_residual(nc, k, QK, d["L0x_woT"], "l0_o", bias=d["L0x_bo"])


def linear_T(nc, k, srcT, dstT, w, name, bias=None, out_chunks=KC, in_chunks=KC):
    with Tensors(nc) as t, stage(nc, name + "_load", name + "_mm", name + "_ev") as (block, load, mm, ev):
        wt = t.sb(name + "_w", [P, in_chunks, out_chunks * P])
        bt = t.sb(name + "_b", [P, out_chunks])
        ps = t.ps(name + "_ps", [P, 2, T])
        loads = 16 + 16 * (bias is not None)

        @block.sync
        def _(sp):
            sp.dma_start(wt[:, :, :], w).then_inc(load, 16)
            if bias is not None:
                sp.dma_start(bt[:, :], bias).then_inc(load, 16)

        @block.tensor
        def _(pe):
            pe.wait_ge(load, loads)
            for m in range(out_chunks):
                if m >= 2:
                    pe.wait_ge(ev, m - 1)
                for c in range(in_chunks):
                    i = nc.tensor.matmul(ps[:, m % 2, :], wt[:, c, m * P:(m + 1) * P], srcT[:, c, :],
                                         start=(c == 0), stop=(c == in_chunks - 1))
                i.then_inc(mm, 1)

        @block.scalar
        def _(act):
            act.wait_ge(load, loads)
            for m in range(out_chunks):
                act.wait_ge(mm, m + 1)
                if bias is not None:
                    nc.scalar.activation(dstT[:, m, :], ps[:, m % 2, :], ACT.Identity, bias=bt[:, m:m + 1]).then_inc(ev, 1)
                else:
                    nc.scalar.copy(dstT[:, m, :], ps[:, m % 2, :]).then_inc(ev, 1)


def layer0_cross(nc, k, d):
    layer_norm(nc, k, k.X, k.N, "n0")
    transpose_tokens(nc, k, k.N, k.NT, "t0")
    context_attention_one_head(nc, k, d)



HD16, HD64 = 16, 64


def context_attention(nc, k, d, pre, keysT, n_keys, hd, groups, out_tokens, biased):
    small = hd == HD16
    HPC = P // hd
    KT = n_keys // P
    SCALE = float(hd) ** -0.5
    G = KC * P
    UH = min(HPC, 4)
    SK = 4 // UH
    STEPS = KT // SK
    UNITS = [(c, h) for c in range(KC) for h in range(0, HPC, UH)]
    NQ = [(j * 512, min(512, n_keys - j * 512)) for j in range((n_keys + 511) // 512)]
    NB = len(NQ)
    VW = hd + 1 if small else hd
    GH = G // hd
    VOFF = P // UH
    NK = KC * NB
    NV = KT // 2
    NP = UH * QT * NB
    RING = 3 if small else 2
    KPART = (0, 1, 0, 1, 0, 2)
    QPART = (0, 0, 1, 1, 2, 0)
    NPART = len(KPART)
    ONE = NPART * HD16

    with Tensors(nc) as t:
        V = t.sb(pre + "_V", [P, KT, GH, VW])
        Kb = t.sb(pre + "_Kb", [P, KC, n_keys], BF16)
        qzb = t.sb(pre + "_qzb", [P, KC, HPC, S], BF16)
        if small:
            K2 = t.sb(pre + "_K2", [P, KC, n_keys], BF16)
            K3 = t.sb(pre + "_K3", [P, KC, n_keys], BF16)
            KS0 = t.sb(pre + "_KS0", [P, UH, n_keys], BF16)
            cT = t.sb(pre + "_cT", [P, KC, n_keys])
            KS = (KS0, cT[:, :, :].rearrange("p c n -> p (c n)").bitcast(BF16).rearrange("p (h n) -> p h n", h=UH))
            QS = t.sb(pre + "_QS", [P, GH, S], BF16)
            qscratch = nc.dram_tensor(pre + "_query_parts", (3, KC, P, S), BF16, kind="Internal").ap()
        else:
            cT = t.sb(pre + "_cT", [P, KC, n_keys])
            Ke = t.sb(pre + "_Ke", [P, KC, n_keys])
            Ko = t.sb(pre + "_Ko", [P, KC, n_keys])
            Q = t.sb(pre + "_Q", [P, KC, 2, S])
        with stage(nc, pre + "_fill", pre + "_fill1") as (block, filled, _v):
            @block.gpsimd
            def _(pool):
                if small:
                    nc.gpsimd.memset(V[:, :, :, hd:hd + 1], 1.0)

            @block.vector
            def _(dve):
                if not small:
                    nc.vector.memset(Q[:, :, :, :], 0.0)

        with nc.Fori(0, B) as b:
            if not small:
                normed_context(nc, k, d, "L1c", b, cT, V[:, :, :, :].rearrange("p t h e -> p (t h e)"), k.NTq, (Ke[64:128, :, :], Ko[0:64, :, :]))
            with nc.Fori(0, groups) as g:
                attend_group(nc, k, d, pre, locals(), b, g)


def attend_group(nc, k, d, pre, env, b, g):
    (keysT, n_keys, hd, out_tokens, biased, small, HPC, KT, SCALE, G, UH, SK, STEPS, UNITS, NQ, NB, VW, GH, VOFF, NK, NV, NP, RING,
     KPART, QPART, NPART, ONE, V, Kb, qzb, cT) = [env[n] for n in (
         "keysT n_keys hd out_tokens biased small HPC KT SCALE G UH SK STEPS UNITS NQ NB VW GH VOFF NK NV NP RING "
         "KPART QPART NPART ONE V Kb qzb cT").split()]
    if small:
        K2, K3, KS, QS, qscratch = [env[n] for n in ("K2", "K3", "KS", "QS", "qscratch")]
    else:
        Ke, Ko, Q = env["Ke"], env["Ko"], env["Q"]
    AHEAD = STEPS - 3
    names = ("wload cload0 cload1 cload2 cload3 nt_here q_mm q_ev qp_dve qp_pool q_out q_in k_mm k_act k_dve k_r k_pool v_mm v_ev bv_here ones_rows "
             "stack0 stack1 peaks peak_read peak rows row_in scored exps averaged sum_dve sum_pool o_copied turned normed chain").split()
    with Tensors(nc) as u, stage(nc, *[pre + "_" + n for n in names]) as (block, *sems):
        (wload, cload0, cload1, cload2, cload3, nt_here, q_mm, q_ev, qp_dve, qp_pool, q_out, q_in, k_mm, k_act, k_dve, k_r, k_pool, v_mm, v_ev,
         bv_here, ones_rows, stack0, stack1, peaks, peak_read, peak, rows, row_in, scored, exps, averaged, sum_dve, sum_pool, o_copied, turned,
         normed, chain) = sems
        cloads, stacks = (cload0, cload1, cload2, cload3), (stack0, stack1)
        if small:
            w = u.sb(pre + "_w", [P, 3, KC, G])
        else:
            acc = u.sb(pre + "_acc", [P, 2, SK, UH, S])
            w = acc[:, :, :, :, :].rearrange("p a e h s -> p (a e h s)")[:, 0:3 * KC * G].rearrange("p (x c n) -> p x c n", x=3, c=KC)
        bias = u.sb(pre + "_b2", [P, 2, KC])
        bv = u.sb(pre + "_bv", [P, G])
        mask = u.sb(pre + "_mask", [P, HPC])
        nt = u.sb(pre + "_nt", [P, KC, S])
        pk = u.sb(pre + "_pk", [P, 2, UH * QT, NB])
        mx = u.sb(pre + "_mx", [P, 2, UH * QT])
        pr = u.sb(pre + "_pr", [P, RING, SK, UH, S])
        rec = u.sb(pre + "_rec", [P, QT, UH])
        if small:
            oc = u.sb(pre + "_oc", [P, 2, S])
            tv = u.sb(pre + "_tv", [P, QT, UH, hd])
        else:
            spare = k.N[:, :, :].rearrange("p i f -> p (i f)")
            oc = spare[:, 0:2 * S].rearrange("p (a s) -> p a s", a=2)
            tv = spare[:, 2 * S:3 * S].rearrange("p (t h e) -> p t h e", t=QT, h=UH)
        pss = u.ps(pre + "_pss", [P, 2, 2, 512])
        psm = u.ps(pre + "_psm", [P, 2, 512])
        pso = u.ps(pre + "_pso", [P, 512])
        pst = u.ps(pre + "_pst", [P, 512])
        tiles = pss[:, :, :, :].rearrange("p a x n -> p (a x) n")
        if small:
            slots = [pr[:, x, :, :, :].rearrange("p e h s -> p (e h s)") for x in range(RING)]
            kf, kr = (slots[x].rearrange("p (a n) -> p a n", a=2) for x in range(2))
            qf = slots[2].rearrange("p (a c s) -> p a c s", a=2, c=KC)
            qp = u.sb(pre + "_qp", [P, 3, KC, S], BF16)
        else:
            psd = pst[:, 2 * P:2 * P + UH * QT]

        def unit_share(s):
            return min(NP, (s + 1) * NP // AHEAD)

        def first_share(r):
            return min(NP, (r + 1) * NP // (NV - 1))

        @block.sync
        def _(sp):
            sp.dma_start(w[:, 0, :, :], d[pre + "_w3"][g][:, 0]).then_inc(wload, 16)
            sp.dma_start(w[:, 1, :, :], d[pre + "_w3"][g][:, 1]).then_inc(wload, 16)
            sp.dma_start(mask[:, :], d["mask%d" % hd]).then_inc(wload, 16)
            sp.dma_start(bias[:, :, :], d[pre + "_b2"][g]).then_inc(wload, 16)
            sp.dma_start(w[:, 2, :, :], d[pre + "_w3"][g][:, 2]).then_inc(cloads[0] if not small else nt_here, 16)
            if small:
                for x in range(4):
                    n = n_keys // 4
                    sp.dma_start(cT[:, :, x * n:(x + 1) * n], keysT[b][:, :, x * n:(x + 1) * n]).then_inc(cloads[x], 16)
            sp.dma_start(bv[:, :], d[pre + "_bv"][g]).then_inc(bv_here, 16)
            if small:
                sp.wait_ge(qp_pool, 1)
                sp.wait_ge(qp_dve, 2)
                for c in range(KC):
                    sp.dma_start(qscratch[:, c].rearrange("x p s -> p x s"), qp[:, :, c, :]).then_inc(q_out, 16)
                sp.wait_ge(q_out, 16 * KC)
                for s, part in enumerate(QPART):
                    sp.dma_start(QS[s * hd:(s + 1) * hd, :, :],
                                 qscratch[part].rearrange("c (h r) s -> r (c h) s", r=hd)).then_inc(q_in, 16)
                for n, (c, h0) in enumerate(UNITS):
                    sp.wait_ge(k_act, NK)
                    sp.wait_ge(k_pool, NK)
                    sp.wait_ge(k_dve, NK)
                    if n == 1:
                        sp.wait_ge(v_mm, NV)
                    if n >= 2:
                        sp.wait_ge(scored, (n - 1) * STEPS)
                    for h in range(UH):
                        p0 = (h0 + h) * hd
                        for s, part in enumerate(KPART):
                            sp.dma_start(KS[n % 2][s * hd:(s + 1) * hd, h, :], (Kb, K2, K3)[part][p0:p0 + hd, c, :]).then_inc(stacks[n % 2], 16)

        @block.gpsimd
        def _(pool):
            nc.gpsimd.tensor_copy(nt[:, :, :], k.NTq[:, :, bass.ds(b * S, S)]).then_inc(nt_here, 1)
            if small:
                pool.wait_ge(qp_dve, 1)
                nc.gpsimd.tensor_copy(qp[:, 1, :, :], qf[:, 1, :, :]).then_inc(qp_pool, 1)
                for n in range(NK):
                    j, m = divmod(n, KC)
                    pool.wait_ge(k_r, n + 1)
                    nc.gpsimd.tensor_copy(K2[:, m, j * 512:(j + 1) * 512], kr[:, n % 2, :]).then_inc(k_pool, 1)
                pool.wait_ge(k_pool, NK)
                nc.gpsimd.memset(KS[0][ONE:ONE + 1, :, :], 1.0).then_inc(ones_rows, 1)
                pool.wait_ge(ones_rows, 1)
                pool.wait_ge(v_mm, NV)
                nc.gpsimd.memset(KS[1][ONE:ONE + 1, :, :], 1.0).then_inc(ones_rows, 1)
            else:
                for n in range(len(UNITS)):
                    for s in range(STEPS):
                        a = n * STEPS + s
                        pool.wait_ge(exps, a + 1)
                        if s:
                            pool.wait_ge(sum_pool, a)
                            i = nc.gpsimd.tensor_tensor(acc[:, n % 2, 1, :, :], acc[:, n % 2, 1, :, :], pr[:, a % RING, 1, :, :], ALU.add)
                        else:
                            i = nc.gpsimd.tensor_copy(acc[:, n % 2, 1, :, :], pr[:, a % RING, 1, :, :])
                        i.then_inc(sum_pool, 1)

        @block.tensor
        def _(pe):
            pe.wait_ge(wload, 64)
            pe.wait_ge(nt_here, 1 + 16 * small)
            for m in range(KC):
                for c in range(KC):
                    i = nc.tensor.matmul(pso[:, m * S:(m + 1) * S], w[:, 0, c, m * P:(m + 1) * P], nt[:, c, :],
                                         start=(c == 0), stop=(c == KC - 1))
            i.then_inc(q_mm, 1)

            def bank_free(n):
                if 4 <= n < NK + 4:
                    pe.wait_ge(k_act, n - 3)
                    if not small:
                        pe.wait_ge(k_dve, n - 3)
                elif n >= NK + 4:
                    pe.wait_ge(v_ev, n - 3 - NK)

            def peak_products(n, first, last):
                c, h0 = UNITS[n]
                for i in range(first, last):
                    hq, j = divmod(i, NB)
                    h, qt = divmod(hq, QT)
                    o, w_ = NQ[j]
                    if n * (NP + 1) + i >= 2:
                        pe.wait_ge(peak_read, n * (NP + 1) + max(i - 1, 0))
                    nc.tensor.matmul(psm[:, i % 2, 0:w_], qzb[:, c, h0 + h, qt * P:(qt + 1) * P], Kb[:, c, o:o + w_],
                                     start=True, stop=True).then_inc(peaks, 1)

            def peak_rows(n):
                pe.wait_ge(peak, n + 1)
                for h in range(UH):
                    p0 = ONE if small else (64, 0)[h]
                    for qt in range(QT):
                        hq = h * QT + qt
                        o = (h % 2) * S + qt * P if small else qt * P
                        i = nc.tensor.matmul(psm[p0:p0 + 1, h // 2 if small else h, o:o + P], mx[:, n % 2, hq:hq + 1], k.ident[:, :],
                                             start=True, stop=True)
                i.then_inc(rows, 1)

            for n in range(NK):
                j, m = divmod(n, KC)
                o, w_ = NQ[j]
                if small and m == 0 and j % (NB // 4) == 0:
                    pe.wait_ge(cloads[j // (NB // 4)], 16)
                bank_free(n)
                for c in range(KC):
                    i = nc.tensor.matmul(tiles[:, n % 4, 0:w_], w[:, 1, c, m * P:(m + 1) * P], cT[:, c, o:o + w_],
                                         start=(c == 0), stop=(c == KC - 1))
                i.then_inc(k_mm, 1)
            if not small:
                pe.wait_ge(cloads[0], 16)
            for r in range(NV):
                bank_free(NK + r)
                done, share = (first_share(r - 1), first_share(r) - first_share(r - 1)) if r else (0, first_share(0))
                for h in range(2):
                    for c in range(KC):
                        i = nc.tensor.matmul(tiles[:, (NK + r) % 4, h * G:(h + 1) * G], cT[:, c, (2 * r + h) * P:(2 * r + h + 1) * P],
                                             w[:, 2, c, :], start=(c == 0), stop=(c == KC - 1))
                        if h * KC + c == 3:
                            i.then_inc(v_mm, 1)
                        if r:
                            q = h * KC + c
                            peak_products(0, done + q * share // 4, done + (q + 1) * share // 4)
                if r == 0:
                    pe.wait_ge(k_act, NK)
                    pe.wait_ge(q_ev, KC * HPC)
                    peak_products(0, 0, share)
            peak_rows(0)

            def average(n, s):
                c, h0 = UNITS[n]
                pe.wait_ge(exps, n * STEPS + s + 1)
                if s == 0:
                    pe.wait_ge(o_copied, n) if n else pe.wait_ge(q_ev, KC * HPC)
                for e in range(SK):
                    for h in range(UH):
                        kt = s * SK + e
                        i = nc.tensor.matmul(pso[VOFF * h:VOFF * h + VW, 0:S], V[:, kt, c * HPC + h0 + h, :],
                                             pr[:, (n * STEPS + s) % RING, e, h, :], start=(kt == 0), stop=(kt == KT - 1),
                                             skip_group_check=True)
                i.then_inc(averaged, 1)

            def finish(n):
                pe.wait_ge(o_copied, n + 1)
                if n >= 1:
                    pe.wait_ge(normed, n)
                if not small:
                    pe.wait_ge(sum_dve, STEPS * (n + 1))
                    pe.wait_ge(sum_pool, STEPS * (n + 1))
                    for h in range(UH):
                        for qt in range(QT):
                            for e in range(SK):
                                nc.tensor.matmul(psd[:, qt * UH + h:qt * UH + h + 1], acc[:, n % 2, e, h, qt * P:(qt + 1) * P],
                                                 k.ones[:, 0:1], start=(e == 0), stop=(e == SK - 1), skip_group_check=True)
                for qt in range(QT):
                    i = nc.tensor.transpose(pst[:, qt * P:(qt + 1) * P], oc[:, n % 2, qt * P:(qt + 1) * P], k.ident[:, :])
                i.then_inc(turned, 1)

            pe.wait_ge(v_ev, NV)
            if small:
                pe.wait_ge(q_in, 16 * NPART)
            for n, (c, h0) in enumerate(UNITS):
                for s in range(STEPS):
                    a = n * STEPS + s
                    if s == 0:
                        pe.wait_ge(row_in, n + 1)
                        if small:
                            pe.wait_ge(stacks[n % 2], 16 * UH * NPART * (n // 2 + 1))
                            if n < 2:
                                pe.wait_ge(ones_rows, n + 1)
                    if a >= 2:
                        pe.wait_ge(exps, a - 1)
                    for e in range(SK):
                        for h in range(UH):
                            i_ = e * UH + h
                            kt = s * SK + e
                            o = pss[:, a % 2, i_ // 2, (i_ % 2) * S:(i_ % 2 + 1) * S]
                            if small:
                                i = nc.tensor.matmul(o, KS[n % 2][0:ONE + 1, h, kt * P:(kt + 1) * P], QS[0:ONE + 1, c * HPC + h0 + h, :],
                                                     start=True, stop=True)
                            else:
                                i = nc.tensor.matmul(o, (Ke, Ko)[h][:, c, kt * P:(kt + 1) * P], Q[:, c, h, :], start=True, stop=True)
                    i.then_inc(scored, 1)
                    first, last = unit_share(s - 1) if s else 0, unit_share(s)
                    if n + 1 < len(UNITS):
                        peak_products(n + 1, first, (first + last) // 2)
                    if s >= 1:
                        average(n, s - 1)
                    elif n >= 1:
                        average(n - 1, STEPS - 1)
                    if n + 1 < len(UNITS):
                        peak_products(n + 1, (first + last) // 2, last)
                        if s == STEPS - 2:
                            peak_rows(n + 1)
                    if s == 2 and n >= 1:
                        finish(n - 1)
            average(len(UNITS) - 1, STEPS - 1)
            finish(len(UNITS) - 1)

        @block.scalar
        def _(act):
            act.wait_ge(wload, 64)
            for n in range(NK):
                j, m = divmod(n, KC)
                o, w_ = NQ[j]
                act.wait_ge(k_mm, n + 1)
                kb = bias[:, 1, m:m + 1]
                if small:
                    if n >= 2:
                        act.wait_ge(k_r, n - 1)
                    nc.scalar.activation(kf[:, n % 2, 0:w_], tiles[:, n % 4, 0:w_], ACT.Identity, bias=kb)
                else:
                    nc.scalar.activation(Ke[0:64, m, o:o + w_], tiles[0:64, n % 4, 0:w_], ACT.Identity, bias=bias[0:64, 1, m:m + 1])
                nc.scalar.activation(Kb[:, m, o:o + w_], tiles[:, n % 4, 0:w_], ACT.Identity, bias=kb).then_inc(k_act, 1)
            for r in range(NV):
                act.wait_ge(v_mm, r + 1)
                nc.scalar.copy(V[:, 2 * r:2 * r + 2, :, 0:hd],
                               tiles[:, (NK + r) % 4, :].rearrange("p (t h e) -> p t h e", t=2, h=GH)).then_inc(v_ev, 1)
            for n in range(len(UNITS)):
                for s in range(STEPS):
                    a = n * STEPS + s
                    act.wait_ge(scored, a + 1)
                    if a >= RING:
                        act.wait_ge(averaged, a - RING + 1)
                        if not small:
                            act.wait_ge(sum_dve, a - RING + 1)
                            act.wait_ge(sum_pool, a - RING + 1)
                    nc.scalar.activation(pr[:, a % RING, :, :, :].rearrange("p e h q -> p (e h q)"),
                                         pss[:, a % 2, :, :].rearrange("p x q -> p (x q)"), ACT.Exp, scale=SCALE).then_inc(exps, 1)

        @block.vector
        def _(dve):
            links = [0]

            def link(i):
                links[0] += 1
                i.then_inc(chain, 1)
                dve.wait_ge(chain, links[0])

            dve.wait_ge(wload, 64)
            dve.wait_ge(q_mm, 1)
            for m in range(KC):
                for h in range(HPC):
                    nc.vector.tensor_scalar(qzb[:, m, h, :], pso[:, m * S:(m + 1) * S], bias[:, 0, m:m + 1], mask[:, h:h + 1],
                                            ALU.add, ALU.mult).then_inc(q_ev, 1)
                    if not small:
                        half = slice(64 * h, 64 * h + 64)
                        nc.vector.tensor_scalar(Q[half, m, h, :], pso[half, m * S:(m + 1) * S], bias[half, 0, m:m + 1], None,
                                                ALU.add).then_inc(chain, 1)
                        links[0] += 1
                if small:
                    nc.vector.tensor_scalar(qf[:, 0, m, :], pso[:, m * S:(m + 1) * S], bias[:, 0, m:m + 1], None, ALU.add).then_inc(chain, 1)
                    links[0] += 1
            dve.wait_ge(chain, links[0])
            if small:
                link(nc.vector.tensor_copy(qp[:, 0, :, :], qf[:, 0, :, :]))
                nc.vector.tensor_tensor(qf[:, 1, :, :], qf[:, 0, :, :], qp[:, 0, :, :], ALU.subtract).then_inc(qp_dve, 1)
                dve.wait_ge(qp_pool, 1)
                nc.vector.tensor_tensor(qp[:, 2, :, :], qf[:, 1, :, :], qp[:, 1, :, :], ALU.subtract).then_inc(qp_dve, 1)
            for n in range(NK + 1):
                j, m = divmod(n, KC)
                if small:
                    if n < NK:
                        dve.wait_ge(k_act, n + 1)
                        if n >= 2:
                            dve.wait_ge(k_pool, n - 1)
                            dve.wait_ge(k_dve, n - 1)
                        nc.vector.tensor_tensor(kr[:, n % 2, :], kf[:, n % 2, :], Kb[:, m, j * 512:(j + 1) * 512], ALU.subtract).then_inc(k_r, 1)
                    if n >= 1:
                        j, m = divmod(n - 1, KC)
                        dve.wait_ge(k_pool, n)
                        nc.vector.tensor_tensor(K3[:, m, j * 512:(j + 1) * 512], kr[:, (n - 1) % 2, :], K2[:, m, j * 512:(j + 1) * 512],
                                                ALU.subtract).then_inc(k_dve, 1)
                elif n < NK:
                    o, w_ = NQ[j]
                    dve.wait_ge(k_act, n + 1)
                    nc.vector.tensor_scalar(Ko[64:128, m, o:o + w_], tiles[64:128, n % 4, 0:w_], bias[64:128, 1, m:m + 1], None,
                                            ALU.add).then_inc(k_dve, 1)

            def read_peaks(n, first, last):
                for i in range(first, last):
                    hq, j = divmod(i, NB)
                    dve.wait_ge(peaks, n * NP + i + 1)
                    nc.vector.reduce_max(pk[:, n % 2, hq, j:j + 1], psm[:, i % 2, 0:NQ[j][1]], AX).then_inc(peak_read, 1)
                if first < NP <= last:
                    dve.wait_ge(peak_read, n * (NP + 1) + NP)
                    link(nc.vector.reduce_max(mx[:, n % 2, :], pk[:, n % 2, :, :], AX))
                    nc.vector.tensor_scalar(mx[:, n % 2, :], mx[:, n % 2, :], -1.0, None, ALU.mult).then_inc(peak, 1)

            def take_rows(n):
                c, h0 = UNITS[n]
                dve.wait_ge(rows, n + 1)
                if small:
                    i = nc.vector.tensor_copy(QS[ONE:ONE + 1, c * HPC + h0:c * HPC + h0 + UH, :].rearrange("p h q -> p (h q)"),
                                              psm[ONE:ONE + 1, :, :].rearrange("p x q -> p (x q)"))
                else:
                    link(nc.vector.tensor_copy(Q[64:65, c, 0, :], psm[64:65, 0, 0:S]))
                    i = nc.vector.tensor_copy(Q[0:1, c, 1, :], psm[0:1, 1, 0:S])
                link(i)
                nc.vector.tensor_copy(mx[:, n % 2, 0:1], mx[:, n % 2, 0:1]).then_inc(peak_read, 1)
                nc.vector.tensor_copy(pk[:, n % 2, 0, 0:1], pk[:, n % 2, 0, 0:1]).then_inc(row_in, 1)

            def sum_step(n, s):
                a = n * STEPS + s
                dve.wait_ge(exps, a + 1)
                if s == 0:
                    if n >= 2:
                        dve.wait_ge(turned, n - 1)
                    i = nc.vector.tensor_copy(acc[:, n % 2, 0, :, :], pr[:, a % RING, 0, :, :])
                else:
                    dve.wait_ge(sum_dve, a)
                    i = nc.vector.tensor_tensor(acc[:, n % 2, 0, :, :], acc[:, n % 2, 0, :, :], pr[:, a % RING, 0, :, :], ALU.add)
                i.then_inc(sum_dve, 1)

            def copy_out(n):
                dve.wait_ge(averaged, (n + 1) * STEPS)
                if n >= 2:
                    dve.wait_ge(turned, n - 1)
                for h in range(UH):
                    i = nc.vector.tensor_copy(oc[VOFF * h:VOFF * h + VW, n % 2, :], pso[VOFF * h:VOFF * h + VW, 0:S])
                    if h < UH - 1:
                        link(i)
                i.then_inc(o_copied, 1)

            def normalize(n):
                c, h0 = UNITS[n]
                dve.wait_ge(turned, n + 1)
                turn = pst[:, 0:2 * P].rearrange("p (t h e) -> p t h e", t=QT, h=UH)
                if small:
                    link(nc.vector.reciprocal(rec[:, :, :], turn[:, :, :, hd]))
                else:
                    link(nc.vector.reciprocal(rec[:, :, :], psd.rearrange("p (t h) -> p t h", t=QT)))
                i = nc.vector.tensor_tensor(tv[:, :, :, :], turn[:, :, :, 0:hd],
                                            rec[:, :, :].unsqueeze(3).broadcast_to([P, QT, UH, hd]), ALU.mult)
                i.then_inc(normed, 1)
                dve.wait_ge(normed, n + 1)
                f = c * P + h0 * hd
                for qt in range(QT):
                    if biased:
                        i = nc.vector.tensor_tensor(out_tokens[:, bass.ds(b * QT + qt, 1), bass.ds(g * G + f, UH * hd)],
                                                    tv[:, qt:qt + 1, :, :].rearrange("p t h e -> p t (h e)"),
                                                    bv[:, f:f + UH * hd].unsqueeze(1), ALU.add)
                    else:
                        i = nc.vector.tensor_copy(out_tokens[:, bass.ds(b * QT + qt, 1), bass.ds(g * G + f, UH * hd)],
                                                  tv[:, qt:qt + 1, :, :].rearrange("p t h e -> p t (h e)"))
                link(i)

            if VW < VOFF:
                link(nc.vector.memset(oc[:, :, :], 0.0))
            dve.wait_ge(bv_here, 16)
            for r in range(NV):
                read_peaks(0, first_share(r - 1) if r else 0, first_share(r))
            take_rows(0)
            for n in range(len(UNITS)):
                for s in range(STEPS):
                    if s == 1 and n >= 1:
                        copy_out(n - 1)
                    if n + 1 < len(UNITS):
                        read_peaks(n + 1, unit_share(s - 1) if s else 0, unit_share(s))
                    if not small:
                        sum_step(n, s)
                    if s == STEPS - 1 and n + 1 < len(UNITS):
                        take_rows(n + 1)
                    if s == 3 and n >= 1:
                        normalize(n - 1)
            copy_out(len(UNITS) - 1)
            normalize(len(UNITS) - 1)


def layer2_cross(nc, k, d):
    cross16(nc, k, d, "L2x")


def layer3_cross(nc, k, d):
    cross16(nc, k, d, "L3x")


def cross16(nc, k, d, pre):
    layer_norm(nc, k, k.X, k.N, pre + "n")
    transpose_tokens(nc, k, k.N, k.NT, pre + "t")
    k.NTq = k.NT
    with Tensors(nc) as t:
        context_attention(nc, k, d, pre, d["ctxT"], CTX, HD16, 1, k.N, True)
        OT = t.sb(pre + "_OT", [P, KC, T])
        transpose_tokens(nc, k, k.N, OT, pre + "o")
        project_residual(nc, k, OT, d[pre + "_woT"], pre + "p", bias=d[pre + "_bo"])


def cross_layouts(a, i, rows, cols, spread):
    for hd in (HD16, HD64):
        m = np.zeros((P, P // hd), np.float32)
        for h in range(P // hd):
            m[h * hd:(h + 1) * hd, h] = 1
        a["mask%d" % hd] = m
    for n, pre in (("L2_xattn_", "L2x"), ("L3_xattn_", "L3x")):
        a[pre + "_w3"] = np.stack([rows(i[n + w].T) for w in ("Wq", "Wk", "Wv")], 1)[None]
        a[pre + "_b2"] = np.stack([cols(i[n + w]) for w in ("bq", "bk")], 1)[None]
        a[pre + "_bv"] = spread(i[n + "bv"])[None]
        a[pre + "_woT"], a[pre + "_bo"] = rows(i[n + "Wo"].T), spread(i[n + "bo"])



def normed_context(nc, k, d, pre, b, cT, room, latents, ones):
    KT = CTX // P
    R = 8
    x = room[:, 0:KT * D].rearrange("p (i f) -> p i f", i=KT)
    with Tensors(nc) as t, stage(nc, *[pre + f"_load{i}" for i in range(KT // R)], pre + "_gb_load", pre + "_stat", pre + "_var", pre + "_std",
                                 pre + "_rstd", pre + "_norm", pre + "_turned", pre + "_copied", pre + "_filled") as (block, *sems):
        loads, (gb_load, stat, var, std_done, rstd_done, norm, turned, copied, filled) = sems[:KT // R], sems[KT // R:]
        gb = t.sb(pre + "_gb", [P, 2, KC])
        st = t.sb(pre + "_st", [P, 2, R, 6])
        mv = t.sb(pre + "_mv", [P, 2, R, 2])
        sd = t.sb(pre + "_sd", [P, 2, R])
        ps = t.ps(pre + "_ps", [P, 8, 512])

        @block.sync
        def _(sp):
            for i in range(KT // R):
                sp.dma_start(x[:, i * R:(i + 1) * R, :], d["ctx_rows"][b][:, i * R:(i + 1) * R, :]).then_inc(loads[i], 16)
            sp.dma_start(gb[:, 0, :], d[pre + "_mg"]).then_inc(gb_load, 16)
            sp.dma_start(gb[:, 1, :], d[pre + "_mb"]).then_inc(gb_load, 16)

        @block.gpsimd
        def _(pool):
            nc.gpsimd.tensor_copy(cT[:, :, CTX:CTX + S], latents[:, :, bass.ds(b * S, S)]).then_inc(filled, 1)
            for i, rows in enumerate(ones):
                pool.wait_ge(filled, i + 1)
                nc.gpsimd.memset(rows, 1.0).then_inc(filled, 1)

        @block.vector
        def _(dve):
            def norm_rows(r):
                dve.wait_ge(std_done, r + 1)
                nc.vector.reciprocal(sd[:, r % 2, :], sd[:, r % 2, :]).then_inc(rstd_done, 1)
                dve.wait_ge(rstd_done, r + 1)
                for i in range(R):
                    n = r * R + i
                    nc.vector.tensor_scalar(x[:, n, :], x[:, n, :], mv[:, r % 2, i, 0:1], sd[:, r % 2, i:i + 1],
                                            ALU.subtract, ALU.mult).then_inc(norm, 1)

            for r in range(KT // R):
                dve.wait_ge(loads[r], 16)
                if r >= 2:
                    dve.wait_ge(norm, (r - 1) * R)
                for i in range(R):
                    nc.vector.bn_stats(st[:, r % 2, i, :], x[:, r * R + i, :]).then_inc(stat, 1)
                for i in range(R):
                    dve.wait_ge(stat, r * R + i + 1)
                    nc.vector.bn_aggr(mv[:, r % 2, i, :], st[:, r % 2, i, :]).then_inc(var, 1)
                dve.wait_ge(var, r * (R + 1) + R)
                nc.vector.tensor_scalar(sd[:, r % 2, :], mv[:, r % 2, :, 1], 1e-5, None, ALU.add).then_inc(var, 1)
                if r >= 1:
                    norm_rows(r - 1)
            norm_rows(KT // R - 1)

        @block.tensor
        def _(pe):
            for q in range(KT // 4):
                pe.wait_ge(norm, 4 * q + 4)
                if q >= 4:
                    pe.wait_ge(copied, KC * (q - 3))
                for c in range(KC):
                    for e in range(4):
                        m = nc.tensor.transpose(ps[:, (KC * q + c) % 8, e * P:(e + 1) * P], x[:, 4 * q + e, c * P:(c + 1) * P], k.ident[:, :])
                    m.then_inc(turned, 1)

        @block.scalar
        def _(act):
            act.wait_ge(gb_load, 32)

            def copy_banks(q):
                for c in range(KC):
                    n = KC * q + c
                    act.wait_ge(turned, n + 1)
                    nc.scalar.activation(cT[:, c, q * 512:(q + 1) * 512], ps[:, n % 8, :], ACT.Identity, bias=gb[:, 1, c:c + 1],
                                         scale=gb[:, 0, c:c + 1]).then_inc(copied, 1)

            for r in range(KT // R):
                act.wait_ge(var, (r + 1) * (R + 1))
                nc.scalar.activation(sd[:, r % 2, :], sd[:, r % 2, :], ACT.Sqrt).then_inc(std_done, 1)
                if r >= 1:
                    copy_banks(2 * r - 2)
                    copy_banks(2 * r - 1)
            copy_banks(KT // 4 - 2)
            copy_banks(KT // 4 - 1)


def layer1_cross(nc, k, d):
    layer_norm(nc, k, k.X, k.N, "L1na")
    layer_norm(nc, k, k.N, k.N, "L1nb")
    transpose_tokens(nc, k, k.N, k.NT, "L1t", gain=d["L1x_lg"], shift=d["L1x_lb"])
    k.NTq = k.NT
    with Tensors(nc) as t:
        O = t.sb("L1x_O", [P, TT, NH * HD64])
        context_attention(nc, k, d, "L1x", None, CTX + S, HD64, 4, O, False)
        OT = t.sb("L1x_OT", [P, NH * HD64 // P, T])
        transpose_tokens(nc, k, O, OT, "L1o", chunks=NH * HD64 // P)
        project_residual(nc, k, OT, d["L1x_wo"], "L1p", chunks=NH * HD64 // P)


def cross64_layouts(a, i, rows, cols, spread):
    n = "L1_xattn_"
    a["L1c_mg"], a["L1c_mb"] = cols(i[n + "ln_m_g"]), cols(i[n + "ln_m_b"])
    a["L1x_lg"], a["L1x_lb"] = cols(i[n + "ln_l_g"]), cols(i[n + "ln_l_b"])
    inner = NH * HD64
    ws = (i[n + "Wq"], i[n + "Wkv"][:, :inner], i[n + "Wkv"][:, inner:])
    a["L1x_w3"] = np.stack([np.stack([rows(w[:, g * D:(g + 1) * D]) for w in ws], 1) for g in range(4)])
    a["L1x_b2"] = np.zeros((4, P, 2, KC), np.float32)
    a["L1x_bv"] = np.zeros((4, P, D), np.float32)
    a["L1x_wo"] = rows(i[n + "Wout"])



def experts(nc, k, pieces, name, n_experts, chunks, body, kind, weights, b1=None):
    gated = kind == "swiglu"
    NIN = 2 if gated else 1
    PW = 2 * (NIN * KC * P + D)
    PIECES = body * chunks // 2
    STEPS = body * chunks
    NR = 2
    with nc.Fori(0, n_experts // body) as it, Tensors(nc) as t:
        with stage(nc, *[name + f"_load{i}" for i in range(PIECES)], name + "_w", name + "_in", name + "_act", name + "_hid",
                   name + "_out", name + "_added") as (block, *sems):
            loads, (w_here, in_done, act_done, hid_done, out_done, added) = sems[:PIECES], sems[PIECES:]
            wt = t.sb(name + "_wt", [P, PIECES, PW])
            wi = t.sb(name + "_wi", [P, TT, body])
            g_act = t.sb(name + "_g", [P, 2, T])
            hT = t.sb(name + "_h", [P, 3, T])
            if b1 is not None:
                bt = t.sb(name + "_b1", [P, STEPS])
            pin = t.ps(name + "_pin", [P, NR, NIN, T])
            pout = t.ps(name + "_pout", [P, TT, 512])

            def w_in(s, part, c):
                p, half = divmod(s, 2)
                o = (part * KC + c) * 2 * P + half * P
                return wt[:, p, o:o + P]

            def w_out(s):
                p, half = divmod(s, 2)
                o = NIN * KC * 2 * P + half * D
                return wt[:, p, o:o + D]

            @block.sync
            def _(sp):
                if b1 is not None:
                    sp.dma_start(bt[:, :], b1[it]).then_inc(w_here, 16)
                for p in range(PIECES):
                    sp.dma_start(wt[:, p, :], pieces[it * PIECES + p]).then_inc(loads[p], 16)

            @block.gpsimd
            def _(pool):
                nc.gpsimd.tensor_copy(wi[:, :, :], weights[:, :, bass.ds(it * body, body)]).then_inc(w_here, 1)

            @block.tensor
            def _(pe):
                for s in range(STEPS + 1):
                    if s < STEPS:
                        if s % 2 == 0:
                            pe.wait_ge(loads[s // 2], 16)
                        if s >= NR:
                            pe.wait_ge(hid_done, s - NR + 1)
                        for part in range(NIN):
                            for c in range(KC):
                                m = nc.tensor.matmul(pin[:, s % NR, part, :], w_in(s, part, c), k.NT[:, c, :],
                                                     start=(c == 0), stop=(c == KC - 1))
                        m.then_inc(in_done, 1)
                    if s >= 1:
                        r = s - 1
                        pe.wait_ge(hid_done, r + 1)
                        e, j = divmod(r, chunks)
                        for i in range(TT):
                            if j == 0 and e >= 1:
                                pe.wait_ge(added, TT * (e - 1) + i + 1)
                            m = nc.tensor.matmul(pout[:, i, 0:D], hT[:, r % 3, i * P:(i + 1) * P], w_out(r),
                                                 start=(j == 0), stop=(j == chunks - 1))
                            m.then_inc(out_done, 1)

            @block.scalar
            def _(act):
                if b1 is not None:
                    act.wait_ge(w_here, 17)
                for s in range(STEPS):
                    act.wait_ge(in_done, s + 1)
                    if gated:
                        if s >= 2:
                            act.wait_ge(hid_done, s - 1)
                        nc.scalar.activation(g_act[:, s % 2, :], pin[:, s % NR, 1, :], ACT.Silu).then_inc(act_done, 1)
                    else:
                        if s >= 3:
                            act.wait_ge(out_done, TT * (s - 2))
                        if kind == "gelu":
                            nc.scalar.activation(hT[:, s % 3, :], pin[:, s % NR, 0, :], ACT.Gelu_apprx_tanh,
                                                 bias=bt[:, s:s + 1]).then_inc(hid_done, 1)
                        elif kind == "gelu_erf":
                            nc.scalar.activation(hT[:, s % 3, :], pin[:, s % NR, 0, :], ACT.Gelu,
                                                 bias=bt[:, s:s + 1]).then_inc(hid_done, 1)
                        else:
                            nc.scalar.activation(hT[:, s % 3, :], pin[:, s % NR, 0, :], ACT.Relu).then_inc(hid_done, 1)

            @block.vector
            def _(dve):
                dve.wait_ge(w_here, 17 if b1 is not None else 1)

                def add_expert(e):
                    for i in range(TT):
                        dve.wait_ge(out_done, TT * chunks * e + TT * (chunks - 1) + i + 1)
                        nc.vector.scalar_tensor_tensor(k.X[:, i, :], pout[:, i, 0:D], wi[:, i, e:e + 1], k.X[:, i, :],
                                                       ALU.mult, ALU.add).then_inc(added, 1)

                done = 0
                for s in range(STEPS):
                    if gated:
                        dve.wait_ge(act_done, s + 1)
                        if s >= 3:
                            dve.wait_ge(out_done, TT * (s - 2))
                        nc.vector.tensor_tensor(hT[:, s % 3, :], pin[:, s % NR, 0, :], g_act[:, s % 2, :], ALU.mult).then_inc(hid_done, 1)
                    if s >= 1 and s % chunks == 0:
                        if done:
                            dve.wait_ge(added, TT * done)
                        add_expert(done)
                        done += 1
                if done:
                    dve.wait_ge(added, TT * done)
                add_expert(done)


def route(nc, k, d, name, E, kind, W, capacity=0):
    K2 = kind in ("capacity_slots", "capacity_tokens")
    with Tensors(nc) as t, stage(nc, name + "_load", name + "_mm", name + "_chain", name + "_act", name + "_shifted", name + "_choices") as (
            block, load, mm, chain, act_done, shifted, choices):
        wr = t.sb(name + "_wr", [P, KC, E])
        tri = t.sb(name + "_tri", [P, P])
        bg = t.sb(name + "_bg", [P, E])
        lg = t.sb(name + "_lg", [P, TT, E])
        ex = t.sb(name + "_ex", [P, TT, E])
        m8 = t.sb(name + "_m8", [P, TT, 8])
        i8 = t.sb(name + "_i8", [P, TT, 8], U32)
        f8 = t.sb(name + "_f8", [P, TT, 8])
        sm = t.sb(name + "_sm", [P, TT])
        g1 = t.sb(name + "_g1", [P, TT, 2])
        oh = t.sb(name + "_oh", [P, TT, 4, E])
        kp = t.sb(name + "_kp", [P, TT, 2, E])
        ps = t.ps(name + "_ps", [P, TT, E])
        pc = t.ps(name + "_pc", [P, TT, 512])
        CW = 2 * E if kind == "capacity_slots" else E

        @block.sync
        def _(sp):
            sp.dma_start(wr[:, :, :], d[name + "_wr"]).then_inc(load, 16)
            if K2:
                sp.dma_start(tri[:, :], d["tri_below" if kind == "capacity_slots" else "tri_upto"]).then_inc(load, 16)
            if kind == "capacity_slots":
                sp.dma_start(bg[:, :], d[name + "_bg"]).then_inc(load, 16)

        LOADS = 16 * (1 + K2 + (kind == "capacity_slots"))

        @block.tensor
        def _(pe):
            pe.wait_ge(load, LOADS)
            for i in range(TT):
                for c in range(KC):
                    m = nc.tensor.matmul(ps[:, i, :], k.NT[:, c, i * P:(i + 1) * P], wr[:, c, :], start=(c == 0), stop=(c == KC - 1))
            m.then_inc(mm, 1)
            if K2:
                pe.wait_ge(choices, 1)

                def chosen(j):
                    slots = oh[:, j, 0:2, :] if kind == "capacity_slots" else oh[:, j, 2:3, :]
                    return slots.rearrange("p a e -> p (a e)")

                for i in range(TT):
                    terms = [(pc[:, i, 0:CW], tri, chosen(i))] + [(pc[:, i, 0:CW], k.ones, chosen(j)) for j in range(i)]
                    if kind == "capacity_slots":
                        terms += [(pc[:, i, E:2 * E], k.ones, oh[:, j, 0, :]) for j in range(TT)]
                    for n, (o, left, right) in enumerate(terms):
                        m = nc.tensor.matmul(o, left[:, :], right, start=(n == 0), stop=(n == len(terms) - 1), skip_group_check=True)
                m.then_inc(mm, 1)

        @block.scalar
        def _(act):
            if kind == "sigmoid_top4":
                act.wait_ge(mm, 1)
                nc.scalar.activation(lg[:, :, :], ps[:, :, :], ACT.Sigmoid).then_inc(act_done, 1)
            else:
                act.wait_ge(shifted, 1)
                nc.scalar.activation(ex[:, :, :], ex[:, :, :], ACT.Exp).then_inc(act_done, 1)

        @block.vector
        def _(dve):
            links = [0]

            def link(i):
                links[0] += 1
                i.then_inc(chain, 1)
                dve.wait_ge(chain, links[0])

            def one_hot(slot, i, j):
                return nc.vector.tensor_scalar(oh[:, i, slot, :], k.iota[:, 0:E], f8[:, i, j:j + 1], None, ALU.is_equal)

            dve.wait_ge(load, LOADS)
            dve.wait_ge(mm, 1)
            if kind == "sigmoid_top4":
                dve.wait_ge(act_done, 1)
            elif kind == "capacity_slots":
                link(nc.vector.tensor_tensor(lg[:, :, :], ps[:, :, :], bg[:, :].unsqueeze(1).broadcast_to([P, TT, E]), ALU.add))
            else:
                link(nc.vector.tensor_copy(lg[:, :, :], ps[:, :, :]))
            for i in range(TT):
                m = nc.vector.max(m8[:, i, :], lg[:, i, :])
            link(m)
            for i in range(TT):
                m = nc.vector.max_index(i8[:, i, :], m8[:, i, :], lg[:, i, :])
            link(m)
            link(nc.vector.tensor_copy(f8[:, :, :], i8[:, :, :]))
            if kind == "top1":
                for i in range(TT):
                    nc.vector.tensor_scalar(ex[:, i, :], lg[:, i, :], m8[:, i, 0:1], None, ALU.subtract)
                    m = one_hot(0, i, 0)
                m.then_inc(shifted, 1)
                dve.wait_ge(act_done, 1)
                link(nc.vector.reduce_sum(sm[:, :], ex[:, :, :], AX))
                link(nc.vector.reciprocal(sm[:, :], sm[:, :]))
                link(nc.vector.tensor_scalar(sm[:, :], sm[:, :], 2.0, None, ALU.mult))
                for i in range(TT):
                    m = nc.vector.tensor_scalar(W[:, i, 0:E], oh[:, i, 0, :], sm[:, i:i + 1], None, ALU.mult)
                link(m)
                nc.vector.memset(W[:, :, E - 1:E], 1.0)
            elif kind == "sigmoid_top4":
                link(nc.vector.reduce_sum(sm[:, :], m8[:, :, 0:4], AX))
                link(nc.vector.reciprocal(sm[:, :], sm[:, :]))
                for i in range(TT):
                    for j in range(4):
                        m = one_hot(j, i, j)
                link(m)
                link(nc.vector.tensor_tensor(kp[:, :, :, :], oh[:, :, 0:2, :], oh[:, :, 2:4, :], ALU.add))
                link(nc.vector.tensor_tensor(ex[:, :, :], kp[:, :, 0, :], kp[:, :, 1, :], ALU.add))
                for i in range(TT):
                    m = nc.vector.scalar_tensor_tensor(W[:, i, 0:E], lg[:, i, :], sm[:, i:i + 1], ex[:, i, :], ALU.mult, ALU.mult)
                nc.vector.memset(W[:, :, E:E + 2], 1.0)
            else:
                for i in range(TT):
                    nc.vector.tensor_scalar(ex[:, i, :], m8[:, i, :], m8[:, i, 0:1], None, ALU.subtract)
                    one_hot(0, i, 0)
                    m = one_hot(1, i, 1)
                m.then_inc(shifted, 1)
                if kind == "capacity_slots":
                    dve.wait_ge(shifted, 1)
                    nc.vector.tensor_copy(f8[:, :, 0:1], f8[:, :, 0:1]).then_inc(choices, 1)
                dve.wait_ge(act_done, 1)
                link(nc.vector.tensor_scalar(sm[:, :], ex[:, :, 1], 1.0, None, ALU.add))
                link(nc.vector.reciprocal(g1[:, :, 0], sm[:, :]))
                link(nc.vector.tensor_tensor(g1[:, :, 1], g1[:, :, 0], ex[:, :, 1], ALU.mult))
                if kind == "capacity_slots":
                    dve.wait_ge(mm, 2)
                    for i in range(TT):
                        m = nc.vector.tensor_scalar(kp[:, i, :, :].rearrange("p a e -> p (a e)"), pc[:, i, 0:2 * E], float(capacity), None,
                                                    ALU.is_lt)
                    link(m)
                    link(nc.vector.tensor_tensor(kp[:, :, :, :], kp[:, :, :, :], oh[:, :, 0:2, :], ALU.mult))
                else:
                    link(nc.vector.tensor_scalar(sm[:, :], g1[:, :, 1], 0.0, None, ALU.is_gt))
                    for i in range(TT):
                        m = nc.vector.scalar_tensor_tensor(oh[:, i, 2, :], oh[:, i, 1, :], sm[:, i:i + 1], oh[:, i, 0, :],
                                                           ALU.mult, ALU.add)
                    m.then_inc(choices, 1)
                    dve.wait_ge(mm, 2)
                    for i in range(TT):
                        m = nc.vector.tensor_scalar(ex[:, i, :], pc[:, i, 0:E], float(capacity), None, ALU.is_le)
                    link(m)
                    for a in range(2):
                        m = nc.vector.tensor_tensor(kp[:, :, a, :], ex[:, :, :], oh[:, :, a, :], ALU.mult)
                    link(m)
                for i in range(TT):
                    for a in range(2):
                        m = nc.vector.tensor_scalar(oh[:, i, 2 + a, :], kp[:, i, a, :], g1[:, i, a:a + 1], None, ALU.mult)
                link(m)
                nc.vector.tensor_tensor(W[:, :, 0:E], oh[:, :, 2, :], oh[:, :, 3, :], ALU.add)


def layer0_ff(nc, k, d):
    layer_norm(nc, k, k.X, k.N, "f0n")
    transpose_tokens(nc, k, k.N, k.NT, "f0t")
    with Tensors(nc) as t:
        W = t.sb("f0_W", [P, TT, 8])
        route(nc, k, d, "f0r", 8, "top1", W)
        experts(nc, k, d["f0_pieces"], "f0e", 8, 8, 2, "swiglu", W)


def layer1_ff(nc, k, d):
    layer_norm(nc, k, k.X, k.N, "f1n")
    transpose_tokens(nc, k, k.N, k.NT, "f1t")
    with Tensors(nc) as t:
        W = t.sb("f1_W", [P, TT, 8])
        route(nc, k, d, "f1r", 8, "capacity_slots", W, capacity=-(-12 * T * 2 // 80))
        weighted_bias(nc, k, d, W)
        experts(nc, k, d["f1_pieces"], "f1e", 8, 8, 2, "gelu", W, b1=d["f1_b1"])


def weighted_bias(nc, k, d, W):
    E = 8
    with Tensors(nc) as t, stage(nc, "wb_load", "wb_turned", "wb_copied", "wb_mm") as (block, load, turned, copied, mm):
        b2 = t.sb("wb_b2", [E, D])
        wT = t.sb("wb_wT", [E, T])
        pt = t.ps("wb_pt", [P, T])
        po = t.ps("wb_po", [P, TT, 512])

        @block.sync
        def _(sp):
            sp.dma_start(b2[:, :], d["f1_b2"]).then_inc(load, 16)

        @block.tensor
        def _(pe):
            for i in range(TT):
                m = nc.tensor.transpose(pt[0:E, i * P:(i + 1) * P], W[:, i, :], k.ident[:, :])
            m.then_inc(turned, 1)
            pe.wait_ge(load, 16)
            pe.wait_ge(copied, 1)
            for i in range(TT):
                nc.tensor.matmul(po[:, i, 0:D], wT[:, i * P:(i + 1) * P], b2[:, :], start=True, stop=True).then_inc(mm, 1)

        @block.scalar
        def _(act):
            act.wait_ge(turned, 1)
            nc.scalar.copy(wT[:, :], pt[0:E, :]).then_inc(copied, 1)

        @block.vector
        def _(dve):
            for i in range(TT):
                dve.wait_ge(mm, i + 1)
                nc.vector.tensor_tensor(k.X[:, i, :], po[:, i, 0:D], k.X[:, i, :], ALU.add)


def layer2_ff(nc, k, d):
    layer_norm(nc, k, k.X, k.N, "f2n")
    transpose_tokens(nc, k, k.N, k.NT, "f2t")
    with Tensors(nc) as t:
        W = t.sb("f2_W", [P, TT, 8])
        route(nc, k, d, "f2r", 8, "capacity_tokens", W, capacity=T // 8)
        experts(nc, k, d["f2_pieces"], "f2e", 8, 4, 4, "relu", W)


def layer3_ff(nc, k, d):
    layer_norm(nc, k, k.X, k.N, "f3n")
    transpose_tokens(nc, k, k.N, k.NT, "f3t")
    with Tensors(nc) as t:
        W = t.sb("f3_W", [P, TT, 18])
        route(nc, k, d, "f3r", 16, "sigmoid_top4", W)
        experts(nc, k, d["f3_pieces"], "f3e", 18, 1, 6, "swiglu", W)


def expert_layouts(a, i, rows, cols, spread):
    def pieces(ins, w_out):
        e, _, h = ins[0].shape
        n = e * h // (2 * P)
        parts = [w.transpose(1, 0, 2).reshape(KC, P, n, 2 * P).transpose(2, 1, 0, 3).reshape(n, P, -1) for w in ins]
        parts.append(w_out.reshape(n, 2, P, D).transpose(0, 2, 1, 3).reshape(n, P, -1))
        return np.ascontiguousarray(np.concatenate(parts, 2))

    def with_shared(w, s):
        return np.concatenate([w, s], 0)

    n = "L0_ffn_"
    a["f0r_wr"] = rows(i[n + "w_router"])
    a["f0_pieces"] = pieces([with_shared(i[n + "w_up"], i[n + "ws_up"][None]), with_shared(i[n + "w_gate"], i[n + "ws_gate"][None])],
                            with_shared(i[n + "w_down"], i[n + "ws_down"][None]))
    n = "L1_ffn_"
    a["f1r_wr"], a["f1r_bg"] = rows(i[n + "Wg"]), spread(i[n + "bg"])
    a["f1_pieces"] = pieces([i[n + "W1"]], i[n + "W2"])
    a["f1_b1"] = np.ascontiguousarray(i[n + "b1"].reshape(4, 16, P).transpose(0, 2, 1))
    a["f1_b2"] = i[n + "b2"]
    n = "L2_ffn_"
    a["f2r_wr"] = rows(i[n + "expert_embeddings"].T)
    a["f2_pieces"] = pieces([i[n + "first_linear"].transpose(0, 2, 1)], i[n + "second_linear"].transpose(0, 2, 1))
    n = "L3_ffn_"
    a["f3r_wr"] = rows(i[n + "gate_w"].T)

    def halves(w):
        return w.reshape(D, 2, P).transpose(1, 0, 2)

    a["f3_pieces"] = pieces([with_shared(i[n + "e_vin"], halves(i[n + "vs_in"])), with_shared(i[n + "e_win"], halves(i[n + "ws_in"]))],
                            with_shared(i[n + "e_wout"], i[n + "ws_out"].reshape(2, P, D)))
    one = np.ones((P, P), np.float32)
    a["tri_below"], a["tri_upto"] = np.triu(one, 1), np.triu(one)



def linear_tokens(nc, k, srcT, dst, w, name, bias, width=D, wide=D, chunks=KC, func=None):
    with Tensors(nc) as t, stage(nc, name + "_load", name + "_mm", name + "_ev") as (block, load, mm, ev):
        wt = t.sb(name + "_w", [P, chunks, width])
        bt = t.sb(name + "_b", [P, width])
        ps = t.ps(name + "_ps", [P, TT, 512])

        @block.sync
        def _(sp):
            sp.dma_start(wt[:, :, :], w).then_inc(load, 16)
            if bias is not None:
                sp.dma_start(bt[:, :], bias).then_inc(load, 16)

        @block.tensor
        def _(pe):
            pe.wait_ge(load, 16 * (1 + (bias is not None)))
            for i in range(TT):
                for c in range(chunks):
                    m = nc.tensor.matmul(ps[:, i, 0:width], srcT[:, c, i * P:(i + 1) * P], wt[:, c, :],
                                         start=(c == 0), stop=(c == chunks - 1))
                m.then_inc(mm, 1)

        @block.vector
        def _(dve):
            for i in range(TT):
                dve.wait_ge(mm, i + 1)
                if bias is not None:
                    nc.vector.tensor_tensor(dst[:, i, 0:width], ps[:, i, 0:width], bt[:, :], ALU.add)
                else:
                    nc.vector.tensor_copy(dst[:, i, 0:width], ps[:, i, 0:width])


def self_attention(nc, k, d, pre, qT, kT, V, O, relative):
    hd, HPC, RW = HD16, P // HD16, 3 * P
    with nc.Fori(0, B) as b, nc.Fori(0, KC) as c, Tensors(nc) as t:
        qz = t.sb(pre + "_qz", [P, HPC, S])
        keys = t.sb(pre + "_keys", [P, S])
        vals = t.sb(pre + "_vals", [P, QT, P])
        mask = t.sb(pre + "_mask", [P, HPC])
        if relative:
            kz = t.sb(pre + "_kz", [P, HPC, S])
            emb = t.sb(pre + "_emb", [P, 2, 512])
            rows = t.sb(pre + "_rows", [P, 4, 4, RW])
            scratch = k.rel_scratch
        names = ("load masked rel rel_dve rel_act out0 out1 add0 add1 ready scored sum peak exp turned pT av chain scaled static").split()
        with Tensors(nc) as u, stage(nc, *[pre + "_" + n for n in names]) as (
                block, load, masked, rel, rel_dve, rel_act, out0, out1, add0, add1, ready, scored, summed, peak, expd, turned, pT_done, av,
                chain, scaled, static):
            LAG = 3 if relative else 0
            outs = (out0, out1)
            sc = u.sb(pre + "_sc", [P, 2, QT, S])
            pr = u.sb(pre + "_pr", [P, 2, QT, S])
            pT = u.sb(pre + "_pT", [P, 2, QT, QT, P])
            mx = u.sb(pre + "_mx", [P, HPC, QT])
            nm = u.sb(pre + "_nm", [P, HPC, QT])
            sums = u.sb(pre + "_sums", [P, HPC, QT])
            rec = u.sb(pre + "_rec", [P, HPC, QT])
            add = u.sb(pre + "_add", [P, 2, 4, S])
            pss = u.ps(pre + "_pss", [P, 2, QT, S])
            pst = u.ps(pre + "_pst", [P, 2, QT, QT, P])
            pso = u.ps(pre + "_pso", [P, 2, 512])
            if relative:
                psr = u.ps(pre + "_psr", [P, 2, 512])
            SC = 1.0 if relative else 0.25
            HEADS = range(HPC)

            @block.sync
            def _(sp):
                if not relative:
                    sp.dma_start(mask[:, :], d["mask16"]).then_inc(load, 16)
                    sp.dma_start(add[:, 0, 0:QT, :], d["causal"]).then_inc(load, 16)
                else:
                    sp.dma_start(mask[:, :], d["mask16"]).then_inc(load, 16)
                    sp.dma_start(emb[:, :, :], d["rel_emb"]).then_inc(load, 16)
                    for t_ in range(HPC + 1):
                        if t_ < HPC:
                            sp.wait_ge(rel_dve, 2 * (t_ + 1))
                            sp.wait_ge(rel_act, 2 * (t_ + 1))
                            sp.dma_start(scratch[t_].rearrange("x p w -> p x w"), rows[:, t_ % 4, :, :]).then_inc(outs[t_ % 2], 16)
                        if t_ >= 1:
                            h = t_ - 1
                            sp.wait_ge(outs[h % 2], 16 * (h // 2 + 1))
                            if h >= 2:
                                sp.wait_ge(summed, h - 1)
                                sp.wait_ge(scored, h - 1)
                            src = scratch[h]
                            skew = bass.AP(tensor=src.tensor, offset=src.offset + P - 1, ap=[[RW - 1, P], [P * RW, 4], [1, S]])
                            sp.dma_start(add[:, h % 2, :, :], skew).then_inc((add0, add1)[h % 2], 16)

            @block.gpsimd
            def _(pool):
                nc.gpsimd.tensor_copy(keys[:, :].unsqueeze(1), kT[:, bass.ds(c, 1), bass.ds(b * S, S)]).then_inc(static, 1)
                nc.gpsimd.tensor_copy(vals[:, :, :], V[:, bass.ds(b * QT, QT), bass.ds(c * P, P)]).then_inc(static, 1)
                if relative:
                    pool.wait_ge(static, 2)
                    nc.gpsimd.tensor_scalar(keys[:, :], keys[:, :], 0.25, None, ALU.mult).then_inc(static, 1)

            def added(eng, h):
                if relative:
                    eng.wait_ge((add0, add1)[h % 2], 16 * (h // 2 + 1))

            def rows_free(eng, h):
                if h >= 4:
                    eng.wait_ge(outs[h % 2], 16 * (h // 2 - 1))

            @block.tensor
            def _(pe):
                if relative:
                    pe.wait_ge(load, 32)
                else:
                    pe.wait_ge(static, 2)
                if not relative:
                    pe.wait_ge(ready, HPC)

                def turn(h):
                    pe.wait_ge(expd, QT * (h + 1))
                    if h >= 2:
                        pe.wait_ge(pT_done, h - 1)
                    for kt in range(QT):
                        for qt in range(QT):
                            m = nc.tensor.transpose(pst[:, h % 2, kt, qt, :], pr[:, h % 2, qt, kt * P:(kt + 1) * P], k.ident[:, :])
                    m.then_inc(turned, 1)

                def average(h):
                    pe.wait_ge(pT_done, h + 1)
                    if h >= 2:
                        pe.wait_ge(scaled, QT * (h - 1))
                    for qt in range(QT):
                        for kt in range(QT):
                            m = nc.tensor.matmul(pso[:, h % 2, qt * hd:(qt + 1) * hd], pT[:, h % 2, kt, qt, :], vals[:, kt, h * hd:(h + 1) * hd],
                                                 start=(kt == 0), stop=(kt == QT - 1))
                    m.then_inc(av, 1)

                def products(h):
                    pe.wait_ge(masked, 2 * (h + 1))
                    for x in range(4):
                        side, i = divmod(x, 2)
                        n = 4 * h + x
                        if n >= 2:
                            pe.wait_ge((rel_act, rel_dve)[n % 2], n // 2)
                        nc.tensor.matmul(psr[:, n % 2, 0:RW], (qz, kz)[side][:, h, i * P:(i + 1) * P],
                                         emb[:, side, P * (1 - i):P * (1 - i) + RW], start=True, stop=True).then_inc(rel, 1)

                for step in range(HPC + 2 + LAG):
                    h = step - LAG
                    if relative and step < HPC:
                        products(step)
                    if h < 0:
                        continue
                    if relative and h == 0:
                        pe.wait_ge(static, 3)
                    if h < HPC:
                        added(pe, h)
                        if h >= 2:
                            pe.wait_ge(summed, h - 1)
                        for qt in range(QT):
                            m = nc.tensor.matmul(pss[:, h % 2, qt, :], qz[:, h, qt * P:(qt + 1) * P], keys[:, :], start=True, stop=not relative,
                                                 skip_group_check=True)
                            if relative:
                                for kt in range(QT):
                                    m = nc.tensor.matmul(pss[:, h % 2, qt, kt * P:(kt + 1) * P], add[:, h % 2, 2 + kt, qt * P:(qt + 1) * P],
                                                         k.ident[:, :], start=False, stop=(kt == QT - 1), skip_group_check=True)
                        m.then_inc(scored, 1)
                    if 1 <= h <= HPC:
                        turn(h - 1)
                    if h >= 2:
                        average(h - 2)

            @block.vector
            def _(dve):
                links = [0]

                def link(i):
                    links[0] += 1
                    i.then_inc(chain, 1)
                    dve.wait_ge(chain, links[0])

                dve.wait_ge(load, 32)
                if relative:
                    for h in HEADS:
                        for src, dst in ((qT, qz), (kT, kz)):
                            nc.vector.tensor_scalar(dst[:, h:h + 1, :], src[:, bass.ds(c, 1), bass.ds(b * S, S)], mask[:, h:h + 1], None,
                                                    ALU.mult).then_inc(masked, 1)
                else:
                    for h in HEADS:
                        nc.vector.tensor_scalar(qz[:, h:h + 1, :], qT[:, bass.ds(c, 1), bass.ds(b * S, S)], mask[:, h:h + 1], None,
                                                ALU.mult).then_inc(ready, 1)

                def normalize(h):
                    dve.wait_ge(av, h + 1)
                    link(nc.vector.reciprocal(rec[:, h, :], sums[:, h, :]))
                    for qt in range(QT):
                        nc.vector.tensor_scalar(O[:, bass.ds(b * QT + qt, 1), bass.ds(c * P + h * hd, hd)],
                                                pso[:, h % 2:h % 2 + 1, qt * hd:(qt + 1) * hd], rec[:, h, qt:qt + 1], None,
                                                ALU.mult).then_inc(scaled, 1)

                for step in range(HPC + 3 + LAG):
                    h = step - LAG
                    if relative and step < HPC:
                        rows_free(dve, step)
                        for n in (4 * step + 1, 4 * step + 3):
                            dve.wait_ge(rel, n + 1)
                            nc.vector.tensor_copy(rows[:, step % 4, n % 4, :], psr[:, n % 2, 0:RW]).then_inc(rel_dve, 1)
                    if h < 0:
                        continue
                    if h < HPC:
                        dve.wait_ge(scored, h + 1)
                        added(dve, h)
                        if h >= 2:
                            dve.wait_ge(expd, QT * (h - 1))
                        m = nc.vector.tensor_tensor(sc[:, h % 2, :, :], pss[:, h % 2, :, :], add[:, h % 2 if relative else 0, 0:QT, :], ALU.add)
                        m.then_inc(summed, 1)
                        dve.wait_ge(summed, h + 1)
                        link(nc.vector.reduce_max(mx[:, h, :], sc[:, h % 2, :, :], AX))
                        nc.vector.tensor_scalar(nm[:, h, :], mx[:, h, :], -SC, None, ALU.mult).then_inc(peak, 1)
                    if h >= 3:
                        normalize(h - 3)

            @block.scalar
            def _(act):
                for step in range(HPC + 1 + LAG):
                    h = step - LAG
                    if relative and step < HPC:
                        rows_free(act, step)
                        for n in (4 * step, 4 * step + 2):
                            act.wait_ge(rel, n + 1)
                            nc.scalar.copy(rows[:, step % 4, n % 4, :], psr[:, n % 2, 0:RW]).then_inc(rel_act, 1)
                    if h < 0:
                        continue
                    if h < HPC:
                        act.wait_ge(peak, h + 1)
                        if h >= 2:
                            act.wait_ge(turned, h - 1)
                        for qt in range(QT):
                            nc.scalar.activation(pr[:, h % 2, qt, :], sc[:, h % 2, qt, :], ACT.Exp, bias=nm[:, h, qt:qt + 1], scale=SC,
                                                 accum_out=sums[:, h, qt:qt + 1]).then_inc(expd, 1)
                    if h >= 1:
                        act.wait_ge(turned, h)
                        if h >= 3:
                            act.wait_ge(av, h - 2)
                        nc.scalar.copy(pT[:, (h - 1) % 2, :, :, :], pst[:, (h - 1) % 2, :, :, :]).then_inc(pT_done, 1)


def layer0_self(nc, k, d):
    layer_norm(nc, k, k.X, k.N, "s0n")
    transpose_tokens(nc, k, k.N, k.NT, "s0t")
    k.rel_scratch = nc.dram_tensor("offset_rows", (P // HD16, 4, P, 3 * P), F32, kind="Internal").ap()
    with Tensors(nc) as t:
        qT = t.sb("s0_qT", [P, KC, T])
        kT = t.sb("s0_kT", [P, KC, T])
        V = t.sb("s0_V", [P, TT, D])
        O = t.sb("s0_O", [P, TT, D])
        linear_T(nc, k, k.NT, qT, d["s0_wq"], "s0q", bias=d["s0_bq"])
        linear_T(nc, k, k.NT, kT, d["s0_wk"], "s0k", bias=d["s0_bk"])
        linear_tokens(nc, k, k.NT, V, d["s0_wv"], "s0v", d["s0_bv"])
        self_attention(nc, k, d, "s0", qT, kT, V, O, True)
        add_to(nc, k.X, O, "s0a")


def add_to(nc, dst, src, name):
    with stage(nc, name + "_unused", name + "_unused1") as (block, _u, _v):
        @block.vector
        def _(dve):
            nc.vector.tensor_tensor(dst[:, :, :], dst[:, :, :], src[:, :, :], ALU.add)


def rotate(nc, k, d, xT, name):
    with Tensors(nc) as t, stage(nc, name + "_load", name + "_mm", name + "_a", name + "_b") as (block, load, mm, ca, cb):
        rot = t.sb(name + "_r", [P, P])
        tab = t.sb(name + "_tab", [P, 2, T])
        tmp = t.sb(name + "_tmp", [P, KC, T])
        ps = t.ps(name + "_ps", [P, KC, T])

        @block.sync
        def _(sp):
            sp.dma_start(rot[:, :], d["rope_swap"]).then_inc(load, 16)
            sp.dma_start(tab[:, :, :], d["rope_tables"]).then_inc(load, 16)

        @block.tensor
        def _(pe):
            pe.wait_ge(load, 32)
            for c in range(KC):
                nc.tensor.matmul(ps[:, c, :], rot[:, :], xT[:, c, :], start=True, stop=True).then_inc(mm, 1)

        @block.vector
        def _(dve):
            dve.wait_ge(load, 32)
            for c in range(KC):
                dve.wait_ge(mm, c + 1)
                nc.vector.tensor_tensor(tmp[:, c, :], ps[:, c, :], tab[:, 1, :], ALU.mult).then_inc(ca, 1)
                nc.vector.tensor_tensor(xT[:, c, :], xT[:, c, :], tab[:, 0, :], ALU.mult).then_inc(cb, 1)
            for c in range(KC):
                dve.wait_ge(ca, KC)
                dve.wait_ge(cb, KC)
                nc.vector.tensor_tensor(xT[:, c, :], xT[:, c, :], tmp[:, c, :], ALU.add)


def layer2_self(nc, k, d):
    with Tensors(nc) as t:
        X0 = t.sb("s2_X0", [P, TT, D])
        with stage(nc, "s2_keep", "s2_keep1") as (block, _u, _v):
            @block.vector
            def _(dve):
                nc.vector.tensor_copy(X0[:, :, :], k.X[:, :, :])
        layer_norm(nc, k, X0, k.X, "s2i")
        layer_norm(nc, k, k.X, k.N, "s2n")
        transpose_tokens(nc, k, k.N, k.NT, "s2t", gain=d["s2_g1"], shift=d["s2_h1"])
        with Tensors(nc) as u:
            qT = u.sb("s2_qT", [P, KC, T])
            kT = u.sb("s2_kT", [P, KC, T])
            V = u.sb("s2_V", [P, TT, D])
            O = u.sb("s2_O", [P, TT, D])
            OT = u.sb("s2_OT", [P, KC, T])
            linear_T(nc, k, k.NT, qT, d["s2_wq"], "s2q", bias=d["s2_bq"])
            linear_T(nc, k, k.NT, kT, d["s2_wk"], "s2k", bias=d["s2_bk"])
            linear_tokens(nc, k, k.NT, V, d["s2_wv"], "s2v", d["s2_bv"])
            rotate(nc, k, d, qT, "s2rq")
            rotate(nc, k, d, kT, "s2rk")
            self_attention(nc, k, d, "s2", qT, kT, V, O, False)
            transpose_tokens(nc, k, O, OT, "s2o")
            project_residual(nc, k, OT, d["s2_wo"], "s2p", bias=d["s2_bo"])
        layer_norm(nc, k, k.X, k.N, "s2m")
        transpose_tokens(nc, k, k.N, k.NT, "s2u", gain=d["s2_g2"], shift=d["s2_h2"])
        W = t.sb("s2_W", [P, TT, 1])
        b2 = t.sb("s2_b2", [P, D])
        with stage(nc, "s2_b2_load", "s2_b2_unused") as (block, load, _u):
            @block.sync
            def _(sp):
                sp.dma_start(b2[:, :], d["s2_b2"]).then_inc(load, 16)

            @block.vector
            def _(dve):
                nc.vector.memset(W[:, :, :], 1.0)
                dve.wait_ge(load, 16)
                nc.vector.tensor_tensor(X0[:, :, :], X0[:, :, :], b2[:, :].unsqueeze(1).broadcast_to([P, TT, D]), ALU.add)
        experts(nc, k, d["s2_pieces"], "s2e", 1, 8, 1, "gelu_erf", W, b1=d["s2_b1"])
        add_to(nc, k.X, X0, "s2a")


def self_layouts(a, i, rows, cols, spread):
    n = "L0_attn_"
    for w in "qk":
        a["s0_w" + w], a["s0_b" + w] = rows(i[n + "W" + w].T), cols(i[n + "b" + w])
    a["s0_wv"], a["s0_bv"] = rows(i[n + "Wv"].T), spread(i[n + "bv"])
    e = i[n + "dist_emb"]
    two = np.stack([e[255:767][::-1], e[256:768]])
    a["rel_emb"] = np.ascontiguousarray(np.tile(two.transpose(2, 0, 1), (P // HD16, 1, 1)))
    n = "L2_attn_"
    wqkv = i[n + "Wqkv"]
    bqkv = i[n + "bqkv"]
    a["s2_wq"], a["s2_wk"], a["s2_wv"] = (rows(wqkv[:, x * D:(x + 1) * D]) for x in range(3))
    a["s2_bq"], a["s2_bk"], a["s2_bv"] = cols(bqkv[:D]), cols(bqkv[D:2 * D]), spread(bqkv[2 * D:])
    for x in "12":
        a["s2_g" + x], a["s2_h" + x] = cols(i[n + f"ln{x}_g"]), cols(i[n + f"ln{x}_b"])
    a["s2_wo"], a["s2_bo"] = rows(i[n + "Wo"]), spread(i[n + "bo"])
    w1, w2 = i[n + "W1"], i[n + "W2"]
    parts = [w1.reshape(KC, P, 4, 2 * P).transpose(2, 1, 0, 3).reshape(4, P, -1), w2.reshape(4, 2, P, D).transpose(0, 2, 1, 3).reshape(4, P, -1)]
    a["s2_pieces"] = np.ascontiguousarray(np.concatenate(parts, 2))
    a["s2_b1"] = cols(i[n + "b1"])[None]
    a["s2_b2"] = spread(i[n + "b2"])
    q = np.arange(S)
    causal = np.where(q[None, :] > q[:, None], np.float32(-1e30), np.float32(0)).astype(np.float32)
    a["causal"] = np.ascontiguousarray(causal.reshape(QT, P, S).transpose(1, 0, 2))
    swap = np.zeros((P, P), np.float32)
    for f in range(P):
        h, r = divmod(f, HD16)
        if r < HD16 // 2:
            swap[h * HD16 + r + HD16 // 2, f] = -1
        else:
            swap[h * HD16 + r - HD16 // 2, f] = 1
    a["rope_swap"] = swap
    inv = (1.0 / 10000.0 ** (np.arange(0, HD16, 2, dtype=np.float32) / HD16)).astype(np.float32)
    fr = np.arange(S, dtype=np.float32)[:, None] * inv[None, :]
    emb = np.concatenate([fr, fr], -1).astype(np.float32)
    tab = np.stack([np.cos(emb), np.sin(emb)]).astype(np.float32).transpose(2, 0, 1)
    a["rope_tables"] = np.ascontiguousarray(np.tile(tab, (P // HD16, 1, B)))



VL = 4
VH = HD16 // VL
C8 = 8
GROUP = 64
ROW = 3 * HD16 + C8 + 1


def delta_blocks(nc, k, heads, gates, packed, own):
    NB = GROUP // C8
    NG = S // GROUP
    with Tensors(nc) as t, stage(nc, "b_load", "b_zero", "b_chain", "b_prod", "b_used", "b_done", "b_out") as (
            block, load, zeroed, chain, prod, used, done, stored):
        qkv = t.sb("b_qkv", [P, 3, NB, C8, HD16])
        ga = t.sb("b_gates", [P, 2, NB, C8])
        E = t.sb("b_E", [P, NB, C8, C8 + 1])
        bg = t.sb("b_bg", [P, NB, C8])
        G = t.sb("b_G", [P, NB, C8, C8])
        H = t.sb("b_H", [P, NB, C8, C8])
        X = t.sb("b_X", [P, NB, C8, 2 * HD16])
        kp = t.sb("b_kp", [P, NB, C8, HD16])
        qp = t.sb("b_qp", [P, 2, NB, C8, HD16])
        tmp = t.sb("b_tmp", [P, NB, C8, 2 * HD16])
        pk = t.sb("b_packed", [P, NB, C8, ROW])
        ow = t.sb("b_own", [P, VH, NB, C8, VL])
        Q, K, V = (qkv[:, n, :, :, :] for n in range(3))
        decay, beta = ga[:, 0, :, :], ga[:, 1, :, :]
        WQ = slice(HD16, 2 * HD16)
        WA = slice(2 * HD16, 2 * HD16 + C8)
        WK = slice(2 * HD16 + C8, 3 * HD16 + C8)

        @block.sync
        def _(sp):
            for b in range(B):
                for g in range(NG):
                    part = slice((b * NG + g) * NH, (b * NG + g + 1) * NH)
                    for n in range(2):
                        sp.dma_start(ga[part, n, :, :], gates[n, b][:, g * GROUP:(g + 1) * GROUP].rearrange("h (c t) -> h c t", t=C8)).then_inc(load, 16)
                    for n in range(3):
                        sp.dma_start(qkv[part, n, :, :, :].rearrange("p c t e -> p (c t e)"),
                                     heads[n, b][:, g * GROUP:(g + 1) * GROUP, :].rearrange("h s e -> h (s e)")).then_inc(load, 16)
            sp.wait_ge(done, 3)
            for b in range(B):
                for g in range(NG):
                    part = slice((b * NG + g) * NH, (b * NG + g + 1) * NH)
                    span = slice(g * GROUP, (g + 1) * GROUP)
                    sp.dma_start(packed[b][:, span, :].rearrange("h s e -> h (s e)"),
                                 pk[part, :, :, :].rearrange("p c t e -> p (c t e)")).then_inc(stored, 16)
                    sp.dma_start(own[b][:, :, span, :].rearrange("x h s e -> h x (s e)"),
                                 ow[part, :, :, :, :].rearrange("p x c t e -> p x (c t e)")).then_inc(stored, 16)
            sp.wait_ge(stored, 16 * 2 * B * NG)

        @block.gpsimd
        def _(pool):
            nc.gpsimd.memset(H[:, :, :, :], 0.0).then_inc(zeroed, 1)
            pool.wait_ge(load, 16 * 5 * B * NG)
            for s in range(C8):
                if s >= 2:
                    pool.wait_ge(used, s - 1)
                nc.gpsimd.tensor_tensor(qp[:, s % 2, :, s:C8, :], Q[:, :, s:C8, :],
                                        K[:, :, s, :].unsqueeze(2).broadcast_to([P, NB, C8 - s, HD16]), ALU.mult).then_inc(prod, 1)

        @block.scalar
        def _(act):
            act.wait_ge(load, 16 * 5 * B * NG)
            act.wait_ge(zeroed, 3)
            nc.scalar.copy(pk[:, :, :, ROW - 1], E[:, :, C8 - 1, 0].unsqueeze(2).broadcast_to([P, NB, C8])).then_inc(done, 1)

        @block.vector
        def _(dve):
            links = [0]

            def link(i):
                links[0] += 1
                i.then_inc(chain, 1)
                dve.wait_ge(chain, links[0])

            nc.vector.memset(E[:, :, :, :], 0.0)
            link(nc.vector.memset(G[:, :, :, :], 0.0))
            diagonal = E[:, :, :, :].rearrange("p c t s -> p c (t s)")[:, :, 1:C8 * (C8 + 1):C8 + 2]
            link(nc.vector.memset(diagonal, 1.0))
            dve.wait_ge(load, 16 * 5 * B * NG)
            link(nc.vector.tensor_copy(E[:, :, 0, 0], decay[:, :, 0]))
            for s in range(1, C8):
                link(nc.vector.tensor_tensor(E[:, :, s, 0:s + 1], E[:, :, s - 1, 0:s + 1],
                                             decay[:, :, s].unsqueeze(2).broadcast_to([P, NB, s + 1]), ALU.mult))
            dve.wait_ge(zeroed, 1)
            nc.vector.tensor_tensor(bg[:, :, :], E[:, :, :, 0], beta, ALU.mult).then_inc(zeroed, 1)
            dve.wait_ge(zeroed, 2)
            nc.vector.tensor_tensor(X[:, :, :, 0:HD16], K, bg[:, :, :].unsqueeze(3).broadcast_to([P, NB, C8, HD16]), ALU.mult).then_inc(zeroed, 1)
            nc.vector.tensor_tensor(X[:, :, :, HD16:2 * HD16], V, beta.unsqueeze(3).broadcast_to([P, NB, C8, HD16]), ALU.mult)
            nc.vector.tensor_tensor(pk[:, :, :, WQ], Q, E[:, :, :, 0].unsqueeze(3).broadcast_to([P, NB, C8, HD16]), ALU.mult)
            nc.vector.tensor_tensor(pk[:, :, :, WK], K, E[:, :, C8 - 1, 1:C8 + 1].unsqueeze(3).broadcast_to([P, NB, C8, HD16]), ALU.mult)
            for s in range(C8 - 1):
                link(nc.vector.tensor_tensor(kp[:, :, s + 1:C8, :], K[:, :, s + 1:C8, :],
                                             K[:, :, s, :].unsqueeze(2).broadcast_to([P, NB, C8 - 1 - s, HD16]), ALU.mult))
                link(nc.vector.reduce_sum(G[:, :, s + 1:C8, s], kp[:, :, s + 1:C8, :], AX))
            link(nc.vector.tensor_tensor(G[:, :, :, :], G[:, :, :, :], E[:, :, :, 1:C8 + 1], ALU.mult))
            link(nc.vector.tensor_tensor(G[:, :, :, :], G[:, :, :, :], beta.unsqueeze(3).broadcast_to([P, NB, C8, C8]), ALU.mult))
            for s in range(C8 - 1):
                rest = C8 - 1 - s
                link(nc.vector.tensor_tensor(tmp[:, :, s + 1:C8, :], X[:, :, s, :].unsqueeze(2).broadcast_to([P, NB, rest, 2 * HD16]),
                                             G[:, :, s + 1:C8, s].unsqueeze(3).broadcast_to([P, NB, rest, 2 * HD16]), ALU.mult))
                link(nc.vector.tensor_tensor(X[:, :, s + 1:C8, :], X[:, :, s + 1:C8, :], tmp[:, :, s + 1:C8, :], ALU.subtract))
            nc.vector.tensor_scalar(pk[:, :, :, 0:HD16], X[:, :, :, 0:HD16], -1.0, None, ALU.mult)
            for x in range(VH):
                m = nc.vector.tensor_copy(ow[:, x, :, :, :], X[:, :, :, HD16 + x * VL:HD16 + (x + 1) * VL])
            m.then_inc(done, 1)
            for s in range(C8):
                dve.wait_ge(prod, s + 1)
                nc.vector.reduce_sum(H[:, :, s:C8, s], qp[:, s % 2, :, s:C8, :], AX).then_inc(used, 1)
            dve.wait_ge(used, C8)
            nc.vector.tensor_tensor(pk[:, :, :, WA], H[:, :, :, :], E[:, :, :, 1:C8 + 1], ALU.mult).then_inc(done, 1)


def delta_load(sp, rows, u0, packed, own, r, load):
    span = bass.ds(r * GROUP, GROUP)
    for b in range(B):
        for x in range(VH):
            part = slice((b * VH + x) * NH, (b * VH + x + 1) * NH)
            sp.dma_start(rows[part, span, :].rearrange("p s e -> p (s e)"),
                         packed[b][:, span, :].rearrange("h s e -> h (s e)")).then_inc(load, 16)
            sp.dma_start(u0[part, span, :].rearrange("p s e -> p (s e)"),
                         own[b, x][:, span, :].rearrange("h s e -> h (s e)")).then_inc(load, 16)


def delta_group(nc, name, r, more, rows, u0, hist, packed, own, oA):
    NB = GROUP // C8
    WQA = slice(HD16, 2 * HD16 + C8)
    WK = slice(2 * HD16 + C8, 3 * HD16 + C8)
    with Tensors(nc) as t, stage(nc, name + "_next", name + "_chain", name + "_side", name + "_update", name + "_state", name + "_prod", name + "_out") as (
            block, load, chain, side, update, state, prod, out):
        pu = t.sb(name + "_pu", [P, 2, VL, C8, HD16 + 1])
        pst = t.sb(name + "_ps", [P, 2, VL, HD16, C8 + 1])
        po = t.sb(name + "_po", [P, 2, C8, VL, HD16 + C8])

        def tokens(c):
            return bass.ds(r * GROUP + c * C8, C8)

        def state_of(c):
            return hist[:, bass.ds(r * NB + c, 1), :, 0:HD16].rearrange("p o v e -> p (o v) e")

        def updates_of(c):
            return hist[:, bass.ds(r * NB + c, 1), :, HD16:HD16 + C8].rearrange("p o v e -> p (o v) e")

        @block.sync
        def _(sp):
            if more:
                delta_load(sp, rows, u0, packed, own, r + 1, load)
                sp.wait_ge(load, 16 * 2 * B * VH)

        @block.scalar
        def _(act):
            for c in range(NB):
                if c >= 2:
                    act.wait_ge(update, c - 1)
                nc.scalar.copy(pu[:, c % 2, :, :, HD16], u0[:, tokens(c), :].rearrange("p t v -> p v t")).then_inc(side, 1)
                if c >= 1:
                    act.wait_ge(state, c)
                decay = rows[:, bass.ds(r * GROUP + c * C8, 1), ROW - 1:ROW].rearrange("p o e -> p (o e)")
                nc.scalar.activation(pst[:, c % 2, :, :, C8], state_of(c), ACT.Copy, scale=decay).then_inc(side, 1)

        @block.vector
        def _(dve):
            for c in range(NB):
                if c >= 1:
                    dve.wait_ge(state, c)
                nc.vector.tensor_tensor(pu[:, c % 2, :, :, 0:HD16], rows[:, tokens(c), 0:HD16].unsqueeze(1).broadcast_to([P, VL, C8, HD16]),
                                        state_of(c).unsqueeze(2).broadcast_to([P, VL, C8, HD16]), ALU.mult).then_inc(chain, 1)
                if c >= 1:
                    dve.wait_ge(prod, c)
                    nc.vector.reduce_sum(oA[:, bass.ds(r * GROUP + (c - 1) * C8, C8), :], po[:, (c - 1) % 2, :, :, :], AX).then_inc(out, 1)
                dve.wait_ge(chain, 2 * c + 1)
                dve.wait_ge(side, 2 * c + 1)
                nc.vector.reduce_sum(updates_of(c), pu[:, c % 2, :, :, :], AX).then_inc(update, 1)
                dve.wait_ge(update, c + 1)
                nc.vector.tensor_tensor(pst[:, c % 2, :, :, 0:C8],
                                        rows[:, tokens(c), WK].rearrange("p t e -> p e t").unsqueeze(1).broadcast_to([P, VL, HD16, C8]),
                                        updates_of(c).unsqueeze(2).broadcast_to([P, VL, HD16, C8]), ALU.mult).then_inc(chain, 1)
                dve.wait_ge(chain, 2 * c + 2)
                dve.wait_ge(side, 2 * c + 2)
                nc.vector.reduce_sum(state_of(c + 1), pst[:, c % 2, :, :, :], AX).then_inc(state, 1)
            dve.wait_ge(prod, NB)
            nc.vector.reduce_sum(oA[:, bass.ds(r * GROUP + (NB - 1) * C8, C8), :], po[:, (NB - 1) % 2, :, :, :], AX).then_inc(out, 1)

        @block.gpsimd
        def _(pool):
            for c in range(NB):
                pool.wait_ge(update, c + 1)
                if c >= 2:
                    pool.wait_ge(out, c - 1)
                both = hist[:, bass.ds(r * NB + c, 1), :, :].rearrange("p o v e -> p (o v) e")
                nc.gpsimd.tensor_tensor(po[:, c % 2, :, :, :], rows[:, tokens(c), WQA].unsqueeze(2).broadcast_to([P, C8, VL, HD16 + C8]),
                                        both.unsqueeze(1).broadcast_to([P, C8, VL, HD16 + C8]), ALU.mult).then_inc(prod, 1)


def layer1_self(nc, k, d):
    layer_norm(nc, k, k.X, k.N, "dn")
    transpose_tokens(nc, k, k.N, k.NT, "dt")
    heads = nc.dram_tensor("delta_heads", (3, B, NH, S, HD16), F32, kind="Internal").ap()
    gates = nc.dram_tensor("delta_gates", (2, B, NH, S), F32, kind="Internal").ap()
    with Tensors(nc) as t:
        oA = t.sb("d_oA", [P, S, VL])
        with Tensors(nc) as u, stage(nc, "d_load", "d_mm", "d_gmm", "d_silu", "d_sq", "d_root", "d_gate", "d_ready", "d_vready", "d_out") as (
                block, load, mm, gmm, silu, sq, root, gate, ready, vready, stored):
            w = u.sb("d_w", [P, 3, KC, D])
            wg = u.sb("d_wg", [P, KC, 2 * HD16])
            q = u.sb("d_q", [P, TT, D])
            kk = u.sb("d_k", [P, TT, D])
            v = u.sb("d_v", [P, TT, D])
            ss = u.sb("d_ss", [P, TT, D])
            nrm = u.sb("d_nrm", [P, TT, NH])
            g = u.sb("d_g", [2 * HD16, T])
            ps = u.ps("d_ps", [P, 3, 2, 512])
            pg = u.ps("d_pg", [2 * HD16, T])

            @block.sync
            def _(sp):
                sp.dma_start(w[:, :, :, :], d["d_w3"]).then_inc(load, 16)
                sp.dma_start(wg[:, :, :], d["d_wg"]).then_inc(load, 16)

                def store(n, src):
                    for b in range(B):
                        for i in range(QT):
                            sp.dma_start(heads[n, b][:, i * P:(i + 1) * P, :].rearrange("h p e -> p h e"),
                                         src[:, b * QT + i, :].rearrange("p (h e) -> p h e", h=NH)).then_inc(stored, 16)

                sp.wait_ge(gate, 2)
                for n in range(2):
                    sp.dma_start(gates[n].rearrange("b h s -> h b s"), g[n * NH:(n + 1) * NH, :].rearrange("h (b s) -> h b s", b=B)).then_inc(stored, 16)
                sp.wait_ge(vready, TT)
                store(2, v)
                sp.wait_ge(silu, 2 * TT)
                store(0, q)
                sp.wait_ge(ready, 1)
                store(1, kk)
                sp.wait_ge(stored, 16 * (2 + 3 * TT))

            @block.tensor
            def _(pe):
                pe.wait_ge(load, 32)
                for c in range(KC):
                    m = nc.tensor.matmul(pg[:, :], wg[:, c, :], k.NT[:, c, :], start=(c == 0), stop=(c == KC - 1))
                m.then_inc(gmm, 1)
                for i in range(TT):
                    if i >= 2:
                        pe.wait_ge(silu, 2 * (i - 1))
                        pe.wait_ge(vready, i - 1)
                    for n in range(3):
                        for c in range(KC):
                            m = nc.tensor.matmul(ps[:, n, i % 2, 0:D], k.NT[:, c, i * P:(i + 1) * P], w[:, n, c, :],
                                                 start=(c == 0), stop=(c == KC - 1))
                    m.then_inc(mm, 1)

            @block.scalar
            def _(act):
                act.wait_ge(gmm, 1)
                nc.scalar.activation(g[:, :], pg[:, :], ACT.Sigmoid).then_inc(gate, 1)
                for i in range(TT):
                    act.wait_ge(mm, i + 1)
                    nc.scalar.activation(q[:, i, :], ps[:, 0, i % 2, 0:D], ACT.Silu).then_inc(silu, 1)
                    nc.scalar.activation(kk[:, i, :], ps[:, 1, i % 2, 0:D], ACT.Silu).then_inc(silu, 1)
                act.wait_ge(sq, 3)
                nc.scalar.activation(nrm[:, :, :], nrm[:, :, :], ACT.Sqrt).then_inc(root, 1)

            @block.vector
            def _(dve):
                for i in range(TT):
                    dve.wait_ge(mm, i + 1)
                    nc.vector.tensor_copy(v[:, i, :], ps[:, 2, i % 2, 0:D]).then_inc(vready, 1)
                dve.wait_ge(gate, 1)
                nc.vector.tensor_scalar(g[:, :], g[:, :], k.twos[0:2 * NH, 0:1], None, ALU.mult).then_inc(gate, 1)
                dve.wait_ge(silu, 2 * TT)
                nc.vector.tensor_tensor(ss[:, :, :], kk[:, :, :], kk[:, :, :], ALU.mult).then_inc(sq, 1)
                dve.wait_ge(sq, 1)
                nc.vector.reduce_sum(nrm[:, :, :], ss[:, :, :].rearrange("p i (h e) -> p i h e", h=NH), AX).then_inc(sq, 1)
                dve.wait_ge(sq, 2)
                nc.vector.tensor_scalar(nrm[:, :, :], nrm[:, :, :], 1e-12, None, ALU.add).then_inc(sq, 1)
                dve.wait_ge(root, 1)
                nc.vector.reciprocal(nrm[:, :, :], nrm[:, :, :]).then_inc(root, 1)
                dve.wait_ge(root, 2)
                for i in range(TT):
                    m = nc.vector.tensor_tensor(kk[:, i, :].rearrange("p (h e) -> p h e", h=NH), kk[:, i, :].rearrange("p (h e) -> p h e", h=NH),
                                                nrm[:, i, :].unsqueeze(2).broadcast_to([P, NH, HD16]), ALU.mult)
                m.then_inc(ready, 1)

        packed = nc.dram_tensor("delta_packed", (B, NH, S, ROW), F32, kind="Internal").ap()
        own = nc.dram_tensor("delta_own", (B, VH, NH, S, VL), F32, kind="Internal").ap()
        delta_blocks(nc, k, heads, gates, packed, own)
        with Tensors(nc) as u:
            rows = u.sb("e_rows", [P, S, ROW])
            u0 = u.sb("e_own", [P, S, VL])
            hist = u.sb("e_hist", [P, S // C8 + 1, VL, HD16 + C8])
            with stage(nc, "d_zero", "d_zero_load") as (block, zero, load):
                @block.vector
                def _(dve):
                    nc.vector.memset(hist[:, 0, :, 0:HD16], 0.0)

                @block.sync
                def _(sp):
                    delta_load(sp, rows, u0, packed, own, 0, load)
                    sp.wait_ge(load, 16 * 2 * B * VH)
            with nc.Fori(0, S // GROUP - 1) as r:
                delta_group(nc, "e", r, True, rows, u0, hist, packed, own, oA)
            delta_group(nc, "f", S // GROUP - 1, False, rows, u0, hist, packed, own, oA)

        O = t.sb("d_O", [P, TT, D])
        with Tensors(nc) as u, stage(nc, "g_load", "g_turned", "g_copied", "g_chain", "g_root") as (block, load, turned, copied, chain, root):
            nw = u.sb("g_nw", [P, D])
            sqr = u.sb("g_sq", [P, TT, D])
            ms = u.sb("g_ms", [P, TT, NH])
            ps = u.ps("g_ps", [P, QT, VL, P])

            @block.sync
            def _(sp):
                sp.dma_start(nw[:, :], d["d_norm_w"]).then_inc(load, 16)

            @block.tensor
            def _(pe):
                for i in range(QT):
                    for x in range(VL):
                        m = nc.tensor.transpose(ps[:, i, x, :], oA[:, i * P:(i + 1) * P, x], k.ident[:, :])
                    m.then_inc(turned, 1)

            @block.vector
            def _(dve):
                links = [0]

                def link(i):
                    links[0] += 1
                    i.then_inc(chain, 1)
                    dve.wait_ge(chain, links[0])

                for i in range(QT):
                    dve.wait_ge(turned, i + 1)
                    for b in range(B):
                        for x in range(VL):
                            m = nc.vector.tensor_copy(O[:, b * QT + i, :].rearrange("p (h y x) -> p h y x", h=NH, y=VH)[:, :, :, x],
                                                      ps[:, i, x, b * NH * VH:(b + 1) * NH * VH].rearrange("p (y h) -> p h y", y=VH))
                link(m)
                link(nc.vector.tensor_tensor(sqr[:, :, :], O[:, :, :], O[:, :, :], ALU.mult))
                link(nc.vector.reduce_sum(ms[:, :, :], sqr[:, :, :].rearrange("p i (h e) -> p i h e", h=NH), AX))
                nc.vector.tensor_scalar(ms[:, :, :], ms[:, :, :], 1.0 / HD16, 1e-6, ALU.mult, ALU.add).then_inc(root, 1)
                dve.wait_ge(root, 2)
                link(nc.vector.reciprocal(ms[:, :, :], ms[:, :, :]))
                dve.wait_ge(load, 16)
                for i in range(TT):
                    o3 = O[:, i, :].rearrange("p (h e) -> p h e", h=NH)
                    link(nc.vector.tensor_tensor(o3, o3, ms[:, i, :].unsqueeze(2).broadcast_to([P, NH, HD16]), ALU.mult))
                    nc.vector.tensor_tensor(O[:, i, :], O[:, i, :], nw[:, :], ALU.mult)

            @block.scalar
            def _(act):
                act.wait_ge(root, 1)
                nc.scalar.activation(ms[:, :, :], ms[:, :, :], ACT.Sqrt).then_inc(root, 1)
        OT = t.sb("d_OT", [P, KC, T])
        transpose_tokens(nc, k, O, OT, "do")
        project_residual(nc, k, OT, d["d_wo"], "dp")



def layer3_self(nc, k, d):
    DI, NS, R, KW = 512, 16, 64, 4
    DC = DI // P
    XD = R + 2 * NS
    SEG = B * DC
    layer_norm(nc, k, k.X, k.N, "mn")
    transpose_tokens(nc, k, k.N, k.NT, "mt")
    with Tensors(nc) as t:
        xc = t.sb("m_xc", [P, DC, T])
        zs = t.sb("m_zs", [P, DC, T])
        dt = t.sb("m_dt", [P, DC, T])
        dbl = t.sb("m_dbl", [XD, T])
        A = t.sb("m_A", [P, DC, NS])
        par = t.sb("m_par", [P, DC, 3 + KW])
        with Tensors(nc) as u, stage(nc, "m_load", "m_mm", "m_ev", "m_zero", "m_conv", "m_xc_done") as (block, load, mm, ev, zero, conv, xc_done):
            w = u.sb("m_win", [P, KC, 2 * DI])
            xp = u.sb("m_xp", [P, DC, B, KW - 1 + S])
            cv = u.sb("m_cv", [P, 2, T])
            ps = u.ps("m_ps", [P, 2, T])

            @block.sync
            def _(sp):
                sp.dma_start(w[:, :, :], d["m_win"]).then_inc(load, 16)
                sp.dma_start(par[:, :, :], d["m_par"]).then_inc(load, 16)
                sp.dma_start(A[:, :, :], d["m_A_log"]).then_inc(load, 16)

            @block.tensor
            def _(pe):
                pe.wait_ge(load, 48)
                for m in range(2 * DC):
                    if m >= 2:
                        pe.wait_ge(ev, m - 1)
                    for c in range(KC):
                        i = nc.tensor.matmul(ps[:, m % 2, :], w[:, c, m * P:(m + 1) * P], k.NT[:, c, :], start=(c == 0), stop=(c == KC - 1))
                    i.then_inc(mm, 1)

            @block.scalar
            def _(act):
                for m in range(2 * DC):
                    act.wait_ge(mm, m + 1)
                    if m < DC:
                        nc.scalar.copy(xp[:, m, :, KW - 1:KW - 1 + S], ps[:, m % 2, :].rearrange("p (b s) -> p b s", b=B)).then_inc(ev, 1)
                    else:
                        nc.scalar.activation(zs[:, m - DC, :], ps[:, m % 2, :], ACT.Silu).then_inc(ev, 1)
                for m in range(DC):
                    act.wait_ge(conv, KW * (m + 1))
                    nc.scalar.activation(xc[:, m, :], cv[:, m % 2, :], ACT.Silu, bias=par[:, m, 0:1]).then_inc(xc_done, 1)
                act.wait_ge(load, 48)
                nc.scalar.activation(A[:, :, :], A[:, :, :], ACT.Exp)

            @block.vector
            def _(dve):
                nc.vector.memset(xp[:, :, :, 0:KW - 1], 0.0).then_inc(zero, 1)
                dve.wait_ge(zero, 1)
                dve.wait_ge(load, 48)
                for m in range(DC):
                    dve.wait_ge(ev, m + 1)
                    if m >= 2:
                        dve.wait_ge(xc_done, m - 1)
                    o = cv[:, m % 2, :].rearrange("p (b s) -> p b s", b=B)
                    for j in range(KW):
                        tap = par[:, m, 3 + j:4 + j]
                        if j == 0:
                            i = nc.vector.tensor_scalar(o, xp[:, m, :, 0:S], tap, None, ALU.mult)
                        else:
                            i = nc.vector.scalar_tensor_tensor(o, xp[:, m, :, j:j + S], tap, o, ALU.mult, ALU.add)
                        i.then_inc(conv, 1)
                        dve.wait_ge(conv, KW * m + j + 1)

        with Tensors(nc) as u, stage(nc, "n_load", "n_mm", "n_ev", "n_dmm", "n_pre", "n_exp", "n_chain") as (block, load, mm, ev, dmm, pre, expd, chain):
            wx = u.sb("n_wx", [P, DC, XD])
            wdt = u.sb("n_wdt", [R, DI])
            e = u.sb("n_e", [P, DC, T])
            w1 = u.sb("n_w1", [P, DC, T])
            ln = u.sb("n_ln", [P, DC, T])
            is1 = u.sb("n_is1", [P, DC, T])
            px = u.ps("n_px", [XD, T])
            pd = u.ps("n_pd", [P, DC, T])

            @block.sync
            def _(sp):
                sp.dma_start(wx[:, :, :], d["m_wx"]).then_inc(load, 16)
                sp.dma_start(wdt[:, :], d["m_wdt"]).then_inc(load, 16)

            @block.tensor
            def _(pe):
                pe.wait_ge(load, 32)
                for c in range(DC):
                    m = nc.tensor.matmul(px[:, :], wx[:, c, :], xc[:, c, :], start=(c == 0), stop=(c == DC - 1))
                m.then_inc(mm, 1)
                pe.wait_ge(ev, 1)
                for c in range(DC):
                    nc.tensor.matmul(pd[:, c, :], wdt[:, c * P:(c + 1) * P], dbl[0:R, :], start=True, stop=True).then_inc(dmm, 1)

            @block.scalar
            def _(act):
                act.wait_ge(mm, 1)
                nc.scalar.copy(dbl[:, :], px[:, :]).then_inc(ev, 1)
                act.wait_ge(pre, 2)
                nc.scalar.activation(e[:, :, :], e[:, :, :], ACT.Exp, scale=-1.0).then_inc(expd, 1)
                act.wait_ge(pre, 3)
                nc.scalar.activation(ln[:, :, :], w1[:, :, :], ACT.Ln).then_inc(expd, 1)

            @block.vector
            def _(dve):
                links = [0]

                def link(i):
                    links[0] += 1
                    i.then_inc(chain, 1)
                    dve.wait_ge(chain, links[0])

                for c in range(DC):
                    dve.wait_ge(dmm, c + 1)
                    i = nc.vector.tensor_scalar(dt[:, c, :], pd[:, c, :], par[:, c, 1:2], None, ALU.add)
                link(i)
                nc.vector.scalar_tensor_tensor(e[:, :, :], dt[:, :, :], -1.0, dt[:, :, :], ALU.mult, ALU.max).then_inc(pre, 1)
                dve.wait_ge(pre, 1)
                nc.vector.tensor_scalar(dt[:, :, :], dt[:, :, :], 0.0, None, ALU.max).then_inc(pre, 1)
                dve.wait_ge(expd, 1)
                nc.vector.tensor_scalar(w1[:, :, :], e[:, :, :], 1.0, None, ALU.add).then_inc(pre, 1)
                dve.wait_ge(pre, 3)
                link(nc.vector.tensor_scalar(is1[:, :, :], w1[:, :, :], 1.0, None, ALU.is_equal))
                dve.wait_ge(expd, 2)
                link(nc.vector.tensor_tensor(ln[:, :, :], ln[:, :, :], is1[:, :, :], ALU.add))
                link(nc.vector.scalar_tensor_tensor(w1[:, :, :], w1[:, :, :], 1.0, is1[:, :, :], ALU.subtract, ALU.add))
                link(nc.vector.reciprocal(w1[:, :, :], w1[:, :, :]))
                link(nc.vector.tensor_tensor(ln[:, :, :], ln[:, :, :], e[:, :, :], ALU.mult))
                link(nc.vector.tensor_tensor(ln[:, :, :], ln[:, :, :], w1[:, :, :], ALU.mult))
                link(nc.vector.tensor_tensor(dt[:, :, :], dt[:, :, :], ln[:, :, :], ALU.add))
                nc.vector.tensor_scalar(A[:, :, :], A[:, :, :], -1.0, None, ALU.mult)

        y = t.sb("m_y", [P, DC, T])
        with Tensors(nc) as u, stage(nc, "o_dx", "o_rows", "o_crow", "o_abar", "o_seg", "o_bu", "o_scan", "o_prod", "o_sum", "o_chain") as (
                block, dx_done, rows_done, crow, abar, seg, bu_done, scan, prod, summed, chain):
            dx = u.sb("o_dxs", [P, DC, T])
            ab = u.sb("o_ab", [P, 2, DC, T])
            bu = u.sb("o_bus", [P, DC, T])
            h = u.sb("o_h", [P, 2, DC, T])
            cr = u.sb("o_cr", [P, 2, T])
            pr = u.sb("o_pr", [P, 2, DC, T])
            pb = u.ps("o_pb", [P, 2, 2, T])
            py = u.ps("o_py", [P, DC, T])

            @block.tensor
            def _(pe):
                for n in range(NS + 1):
                    if n < NS:
                        if n >= 2:
                            pe.wait_ge(bu_done, n - 1)
                            pe.wait_ge(crow, n - 1)
                        for x in range(2):
                            r = R + NS * x + n
                            m = nc.tensor.matmul(pb[:, n % 2, x, :], k.ident[0:XD, r:r + 1].broadcast_to([XD, P]), dbl[:, :], start=True, stop=True)
                        m.then_inc(rows_done, 1)
                    if n >= 1:
                        pe.wait_ge(prod, n)
                        for c in range(DC):
                            m = nc.tensor.matmul(py[:, c, :], k.ident[:, :], pr[:, (n - 1) % 2, c, :], start=(n == 1), stop=(n == NS))
                        m.then_inc(summed, 1)

            @block.scalar
            def _(act):
                for n in range(NS):
                    if n >= 2:
                        act.wait_ge(scan, n - 1)
                    for c in range(DC):
                        m = nc.scalar.activation(ab[:, n % 2, c, :], dt[:, c, :], ACT.Exp, scale=A[:, c, n:n + 1])
                    m.then_inc(abar, 1)
                    act.wait_ge(rows_done, n + 1)
                    if n >= 2:
                        act.wait_ge(prod, n - 1)
                    nc.scalar.copy(cr[:, n % 2, :], pb[:, n % 2, 1, :]).then_inc(crow, 1)

            @block.gpsimd
            def _(pool):
                for n in range(NS + 1):
                    if n < NS:
                        pool.wait_ge(abar, n + 1)
                        nc.gpsimd.memset(ab[:, n % 2, :, :].rearrange("p c (b s) -> p (c b) s", b=B)[:, :, 0:1], 0.0).then_inc(seg, 1)
                    if n >= 1:
                        j = n - 1
                        pool.wait_ge(scan, j + 1)
                        pool.wait_ge(crow, j + 1)
                        if j >= 2:
                            pool.wait_ge(summed, j - 1)
                        nc.gpsimd.tensor_tensor(pr[:, j % 2, :, :], h[:, j % 2, :, :], cr[:, j % 2, :].unsqueeze(1).broadcast_to([P, DC, T]),
                                                ALU.mult).then_inc(prod, 1)

            @block.vector
            def _(dve):
                nc.vector.tensor_tensor(dx[:, :, :], dt[:, :, :], xc[:, :, :], ALU.mult).then_inc(dx_done, 1)
                dve.wait_ge(dx_done, 1)
                for n in range(NS):
                    dve.wait_ge(rows_done, n + 1)
                    if n >= 1:
                        dve.wait_ge(scan, n)
                    nc.vector.tensor_tensor(bu[:, :, :], dx[:, :, :], pb[:, n % 2, 0, :].unsqueeze(1).broadcast_to([P, DC, T]),
                                            ALU.mult).then_inc(bu_done, 1)
                    dve.wait_ge(bu_done, n + 1)
                    dve.wait_ge(seg, n + 1)
                    if n >= 2:
                        dve.wait_ge(prod, n - 1)
                    flat = "p c s -> p (c s)"
                    nc.vector.tensor_tensor_scan(h[:, n % 2, :, :].rearrange(flat), ab[:, n % 2, :, :].rearrange(flat), bu[:, :, :].rearrange(flat),
                                                 0.0, ALU.mult, ALU.add).then_inc(scan, 1)
                for c in range(DC):
                    nc.vector.tensor_scalar(y[:, c, :], xc[:, c, :], par[:, c, 2:3], None, ALU.mult).then_inc(chain, 1)
                dve.wait_ge(chain, DC)
                dve.wait_ge(summed, NS)
                nc.vector.tensor_tensor(y[:, :, :], py[:, :, :], y[:, :, :], ALU.add).then_inc(chain, 1)
                dve.wait_ge(chain, DC + 1)
                nc.vector.tensor_tensor(y[:, :, :], y[:, :, :], zs[:, :, :], ALU.mult)
        project_residual(nc, k, y, d["m_wout"], "mp", chunks=DC)


def scan_layouts(a, i, rows, cols, spread):
    n = "L1_attn_"
    a["d_w3"] = np.ascontiguousarray(np.stack([rows(i[n + w]) for w in ("Wq", "Wk", "Wv")], 1))
    a["d_wg"] = rows(np.concatenate([i[n + "Wf"], i[n + "Wbet"]], 1))
    a["d_norm_w"] = spread(i[n + "norm_w"])
    a["d_wo"] = rows(i[n + "Wo"])
    fourth = np.zeros((P, VH), np.float32)
    for p in range(P):
        fourth[p, p % (NH * VH) // NH] = 1
    a["d_fourth"] = fourth
    two = np.ones((P, 1), np.float32)
    two[NH:2 * NH] = 2
    a["twos"] = two
    n = "L3_attn_"
    a["m_win"] = rows(i[n + "W_in"].T)

    def lane(v):
        return np.ascontiguousarray(v.reshape(4, P, -1).transpose(1, 0, 2))

    a["m_par"] = np.concatenate([lane(i[n + "conv_b"]), lane(i[n + "b_dt"]), lane(i[n + "D_param"]), lane(i[n + "conv_w"])], 2)
    a["m_A_log"] = lane(i[n + "A_log"])
    a["m_wx"], a["m_wdt"], a["m_wout"] = rows(i[n + "W_x"].T), np.ascontiguousarray(i[n + "W_dt"].T), rows(i[n + "W_out"].T)



class Kernel:
    pass


def program(nc, d, out):
    k = Kernel()
    with Tensors(nc) as t:
        k.X = t.sb("X", [P, TT, D])
        k.N = t.sb("N", [P, TT, D])
        k.NT = t.sb("NT", [P, KC, T])
        k.ident = t.sb("ident", [P, P])
        k.onesb = t.sb("ones_bf16", [P, P], BF16)
        k.ones = t.sb("ones_f32", [P, P])
        k.iota = t.sb("iota16", [P, NH])
        k.twos = t.sb("twos", [P, 1])
        with stage(nc, "x_load", "unused") as (block, load, _unused):
            @block.sync
            def _(sp):
                sp.dma_start(k.X[:, :, :], d["x"]).then_inc(load, 16)
                sp.dma_start(k.ident[:, :], d["ident"]).then_inc(load, 16)
                sp.dma_start(k.iota[:, :], d["iota16"]).then_inc(load, 16)
                sp.dma_start(k.twos[:, :], d["twos"]).then_inc(load, 16)
                sp.wait_ge(load, 64)

            @block.gpsimd
            def _(pool):
                nc.gpsimd.memset(k.onesb[:, :], 1.0)
                nc.gpsimd.memset(k.ones[:, :], 1.0)

        for layer in (layer0_cross, layer0_self, layer0_ff, layer1_cross, layer1_self, layer1_ff,
                      layer2_cross, layer2_self, layer2_ff, layer3_cross, layer3_self, layer3_ff):
            layer(nc, k, d)

        with stage(nc, "stored", "unused2") as (block, stored, _unused):
            @block.sync
            def _(sp):
                sp.dma_start(out.rearrange("b (i p) f -> p (b i) f", p=P), k.X[:, :, :]).then_inc(stored, 16)
                sp.wait_ge(stored, 16)


def layouts(inp):
    def rows(w):
        return np.ascontiguousarray(np.asarray(w).reshape(-1, P, np.asarray(w).shape[-1]).transpose(1, 0, 2))

    def cols(v):
        return np.ascontiguousarray(np.asarray(v).reshape(-1, P).T)

    def spread(v):
        return np.ascontiguousarray(np.broadcast_to(np.asarray(v).reshape(1, -1), (P, np.asarray(v).size)))

    i = {n: np.asarray(a) for n, a in inp.items()}
    a = {}
    a["x"] = rows(i["x"].reshape(T, D))
    ctx = i["ctx_1024"]
    a["ctxT"] = np.stack([rows(np.ascontiguousarray(ctx[b].T)) for b in range(B)])
    a["ctx_rows"] = np.stack([rows(ctx[b]) for b in range(B)])
    a["ident"] = np.eye(P, dtype=np.float32)
    a["iota16"] = np.ascontiguousarray(np.broadcast_to(np.arange(NH, dtype=np.float32), (P, NH)))
    a["L0x_wqT"], a["L0x_wk"] = rows(i["L0_xattn_Wq"].T), rows(i["L0_xattn_Wk"])
    a["L0x_bq"] = cols(i["L0_xattn_bq"])
    a["L0x_wvT"], a["L0x_bv"] = rows(i["L0_xattn_Wv"].T), cols(i["L0_xattn_bv"])
    a["L0x_woT"], a["L0x_bo"] = rows(i["L0_xattn_Wo"].T), spread(i["L0_xattn_bo"])
    for more in (cross_layouts, cross64_layouts, expert_layouts, self_layouts, scan_layouts):
        more(a, i, rows, cols, spread)
    return a


def kernel(**inputs):
    import concourse.bacc as bacc
    from concourse.bass_utils import run_bass_kernel_spmd

    nc = bacc.Bacc("TRN2", target_bir_lowering=False, num_devices=1)
    arrays = {"in_" + n: a for n, a in layouts(inputs).items()}
    d = {n[3:]: nc.dram_tensor(n, a.shape, mybir.dt.from_np(a.dtype), kind="ExternalInput").ap() for n, a in arrays.items()}
    out = nc.dram_tensor("out", (B, S, D), F32, kind="ExternalOutput").ap()
    program(nc, d, out)
    r = run_bass_kernel_spmd(nc, [arrays], core_ids=[0])
    return r.results[0]["out"]
```

```python
from contextlib import ExitStack, contextmanager

import numpy as np
import concourse.bass as bass
from concourse import mybir

ALU = mybir.AluOpType
ACT = mybir.ActivationFunctionType
F32 = mybir.dt.float32
BF16 = mybir.dt.bfloat16
U32 = mybir.dt.uint32
AX = mybir.AxisListType.X

P = 128
B = 2
S = 256
D = 256
KC = D // P
T = B * S
TT = T // P
QT = S // P
CTX = 4096
NH = 16


@contextmanager
def stage(nc, *names):
    with ExitStack() as held:
        sems = [held.enter_context(nc.semaphore(n)) for n in names]
        with nc.Block(no_gpsimd_drain=True) as block:
            yield (block, *sems)
        numbers = sorted(s.num for s in sems)
        starts = [n for n in numbers if n - 1 not in numbers]
        runs = [range(n, next(m for m in range(n, n + len(numbers) + 1) if m not in numbers)) for n in starts]
        for run in runs:
            nc.all_engine_barrier(sems_to_clear=run)


class Tensors:

    def __init__(self, nc):
        self.nc, self.held = nc, ExitStack()

    def __enter__(self):
        return self

    def __exit__(self, *said):
        return self.held.__exit__(*said)

    def sb(self, name, shape, dt=F32):
        return self.held.enter_context(self.nc.sbuf_tensor(name, shape, dt))

    def ps(self, name, shape, dt=F32):
        return self.held.enter_context(self.nc.psum_tensor(name, shape, dt))



def layer_norm(nc, k, src, dst, name, dstT=None, gain=None, shift=None, eps=1e-5):
    with Tensors(nc) as t, stage(nc, name + "_load", name + "_stats", name + "_var", name + "_std", name + "_rstd", name + "_normed",
                                 name + "_turned") as (block, load, stats_done, var_done, std_done, rstd_done, normed, turned):
        stats = t.sb(name + "_bn", [P, TT, 6])
        mv = t.sb(name + "_mv", [P, TT, 2])
        std = t.sb(name + "_sd", [P, TT])
        rstd = t.sb(name + "_rs", [P, TT])
        HT = TT // 2
        if dstT is not None:
            flip = t.ps(name + "_flip", [P, 2, KC, 512])
        if gain is not None:
            gb = t.sb(name + "_gb", [P, 2, KC])

            @block.sync
            def _(sp):
                sp.dma_start(gb[:, 0, :], gain).then_inc(load, 16)
                sp.dma_start(gb[:, 1, :], shift).then_inc(load, 16)

        @block.vector
        def _(dve):
            for i in range(TT):
                nc.vector.bn_stats(stats[:, i, :], src[:, i, :]).then_inc(stats_done, 1)
            for i in range(TT):
                dve.wait_ge(stats_done, i + 1)
                nc.vector.bn_aggr(mv[:, i, :], stats[:, i, :]).then_inc(var_done, 1)
            dve.wait_ge(var_done, TT)
            nc.vector.tensor_scalar(std[:, :], mv[:, :, 1], eps, None, ALU.add).then_inc(var_done, 1)
            dve.wait_ge(std_done, 1)
            nc.vector.reciprocal(rstd[:, :], std[:, :]).then_inc(rstd_done, 1)
            dve.wait_ge(rstd_done, 1)
            for i in range(TT):
                nc.vector.tensor_scalar(dst[:, i, :], src[:, i, :], mv[:, i, 0:1], rstd[:, i:i + 1],
                                        ALU.subtract, ALU.mult).then_inc(normed, 1)

        @block.tensor
        def _(pe):
            if dstT is not None:
                for i in range(TT):
                    pe.wait_ge(normed, i + 1)
                    for c in range(KC):
                        m = nc.tensor.transpose(flip[:, i // HT, c, i % HT * P:(i % HT + 1) * P], dst[:, i, c * P:(c + 1) * P], k.ident[:, :])
                    m.then_inc(turned, 1)

        @block.scalar
        def _(act):
            act.wait_ge(var_done, TT + 1)
            nc.scalar.activation(std[:, :], std[:, :], ACT.Sqrt).then_inc(std_done, 1)
            if gain is not None:
                act.wait_ge(load, 32)
            if dstT is not None:
                for half in range(2):
                    act.wait_ge(turned, HT * (half + 1))
                    for c in range(KC):
                        o, i = dstT[:, c, half * HT * P:(half + 1) * HT * P], flip[:, half, c, 0:HT * P]
                        if gain is not None:
                            nc.scalar.activation(o, i, ACT.Identity, bias=gb[:, 1, c:c + 1], scale=gb[:, 0, c:c + 1])
                        else:
                            nc.scalar.copy(o, i)


def transpose_tokens(nc, k, src, dst, name, chunks=KC):
    with Tensors(nc) as t, stage(nc, name + "_turned", name + "_copied") as (block, turned, copied):
        flip = t.ps(name + "_flip", [P, 2, T])

        @block.tensor
        def _(pe):
            turn_chunks(nc, k, pe, src, flip, chunks, turned, copied)

        @block.scalar
        def _(act):
            copy_chunks(nc, act, flip, dst, chunks, turned, copied)


def turn_chunk(nc, k, pe, src, flip, c, turned, copied):
    if c >= 2:
        pe.wait_ge(copied, c - 1)
    for i in range(TT):
        m = nc.tensor.transpose(flip[:, c % 2, i * P:(i + 1) * P], src[:, i, c * P:(c + 1) * P], k.ident[:, :])
    m.then_inc(turned, 1)


def turn_chunks(nc, k, pe, src, flip, chunks, turned, copied):
    for c in range(chunks):
        turn_chunk(nc, k, pe, src, flip, c, turned, copied)


def copy_chunks(nc, act, flip, dst, chunks, turned, copied):
    for c in range(chunks):
        act.wait_ge(turned, c + 1)
        nc.scalar.copy(dst[:, c, :], flip[:, c % 2, :]).then_inc(copied, 1)


def project_tokens(nc, k, src, w, name, chunks=KC, bias=None):
    with Tensors(nc) as t, stage(nc, name + "_load", name + "_turned", name + "_copied", name + "_mm", name + "_sum") as (
            block, load, turned, copied, mm, summed):
        wt = t.sb(name + "_w", [P, chunks, D])
        br = t.sb(name + "_b", [P, D])
        srcT = t.sb(name + "_T", [P, chunks, T])
        flip = t.ps(name + "_flip", [P, 2, T])
        out = t.ps(name + "_o", [P, TT, 512])
        loads = 16 + 16 * (bias is not None)

        @block.sync
        def _(sp):
            sp.dma_start(wt[:, :, :], w).then_inc(load, 16)
            if bias is not None:
                sp.dma_start(br[:, :], bias).then_inc(load, 16)

        @block.tensor
        def _(pe):
            for c in range(chunks + 1):
                if c < chunks:
                    turn_chunk(nc, k, pe, src, flip, c, turned, copied)
                if c == 1:
                    pe.wait_ge(load, loads)
                if c >= 1:
                    pe.wait_ge(copied, c)
                    for i in range(TT):
                        m = nc.tensor.matmul(out[:, i, 0:D], srcT[:, c - 1, i * P:(i + 1) * P], wt[:, c - 1, :],
                                             start=(c == 1), stop=(c == chunks))
                        if c == chunks:
                            m.then_inc(mm, 1)

        @block.scalar
        def _(act):
            copy_chunks(nc, act, flip, srcT, chunks, turned, copied)

        @block.vector
        def _(dve):
            if bias is not None:
                dve.wait_ge(load, loads)
                nc.vector.tensor_tensor(k.X[:, :, :], k.X[:, :, :], br[:, :].unsqueeze(1).broadcast_to([P, TT, D]), ALU.add).then_inc(summed, 1)
                dve.wait_ge(summed, 1)
            for i in range(TT):
                dve.wait_ge(mm, i + 1)
                nc.vector.tensor_tensor(k.X[:, i, :], out[:, i, 0:D], k.X[:, i, :], ALU.add)


def project_residual(nc, k, srcT, w, name, chunks=KC, bias=None):
    with Tensors(nc) as t, stage(nc, name + "_load", name + "_mm", name + "_sum") as (block, load, mm, summed):
        wt = t.sb(name + "_w", [P, chunks, D])
        br = t.sb(name + "_b", [P, D])
        out = t.ps(name + "_o", [P, TT, 512])

        @block.sync
        def _(sp):
            sp.dma_start(wt[:, :, :], w).then_inc(load, 16)
            if bias is not None:
                sp.dma_start(br[:, :], bias).then_inc(load, 16)

        @block.tensor
        def _(pe):
            pe.wait_ge(load, 32 if bias is not None else 16)
            for i in range(TT):
                for c in range(chunks):
                    m = nc.tensor.matmul(out[:, i, 0:D], srcT[:, c, i * P:(i + 1) * P], wt[:, c, :],
                                         start=(c == 0), stop=(c == chunks - 1))
                m.then_inc(mm, 1)

        @block.vector
        def _(dve):
            if bias is not None:
                dve.wait_ge(load, 32)
                for i in range(TT):
                    last = nc.vector.tensor_tensor(k.X[:, i, :], k.X[:, i, :], br[:, :], ALU.add)
                last.then_inc(summed, 1)
                dve.wait_ge(summed, 1)
            for i in range(TT):
                dve.wait_ge(mm, i + 1)
                nc.vector.tensor_tensor(k.X[:, i, :], out[:, i, 0:D], k.X[:, i, :], ALU.add)



def context_attention_one_head(nc, k, d):
    KT = CTX // P
    STEPS = KT // 2
    SCALE = float(D) ** -0.5
    with Tensors(nc) as t:
        QK = t.sb("l0q_keys", [P, KC, T])
        OT = t.sb("l0_out", [P, KC, T])
        V = t.sb("l0_values", [P, TT, D])
        with Tensors(nc) as u, stage(nc, "l0q_load", "l0q_mm", "l0q_ev") as (block, load, mm, ev):
            wq = u.sb("l0_wq", [P, KC, D])
            wk = u.sb("l0_wk", [P, KC, D])
            bq = u.sb("l0_bq", [P, KC])
            qT = u.sb("l0_qT", [P, KC, T])
            ps = u.ps("l0_qps", [P, 2 * KC, T])

            @block.sync
            def _(sp):
                sp.dma_start(wq[:, :, :], d["L0x_wqT"]).then_inc(load, 16)
                sp.dma_start(wk[:, :, :], d["L0x_wk"]).then_inc(load, 16)
                sp.dma_start(bq[:, :], d["L0x_bq"]).then_inc(load, 16)

            @block.tensor
            def _(pe):
                pe.wait_ge(load, 48)
                for half, (w, src) in enumerate(((wq, k.NT), (wk, qT))):
                    if half:
                        pe.wait_ge(ev, KC)
                    for m in range(KC):
                        for c in range(KC):
                            i = nc.tensor.matmul(ps[:, KC * half + m, :], w[:, c, m * P:(m + 1) * P], src[:, c, :],
                                                 start=(c == 0), stop=(c == KC - 1))
                        i.then_inc(mm, 1)

            @block.scalar
            def _(act):
                act.wait_ge(load, 48)
                for m in range(KC):
                    act.wait_ge(mm, m + 1)
                    nc.scalar.activation(qT[:, m, :], ps[:, m, :], ACT.Identity, bias=bq[:, m:m + 1]).then_inc(ev, 1)
                for m in range(KC):
                    act.wait_ge(mm, KC + m + 1)
                    nc.scalar.copy(QK[:, m, :], ps[:, KC + m, :]).then_inc(ev, 1)

        with nc.Fori(0, B) as b:
            with Tensors(nc) as u, stage(nc, "l0_load0", "l0_load1", "l0_load2", "l0_load3", "l0_rows_load", "l0_casts", "l0_peaks", "l0_peak_read", "l0_diag", "l0_scored",
                                         "l0_exps", "l0_averaged", "l0_normed") as (
                    block, load0, load1, load2, load3, rows_load, casts, peaks, peak_read, diag, scored, exps, averaged, normed):
                NB = CTX // 512
                loads = (load0, load1, load2, load3)
                cT = u.sb("l0_cT", [P, KC, CTX])
                cTb = u.sb("l0_cTb", [P, KC, CTX], BF16)
                V1 = u.sb("l0_V1", [P, KT, D + 1])
                q = u.sb("l0_q", [P, KC, S])
                qb = u.sb("l0_qb", [P, KC, S], BF16)
                pk = u.sb("l0_pk", [P, QT, NB])
                mx = u.sb("l0_mx", [P, QT])
                dg = u.sb("l0_dg", [P, QT, P], BF16)
                pr = u.sb("l0_pr", [P, 2, 2, S])
                rec = u.sb("l0_rec", [P, QT])
                psm = u.ps("l0_psm", [P, 2, 512])
                pss = u.ps("l0_pss", [P, 2, 2, S])
                pso = u.ps("l0_pso", [P, QT, 512])

                @block.sync
                def _(sp):
                    for x, load in enumerate(loads):
                        span = slice(x * CTX // 4, (x + 1) * CTX // 4)
                        sp.dma_start(cT[:, :, span], d["ctxT"][b][:, :, span]).then_inc(load, 16)
                    sp.dma_start(V1[:, :, 0:D], d["ctx_rows"][b]).then_inc(rows_load, 16)

                @block.gpsimd
                def _(pool):
                    nc.gpsimd.tensor_copy(q[:, :, :], QK[:, :, bass.ds(b * S, S)]).then_inc(casts, 1)
                    nc.gpsimd.memset(V1[:, :, D:D + 1], 1.0).then_inc(casts, 1)
                    pool.wait_ge(casts, 2)
                    nc.gpsimd.tensor_copy(qb[:, :, :], q[:, :, :]).then_inc(casts, 1)

                @block.tensor
                def _(pe):
                    pe.wait_ge(casts, 3)
                    for n in range(QT * NB):
                        j, qt = divmod(n, QT)
                        if qt == 0:
                            pe.wait_ge(exps, j + 1)
                        if n >= 2:
                            pe.wait_ge(peak_read, n - 1)
                        for c in range(KC):
                            m = nc.tensor.matmul(psm[:, n % 2, :], qb[:, c, qt * P:(qt + 1) * P],
                                                 cTb[:, c, j * 512:(j + 1) * 512], start=(c == 0), stop=(c == KC - 1))
                        m.then_inc(peaks, 1)
                    pe.wait_ge(diag, 1)
                    for s in range(STEPS + 1):
                        if s < STEPS:
                            if s >= 2:
                                pe.wait_ge(exps, NB + s - 1)
                            for qt in range(QT):
                                nc.tensor.matmul(pss[:, s % 2, :, qt * P:(qt + 1) * P], k.onesb[:, :],
                                                 dg[:, qt, :].unsqueeze(1).broadcast_to([P, 2, P]), start=(qt == 0), stop=False,
                                                 skip_group_check=True)
                            for h in range(2):
                                for c in range(KC):
                                    m = nc.tensor.matmul(pss[:, s % 2, h, :], cT[:, c, (2 * s + h) * P:(2 * s + h + 1) * P],
                                                         q[:, c, :], start=False, stop=(c == KC - 1), skip_group_check=True)
                            m.then_inc(scored, 1)
                        if s >= 1:
                            pe.wait_ge(exps, NB + s)
                            if s == 1:
                                pe.wait_ge(rows_load, 16)
                            for h in range(2):
                                kt = 2 * (s - 1) + h
                                for qt in range(QT):
                                    m = nc.tensor.matmul(pso[:, qt, 0:D + 1], pr[:, (s - 1) % 2, h, qt * P:(qt + 1) * P],
                                                         V1[:, kt, :], start=(kt == 0), stop=(kt == KT - 1))
                            m.then_inc(averaged, 1)

                @block.vector
                def _(dve):
                    for n in range(QT * NB):
                        dve.wait_ge(peaks, n + 1)
                        nc.vector.reduce_max(pk[:, n % QT, n // QT:n // QT + 1], psm[:, n % 2, :], AX).then_inc(peak_read, 1)
                    dve.wait_ge(peak_read, QT * NB)
                    nc.vector.reduce_max(mx[:, :], pk[:, :, :], AX).then_inc(peak_read, 1)
                    dve.wait_ge(peak_read, QT * NB + 1)
                    for qt in range(QT):
                        m = nc.vector.tensor_scalar(dg[:, qt, :], k.ident[:, :], mx[:, qt:qt + 1], -1.0, ALU.mult, ALU.mult)
                    m.then_inc(diag, 1)
                    dve.wait_ge(averaged, STEPS)
                    nc.vector.reciprocal(rec[:, :], pso[:, :, D]).then_inc(normed, 1)
                    dve.wait_ge(normed, 1)
                    for qt in range(QT):
                        nc.vector.tensor_scalar(V[:, bass.ds(b * QT + qt, 1), :], pso[:, qt:qt + 1, 0:D], rec[:, qt:qt + 1], None,
                                                ALU.mult)

                @block.scalar
                def _(act):
                    for j in range(NB):
                        act.wait_ge(loads[j // (NB // 4)], 16)
                        nc.scalar.copy(cTb[:, :, j * 512:(j + 1) * 512], cT[:, :, j * 512:(j + 1) * 512]).then_inc(exps, 1)
                    for s in range(STEPS):
                        act.wait_ge(scored, s + 1)
                        if s >= 2:
                            act.wait_ge(averaged, s - 1)
                        nc.scalar.activation(pr[:, s % 2, :, :], pss[:, s % 2, :, :], ACT.Exp, scale=SCALE).then_inc(exps, 1)

        transpose_tokens(nc, k, V, OT, "l0_avg")
        linear_T(nc, k, OT, QK, d["L0x_wvT"], "l0_v", bias=d["L0x_bv"])
        project_residual(nc, k, QK, d["L0x_woT"], "l0_o", bias=d["L0x_bo"])


def linear_T(nc, k, srcT, dstT, w, name, bias=None, out_chunks=KC, in_chunks=KC):
    with Tensors(nc) as t, stage(nc, name + "_load", name + "_mm", name + "_ev") as (block, load, mm, ev):
        wt = t.sb(name + "_w", [P, in_chunks, out_chunks * P])
        bt = t.sb(name + "_b", [P, out_chunks])
        ps = t.ps(name + "_ps", [P, 2, T])
        loads = 16 + 16 * (bias is not None)

        @block.sync
        def _(sp):
            sp.dma_start(wt[:, :, :], w).then_inc(load, 16)
            if bias is not None:
                sp.dma_start(bt[:, :], bias).then_inc(load, 16)

        @block.tensor
        def _(pe):
            pe.wait_ge(load, loads)
            for m in range(out_chunks):
                if m >= 2:
                    pe.wait_ge(ev, m - 1)
                for c in range(in_chunks):
                    i = nc.tensor.matmul(ps[:, m % 2, :], wt[:, c, m * P:(m + 1) * P], srcT[:, c, :],
                                         start=(c == 0), stop=(c == in_chunks - 1))
                i.then_inc(mm, 1)

        @block.scalar
        def _(act):
            act.wait_ge(load, loads)
            for m in range(out_chunks):
                act.wait_ge(mm, m + 1)
                if bias is not None:
                    nc.scalar.activation(dstT[:, m, :], ps[:, m % 2, :], ACT.Identity, bias=bt[:, m:m + 1]).then_inc(ev, 1)
                else:
                    nc.scalar.copy(dstT[:, m, :], ps[:, m % 2, :]).then_inc(ev, 1)


def layer0_cross(nc, k, d):
    layer_norm(nc, k, k.X, k.N, "n0", k.NT)
    context_attention_one_head(nc, k, d)



HD16, HD64 = 16, 64


def context_attention(nc, k, d, pre, keysT, n_keys, hd, groups, out_tokens, biased):
    small = hd == HD16
    HPC = P // hd
    KT = n_keys // P
    SCALE = float(hd) ** -0.5
    G = KC * P
    UH = min(HPC, 4)
    SK = 4 // UH
    STEPS = KT // SK
    UNITS = [(c, h) for c in range(KC) for h in range(0, HPC, UH)]
    NQ = [(j * 512, min(512, n_keys - j * 512)) for j in range((n_keys + 511) // 512)]
    NB = len(NQ)
    VW = hd + 1 if small else hd
    GH = G // hd
    VOFF = P // UH
    NK = KC * NB
    NV = KT // 2
    NP = UH * QT * NB
    RING = 3 if small else 2
    KPART = (0, 1, 0, 1, 0, 2)
    QPART = (0, 0, 1, 1, 2, 0)
    NPART = len(KPART)
    ONE = NPART * HD16
    assert not small or NK == KC * HPC

    with Tensors(nc) as t:
        V = t.sb(pre + "_V", [P, KT, GH, VW])
        Kb = t.sb(pre + "_Kb", [P, KC, n_keys], BF16)
        qzb = t.sb(pre + "_qzb", [P, KC, HPC, S], BF16)
        if small:
            K2 = t.sb(pre + "_K2", [P, KC, n_keys], BF16)
            K3 = t.sb(pre + "_K3", [P, KC, n_keys], BF16)
            KS0 = t.sb(pre + "_KS0", [P, UH, n_keys], BF16)
            cT = t.sb(pre + "_cT", [P, KC, n_keys])
            KS = (KS0, cT[:, :, :].rearrange("p c n -> p (c n)").bitcast(BF16).rearrange("p (h n) -> p h n", h=UH))
            QS = t.sb(pre + "_QS", [P, GH, S], BF16)
            qscratch = nc.dram_tensor(pre + "_query_parts", (3, KC, P, S), BF16, kind="Internal").ap()
        else:
            cT = t.sb(pre + "_cT", [P, KC, n_keys])
            Ke = t.sb(pre + "_Ke", [P, KC, n_keys])
            Ko = t.sb(pre + "_Ko", [P, KC, n_keys])
            Q = t.sb(pre + "_Q", [P, KC, 2, S])
        env = dict(keysT=keysT, n_keys=n_keys, hd=hd, out_tokens=out_tokens, biased=biased, small=small, HPC=HPC, KT=KT, SCALE=SCALE, G=G, UH=UH, SK=SK, STEPS=STEPS, UNITS=UNITS,
                   NQ=NQ, NB=NB, VW=VW, GH=GH, VOFF=VOFF, NK=NK, NV=NV, NP=NP, RING=RING, KPART=KPART, QPART=QPART, NPART=NPART, ONE=ONE, V=V, Kb=Kb, qzb=qzb, cT=cT)
        if small:
            env.update(K2=K2, K3=K3, KS=KS, QS=QS, qscratch=qscratch)
        else:
            env.update(Ke=Ke, Ko=Ko, Q=Q)
        with stage(nc, pre + "_fill", pre + "_fill1") as (block, filled, _v):
            @block.gpsimd
            def _(pool):
                if small:
                    nc.gpsimd.memset(V[:, :, :, hd:hd + 1], 1.0)

            @block.vector
            def _(dve):
                if not small:
                    nc.vector.memset(Q[:, :, :, :], 0.0)

        with nc.Fori(0, B) as b:
            if not small:
                normed_context(nc, k, d, "L1c", b, cT, V[:, :, :, :].rearrange("p t h e -> p (t h e)"), k.NT, (Ke[64:128, :, :], Ko[0:64, :, :]))
            with nc.Fori(0, groups) as g:
                attend_group(nc, k, d, pre, env, b, g)


def attend_group(nc, k, d, pre, env, b, g):
    (keysT, n_keys, hd, out_tokens, biased, small, HPC, KT, SCALE, G, UH, SK, STEPS, UNITS, NQ, NB, VW, GH, VOFF, NK, NV, NP, RING,
     KPART, QPART, NPART, ONE, V, Kb, qzb, cT) = [env[n] for n in (
         "keysT n_keys hd out_tokens biased small HPC KT SCALE G UH SK STEPS UNITS NQ NB VW GH VOFF NK NV NP RING "
         "KPART QPART NPART ONE V Kb qzb cT").split()]
    if small:
        K2, K3, KS, QS, qscratch = [env[n] for n in ("K2", "K3", "KS", "QS", "qscratch")]
    else:
        Ke, Ko, Q = env["Ke"], env["Ko"], env["Q"]
    AHEAD = STEPS - 3
    names = ("wload cload0 cload1 cload2 cload3 nt_here q_mm q_ev qp_dve qp_pool q_out q_in k_mm k_act k_dve k_r k_pool v_mm v_ev bv_here ones_rows "
             "stack0 stack1 peaks peak_read peak rows row_in scored exps averaged sum_dve sum_pool o_copied turned normed chain").split()
    with Tensors(nc) as u, stage(nc, *[pre + "_" + n for n in names]) as (block, *sems):
        (wload, cload0, cload1, cload2, cload3, nt_here, q_mm, q_ev, qp_dve, qp_pool, q_out, q_in, k_mm, k_act, k_dve, k_r, k_pool, v_mm, v_ev,
         bv_here, ones_rows, stack0, stack1, peaks, peak_read, peak, rows, row_in, scored, exps, averaged, sum_dve, sum_pool, o_copied, turned,
         normed, chain) = sems
        cloads, stacks = (cload0, cload1, cload2, cload3), (stack0, stack1)
        if small:
            w = u.sb(pre + "_w", [P, 3, KC, G])
        else:
            acc = u.sb(pre + "_acc", [P, 2, SK, UH, S])
            w = acc[:, :, :, :, :].rearrange("p a e h s -> p (a e h s)")[:, 0:3 * KC * G].rearrange("p (x c n) -> p x c n", x=3, c=KC)
        bias = u.sb(pre + "_b2", [P, 2, KC])
        bv = u.sb(pre + "_bv", [P, G])
        mask = u.sb(pre + "_mask", [P, HPC])
        nt = u.sb(pre + "_nt", [P, KC, S])
        pk = u.sb(pre + "_pk", [P, 2, UH * QT, NB])
        mx = u.sb(pre + "_mx", [P, 2, UH * QT])
        pr = u.sb(pre + "_pr", [P, RING, SK, UH, S])
        rec = u.sb(pre + "_rec", [P, QT, UH])
        if small:
            oc = u.sb(pre + "_oc", [P, 2, S])
            tv = u.sb(pre + "_tv", [P, QT, UH, hd])
        else:
            spare = k.N[:, :, :].rearrange("p i f -> p (i f)")
            oc = spare[:, 0:2 * S].rearrange("p (a s) -> p a s", a=2)
            tv = spare[:, 2 * S:3 * S].rearrange("p (t h e) -> p t h e", t=QT, h=UH)
        pss = u.ps(pre + "_pss", [P, 2, 2, 512])
        psm = u.ps(pre + "_psm", [P, 2, 512])
        pso = u.ps(pre + "_pso", [P, 512])
        pst = u.ps(pre + "_pst", [P, 512])
        tiles = pss[:, :, :, :].rearrange("p a x n -> p (a x) n")
        if small:
            slots = [pr[:, x, :, :, :].rearrange("p e h s -> p (e h s)") for x in range(RING)]
            kf, kr = (slots[x].rearrange("p (a n) -> p a n", a=2) for x in range(2))
            qf = slots[2].rearrange("p (a c s) -> p a c s", a=2, c=KC)
            qp = u.sb(pre + "_qp", [P, 3, KC, S], BF16)
        else:
            psd = pst[:, 2 * P:2 * P + UH * QT]

        def pool_casts(n):
            return n - n // 4

        def unit_share(s):
            return min(NP, (s + 1) * NP // AHEAD)

        PLAIN = 4

        def first_share(r):
            return min(NP, max(0, r + 1 - PLAIN) * NP // (NV - 1 - PLAIN))

        @block.sync
        def _(sp):
            sp.dma_start(w[:, 0, :, :], d[pre + "_w3"][g][:, 0]).then_inc(wload, 16)
            sp.dma_start(w[:, 1, :, :], d[pre + "_w3"][g][:, 1]).then_inc(wload, 16)
            sp.dma_start(mask[:, :], d["mask%d" % hd]).then_inc(wload, 16)
            sp.dma_start(bias[:, :, :], d[pre + "_b2"][g]).then_inc(wload, 16)
            sp.dma_start(w[:, 2, :, :], d[pre + "_w3"][g][:, 2]).then_inc(cloads[0] if not small else nt_here, 16)
            if small:
                for x in range(4):
                    n = n_keys // 4
                    sp.dma_start(cT[:, :, x * n:(x + 1) * n], keysT[b][:, :, x * n:(x + 1) * n]).then_inc(cloads[x], 16)
            sp.dma_start(bv[:, :], d[pre + "_bv"][g]).then_inc(bv_here, 16)
            if small:
                sp.wait_ge(qp_pool, 1)
                sp.wait_ge(qp_dve, 2)
                for c in range(KC):
                    sp.dma_start(qscratch[:, c].rearrange("x p s -> p x s"), qp[:, :, c, :]).then_inc(q_out, 16)
                sp.wait_ge(q_out, 16 * KC)
                for s, part in enumerate(QPART):
                    sp.dma_start(QS[s * hd:(s + 1) * hd, :, :],
                                 qscratch[part].rearrange("c (h r) s -> r (c h) s", r=hd)).then_inc(q_in, 16)
                for n, (c, h0) in enumerate(UNITS):
                    sp.wait_ge(k_act, NK)
                    sp.wait_ge(k_pool, pool_casts(NK))
                    sp.wait_ge(k_dve, NK)
                    if n == 1:
                        sp.wait_ge(v_mm, NV)
                    if n >= 2:
                        sp.wait_ge(scored, (n - 1) * STEPS)
                    for h in range(UH):
                        p0 = (h0 + h) * hd
                        for s, part in enumerate(KPART):
                            sp.dma_start(KS[n % 2][s * hd:(s + 1) * hd, h, :], (Kb, K2, K3)[part][p0:p0 + hd, c, :]).then_inc(stacks[n % 2], 16)

        @block.gpsimd
        def _(pool):
            nc.gpsimd.tensor_copy(nt[:, :, :], k.NT[:, :, bass.ds(b * S, S)]).then_inc(nt_here, 1)
            if small:
                pool.wait_ge(qp_dve, 1)
                nc.gpsimd.tensor_copy(qp[:, 1, :, :], qf[:, 1, :, :]).then_inc(qp_pool, 1)
                for n in [n for n in range(NK) if n % 4 < 3]:
                    j, m = divmod(n, KC)
                    pool.wait_ge(k_r, n + 1)
                    nc.gpsimd.tensor_copy(K2[:, m, j * 512:(j + 1) * 512], kr[:, n % 2, :]).then_inc(k_pool, 1)
                pool.wait_ge(k_pool, pool_casts(NK))
                nc.gpsimd.memset(KS[0][ONE:ONE + 1, :, :], 1.0).then_inc(ones_rows, 1)
                pool.wait_ge(ones_rows, 1)
                pool.wait_ge(v_mm, NV)
                nc.gpsimd.memset(KS[1][ONE:ONE + 1, :, :], 1.0).then_inc(ones_rows, 1)
            else:
                for n in range(len(UNITS)):
                    for s in range(STEPS):
                        a = n * STEPS + s
                        pool.wait_ge(exps, a + 1)
                        if s:
                            pool.wait_ge(sum_pool, a)
                            i = nc.gpsimd.tensor_tensor(acc[:, n % 2, 1, :, :], acc[:, n % 2, 1, :, :], pr[:, a % RING, 1, :, :], ALU.add)
                        else:
                            i = nc.gpsimd.tensor_copy(acc[:, n % 2, 1, :, :], pr[:, a % RING, 1, :, :])
                        i.then_inc(sum_pool, 1)

        @block.tensor
        def _(pe):
            pe.wait_ge(wload, 64)
            pe.wait_ge(nt_here, 1 + 16 * small)
            for m in range(KC):
                for c in range(KC):
                    i = nc.tensor.matmul(pso[:, m * S:(m + 1) * S], w[:, 0, c, m * P:(m + 1) * P], nt[:, c, :],
                                         start=(c == 0), stop=(c == KC - 1))
            i.then_inc(q_mm, 1)

            def bank_free(n):
                if 4 <= n < NK + 4:
                    pe.wait_ge(k_act, n - 3)
                    if not small:
                        pe.wait_ge(k_dve, n - 3)
                elif n >= NK + 4:
                    pe.wait_ge(v_ev, n - 3 - NK)

            def peak_products(n, first, last):
                c, h0 = UNITS[n]
                for i in range(first, last):
                    hq, j = divmod(i, NB)
                    h, qt = divmod(hq, QT)
                    o, w_ = NQ[j]
                    if n * (NP + 1) + i >= 2:
                        pe.wait_ge(peak_read, n * (NP + 1) + max(i - 1, 0))
                    nc.tensor.matmul(psm[:, i % 2, 0:w_], qzb[:, c, h0 + h, qt * P:(qt + 1) * P], Kb[:, c, o:o + w_],
                                     start=True, stop=True).then_inc(peaks, 1)

            def peak_rows(n):
                pe.wait_ge(peak, n + 1)
                for h in range(UH):
                    p0 = ONE if small else (64, 0)[h]
                    for qt in range(QT):
                        hq = h * QT + qt
                        o = (h % 2) * S + qt * P if small else qt * P
                        i = nc.tensor.matmul(psm[p0:p0 + 1, h // 2 if small else h, o:o + P], mx[:, n % 2, hq:hq + 1], k.ident[:, :],
                                             start=True, stop=True)
                i.then_inc(rows, 1)

            for n in range(NK):
                j, m = divmod(n, KC)
                o, w_ = NQ[j]
                if small and m == 0 and j % (NB // 4) == 0:
                    pe.wait_ge(cloads[j // (NB // 4)], 16)
                bank_free(n)
                for c in range(KC):
                    i = nc.tensor.matmul(tiles[:, n % 4, 0:w_], w[:, 1, c, m * P:(m + 1) * P], cT[:, c, o:o + w_],
                                         start=(c == 0), stop=(c == KC - 1))
                i.then_inc(k_mm, 1)
            if not small:
                pe.wait_ge(cloads[0], 16)
            for r in range(NV):
                bank_free(NK + r)
                if r == PLAIN:
                    pe.wait_ge(k_act, NK)
                    pe.wait_ge(q_ev, KC * HPC)
                done = first_share(r - 1)
                share = first_share(r) - done
                for h in range(2):
                    for c in range(KC):
                        i = nc.tensor.matmul(tiles[:, (NK + r) % 4, h * G:(h + 1) * G], cT[:, c, (2 * r + h) * P:(2 * r + h + 1) * P],
                                             w[:, 2, c, :], start=(c == 0), stop=(c == KC - 1))
                        q = h * KC + c
                        if q == 3:
                            i.then_inc(v_mm, 1)
                        peak_products(0, done + q * share // 4, done + (q + 1) * share // 4)
            peak_rows(0)

            def average(n, s):
                c, h0 = UNITS[n]
                pe.wait_ge(exps, n * STEPS + s + 1)
                if s == 0:
                    pe.wait_ge(o_copied, n) if n else pe.wait_ge(q_ev, KC * HPC)
                for e in range(SK):
                    for h in range(UH):
                        kt = s * SK + e
                        i = nc.tensor.matmul(pso[VOFF * h:VOFF * h + VW, 0:S], V[:, kt, c * HPC + h0 + h, :],
                                             pr[:, (n * STEPS + s) % RING, e, h, :], start=(kt == 0), stop=(kt == KT - 1),
                                             skip_group_check=True)
                i.then_inc(averaged, 1)

            def finish(n):
                pe.wait_ge(o_copied, n + 1)
                if n >= 1:
                    pe.wait_ge(normed, n)
                if not small:
                    pe.wait_ge(sum_dve, STEPS * (n + 1))
                    pe.wait_ge(sum_pool, STEPS * (n + 1))
                    for h in range(UH):
                        for qt in range(QT):
                            for e in range(SK):
                                nc.tensor.matmul(psd[:, qt * UH + h:qt * UH + h + 1], acc[:, n % 2, e, h, qt * P:(qt + 1) * P],
                                                 k.ones[:, 0:1], start=(e == 0), stop=(e == SK - 1), skip_group_check=True)
                for qt in range(QT):
                    i = nc.tensor.transpose(pst[:, qt * P:(qt + 1) * P], oc[:, n % 2, qt * P:(qt + 1) * P], k.ident[:, :])
                i.then_inc(turned, 1)

            pe.wait_ge(v_ev, NV)
            if small:
                pe.wait_ge(q_in, 16 * NPART)
            for n, (c, h0) in enumerate(UNITS):
                for s in range(STEPS):
                    a = n * STEPS + s
                    if s == 0:
                        pe.wait_ge(row_in, n + 1)
                        if small:
                            pe.wait_ge(stacks[n % 2], 16 * UH * NPART * (n // 2 + 1))
                            if n < 2:
                                pe.wait_ge(ones_rows, n + 1)
                    if a >= 2:
                        pe.wait_ge(exps, a - 1)
                    for e in range(SK):
                        for h in range(UH):
                            i_ = e * UH + h
                            kt = s * SK + e
                            o = pss[:, a % 2, i_ // 2, (i_ % 2) * S:(i_ % 2 + 1) * S]
                            if small:
                                i = nc.tensor.matmul(o, KS[n % 2][0:ONE + 1, h, kt * P:(kt + 1) * P], QS[0:ONE + 1, c * HPC + h0 + h, :],
                                                     start=True, stop=True)
                            else:
                                i = nc.tensor.matmul(o, (Ke, Ko)[h][:, c, kt * P:(kt + 1) * P], Q[:, c, h, :], start=True, stop=True)
                    i.then_inc(scored, 1)
                    first, last = unit_share(s - 1) if s else 0, unit_share(s)
                    if n + 1 < len(UNITS):
                        peak_products(n + 1, first, (first + last) // 2)
                    if s >= 1:
                        average(n, s - 1)
                    elif n >= 1:
                        average(n - 1, STEPS - 1)
                    if n + 1 < len(UNITS):
                        peak_products(n + 1, (first + last) // 2, last)
                        if s == STEPS - 2:
                            peak_rows(n + 1)
                    if s == 2 and n >= 1:
                        finish(n - 1)
            average(len(UNITS) - 1, STEPS - 1)
            finish(len(UNITS) - 1)

        @block.scalar
        def _(act):
            act.wait_ge(wload, 64)
            for n in range(NK):
                j, m = divmod(n, KC)
                o, w_ = NQ[j]
                act.wait_ge(k_mm, n + 1)
                kb = bias[:, 1, m:m + 1]
                if small:
                    if n >= 2:
                        act.wait_ge(k_r, n - 1)
                    nc.scalar.activation(kf[:, n % 2, 0:w_], tiles[:, n % 4, 0:w_], ACT.Identity, bias=kb)
                else:
                    nc.scalar.activation(Ke[0:64, m, o:o + w_], tiles[0:64, n % 4, 0:w_], ACT.Identity, bias=bias[0:64, 1, m:m + 1])
                nc.scalar.activation(Kb[:, m, o:o + w_], tiles[:, n % 4, 0:w_], ACT.Identity, bias=kb).then_inc(k_act, 1)
            for r in range(NV):
                act.wait_ge(v_mm, r + 1)
                nc.scalar.copy(V[:, 2 * r:2 * r + 2, :, 0:hd],
                               tiles[:, (NK + r) % 4, :].rearrange("p (t h e) -> p t h e", t=2, h=GH)).then_inc(v_ev, 1)
            for n in range(len(UNITS)):
                for s in range(STEPS):
                    a = n * STEPS + s
                    act.wait_ge(scored, a + 1)
                    if a >= RING:
                        act.wait_ge(averaged, a - RING + 1)
                        if not small:
                            act.wait_ge(sum_dve, a - RING + 1)
                            act.wait_ge(sum_pool, a - RING + 1)
                    nc.scalar.activation(pr[:, a % RING, :, :, :].rearrange("p e h q -> p (e h q)"),
                                         pss[:, a % 2, :, :].rearrange("p x q -> p (x q)"), ACT.Exp, scale=SCALE).then_inc(exps, 1)

        @block.vector
        def _(dve):
            links = [0]

            def link(i):
                links[0] += 1
                i.then_inc(chain, 1)
                dve.wait_ge(chain, links[0])

            dve.wait_ge(wload, 64)
            dve.wait_ge(q_mm, 1)

            def mask_queries(m, h):
                nc.vector.tensor_scalar(qzb[:, m, h, :], pso[:, m * S:(m + 1) * S], bias[:, 0, m:m + 1], mask[:, h:h + 1],
                                        ALU.add, ALU.mult).then_inc(q_ev, 1)

            for m in range(KC):
                for h in range(HPC):
                    if not small:
                        mask_queries(m, h)
                        half = slice(64 * h, 64 * h + 64)
                        nc.vector.tensor_scalar(Q[half, m, h, :], pso[half, m * S:(m + 1) * S], bias[half, 0, m:m + 1], None,
                                                ALU.add).then_inc(chain, 1)
                        links[0] += 1
                if small:
                    nc.vector.tensor_scalar(qf[:, 0, m, :], pso[:, m * S:(m + 1) * S], bias[:, 0, m:m + 1], None, ALU.add).then_inc(chain, 1)
                    links[0] += 1
            dve.wait_ge(chain, links[0])
            if small:
                link(nc.vector.tensor_copy(qp[:, 0, :, :], qf[:, 0, :, :]))
                nc.vector.tensor_tensor(qf[:, 1, :, :], qf[:, 0, :, :], qp[:, 0, :, :], ALU.subtract).then_inc(qp_dve, 1)
                dve.wait_ge(qp_pool, 1)
                nc.vector.tensor_tensor(qp[:, 2, :, :], qf[:, 1, :, :], qp[:, 1, :, :], ALU.subtract).then_inc(qp_dve, 1)
            for n in range(NK + 1):
                j, m = divmod(n, KC)
                if small:
                    if n < NK:
                        dve.wait_ge(k_act, n + 1)
                        if n >= 2:
                            dve.wait_ge(k_pool, pool_casts(n - 1))
                            dve.wait_ge(k_dve, n - 1)
                        nc.vector.tensor_tensor(kr[:, n % 2, :], kf[:, n % 2, :], Kb[:, m, j * 512:(j + 1) * 512], ALU.subtract).then_inc(k_r, 1)
                        mask_queries(*divmod(n, HPC))
                        if n % 4 == 3:
                            dve.wait_ge(k_r, n + 1)
                            link(nc.vector.tensor_copy(K2[:, m, j * 512:(j + 1) * 512], kr[:, n % 2, :]))
                    if n >= 1:
                        j, m = divmod(n - 1, KC)
                        dve.wait_ge(k_pool, pool_casts(n))
                        nc.vector.tensor_tensor(K3[:, m, j * 512:(j + 1) * 512], kr[:, (n - 1) % 2, :], K2[:, m, j * 512:(j + 1) * 512],
                                                ALU.subtract).then_inc(k_dve, 1)
                elif n < NK:
                    o, w_ = NQ[j]
                    dve.wait_ge(k_act, n + 1)
                    nc.vector.tensor_scalar(Ko[64:128, m, o:o + w_], tiles[64:128, n % 4, 0:w_], bias[64:128, 1, m:m + 1], None,
                                            ALU.add).then_inc(k_dve, 1)

            def read_peaks(n, first, last):
                for i in range(first, last):
                    hq, j = divmod(i, NB)
                    dve.wait_ge(peaks, n * NP + i + 1)
                    nc.vector.reduce_max(pk[:, n % 2, hq, j:j + 1], psm[:, i % 2, 0:NQ[j][1]], AX).then_inc(peak_read, 1)
                if first < NP <= last:
                    dve.wait_ge(peak_read, n * (NP + 1) + NP)
                    link(nc.vector.reduce_max(mx[:, n % 2, :], pk[:, n % 2, :, :], AX))
                    nc.vector.tensor_scalar(mx[:, n % 2, :], mx[:, n % 2, :], -1.0, None, ALU.mult).then_inc(peak, 1)

            def take_rows(n):
                c, h0 = UNITS[n]
                dve.wait_ge(rows, n + 1)
                if small:
                    i = nc.vector.tensor_copy(QS[ONE:ONE + 1, c * HPC + h0:c * HPC + h0 + UH, :].rearrange("p h q -> p (h q)"),
                                              psm[ONE:ONE + 1, :, :].rearrange("p x q -> p (x q)"))
                else:
                    link(nc.vector.tensor_copy(Q[64:65, c, 0, :], psm[64:65, 0, 0:S]))
                    i = nc.vector.tensor_copy(Q[0:1, c, 1, :], psm[0:1, 1, 0:S])
                link(i)
                nc.vector.tensor_copy(mx[:, n % 2, 0:1], mx[:, n % 2, 0:1]).then_inc(peak_read, 1)
                nc.vector.tensor_copy(pk[:, n % 2, 0, 0:1], pk[:, n % 2, 0, 0:1]).then_inc(row_in, 1)

            def sum_step(n, s):
                a = n * STEPS + s
                dve.wait_ge(exps, a + 1)
                if s == 0:
                    if n >= 2:
                        dve.wait_ge(turned, n - 1)
                    i = nc.vector.tensor_copy(acc[:, n % 2, 0, :, :], pr[:, a % RING, 0, :, :])
                else:
                    dve.wait_ge(sum_dve, a)
                    i = nc.vector.tensor_tensor(acc[:, n % 2, 0, :, :], acc[:, n % 2, 0, :, :], pr[:, a % RING, 0, :, :], ALU.add)
                i.then_inc(sum_dve, 1)

            def copy_out(n):
                dve.wait_ge(averaged, (n + 1) * STEPS)
                if n >= 2:
                    dve.wait_ge(turned, n - 1)
                for h in range(UH):
                    i = nc.vector.tensor_copy(oc[VOFF * h:VOFF * h + VW, n % 2, :], pso[VOFF * h:VOFF * h + VW, 0:S])
                    if h < UH - 1:
                        link(i)
                i.then_inc(o_copied, 1)

            def normalize(n):
                c, h0 = UNITS[n]
                dve.wait_ge(turned, n + 1)
                turn = pst[:, 0:2 * P].rearrange("p (t h e) -> p t h e", t=QT, h=UH)
                if small:
                    link(nc.vector.reciprocal(rec[:, :, :], turn[:, :, :, hd]))
                else:
                    link(nc.vector.reciprocal(rec[:, :, :], psd.rearrange("p (t h) -> p t h", t=QT)))
                i = nc.vector.tensor_tensor(tv[:, :, :, :], turn[:, :, :, 0:hd],
                                            rec[:, :, :].unsqueeze(3).broadcast_to([P, QT, UH, hd]), ALU.mult)
                i.then_inc(normed, 1)
                dve.wait_ge(normed, n + 1)
                f = c * P + h0 * hd
                for qt in range(QT):
                    if biased:
                        i = nc.vector.tensor_tensor(out_tokens[:, bass.ds(b * QT + qt, 1), bass.ds(g * G + f, UH * hd)],
                                                    tv[:, qt:qt + 1, :, :].rearrange("p t h e -> p t (h e)"),
                                                    bv[:, f:f + UH * hd].unsqueeze(1), ALU.add)
                    else:
                        i = nc.vector.tensor_copy(out_tokens[:, bass.ds(b * QT + qt, 1), bass.ds(g * G + f, UH * hd)],
                                                  tv[:, qt:qt + 1, :, :].rearrange("p t h e -> p t (h e)"))
                link(i)

            if VW < VOFF:
                link(nc.vector.memset(oc[:, :, :], 0.0))
            dve.wait_ge(bv_here, 16)
            for r in range(NV):
                read_peaks(0, first_share(r - 1), first_share(r))
            take_rows(0)
            for n in range(len(UNITS)):
                for s in range(STEPS):
                    if s == 1 and n >= 1:
                        copy_out(n - 1)
                    if n + 1 < len(UNITS):
                        read_peaks(n + 1, unit_share(s - 1) if s else 0, unit_share(s))
                    if not small:
                        sum_step(n, s)
                    if s == STEPS - 1 and n + 1 < len(UNITS):
                        take_rows(n + 1)
                    if s == 3 and n >= 1:
                        normalize(n - 1)
            copy_out(len(UNITS) - 1)
            normalize(len(UNITS) - 1)


def layer2_cross(nc, k, d):
    cross16(nc, k, d, "L2x")


def layer3_cross(nc, k, d):
    cross16(nc, k, d, "L3x")


def cross16(nc, k, d, pre):
    layer_norm(nc, k, k.X, k.N, pre + "n", k.NT)
    with Tensors(nc) as t:
        context_attention(nc, k, d, pre, d["ctxT"], CTX, HD16, 1, k.N, True)
        project_tokens(nc, k, k.N, d[pre + "_woT"], pre + "p", bias=d[pre + "_bo"])


def cross_layouts(a, i, rows, cols, spread):
    for hd in (HD16, HD64):
        m = np.zeros((P, P // hd), np.float32)
        for h in range(P // hd):
            m[h * hd:(h + 1) * hd, h] = 1
        a["mask%d" % hd] = m
    for n, pre in (("L2_xattn_", "L2x"), ("L3_xattn_", "L3x")):
        a[pre + "_w3"] = np.stack([rows(i[n + w].T) for w in ("Wq", "Wk", "Wv")], 1)[None]
        a[pre + "_b2"] = np.stack([cols(i[n + w]) for w in ("bq", "bk")], 1)[None]
        a[pre + "_bv"] = spread(i[n + "bv"])[None]
        a[pre + "_woT"], a[pre + "_bo"] = rows(i[n + "Wo"].T), spread(i[n + "bo"])



def normed_context(nc, k, d, pre, b, cT, room, latents, ones):
    KT = CTX // P
    R = 8
    x = room[:, 0:KT * D].rearrange("p (i f) -> p i f", i=KT)
    with Tensors(nc) as t, stage(nc, *[pre + f"_load{i}" for i in range(KT // R)], pre + "_gb_load", pre + "_stat", pre + "_var", pre + "_std",
                                 pre + "_rstd", pre + "_norm", pre + "_turned", pre + "_copied", pre + "_filled") as (block, *sems):
        loads, (gb_load, stat, var, std_done, rstd_done, norm, turned, copied, filled) = sems[:KT // R], sems[KT // R:]
        gb = t.sb(pre + "_gb", [P, 2, KC])
        st = t.sb(pre + "_st", [P, 2, R, 6])
        mv = t.sb(pre + "_mv", [P, 2, R, 2])
        sd = t.sb(pre + "_sd", [P, 2, R])
        ps = t.ps(pre + "_ps", [P, 8, 512])

        @block.sync
        def _(sp):
            for i in range(KT // R):
                sp.dma_start(x[:, i * R:(i + 1) * R, :], d["ctx_rows"][b][:, i * R:(i + 1) * R, :]).then_inc(loads[i], 16)
            sp.dma_start(gb[:, 0, :], d[pre + "_mg"]).then_inc(gb_load, 16)
            sp.dma_start(gb[:, 1, :], d[pre + "_mb"]).then_inc(gb_load, 16)

        @block.gpsimd
        def _(pool):
            nc.gpsimd.tensor_copy(cT[:, :, CTX:CTX + S], latents[:, :, bass.ds(b * S, S)]).then_inc(filled, 1)
            for i, rows in enumerate(ones):
                pool.wait_ge(filled, i + 1)
                nc.gpsimd.memset(rows, 1.0).then_inc(filled, 1)

        @block.vector
        def _(dve):
            def norm_rows(r):
                dve.wait_ge(std_done, r + 1)
                nc.vector.reciprocal(sd[:, r % 2, :], sd[:, r % 2, :]).then_inc(rstd_done, 1)
                dve.wait_ge(rstd_done, r + 1)
                for i in range(R):
                    n = r * R + i
                    nc.vector.tensor_scalar(x[:, n, :], x[:, n, :], mv[:, r % 2, i, 0:1], sd[:, r % 2, i:i + 1],
                                            ALU.subtract, ALU.mult).then_inc(norm, 1)

            for r in range(KT // R):
                dve.wait_ge(loads[r], 16)
                if r >= 2:
                    dve.wait_ge(norm, (r - 1) * R)
                for i in range(R):
                    nc.vector.bn_stats(st[:, r % 2, i, :], x[:, r * R + i, :]).then_inc(stat, 1)
                for i in range(R):
                    dve.wait_ge(stat, r * R + i + 1)
                    nc.vector.bn_aggr(mv[:, r % 2, i, :], st[:, r % 2, i, :]).then_inc(var, 1)
                dve.wait_ge(var, r * (R + 1) + R)
                nc.vector.tensor_scalar(sd[:, r % 2, :], mv[:, r % 2, :, 1], 1e-5, None, ALU.add).then_inc(var, 1)
                if r >= 1:
                    norm_rows(r - 1)
            norm_rows(KT // R - 1)

        @block.tensor
        def _(pe):
            for q in range(KT // 4):
                pe.wait_ge(norm, 4 * q + 4)
                if q >= 4:
                    pe.wait_ge(copied, KC * (q - 3))
                for c in range(KC):
                    for e in range(4):
                        m = nc.tensor.transpose(ps[:, (KC * q + c) % 8, e * P:(e + 1) * P], x[:, 4 * q + e, c * P:(c + 1) * P], k.ident[:, :])
                    m.then_inc(turned, 1)

        @block.scalar
        def _(act):
            act.wait_ge(gb_load, 32)

            def copy_banks(q):
                for c in range(KC):
                    n = KC * q + c
                    act.wait_ge(turned, n + 1)
                    nc.scalar.activation(cT[:, c, q * 512:(q + 1) * 512], ps[:, n % 8, :], ACT.Identity, bias=gb[:, 1, c:c + 1],
                                         scale=gb[:, 0, c:c + 1]).then_inc(copied, 1)

            for r in range(KT // R):
                act.wait_ge(var, (r + 1) * (R + 1))
                nc.scalar.activation(sd[:, r % 2, :], sd[:, r % 2, :], ACT.Sqrt).then_inc(std_done, 1)
                if r >= 1:
                    copy_banks(2 * r - 2)
                    copy_banks(2 * r - 1)
            copy_banks(KT // 4 - 2)
            copy_banks(KT // 4 - 1)


def layer1_cross(nc, k, d):
    layer_norm(nc, k, k.X, k.N, "L1na")
    layer_norm(nc, k, k.N, k.N, "L1nb", k.NT, gain=d["L1x_lg"], shift=d["L1x_lb"])
    with Tensors(nc) as t:
        O = t.sb("L1x_O", [P, TT, NH * HD64])
        context_attention(nc, k, d, "L1x", None, CTX + S, HD64, 4, O, False)
        project_tokens(nc, k, O, d["L1x_wo"], "L1p", chunks=NH * HD64 // P)


def cross64_layouts(a, i, rows, cols, spread):
    n = "L1_xattn_"
    a["L1c_mg"], a["L1c_mb"] = cols(i[n + "ln_m_g"]), cols(i[n + "ln_m_b"])
    a["L1x_lg"], a["L1x_lb"] = cols(i[n + "ln_l_g"]), cols(i[n + "ln_l_b"])
    inner = NH * HD64
    ws = (i[n + "Wq"], i[n + "Wkv"][:, :inner], i[n + "Wkv"][:, inner:])
    a["L1x_w3"] = np.stack([np.stack([rows(w[:, g * D:(g + 1) * D]) for w in ws], 1) for g in range(4)])
    a["L1x_b2"] = np.zeros((4, P, 2, KC), np.float32)
    a["L1x_bv"] = np.zeros((4, P, D), np.float32)
    a["L1x_wo"] = rows(i[n + "Wout"])



def experts(nc, k, pieces, name, n_experts, chunks, body, kind, weights, b1=None):
    gated = kind == "swiglu"
    NIN = 2 if gated else 1
    PW = 2 * (NIN * KC * P + D)
    PIECES = body * chunks // 2
    STEPS = body * chunks
    NR = 2
    with nc.Fori(0, n_experts // body) as it, Tensors(nc) as t:
        with stage(nc, *[name + f"_load{i}" for i in range(PIECES)], name + "_w", name + "_in", name + "_act", name + "_hid",
                   name + "_out", name + "_added") as (block, *sems):
            loads, (w_here, in_done, act_done, hid_done, out_done, added) = sems[:PIECES], sems[PIECES:]
            wt = t.sb(name + "_wt", [P, PIECES, PW])
            wi = t.sb(name + "_wi", [P, TT, body])
            g_act = t.sb(name + "_g", [P, 2, T])
            hT = t.sb(name + "_h", [P, 3, T])
            if b1 is not None:
                bt = t.sb(name + "_b1", [P, STEPS])
            pin = t.ps(name + "_pin", [P, NR, NIN, T])
            pout = t.ps(name + "_pout", [P, TT, 512])

            def w_in(s, part, c):
                p, half = divmod(s, 2)
                o = (part * KC + c) * 2 * P + half * P
                return wt[:, p, o:o + P]

            def w_out(s):
                p, half = divmod(s, 2)
                o = NIN * KC * 2 * P + half * D
                return wt[:, p, o:o + D]

            @block.sync
            def _(sp):
                if b1 is not None:
                    sp.dma_start(bt[:, :], b1[it]).then_inc(w_here, 16)
                for p in range(PIECES):
                    sp.dma_start(wt[:, p, :], pieces[it * PIECES + p]).then_inc(loads[p], 16)

            @block.gpsimd
            def _(pool):
                nc.gpsimd.tensor_copy(wi[:, :, :], weights[:, :, bass.ds(it * body, body)]).then_inc(w_here, 1)

            @block.tensor
            def _(pe):
                for s in range(STEPS + 1):
                    if s < STEPS:
                        if s % 2 == 0:
                            pe.wait_ge(loads[s // 2], 16)
                        if s >= NR:
                            pe.wait_ge(hid_done, s - NR + 1)
                        for part in range(NIN):
                            for c in range(KC):
                                m = nc.tensor.matmul(pin[:, s % NR, part, :], w_in(s, part, c), k.NT[:, c, :],
                                                     start=(c == 0), stop=(c == KC - 1))
                        m.then_inc(in_done, 1)
                    if s >= 1:
                        r = s - 1
                        pe.wait_ge(hid_done, r + 1)
                        e, j = divmod(r, chunks)
                        for i in range(TT):
                            if j == 0 and e >= 1:
                                pe.wait_ge(added, TT * (e - 1) + i + 1)
                            m = nc.tensor.matmul(pout[:, i, 0:D], hT[:, r % 3, i * P:(i + 1) * P], w_out(r),
                                                 start=(j == 0), stop=(j == chunks - 1))
                            m.then_inc(out_done, 1)

            @block.scalar
            def _(act):
                if b1 is not None:
                    act.wait_ge(w_here, 17)
                for s in range(STEPS):
                    act.wait_ge(in_done, s + 1)
                    if gated:
                        if s >= 2:
                            act.wait_ge(hid_done, s - 1)
                        nc.scalar.activation(g_act[:, s % 2, :], pin[:, s % NR, 1, :], ACT.Silu).then_inc(act_done, 1)
                    else:
                        if s >= 3:
                            act.wait_ge(out_done, TT * (s - 2))
                        if kind == "gelu":
                            nc.scalar.activation(hT[:, s % 3, :], pin[:, s % NR, 0, :], ACT.Gelu_apprx_tanh,
                                                 bias=bt[:, s:s + 1]).then_inc(hid_done, 1)
                        elif kind == "gelu_erf":
                            nc.scalar.activation(hT[:, s % 3, :], pin[:, s % NR, 0, :], ACT.Gelu,
                                                 bias=bt[:, s:s + 1]).then_inc(hid_done, 1)
                        else:
                            nc.scalar.activation(hT[:, s % 3, :], pin[:, s % NR, 0, :], ACT.Relu).then_inc(hid_done, 1)

            @block.vector
            def _(dve):
                dve.wait_ge(w_here, 17 if b1 is not None else 1)

                def add_expert(e):
                    for i in range(TT):
                        dve.wait_ge(out_done, TT * chunks * e + TT * (chunks - 1) + i + 1)
                        nc.vector.scalar_tensor_tensor(k.X[:, i, :], pout[:, i, 0:D], wi[:, i, e:e + 1], k.X[:, i, :],
                                                       ALU.mult, ALU.add).then_inc(added, 1)

                done = 0
                for s in range(STEPS):
                    if gated:
                        dve.wait_ge(act_done, s + 1)
                        if s >= 3:
                            dve.wait_ge(out_done, TT * (s - 2))
                        nc.vector.tensor_tensor(hT[:, s % 3, :], pin[:, s % NR, 0, :], g_act[:, s % 2, :], ALU.mult).then_inc(hid_done, 1)
                    if s >= 1 and s % chunks == 0:
                        if done:
                            dve.wait_ge(added, TT * done)
                        add_expert(done)
                        done += 1
                if done:
                    dve.wait_ge(added, TT * done)
                add_expert(done)


def route(nc, k, d, name, E, kind, W, capacity=0):
    K2 = kind in ("capacity_slots", "capacity_tokens")
    with Tensors(nc) as t, stage(nc, name + "_load", name + "_mm", name + "_chain", name + "_act", name + "_shifted", name + "_choices") as (
            block, load, mm, chain, act_done, shifted, choices):
        wr = t.sb(name + "_wr", [P, KC, E])
        tri = t.sb(name + "_tri", [P, P])
        bg = t.sb(name + "_bg", [P, E])
        lg = t.sb(name + "_lg", [P, TT, E])
        ex = t.sb(name + "_ex", [P, TT, E])
        m8 = t.sb(name + "_m8", [P, TT, 8])
        i8 = t.sb(name + "_i8", [P, TT, 8], U32)
        f8 = t.sb(name + "_f8", [P, TT, 8])
        sm = t.sb(name + "_sm", [P, TT])
        g1 = t.sb(name + "_g1", [P, TT, 2])
        oh = t.sb(name + "_oh", [P, TT, 4, E])
        kp = t.sb(name + "_kp", [P, TT, 2, E])
        ps = t.ps(name + "_ps", [P, TT, E])
        pc = t.ps(name + "_pc", [P, TT, 512])
        CW = 2 * E if kind == "capacity_slots" else E

        @block.sync
        def _(sp):
            sp.dma_start(wr[:, :, :], d[name + "_wr"]).then_inc(load, 16)
            if K2:
                sp.dma_start(tri[:, :], d["tri_below" if kind == "capacity_slots" else "tri_upto"]).then_inc(load, 16)
            if kind == "capacity_slots":
                sp.dma_start(bg[:, :], d[name + "_bg"]).then_inc(load, 16)

        LOADS = 16 * (1 + K2 + (kind == "capacity_slots"))

        @block.tensor
        def _(pe):
            pe.wait_ge(load, LOADS)
            for i in range(TT):
                for c in range(KC):
                    m = nc.tensor.matmul(ps[:, i, :], k.NT[:, c, i * P:(i + 1) * P], wr[:, c, :], start=(c == 0), stop=(c == KC - 1))
            m.then_inc(mm, 1)
            if K2:
                pe.wait_ge(choices, 1)

                def chosen(j):
                    slots = oh[:, j, 0:2, :] if kind == "capacity_slots" else oh[:, j, 2:3, :]
                    return slots.rearrange("p a e -> p (a e)")

                for i in range(TT):
                    terms = [(pc[:, i, 0:CW], tri, chosen(i))] + [(pc[:, i, 0:CW], k.ones, chosen(j)) for j in range(i)]
                    if kind == "capacity_slots":
                        terms += [(pc[:, i, E:2 * E], k.ones, oh[:, j, 0, :]) for j in range(TT)]
                    for n, (o, left, right) in enumerate(terms):
                        m = nc.tensor.matmul(o, left[:, :], right, start=(n == 0), stop=(n == len(terms) - 1), skip_group_check=True)
                m.then_inc(mm, 1)

        @block.scalar
        def _(act):
            if kind == "sigmoid_top4":
                act.wait_ge(mm, 1)
                nc.scalar.activation(lg[:, :, :], ps[:, :, :], ACT.Sigmoid).then_inc(act_done, 1)
            else:
                act.wait_ge(shifted, 1)
                nc.scalar.activation(ex[:, :, :], ex[:, :, :], ACT.Exp).then_inc(act_done, 1)

        @block.vector
        def _(dve):
            links = [0]

            def link(i):
                links[0] += 1
                i.then_inc(chain, 1)
                dve.wait_ge(chain, links[0])

            def one_hot(slot, i, j):
                return nc.vector.tensor_scalar(oh[:, i, slot, :], k.iota[:, 0:E], f8[:, i, j:j + 1], None, ALU.is_equal)

            dve.wait_ge(load, LOADS)
            dve.wait_ge(mm, 1)
            if kind == "sigmoid_top4":
                dve.wait_ge(act_done, 1)
            elif kind == "capacity_slots":
                link(nc.vector.tensor_tensor(lg[:, :, :], ps[:, :, :], bg[:, :].unsqueeze(1).broadcast_to([P, TT, E]), ALU.add))
            else:
                link(nc.vector.tensor_copy(lg[:, :, :], ps[:, :, :]))
            for i in range(TT):
                m = nc.vector.max(m8[:, i, :], lg[:, i, :])
            link(m)
            for i in range(TT):
                m = nc.vector.max_index(i8[:, i, :], m8[:, i, :], lg[:, i, :])
            link(m)
            link(nc.vector.tensor_copy(f8[:, :, :], i8[:, :, :]))
            if kind == "top1":
                for i in range(TT):
                    nc.vector.tensor_scalar(ex[:, i, :], lg[:, i, :], m8[:, i, 0:1], None, ALU.subtract)
                    m = one_hot(0, i, 0)
                m.then_inc(shifted, 1)
                dve.wait_ge(act_done, 1)
                link(nc.vector.reduce_sum(sm[:, :], ex[:, :, :], AX))
                link(nc.vector.reciprocal(sm[:, :], sm[:, :]))
                link(nc.vector.tensor_scalar(sm[:, :], sm[:, :], 2.0, None, ALU.mult))
                for i in range(TT):
                    m = nc.vector.tensor_scalar(W[:, i, 0:E], oh[:, i, 0, :], sm[:, i:i + 1], None, ALU.mult)
                link(m)
                nc.vector.memset(W[:, :, E - 1:E], 1.0)
            elif kind == "sigmoid_top4":
                link(nc.vector.reduce_sum(sm[:, :], m8[:, :, 0:4], AX))
                link(nc.vector.reciprocal(sm[:, :], sm[:, :]))
                for i in range(TT):
                    for j in range(4):
                        m = one_hot(j, i, j)
                link(m)
                link(nc.vector.tensor_tensor(kp[:, :, :, :], oh[:, :, 0:2, :], oh[:, :, 2:4, :], ALU.add))
                link(nc.vector.tensor_tensor(ex[:, :, :], kp[:, :, 0, :], kp[:, :, 1, :], ALU.add))
                for i in range(TT):
                    m = nc.vector.scalar_tensor_tensor(W[:, i, 0:E], lg[:, i, :], sm[:, i:i + 1], ex[:, i, :], ALU.mult, ALU.mult)
                nc.vector.memset(W[:, :, E:E + 2], 1.0)
            else:
                for i in range(TT):
                    nc.vector.tensor_scalar(ex[:, i, :], m8[:, i, :], m8[:, i, 0:1], None, ALU.subtract)
                    one_hot(0, i, 0)
                    m = one_hot(1, i, 1)
                m.then_inc(shifted, 1)
                if kind == "capacity_slots":
                    dve.wait_ge(shifted, 1)
                    nc.vector.tensor_copy(f8[:, :, 0:1], f8[:, :, 0:1]).then_inc(choices, 1)
                dve.wait_ge(act_done, 1)
                link(nc.vector.tensor_scalar(sm[:, :], ex[:, :, 1], 1.0, None, ALU.add))
                link(nc.vector.reciprocal(g1[:, :, 0], sm[:, :]))
                link(nc.vector.tensor_tensor(g1[:, :, 1], g1[:, :, 0], ex[:, :, 1], ALU.mult))
                if kind == "capacity_slots":
                    dve.wait_ge(mm, 2)
                    for i in range(TT):
                        m = nc.vector.tensor_scalar(kp[:, i, :, :].rearrange("p a e -> p (a e)"), pc[:, i, 0:2 * E], float(capacity), None,
                                                    ALU.is_lt)
                    link(m)
                    link(nc.vector.tensor_tensor(kp[:, :, :, :], kp[:, :, :, :], oh[:, :, 0:2, :], ALU.mult))
                else:
                    link(nc.vector.tensor_scalar(sm[:, :], g1[:, :, 1], 0.0, None, ALU.is_gt))
                    for i in range(TT):
                        m = nc.vector.scalar_tensor_tensor(oh[:, i, 2, :], oh[:, i, 1, :], sm[:, i:i + 1], oh[:, i, 0, :],
                                                           ALU.mult, ALU.add)
                    m.then_inc(choices, 1)
                    dve.wait_ge(mm, 2)
                    for i in range(TT):
                        m = nc.vector.tensor_scalar(ex[:, i, :], pc[:, i, 0:E], float(capacity), None, ALU.is_le)
                    link(m)
                    for a in range(2):
                        m = nc.vector.tensor_tensor(kp[:, :, a, :], ex[:, :, :], oh[:, :, a, :], ALU.mult)
                    link(m)
                for i in range(TT):
                    for a in range(2):
                        m = nc.vector.tensor_scalar(oh[:, i, 2 + a, :], kp[:, i, a, :], g1[:, i, a:a + 1], None, ALU.mult)
                link(m)
                nc.vector.tensor_tensor(W[:, :, 0:E], oh[:, :, 2, :], oh[:, :, 3, :], ALU.add)


def layer0_ff(nc, k, d):
    layer_norm(nc, k, k.X, k.N, "f0n", k.NT)
    with Tensors(nc) as t:
        W = t.sb("f0_W", [P, TT, 8])
        route(nc, k, d, "f0r", 8, "top1", W)
        experts(nc, k, d["f0_pieces"], "f0e", 8, 8, 4, "swiglu", W)


def layer1_ff(nc, k, d):
    layer_norm(nc, k, k.X, k.N, "f1n", k.NT)
    with Tensors(nc) as t:
        W = t.sb("f1_W", [P, TT, 8])
        route(nc, k, d, "f1r", 8, "capacity_slots", W, capacity=-(-12 * T * 2 // 80))
        weighted_bias(nc, k, d, W)
        experts(nc, k, d["f1_pieces"], "f1e", 8, 8, 4, "gelu", W, b1=d["f1_b1"])


def weighted_bias(nc, k, d, W):
    E = 8
    with Tensors(nc) as t, stage(nc, "wb_load", "wb_turned", "wb_copied", "wb_mm") as (block, load, turned, copied, mm):
        b2 = t.sb("wb_b2", [E, D])
        wT = t.sb("wb_wT", [E, T])
        pt = t.ps("wb_pt", [P, T])
        po = t.ps("wb_po", [P, TT, 512])

        @block.sync
        def _(sp):
            sp.dma_start(b2[:, :], d["f1_b2"]).then_inc(load, 16)

        @block.tensor
        def _(pe):
            for i in range(TT):
                m = nc.tensor.transpose(pt[0:E, i * P:(i + 1) * P], W[:, i, :], k.ident[:, :])
            m.then_inc(turned, 1)
            pe.wait_ge(load, 16)
            pe.wait_ge(copied, 1)
            for i in range(TT):
                nc.tensor.matmul(po[:, i, 0:D], wT[:, i * P:(i + 1) * P], b2[:, :], start=True, stop=True).then_inc(mm, 1)

        @block.scalar
        def _(act):
            act.wait_ge(turned, 1)
            nc.scalar.copy(wT[:, :], pt[0:E, :]).then_inc(copied, 1)

        @block.vector
        def _(dve):
            for i in range(TT):
                dve.wait_ge(mm, i + 1)
                nc.vector.tensor_tensor(k.X[:, i, :], po[:, i, 0:D], k.X[:, i, :], ALU.add)


def layer2_ff(nc, k, d):
    layer_norm(nc, k, k.X, k.N, "f2n", k.NT)
    with Tensors(nc) as t:
        W = t.sb("f2_W", [P, TT, 8])
        route(nc, k, d, "f2r", 8, "capacity_tokens", W, capacity=T // 8)
        experts(nc, k, d["f2_pieces"], "f2e", 8, 4, 8, "relu", W)


def layer3_ff(nc, k, d):
    layer_norm(nc, k, k.X, k.N, "f3n", k.NT)
    with Tensors(nc) as t:
        W = t.sb("f3_W", [P, TT, 18])
        route(nc, k, d, "f3r", 16, "sigmoid_top4", W)
        experts(nc, k, d["f3_pieces"], "f3e", 18, 1, 18, "swiglu", W)


def expert_layouts(a, i, rows, cols, spread):
    def pieces(ins, w_out):
        e, _, h = ins[0].shape
        n = e * h // (2 * P)
        parts = [w.transpose(1, 0, 2).reshape(KC, P, n, 2 * P).transpose(2, 1, 0, 3).reshape(n, P, -1) for w in ins]
        parts.append(w_out.reshape(n, 2, P, D).transpose(0, 2, 1, 3).reshape(n, P, -1))
        return np.ascontiguousarray(np.concatenate(parts, 2))

    def with_shared(w, s):
        return np.concatenate([w, s], 0)

    n = "L0_ffn_"
    a["f0r_wr"] = rows(i[n + "w_router"])
    a["f0_pieces"] = pieces([with_shared(i[n + "w_up"], i[n + "ws_up"][None]), with_shared(i[n + "w_gate"], i[n + "ws_gate"][None])],
                            with_shared(i[n + "w_down"], i[n + "ws_down"][None]))
    n = "L1_ffn_"
    a["f1r_wr"], a["f1r_bg"] = rows(i[n + "Wg"]), spread(i[n + "bg"])
    a["f1_pieces"] = pieces([i[n + "W1"]], i[n + "W2"])
    a["f1_b1"] = np.ascontiguousarray(i[n + "b1"].reshape(2, 32, P).transpose(0, 2, 1))
    a["f1_b2"] = i[n + "b2"]
    n = "L2_ffn_"
    a["f2r_wr"] = rows(i[n + "expert_embeddings"].T)
    a["f2_pieces"] = pieces([i[n + "first_linear"].transpose(0, 2, 1)], i[n + "second_linear"].transpose(0, 2, 1))
    n = "L3_ffn_"
    a["f3r_wr"] = rows(i[n + "gate_w"].T)

    def halves(w):
        return w.reshape(D, 2, P).transpose(1, 0, 2)

    a["f3_pieces"] = pieces([with_shared(i[n + "e_vin"], halves(i[n + "vs_in"])), with_shared(i[n + "e_win"], halves(i[n + "ws_in"]))],
                            with_shared(i[n + "e_wout"], i[n + "ws_out"].reshape(2, P, D)))
    one = np.ones((P, P), np.float32)
    a["tri_below"], a["tri_upto"] = np.triu(one, 1), np.triu(one)



def latent_projections(nc, k, d, pre, qT, kT, V):
    with Tensors(nc) as t, stage(nc, pre + "q_load", pre + "k_load", pre + "v_load", pre + "qk_mm", pre + "v_mm") as (
            block, q_load, k_load, v_load, qk_mm, v_mm):
        loads = (q_load, k_load, v_load)
        w = t.sb(pre + "_w3", [P, 3, KC, D])
        bqk = t.sb(pre + "_bqk", [P, 2, KC])
        bv = t.sb(pre + "_bv", [P, D])
        psT = t.ps(pre + "_psT", [P, 2 * KC, T])
        psv = t.ps(pre + "_psv", [P, TT, 512])

        @block.sync
        def _(sp):
            for n, name in enumerate("qkv"):
                sp.dma_start(w[:, n, :, :], d[pre + "_w" + name]).then_inc(loads[n], 16)
                sp.dma_start(bqk[:, n, :] if n < 2 else bv[:, :], d[pre + "_b" + name]).then_inc(loads[n], 16)

        @block.tensor
        def _(pe):
            for n in range(2):
                pe.wait_ge(loads[n], 32)
                for m in range(KC):
                    for c in range(KC):
                        i = nc.tensor.matmul(psT[:, n * KC + m, :], w[:, n, c, m * P:(m + 1) * P], k.NT[:, c, :],
                                             start=(c == 0), stop=(c == KC - 1))
                    i.then_inc(qk_mm, 1)
            pe.wait_ge(v_load, 32)
            for i in range(TT):
                for c in range(KC):
                    m = nc.tensor.matmul(psv[:, i, 0:D], k.NT[:, c, i * P:(i + 1) * P], w[:, 2, c, :], start=(c == 0), stop=(c == KC - 1))
                m.then_inc(v_mm, 1)

        @block.scalar
        def _(act):
            for n, dst in enumerate((qT, kT)):
                act.wait_ge(loads[n], 32)
                for m in range(KC):
                    act.wait_ge(qk_mm, n * KC + m + 1)
                    nc.scalar.activation(dst[:, m, :], psT[:, n * KC + m, :], ACT.Identity, bias=bqk[:, n, m:m + 1])

        @block.vector
        def _(dve):
            dve.wait_ge(v_load, 32)
            for i in range(TT):
                dve.wait_ge(v_mm, i + 1)
                nc.vector.tensor_tensor(V[:, i, :], psv[:, i, 0:D], bv[:, :], ALU.add)


def self_attention(nc, k, d, pre, qT, kT, V, O, relative):
    hd, HPC, RW = HD16, P // HD16, 3 * P
    with nc.Fori(0, B) as b, Tensors(nc) as t:
        qz = t.sb(pre + "_qz", [P, NH, S])
        keys = t.sb(pre + "_keys", [P, KC, S])
        vals = t.sb(pre + "_vals", [P, QT, D])
        mask = t.sb(pre + "_mask", [P, HPC])
        if relative:
            kz = t.sb(pre + "_kz", [P, NH, S])
            emb = t.sb(pre + "_emb", [P, 2, 512])
            rows = t.sb(pre + "_rows", [P, 4, 4, RW])
            scratch = k.rel_scratch
        names = ("load masked rel rel_dve rel_act out0 out1 add0 add1 ready scored sum peak exp turned pT av chain scaled static").split()
        with Tensors(nc) as u, stage(nc, *[pre + "_" + n for n in names]) as (
                block, load, masked, rel, rel_dve, rel_act, out0, out1, add0, add1, ready, scored, summed, peak, expd, turned, pT_done, av,
                chain, scaled, static):
            LAG = 3 if relative else 0
            outs = (out0, out1)
            sc = u.sb(pre + "_sc", [P, 2, QT, S])
            pr = u.sb(pre + "_pr", [P, 2, QT, S])
            pT = u.sb(pre + "_pT", [P, 2, QT, QT, P])
            mx = u.sb(pre + "_mx", [P, NH, QT])
            nm = u.sb(pre + "_nm", [P, NH, QT])
            sums = u.sb(pre + "_sums", [P, NH, QT])
            rec = u.sb(pre + "_rec", [P, NH, QT])
            add = u.sb(pre + "_add", [P, 2, 4, S])
            pss = u.ps(pre + "_pss", [P, 2, QT, S])
            pst = u.ps(pre + "_pst", [P, 2, QT, QT, P])
            pso = u.ps(pre + "_pso", [P, 2, 512])
            if relative:
                psr = u.ps(pre + "_psr", [P, 2, 512])
            SC = 1.0 if relative else 0.25
            HEADS = range(NH)

            @block.sync
            def _(sp):
                if not relative:
                    sp.dma_start(mask[:, :], d["mask16"]).then_inc(load, 16)
                    sp.dma_start(add[:, 0, 0:QT, :], d["causal"]).then_inc(load, 16)
                else:
                    sp.dma_start(mask[:, :], d["mask16"]).then_inc(load, 16)
                    sp.dma_start(emb[:, :, :], d["rel_emb"]).then_inc(load, 16)
                    for t_ in range(NH + 1):
                        if t_ < NH:
                            sp.wait_ge(rel_dve, 2 * (t_ + 1))
                            sp.wait_ge(rel_act, 2 * (t_ + 1))
                            sp.dma_start(scratch[t_].rearrange("x p w -> p x w"), rows[:, t_ % 4, :, :]).then_inc(outs[t_ % 2], 16)
                        if t_ >= 1:
                            h = t_ - 1
                            sp.wait_ge(outs[h % 2], 16 * (h // 2 + 1))
                            if h >= 2:
                                sp.wait_ge(summed, h - 1)
                                sp.wait_ge(scored, h - 1)
                            src = scratch[h]
                            skew = bass.AP(tensor=src.tensor, offset=src.offset + P - 1, ap=[[RW - 1, P], [P * RW, 4], [1, S]])
                            sp.dma_start(add[:, h % 2, :, :], skew).then_inc((add0, add1)[h % 2], 16)

            @block.gpsimd
            def _(pool):
                nc.gpsimd.tensor_copy(keys[:, :, :], kT[:, :, bass.ds(b * S, S)]).then_inc(static, 1)
                nc.gpsimd.tensor_copy(vals[:, :, :], V[:, bass.ds(b * QT, QT), :]).then_inc(static, 1)
                if relative:
                    pool.wait_ge(static, 2)
                    nc.gpsimd.tensor_scalar(keys[:, :, :], keys[:, :, :], 0.25, None, ALU.mult).then_inc(static, 1)

            def added(eng, h):
                if relative:
                    eng.wait_ge((add0, add1)[h % 2], 16 * (h // 2 + 1))

            def rows_free(eng, h):
                if h >= 4:
                    eng.wait_ge(outs[h % 2], 16 * (h // 2 - 1))

            @block.tensor
            def _(pe):
                if relative:
                    pe.wait_ge(load, 32)
                else:
                    pe.wait_ge(static, 2)
                if not relative:
                    pe.wait_ge(ready, NH)

                def turn(h):
                    pe.wait_ge(expd, QT * (h + 1))
                    if h >= 2:
                        pe.wait_ge(pT_done, h - 1)
                    for kt in range(QT):
                        for qt in range(QT):
                            m = nc.tensor.transpose(pst[:, h % 2, kt, qt, :], pr[:, h % 2, qt, kt * P:(kt + 1) * P], k.ident[:, :])
                    m.then_inc(turned, 1)

                def average(h):
                    pe.wait_ge(pT_done, h + 1)
                    if h >= 2:
                        pe.wait_ge(scaled, QT * (h - 1))
                    for qt in range(QT):
                        for kt in range(QT):
                            m = nc.tensor.matmul(pso[:, h % 2, qt * hd:(qt + 1) * hd], pT[:, h % 2, kt, qt, :], vals[:, kt, h * hd:(h + 1) * hd],
                                                 start=(kt == 0), stop=(kt == QT - 1))
                    m.then_inc(av, 1)

                def products(h):
                    pe.wait_ge(masked, 2 * (h + 1))
                    for x in range(4):
                        side, i = divmod(x, 2)
                        n = 4 * h + x
                        if n >= 2:
                            pe.wait_ge((rel_act, rel_dve)[n % 2], n // 2)
                        nc.tensor.matmul(psr[:, n % 2, 0:RW], (qz, kz)[side][:, h, i * P:(i + 1) * P],
                                         emb[:, side, P * (1 - i):P * (1 - i) + RW], start=True, stop=True).then_inc(rel, 1)

                for step in range(NH + 3 + LAG):
                    h = step - LAG
                    if relative and step < NH:
                        products(step)
                    if h < 0:
                        continue
                    if relative and h == 0:
                        pe.wait_ge(static, 3)
                    if h < NH:
                        added(pe, h)
                        if h >= 2:
                            pe.wait_ge(summed, h - 1)
                        for qt in range(QT):
                            m = nc.tensor.matmul(pss[:, h % 2, qt, :], qz[:, h, qt * P:(qt + 1) * P], keys[:, h // HPC, :], start=True, stop=not relative,
                                                 skip_group_check=True)
                            if relative:
                                for kt in range(QT):
                                    m = nc.tensor.matmul(pss[:, h % 2, qt, kt * P:(kt + 1) * P], add[:, h % 2, 2 + kt, qt * P:(qt + 1) * P],
                                                         k.ident[:, :], start=False, stop=(kt == QT - 1), skip_group_check=True)
                        m.then_inc(scored, 1)
                    if 2 <= h <= NH + 1:
                        turn(h - 2)
                    if h >= 3:
                        average(h - 3)

            @block.vector
            def _(dve):
                links = [0]

                def link(i):
                    links[0] += 1
                    i.then_inc(chain, 1)
                    dve.wait_ge(chain, links[0])

                dve.wait_ge(load, 32)
                if relative:
                    for h in HEADS:
                        for src, dst in ((qT, qz), (kT, kz)):
                            nc.vector.tensor_scalar(dst[:, h:h + 1, :], src[:, h // HPC:h // HPC + 1, bass.ds(b * S, S)], mask[:, h % HPC:h % HPC + 1], None,
                                                    ALU.mult).then_inc(masked, 1)
                else:
                    for h in HEADS:
                        nc.vector.tensor_scalar(qz[:, h:h + 1, :], qT[:, h // HPC:h // HPC + 1, bass.ds(b * S, S)], mask[:, h % HPC:h % HPC + 1], None,
                                                ALU.mult).then_inc(ready, 1)

                def normalize(h):
                    dve.wait_ge(av, h + 1)
                    link(nc.vector.reciprocal(rec[:, h, :], sums[:, h, :]))
                    for qt in range(QT):
                        nc.vector.tensor_scalar(O[:, bass.ds(b * QT + qt, 1), h * hd:(h + 1) * hd],
                                                pso[:, h % 2:h % 2 + 1, qt * hd:(qt + 1) * hd], rec[:, h, qt:qt + 1], None,
                                                ALU.mult).then_inc(scaled, 1)

                for step in range(NH + 4 + LAG):
                    h = step - LAG
                    if relative and step < NH:
                        rows_free(dve, step)
                        for n in (4 * step + 1, 4 * step + 3):
                            dve.wait_ge(rel, n + 1)
                            nc.vector.tensor_copy(rows[:, step % 4, n % 4, :], psr[:, n % 2, 0:RW]).then_inc(rel_dve, 1)
                    if h < 0:
                        continue
                    if h < NH:
                        dve.wait_ge(scored, h + 1)
                        added(dve, h)
                        if h >= 2:
                            dve.wait_ge(expd, QT * (h - 1))
                        m = nc.vector.tensor_tensor(sc[:, h % 2, :, :], pss[:, h % 2, :, :], add[:, h % 2 if relative else 0, 0:QT, :], ALU.add)
                        m.then_inc(summed, 1)
                        dve.wait_ge(summed, h + 1)
                        link(nc.vector.reduce_max(mx[:, h, :], sc[:, h % 2, :, :], AX))
                        nc.vector.tensor_scalar(nm[:, h, :], mx[:, h, :], -SC, None, ALU.mult).then_inc(peak, 1)
                    if h >= 4:
                        normalize(h - 4)

            @block.scalar
            def _(act):
                for step in range(NH + 2 + LAG):
                    h = step - LAG
                    if relative and step < NH:
                        rows_free(act, step)
                        for n in (4 * step, 4 * step + 2):
                            act.wait_ge(rel, n + 1)
                            nc.scalar.copy(rows[:, step % 4, n % 4, :], psr[:, n % 2, 0:RW]).then_inc(rel_act, 1)
                    if 1 <= h <= NH:
                        e = h - 1
                        act.wait_ge(peak, e + 1)
                        if e >= 2:
                            act.wait_ge(turned, e - 1)
                        for qt in range(QT):
                            nc.scalar.activation(pr[:, e % 2, qt, :], sc[:, e % 2, qt, :], ACT.Exp, bias=nm[:, e, qt:qt + 1], scale=SC,
                                                 accum_out=sums[:, e, qt:qt + 1]).then_inc(expd, 1)
                    if h >= 2:
                        x = h - 2
                        act.wait_ge(turned, x + 1)
                        if x >= 2:
                            act.wait_ge(av, x - 1)
                        nc.scalar.copy(pT[:, x % 2, :, :, :], pst[:, x % 2, :, :, :]).then_inc(pT_done, 1)


def layer0_self(nc, k, d):
    layer_norm(nc, k, k.X, k.N, "s0n", k.NT)
    k.rel_scratch = nc.dram_tensor("offset_rows", (NH, 4, P, 3 * P), F32, kind="Internal").ap()
    with Tensors(nc) as t:
        qT = t.sb("s0_qT", [P, KC, T])
        kT = t.sb("s0_kT", [P, KC, T])
        V = t.sb("s0_V", [P, TT, D])
        O = t.sb("s0_O", [P, TT, D])
        latent_projections(nc, k, d, "s0", qT, kT, V)
        self_attention(nc, k, d, "s0", qT, kT, V, O, True)
        add_to(nc, k.X, O, "s0a")


def add_to(nc, dst, src, name):
    with stage(nc, name + "_unused", name + "_unused1") as (block, _u, _v):
        @block.vector
        def _(dve):
            nc.vector.tensor_tensor(dst[:, :, :], dst[:, :, :], src[:, :, :], ALU.add)


def rotate(nc, k, d, both, name):
    with Tensors(nc) as t, stage(nc, name + "_load", name + "_mm", name + "_a", name + "_b") as (block, load, mm, ca, cb):
        rot = t.sb(name + "_r", [P, P])
        tab = t.sb(name + "_tab", [P, 2, T])
        tmp = t.sb(name + "_tmp", [P, 2, KC, T])
        ps = t.ps(name + "_ps", [P, 2, KC, T])

        @block.sync
        def _(sp):
            sp.dma_start(rot[:, :], d["rope_swap"]).then_inc(load, 16)
            sp.dma_start(tab[:, :, :], d["rope_tables"]).then_inc(load, 16)

        @block.tensor
        def _(pe):
            pe.wait_ge(load, 32)
            for n, xT in enumerate(both):
                for c in range(KC):
                    nc.tensor.matmul(ps[:, n, c, :], rot[:, :], xT[:, c, :], start=True, stop=True).then_inc(mm, 1)

        @block.vector
        def _(dve):
            dve.wait_ge(load, 32)
            for n, xT in enumerate(both):
                for c in range(KC):
                    dve.wait_ge(mm, n * KC + c + 1)
                    nc.vector.tensor_tensor(tmp[:, n, c, :], ps[:, n, c, :], tab[:, 1, :], ALU.mult).then_inc(ca, 1)
                    nc.vector.tensor_tensor(xT[:, c, :], xT[:, c, :], tab[:, 0, :], ALU.mult).then_inc(cb, 1)
                for c in range(KC):
                    dve.wait_ge(ca, (n + 1) * KC)
                    dve.wait_ge(cb, (n + 1) * KC)
                    nc.vector.tensor_tensor(xT[:, c, :], xT[:, c, :], tmp[:, n, c, :], ALU.add)


def layer2_self(nc, k, d):
    with Tensors(nc) as t:
        X0 = t.sb("s2_X0", [P, TT, D])
        with stage(nc, "s2_keep", "s2_keep1") as (block, _u, _v):
            @block.vector
            def _(dve):
                nc.vector.tensor_copy(X0[:, :, :], k.X[:, :, :])
        layer_norm(nc, k, X0, k.X, "s2i")
        layer_norm(nc, k, k.X, k.N, "s2n", k.NT, gain=d["s2_g1"], shift=d["s2_h1"])
        with Tensors(nc) as u:
            qT = u.sb("s2_qT", [P, KC, T])
            kT = u.sb("s2_kT", [P, KC, T])
            V = u.sb("s2_V", [P, TT, D])
            O = u.sb("s2_O", [P, TT, D])
            latent_projections(nc, k, d, "s2", qT, kT, V)
            rotate(nc, k, d, (qT, kT), "s2r")
            self_attention(nc, k, d, "s2", qT, kT, V, O, False)
            project_tokens(nc, k, O, d["s2_wo"], "s2p", bias=d["s2_bo"])
        layer_norm(nc, k, k.X, k.N, "s2m", k.NT, gain=d["s2_g2"], shift=d["s2_h2"])
        W = t.sb("s2_W", [P, TT, 1])
        b2 = t.sb("s2_b2", [P, D])
        with stage(nc, "s2_b2_load", "s2_b2_unused") as (block, load, _u):
            @block.sync
            def _(sp):
                sp.dma_start(b2[:, :], d["s2_b2"]).then_inc(load, 16)

            @block.vector
            def _(dve):
                nc.vector.memset(W[:, :, :], 1.0)
                dve.wait_ge(load, 16)
                nc.vector.tensor_tensor(X0[:, :, :], X0[:, :, :], b2[:, :].unsqueeze(1).broadcast_to([P, TT, D]), ALU.add)
        experts(nc, k, d["s2_pieces"], "s2e", 1, 8, 1, "gelu_erf", W, b1=d["s2_b1"])
        add_to(nc, k.X, X0, "s2a")


def self_layouts(a, i, rows, cols, spread):
    n = "L0_attn_"
    for w in "qk":
        a["s0_w" + w], a["s0_b" + w] = rows(i[n + "W" + w].T), cols(i[n + "b" + w])
    a["s0_wv"], a["s0_bv"] = rows(i[n + "Wv"].T), spread(i[n + "bv"])
    e = i[n + "dist_emb"]
    two = np.stack([e[255:767][::-1], e[256:768]])
    a["rel_emb"] = np.ascontiguousarray(np.tile(two.transpose(2, 0, 1), (P // HD16, 1, 1)))
    n = "L2_attn_"
    wqkv = i[n + "Wqkv"]
    bqkv = i[n + "bqkv"]
    a["s2_wq"], a["s2_wk"], a["s2_wv"] = (rows(wqkv[:, x * D:(x + 1) * D]) for x in range(3))
    a["s2_bq"], a["s2_bk"], a["s2_bv"] = cols(bqkv[:D]), cols(bqkv[D:2 * D]), spread(bqkv[2 * D:])
    for x in "12":
        a["s2_g" + x], a["s2_h" + x] = cols(i[n + f"ln{x}_g"]), cols(i[n + f"ln{x}_b"])
    a["s2_wo"], a["s2_bo"] = rows(i[n + "Wo"]), spread(i[n + "bo"])
    w1, w2 = i[n + "W1"], i[n + "W2"]
    parts = [w1.reshape(KC, P, 4, 2 * P).transpose(2, 1, 0, 3).reshape(4, P, -1), w2.reshape(4, 2, P, D).transpose(0, 2, 1, 3).reshape(4, P, -1)]
    a["s2_pieces"] = np.ascontiguousarray(np.concatenate(parts, 2))
    a["s2_b1"] = cols(i[n + "b1"])[None]
    a["s2_b2"] = spread(i[n + "b2"])
    q = np.arange(S)
    causal = np.where(q[None, :] > q[:, None], np.float32(-1e30), np.float32(0)).astype(np.float32)
    a["causal"] = np.ascontiguousarray(causal.reshape(QT, P, S).transpose(1, 0, 2))
    swap = np.zeros((P, P), np.float32)
    for f in range(P):
        h, r = divmod(f, HD16)
        if r < HD16 // 2:
            swap[h * HD16 + r + HD16 // 2, f] = -1
        else:
            swap[h * HD16 + r - HD16 // 2, f] = 1
    a["rope_swap"] = swap
    inv = (1.0 / 10000.0 ** (np.arange(0, HD16, 2, dtype=np.float32) / HD16)).astype(np.float32)
    fr = np.arange(S, dtype=np.float32)[:, None] * inv[None, :]
    emb = np.concatenate([fr, fr], -1).astype(np.float32)
    tab = np.stack([np.cos(emb), np.sin(emb)]).astype(np.float32).transpose(2, 0, 1)
    a["rope_tables"] = np.ascontiguousarray(np.tile(tab, (P // HD16, 1, B)))



VL = 4
VH = HD16 // VL
C8 = 8
GROUP = 64
ROW = 3 * HD16 + C8 + 1


def delta_blocks(nc, k, heads, gates, packed, own):
    NB = GROUP // C8
    NG = S // GROUP
    with Tensors(nc) as t, stage(nc, "b_load", "b_zero", "b_chain", "b_prod", "b_used", "b_done", "b_out") as (
            block, load, zeroed, chain, prod, used, done, stored):
        qkv = t.sb("b_qkv", [P, 3, NB, C8, HD16])
        ga = t.sb("b_gates", [P, 2, NB, C8])
        E = t.sb("b_E", [P, NB, C8, C8 + 1])
        bg = t.sb("b_bg", [P, NB, C8])
        G = t.sb("b_G", [P, NB, C8, C8])
        H = t.sb("b_H", [P, NB, C8, C8])
        X = t.sb("b_X", [P, NB, C8, 2 * HD16])
        kp = t.sb("b_kp", [P, NB, C8, HD16])
        qp = t.sb("b_qp", [P, C8, NB, C8, HD16])
        tmp = t.sb("b_tmp", [P, NB, C8, 2 * HD16])
        pk = t.sb("b_packed", [P, NB, C8, ROW])
        ow = t.sb("b_own", [P, VH, NB, C8, VL])
        Q, K, V = (qkv[:, n, :, :, :] for n in range(3))
        decay, beta = ga[:, 0, :, :], ga[:, 1, :, :]
        WQ = slice(HD16, 2 * HD16)
        WA = slice(2 * HD16, 2 * HD16 + C8)
        WK = slice(2 * HD16 + C8, 3 * HD16 + C8)

        @block.sync
        def _(sp):
            for b in range(B):
                for g in range(NG):
                    part = slice((b * NG + g) * NH, (b * NG + g + 1) * NH)
                    span = slice(g * GROUP, (g + 1) * GROUP)
                    sp.dma_start(ga[part, :, :, :].rearrange("p n c t -> p n (c t)"), gates[:, b, :, span].rearrange("n h s -> h n s")).then_inc(load, 16)
                    sp.dma_start(qkv[part, :, :, :, :].rearrange("p n c t e -> p n (c t e)"),
                                 heads[:, b, :, span, :].rearrange("n h s e -> h n (s e)")).then_inc(load, 16)
            sp.wait_ge(done, 3)
            for b in range(B):
                for g in range(NG):
                    part = slice((b * NG + g) * NH, (b * NG + g + 1) * NH)
                    span = slice(g * GROUP, (g + 1) * GROUP)
                    sp.dma_start(packed[b][:, span, :].rearrange("h s e -> h (s e)"),
                                 pk[part, :, :, :].rearrange("p c t e -> p (c t e)")).then_inc(stored, 16)
                    sp.dma_start(own[b][:, :, span, :].rearrange("x h s e -> h x (s e)"),
                                 ow[part, :, :, :, :].rearrange("p x c t e -> p x (c t e)")).then_inc(stored, 16)
            sp.wait_ge(stored, 16 * 2 * B * NG)

        @block.gpsimd
        def _(pool):
            nc.gpsimd.memset(H[:, :, :, :], 0.0).then_inc(zeroed, 1)
            pool.wait_ge(load, 16 * 2 * B * NG)
            for s in range(C8):
                nc.gpsimd.tensor_tensor(qp[:, s, :, s:C8, :], Q[:, :, s:C8, :],
                                        K[:, :, s, :].unsqueeze(2).broadcast_to([P, NB, C8 - s, HD16]), ALU.mult).then_inc(prod, 1)

        @block.scalar
        def _(act):
            act.wait_ge(load, 16 * 2 * B * NG)
            act.wait_ge(zeroed, 3)
            nc.scalar.copy(pk[:, :, :, ROW - 1], E[:, :, C8 - 1, 0].unsqueeze(2).broadcast_to([P, NB, C8])).then_inc(done, 1)

        @block.vector
        def _(dve):
            links = [0]

            def link(i):
                links[0] += 1
                i.then_inc(chain, 1)
                dve.wait_ge(chain, links[0])

            nc.vector.memset(E[:, :, :, :], 0.0)
            link(nc.vector.memset(G[:, :, :, :], 0.0))
            diagonal = E[:, :, :, :].rearrange("p c t s -> p c (t s)")[:, :, 1:C8 * (C8 + 1):C8 + 2]
            link(nc.vector.memset(diagonal, 1.0))
            dve.wait_ge(load, 16 * 2 * B * NG)
            link(nc.vector.tensor_copy(E[:, :, 0, 0], decay[:, :, 0]))
            for s in range(1, C8):
                link(nc.vector.tensor_tensor(E[:, :, s, 0:s + 1], E[:, :, s - 1, 0:s + 1],
                                             decay[:, :, s].unsqueeze(2).broadcast_to([P, NB, s + 1]), ALU.mult))
            dve.wait_ge(zeroed, 1)
            nc.vector.tensor_tensor(bg[:, :, :], E[:, :, :, 0], beta, ALU.mult).then_inc(zeroed, 1)
            dve.wait_ge(zeroed, 2)
            nc.vector.tensor_tensor(X[:, :, :, 0:HD16], K, bg[:, :, :].unsqueeze(3).broadcast_to([P, NB, C8, HD16]), ALU.mult).then_inc(zeroed, 1)
            nc.vector.tensor_tensor(X[:, :, :, HD16:2 * HD16], V, beta.unsqueeze(3).broadcast_to([P, NB, C8, HD16]), ALU.mult)
            nc.vector.tensor_tensor(pk[:, :, :, WQ], Q, E[:, :, :, 0].unsqueeze(3).broadcast_to([P, NB, C8, HD16]), ALU.mult)
            nc.vector.tensor_tensor(pk[:, :, :, WK], K, E[:, :, C8 - 1, 1:C8 + 1].unsqueeze(3).broadcast_to([P, NB, C8, HD16]), ALU.mult)
            for s in range(C8 - 1):
                link(nc.vector.tensor_tensor(kp[:, :, s + 1:C8, :], K[:, :, s + 1:C8, :],
                                             K[:, :, s, :].unsqueeze(2).broadcast_to([P, NB, C8 - 1 - s, HD16]), ALU.mult))
                link(nc.vector.reduce_sum(G[:, :, s + 1:C8, s], kp[:, :, s + 1:C8, :], AX))
            link(nc.vector.tensor_tensor(G[:, :, :, :], G[:, :, :, :], E[:, :, :, 1:C8 + 1], ALU.mult))
            link(nc.vector.tensor_tensor(G[:, :, :, :], G[:, :, :, :], beta.unsqueeze(3).broadcast_to([P, NB, C8, C8]), ALU.mult))
            for s in range(C8 - 1):
                rest = C8 - 1 - s
                link(nc.vector.tensor_tensor(tmp[:, :, s + 1:C8, :], X[:, :, s, :].unsqueeze(2).broadcast_to([P, NB, rest, 2 * HD16]),
                                             G[:, :, s + 1:C8, s].unsqueeze(3).broadcast_to([P, NB, rest, 2 * HD16]), ALU.mult))
                link(nc.vector.tensor_tensor(X[:, :, s + 1:C8, :], X[:, :, s + 1:C8, :], tmp[:, :, s + 1:C8, :], ALU.subtract))
            nc.vector.tensor_scalar(pk[:, :, :, 0:HD16], X[:, :, :, 0:HD16], -1.0, None, ALU.mult)
            for x in range(VH):
                m = nc.vector.tensor_copy(ow[:, x, :, :, :], X[:, :, :, HD16 + x * VL:HD16 + (x + 1) * VL])
            m.then_inc(done, 1)
            for s in range(C8):
                dve.wait_ge(prod, s + 1)
                nc.vector.reduce_sum(H[:, :, s:C8, s], qp[:, s, :, s:C8, :], AX).then_inc(used, 1)
            dve.wait_ge(used, C8)
            nc.vector.tensor_tensor(pk[:, :, :, WA], H[:, :, :, :], E[:, :, :, 1:C8 + 1], ALU.mult).then_inc(done, 1)


def delta_load(sp, rows, u0, packed, own, r, load):
    span = bass.ds(r * GROUP, GROUP)
    for b in range(B):
        for x in range(VH):
            part = slice((b * VH + x) * NH, (b * VH + x + 1) * NH)
            sp.dma_start(rows[part, span, :].rearrange("p s e -> p (s e)"),
                         packed[b][:, span, :].rearrange("h s e -> h (s e)")).then_inc(load, 16)
            sp.dma_start(u0[part, span, :].rearrange("p s e -> p (s e)"),
                         own[b, x][:, span, :].rearrange("h s e -> h (s e)")).then_inc(load, 16)


def delta_group(nc, name, r, more, rows, u0, hist, packed, own, oA):
    NB = GROUP // C8
    WQA = slice(HD16, 2 * HD16 + C8)
    HALF = (HD16 + C8) // 2
    WK = slice(2 * HD16 + C8, 3 * HD16 + C8)
    with Tensors(nc) as t, stage(nc, name + "_next", name + "_chain", name + "_side", name + "_update", name + "_state", name + "_half", name + "_prod", name + "_out") as (
            block, load, chain, side, update, state, half, prod, out):
        pu = t.sb(name + "_pu", [P, 2, VL, C8, HD16 + 1])
        pst = t.sb(name + "_ps", [P, 2, VL, HD16, C8 + 1])
        po = t.sb(name + "_po", [P, 3, C8, VL, HD16 + C8])

        def tokens(c):
            return bass.ds(r * GROUP + c * C8, C8)

        def state_of(c):
            return hist[:, bass.ds(r * NB + c, 1), :, 0:HD16].rearrange("p o v e -> p (o v) e")

        def updates_of(c):
            return hist[:, bass.ds(r * NB + c, 1), :, HD16:HD16 + C8].rearrange("p o v e -> p (o v) e")

        @block.sync
        def _(sp):
            if more:
                delta_load(sp, rows, u0, packed, own, r + 1, load)
                sp.wait_ge(load, 16 * 2 * B * VH)

        @block.scalar
        def _(act):
            for c in range(NB):
                if c >= 2:
                    act.wait_ge(update, c - 1)
                nc.scalar.copy(pu[:, c % 2, :, :, HD16], u0[:, tokens(c), :].rearrange("p t v -> p v t")).then_inc(side, 1)
                if c >= 1:
                    act.wait_ge(state, c)
                decay = rows[:, bass.ds(r * GROUP + c * C8, 1), ROW - 1:ROW].rearrange("p o e -> p (o e)")
                nc.scalar.activation(pst[:, c % 2, :, :, C8], state_of(c), ACT.Copy, scale=decay).then_inc(side, 1)

        @block.vector
        def _(dve):
            def outputs(c):
                dve.wait_ge(prod, c + 1)
                nc.vector.reduce_sum(oA[:, bass.ds(r * GROUP + c * C8, C8), :], po[:, c % 3, :, :, 0:HALF], AX).then_inc(out, 1)

            for c in range(NB):
                if c >= 1:
                    dve.wait_ge(state, c)
                nc.vector.tensor_tensor(pu[:, c % 2, :, :, 0:HD16], rows[:, tokens(c), 0:HD16].unsqueeze(1).broadcast_to([P, VL, C8, HD16]),
                                        state_of(c).unsqueeze(2).broadcast_to([P, VL, C8, HD16]), ALU.mult).then_inc(chain, 1)
                if c >= 2:
                    outputs(c - 2)
                dve.wait_ge(chain, 2 * c + 1)
                dve.wait_ge(side, 2 * c + 1)
                nc.vector.reduce_sum(updates_of(c), pu[:, c % 2, :, :, :], AX).then_inc(update, 1)
                dve.wait_ge(update, c + 1)
                nc.vector.tensor_tensor(pst[:, c % 2, :, :, 0:C8],
                                        rows[:, tokens(c), WK].rearrange("p t e -> p e t").unsqueeze(1).broadcast_to([P, VL, HD16, C8]),
                                        updates_of(c).unsqueeze(2).broadcast_to([P, VL, HD16, C8]), ALU.mult).then_inc(chain, 1)
                dve.wait_ge(chain, 2 * c + 2)
                dve.wait_ge(side, 2 * c + 2)
                nc.vector.reduce_sum(state_of(c + 1), pst[:, c % 2, :, :, :], AX).then_inc(state, 1)
            outputs(NB - 2)
            outputs(NB - 1)

        @block.gpsimd
        def _(pool):
            for c in range(NB):
                pool.wait_ge(update, c + 1)
                if c >= 3:
                    pool.wait_ge(out, c - 2)
                both = hist[:, bass.ds(r * NB + c, 1), :, :].rearrange("p o v e -> p (o v) e")
                nc.gpsimd.tensor_tensor(po[:, c % 3, :, :, :], rows[:, tokens(c), WQA].unsqueeze(2).broadcast_to([P, C8, VL, HD16 + C8]),
                                        both.unsqueeze(1).broadcast_to([P, C8, VL, HD16 + C8]), ALU.mult).then_inc(half, 1)
                pool.wait_ge(half, c + 1)
                nc.gpsimd.tensor_tensor(po[:, c % 3, :, :, 0:HALF], po[:, c % 3, :, :, 0:HALF], po[:, c % 3, :, :, HALF:2 * HALF],
                                        ALU.add).then_inc(prod, 1)


def layer1_self(nc, k, d):
    layer_norm(nc, k, k.X, k.N, "dn", k.NT)
    heads = nc.dram_tensor("delta_heads", (3, B, NH, S, HD16), F32, kind="Internal").ap()
    gates = nc.dram_tensor("delta_gates", (2, B, NH, S), F32, kind="Internal").ap()
    with Tensors(nc) as t:
        oA = t.sb("d_oA", [P, S, VL])
        with Tensors(nc) as u, stage(nc, "d_load", "d_mm", "d_gmm", "d_silu", "d_sq", "d_root", "d_gate", "d_ready", "d_vready", "d_out") as (
                block, load, mm, gmm, silu, sq, root, gate, ready, vready, stored):
            w = u.sb("d_w", [P, 3, KC, D])
            wg = u.sb("d_wg", [P, KC, 2 * HD16])
            q = u.sb("d_q", [P, TT, D])
            kk = u.sb("d_k", [P, TT, D])
            v = u.sb("d_v", [P, TT, D])
            ss = u.sb("d_ss", [P, TT, D])
            nrm = u.sb("d_nrm", [P, TT, NH])
            g = u.sb("d_g", [2 * HD16, T])
            ps = u.ps("d_ps", [P, 3, 2, 512])
            pg = u.ps("d_pg", [2 * HD16, T])

            @block.sync
            def _(sp):
                sp.dma_start(w[:, :, :, :], d["d_w3"]).then_inc(load, 16)
                sp.dma_start(wg[:, :, :], d["d_wg"]).then_inc(load, 16)

                def store(n, src, i):
                    b, part = divmod(i, QT)
                    sp.dma_start(heads[n, b][:, part * P:(part + 1) * P, :].rearrange("h p e -> p h e"),
                                 src[:, i, :].rearrange("p (h e) -> p h e", h=NH)).then_inc(stored, 16)

                for i in range(TT):
                    sp.wait_ge(vready, i + 1)
                    store(2, v, i)
                    sp.wait_ge(silu, 2 * (i + 1))
                    store(0, q, i)
                sp.wait_ge(gate, 2)
                for n in range(2):
                    sp.dma_start(gates[n].rearrange("b h s -> h b s"), g[n * NH:(n + 1) * NH, :].rearrange("h (b s) -> h b s", b=B)).then_inc(stored, 16)
                sp.wait_ge(ready, 1)
                for i in range(TT):
                    store(1, kk, i)
                sp.wait_ge(stored, 16 * (2 + 3 * TT))

            @block.tensor
            def _(pe):
                pe.wait_ge(load, 32)
                for c in range(KC):
                    m = nc.tensor.matmul(pg[:, :], wg[:, c, :], k.NT[:, c, :], start=(c == 0), stop=(c == KC - 1))
                m.then_inc(gmm, 1)
                for i in range(TT):
                    if i >= 2:
                        pe.wait_ge(silu, 2 * (i - 1))
                        pe.wait_ge(vready, i - 1)
                    for n in range(3):
                        for c in range(KC):
                            m = nc.tensor.matmul(ps[:, n, i % 2, 0:D], k.NT[:, c, i * P:(i + 1) * P], w[:, n, c, :],
                                                 start=(c == 0), stop=(c == KC - 1))
                    m.then_inc(mm, 1)

            @block.scalar
            def _(act):
                act.wait_ge(gmm, 1)
                nc.scalar.activation(g[:, :], pg[:, :], ACT.Sigmoid).then_inc(gate, 1)
                for i in range(TT):
                    act.wait_ge(mm, i + 1)
                    nc.scalar.activation(q[:, i, :], ps[:, 0, i % 2, 0:D], ACT.Silu).then_inc(silu, 1)
                    nc.scalar.activation(kk[:, i, :], ps[:, 1, i % 2, 0:D], ACT.Silu).then_inc(silu, 1)
                act.wait_ge(sq, 3)
                nc.scalar.activation(nrm[:, :, :], nrm[:, :, :], ACT.Sqrt).then_inc(root, 1)

            @block.vector
            def _(dve):
                for i in range(TT):
                    dve.wait_ge(mm, i + 1)
                    nc.vector.tensor_copy(v[:, i, :], ps[:, 2, i % 2, 0:D]).then_inc(vready, 1)
                dve.wait_ge(gate, 1)
                nc.vector.tensor_scalar(g[:, :], g[:, :], k.twos[0:2 * NH, 0:1], None, ALU.mult).then_inc(gate, 1)
                dve.wait_ge(silu, 2 * TT)
                nc.vector.tensor_tensor(ss[:, :, :], kk[:, :, :], kk[:, :, :], ALU.mult).then_inc(sq, 1)
                dve.wait_ge(sq, 1)
                nc.vector.reduce_sum(nrm[:, :, :], ss[:, :, :].rearrange("p i (h e) -> p i h e", h=NH), AX).then_inc(sq, 1)
                dve.wait_ge(sq, 2)
                nc.vector.tensor_scalar(nrm[:, :, :], nrm[:, :, :], 1e-12, None, ALU.add).then_inc(sq, 1)
                dve.wait_ge(root, 1)
                nc.vector.reciprocal(nrm[:, :, :], nrm[:, :, :]).then_inc(root, 1)
                dve.wait_ge(root, 2)
                for i in range(TT):
                    m = nc.vector.tensor_tensor(kk[:, i, :].rearrange("p (h e) -> p h e", h=NH), kk[:, i, :].rearrange("p (h e) -> p h e", h=NH),
                                                nrm[:, i, :].unsqueeze(2).broadcast_to([P, NH, HD16]), ALU.mult)
                m.then_inc(ready, 1)

        packed = nc.dram_tensor("delta_packed", (B, NH, S, ROW), F32, kind="Internal").ap()
        own = nc.dram_tensor("delta_own", (B, VH, NH, S, VL), F32, kind="Internal").ap()
        delta_blocks(nc, k, heads, gates, packed, own)
        with Tensors(nc) as u:
            rows = u.sb("e_rows", [P, S, ROW])
            u0 = u.sb("e_own", [P, S, VL])
            hist = u.sb("e_hist", [P, S // C8 + 1, VL, HD16 + C8])
            with stage(nc, "d_zero", "d_zero_load") as (block, zero, load):
                @block.vector
                def _(dve):
                    nc.vector.memset(hist[:, 0, :, 0:HD16], 0.0)

                @block.sync
                def _(sp):
                    delta_load(sp, rows, u0, packed, own, 0, load)
                    sp.wait_ge(load, 16 * 2 * B * VH)
            with nc.Fori(0, S // GROUP - 1) as r:
                delta_group(nc, "e", r, True, rows, u0, hist, packed, own, oA)
            delta_group(nc, "f", S // GROUP - 1, False, rows, u0, hist, packed, own, oA)

        O = t.sb("d_O", [P, TT, D])
        with Tensors(nc) as u, stage(nc, "g_load", "g_turned", "g_copied", "g_chain", "g_root") as (block, load, turned, copied, chain, root):
            nw = u.sb("g_nw", [P, D])
            sqr = u.sb("g_sq", [P, TT, D])
            ms = u.sb("g_ms", [P, TT, NH])
            ps = u.ps("g_ps", [P, QT, VL, P])

            @block.sync
            def _(sp):
                sp.dma_start(nw[:, :], d["d_norm_w"]).then_inc(load, 16)

            @block.tensor
            def _(pe):
                for i in range(QT):
                    for x in range(VL):
                        m = nc.tensor.transpose(ps[:, i, x, :], oA[:, i * P:(i + 1) * P, x], k.ident[:, :])
                    m.then_inc(turned, 1)

            @block.vector
            def _(dve):
                links = [0]

                def link(i):
                    links[0] += 1
                    i.then_inc(chain, 1)
                    dve.wait_ge(chain, links[0])

                for i in range(QT):
                    dve.wait_ge(turned, i + 1)
                    for b in range(B):
                        for x in range(VL):
                            m = nc.vector.tensor_copy(O[:, b * QT + i, :].rearrange("p (h y x) -> p h y x", h=NH, y=VH)[:, :, :, x],
                                                      ps[:, i, x, b * NH * VH:(b + 1) * NH * VH].rearrange("p (y h) -> p h y", y=VH))
                link(m)
                link(nc.vector.tensor_tensor(sqr[:, :, :], O[:, :, :], O[:, :, :], ALU.mult))
                link(nc.vector.reduce_sum(ms[:, :, :], sqr[:, :, :].rearrange("p i (h e) -> p i h e", h=NH), AX))
                nc.vector.tensor_scalar(ms[:, :, :], ms[:, :, :], 1.0 / HD16, 1e-6, ALU.mult, ALU.add).then_inc(root, 1)
                dve.wait_ge(root, 2)
                link(nc.vector.reciprocal(ms[:, :, :], ms[:, :, :]))
                dve.wait_ge(load, 16)
                for i in range(TT):
                    o3 = O[:, i, :].rearrange("p (h e) -> p h e", h=NH)
                    link(nc.vector.tensor_tensor(o3, o3, ms[:, i, :].unsqueeze(2).broadcast_to([P, NH, HD16]), ALU.mult))
                    nc.vector.tensor_tensor(O[:, i, :], O[:, i, :], nw[:, :], ALU.mult)

            @block.scalar
            def _(act):
                act.wait_ge(root, 1)
                nc.scalar.activation(ms[:, :, :], ms[:, :, :], ACT.Sqrt).then_inc(root, 1)
        project_tokens(nc, k, O, d["d_wo"], "dp")



def layer3_self(nc, k, d):
    DI, NS, R, KW = 512, 16, 64, 4
    DC = DI // P
    XD = R + 2 * NS
    SEG = B * DC
    layer_norm(nc, k, k.X, k.N, "mn", k.NT)
    with Tensors(nc) as t:
        xc = t.sb("m_xc", [P, DC, T])
        zs = t.sb("m_zs", [P, DC, T])
        dt = t.sb("m_dt", [P, DC, T])
        dbl = t.sb("m_dbl", [XD, T])
        A = t.sb("m_A", [P, DC, NS])
        par = t.sb("m_par", [P, DC, 3 + KW])
        with Tensors(nc) as u, stage(nc, "m_load", "m_mm", "m_ev", "m_zero", "m_conv", "m_xc_done") as (block, load, mm, ev, zero, conv, xc_done):
            w = u.sb("m_win", [P, KC, 2 * DI])
            xp = u.sb("m_xp", [P, DC, B, KW - 1 + S])
            cv = u.sb("m_cv", [P, 2, T])
            ps = u.ps("m_ps", [P, 2, T])

            @block.sync
            def _(sp):
                sp.dma_start(w[:, :, :], d["m_win"]).then_inc(load, 16)
                sp.dma_start(par[:, :, :], d["m_par"]).then_inc(load, 16)
                sp.dma_start(A[:, :, :], d["m_A_log"]).then_inc(load, 16)

            @block.tensor
            def _(pe):
                pe.wait_ge(load, 48)
                for m in range(2 * DC):
                    if m >= 2:
                        pe.wait_ge(ev, m - 1)
                    for c in range(KC):
                        i = nc.tensor.matmul(ps[:, m % 2, :], w[:, c, m * P:(m + 1) * P], k.NT[:, c, :], start=(c == 0), stop=(c == KC - 1))
                    i.then_inc(mm, 1)

            @block.scalar
            def _(act):
                for m in range(2 * DC):
                    act.wait_ge(mm, m + 1)
                    if m < DC:
                        nc.scalar.copy(xp[:, m, :, KW - 1:KW - 1 + S], ps[:, m % 2, :].rearrange("p (b s) -> p b s", b=B)).then_inc(ev, 1)
                    else:
                        nc.scalar.activation(zs[:, m - DC, :], ps[:, m % 2, :], ACT.Silu).then_inc(ev, 1)
                        act.wait_ge(conv, KW * (m - DC + 1))
                        nc.scalar.activation(xc[:, m - DC, :], cv[:, (m - DC) % 2, :], ACT.Silu, bias=par[:, m - DC, 0:1]).then_inc(xc_done, 1)
                act.wait_ge(load, 48)
                nc.scalar.activation(A[:, :, :], A[:, :, :], ACT.Exp)

            @block.vector
            def _(dve):
                nc.vector.memset(xp[:, :, :, 0:KW - 1], 0.0).then_inc(zero, 1)
                dve.wait_ge(zero, 1)
                dve.wait_ge(load, 48)
                for m in range(DC):
                    dve.wait_ge(ev, m + 1)
                    if m >= 2:
                        dve.wait_ge(xc_done, m - 1)
                    o = cv[:, m % 2, :].rearrange("p (b s) -> p b s", b=B)
                    for j in range(KW):
                        tap = par[:, m, 3 + j:4 + j]
                        if j == 0:
                            i = nc.vector.tensor_scalar(o, xp[:, m, :, 0:S], tap, None, ALU.mult)
                        else:
                            i = nc.vector.scalar_tensor_tensor(o, xp[:, m, :, j:j + S], tap, o, ALU.mult, ALU.add)
                        i.then_inc(conv, 1)
                        dve.wait_ge(conv, KW * m + j + 1)

        with Tensors(nc) as u, stage(nc, "n_load", "n_mm", "n_ev", "n_dmm", "n_pre", "n_exp", "n_chain") as (block, load, mm, ev, dmm, pre, expd, chain):
            wx = u.sb("n_wx", [P, DC, XD])
            wdt = u.sb("n_wdt", [R, DI])
            e = u.sb("n_e", [P, DC, T])
            w1 = u.sb("n_w1", [P, DC, T])
            ln = u.sb("n_ln", [P, DC, T])
            inv = u.sb("n_inv", [P, DC, T])
            px = u.ps("n_px", [XD, T])
            pd = u.ps("n_pd", [P, DC, T])

            @block.sync
            def _(sp):
                sp.dma_start(wx[:, :, :], d["m_wx"]).then_inc(load, 16)
                sp.dma_start(wdt[:, :], d["m_wdt"]).then_inc(load, 16)

            @block.tensor
            def _(pe):
                pe.wait_ge(load, 32)
                for c in range(DC):
                    m = nc.tensor.matmul(px[:, :], wx[:, c, :], xc[:, c, :], start=(c == 0), stop=(c == DC - 1))
                m.then_inc(mm, 1)
                pe.wait_ge(ev, 1)
                for c in range(DC):
                    nc.tensor.matmul(pd[:, c, :], wdt[:, c * P:(c + 1) * P], dbl[0:R, :], start=True, stop=True).then_inc(dmm, 1)

            @block.scalar
            def _(act):
                act.wait_ge(mm, 1)
                nc.scalar.copy(dbl[:, :], px[:, :]).then_inc(ev, 1)
                act.wait_ge(pre, 2)
                nc.scalar.activation(e[:, :, :], e[:, :, :], ACT.Exp, scale=-1.0).then_inc(expd, 1)
                act.wait_ge(pre, 3)
                nc.scalar.activation(ln[:, :, :], w1[:, :, :], ACT.Ln).then_inc(expd, 1)
                act.wait_ge(expd, 2)
                nc.scalar.activation(inv[:, :, :], ln[:, :, :], ACT.Exp, scale=-1.0).then_inc(expd, 1)

            @block.vector
            def _(dve):
                links = [0]

                def link(i):
                    links[0] += 1
                    i.then_inc(chain, 1)
                    dve.wait_ge(chain, links[0])

                for c in range(DC):
                    dve.wait_ge(dmm, c + 1)
                    i = nc.vector.tensor_scalar(dt[:, c, :], pd[:, c, :], par[:, c, 1:2], None, ALU.add)
                link(i)
                nc.vector.scalar_tensor_tensor(e[:, :, :], dt[:, :, :], -1.0, dt[:, :, :], ALU.mult, ALU.max).then_inc(pre, 1)
                dve.wait_ge(pre, 1)
                nc.vector.tensor_scalar(dt[:, :, :], dt[:, :, :], 0.0, None, ALU.max).then_inc(pre, 1)
                dve.wait_ge(expd, 1)
                nc.vector.tensor_scalar(w1[:, :, :], e[:, :, :], 1.0, None, ALU.add).then_inc(pre, 1)
                dve.wait_ge(pre, 3)
                link(nc.vector.scalar_tensor_tensor(e[:, :, :], w1[:, :, :], 1.0, e[:, :, :], ALU.subtract, ALU.subtract))
                dve.wait_ge(expd, 2)
                link(nc.vector.tensor_tensor(dt[:, :, :], dt[:, :, :], ln[:, :, :], ALU.add))
                dve.wait_ge(expd, 3)
                link(nc.vector.tensor_tensor(e[:, :, :], e[:, :, :], inv[:, :, :], ALU.mult))
                link(nc.vector.tensor_tensor(dt[:, :, :], dt[:, :, :], e[:, :, :], ALU.subtract))
                nc.vector.tensor_scalar(A[:, :, :], A[:, :, :], -1.0, None, ALU.mult)

        y = t.sb("m_y", [P, DC, T])
        with Tensors(nc) as u, stage(nc, "o_dx", "o_rows", "o_crow", "o_abar", "o_seg", "o_bu", "o_scan", "o_prod", "o_sum", "o_chain") as (
                block, dx_done, rows_done, crow, abar, seg, bu_done, scan, prod, summed, chain):
            dx = u.sb("o_dxs", [P, DC, T])
            ab = u.sb("o_ab", [P, 2, DC, T])
            bu = u.sb("o_bus", [P, DC, T])
            h = u.sb("o_h", [P, 2, DC, T])
            cr = u.sb("o_cr", [P, 2, T])
            pr = u.sb("o_pr", [P, 2, DC, T])
            pb = u.ps("o_pb", [P, 2, 2, T])
            py = u.ps("o_py", [P, DC, T])

            @block.tensor
            def _(pe):
                for n in range(NS + 2):
                    if n < NS:
                        if n >= 2:
                            pe.wait_ge(bu_done, n - 1)
                            pe.wait_ge(crow, n - 1)
                        for x in range(2):
                            r = R + NS * x + n
                            m = nc.tensor.matmul(pb[:, n % 2, x, :], k.ident[0:XD, r:r + 1].broadcast_to([XD, P]), dbl[:, :], start=True, stop=True)
                        m.then_inc(rows_done, 1)
                    if n >= 2:
                        pe.wait_ge(prod, n - 1)
                        for c in range(DC):
                            m = nc.tensor.matmul(py[:, c, :], k.ident[:, :], pr[:, n % 2, c, :], start=(n == 2), stop=(n == NS + 1))
                        m.then_inc(summed, 1)

            @block.scalar
            def _(act):
                for n in range(NS):
                    if n >= 2:
                        act.wait_ge(scan, n - 1)
                    for c in range(DC):
                        m = nc.scalar.activation(ab[:, n % 2, c, :], dt[:, c, :], ACT.Exp, scale=A[:, c, n:n + 1])
                    m.then_inc(abar, 1)
                    act.wait_ge(rows_done, n + 1)
                    if n >= 2:
                        act.wait_ge(prod, n - 1)
                    nc.scalar.copy(cr[:, n % 2, :], pb[:, n % 2, 1, :]).then_inc(crow, 1)

            @block.gpsimd
            def _(pool):
                for n in range(NS + 1):
                    if n < NS:
                        pool.wait_ge(abar, n + 1)
                        nc.gpsimd.memset(ab[:, n % 2, :, :].rearrange("p c (b s) -> p (c b) s", b=B)[:, :, 0:1], 0.0).then_inc(seg, 1)
                    if n >= 1:
                        j = n - 1
                        pool.wait_ge(scan, j + 1)
                        pool.wait_ge(crow, j + 1)
                        if j >= 2:
                            pool.wait_ge(summed, j - 1)
                        nc.gpsimd.tensor_tensor(pr[:, j % 2, :, :], h[:, j % 2, :, :], cr[:, j % 2, :].unsqueeze(1).broadcast_to([P, DC, T]),
                                                ALU.mult).then_inc(prod, 1)

            @block.vector
            def _(dve):
                nc.vector.tensor_tensor(dx[:, :, :], dt[:, :, :], xc[:, :, :], ALU.mult).then_inc(dx_done, 1)
                dve.wait_ge(dx_done, 1)
                for n in range(NS):
                    dve.wait_ge(rows_done, n + 1)
                    if n >= 1:
                        dve.wait_ge(scan, n)
                    nc.vector.tensor_tensor(bu[:, :, :], dx[:, :, :], pb[:, n % 2, 0, :].unsqueeze(1).broadcast_to([P, DC, T]),
                                            ALU.mult).then_inc(bu_done, 1)
                    dve.wait_ge(bu_done, n + 1)
                    dve.wait_ge(seg, n + 1)
                    if n >= 2:
                        dve.wait_ge(prod, n - 1)
                    flat = "p c s -> p (c s)"
                    nc.vector.tensor_tensor_scan(h[:, n % 2, :, :].rearrange(flat), ab[:, n % 2, :, :].rearrange(flat), bu[:, :, :].rearrange(flat),
                                                 0.0, ALU.mult, ALU.add).then_inc(scan, 1)
                for c in range(DC):
                    nc.vector.tensor_scalar(y[:, c, :], xc[:, c, :], par[:, c, 2:3], None, ALU.mult).then_inc(chain, 1)
                dve.wait_ge(chain, DC)
                dve.wait_ge(summed, NS)
                nc.vector.tensor_tensor(y[:, :, :], py[:, :, :], y[:, :, :], ALU.add).then_inc(chain, 1)
                dve.wait_ge(chain, DC + 1)
                nc.vector.tensor_tensor(y[:, :, :], y[:, :, :], zs[:, :, :], ALU.mult)
        project_residual(nc, k, y, d["m_wout"], "mp", chunks=DC)


def scan_layouts(a, i, rows, cols, spread):
    n = "L1_attn_"
    a["d_w3"] = np.ascontiguousarray(np.stack([rows(i[n + w]) for w in ("Wq", "Wk", "Wv")], 1))
    a["d_wg"] = rows(np.concatenate([i[n + "Wf"], i[n + "Wbet"]], 1))
    a["d_norm_w"] = spread(i[n + "norm_w"])
    a["d_wo"] = rows(i[n + "Wo"])
    two = np.ones((P, 1), np.float32)
    two[NH:2 * NH] = 2
    a["twos"] = two
    n = "L3_attn_"
    a["m_win"] = rows(i[n + "W_in"].T)

    def lane(v):
        return np.ascontiguousarray(v.reshape(4, P, -1).transpose(1, 0, 2))

    a["m_par"] = np.concatenate([lane(i[n + "conv_b"]), lane(i[n + "b_dt"]), lane(i[n + "D_param"]), lane(i[n + "conv_w"])], 2)
    a["m_A_log"] = lane(i[n + "A_log"])
    a["m_wx"], a["m_wdt"], a["m_wout"] = rows(i[n + "W_x"].T), np.ascontiguousarray(i[n + "W_dt"].T), rows(i[n + "W_out"].T)



class Kernel:
    pass


def program(nc, d, out):
    k = Kernel()
    with Tensors(nc) as t:
        k.X = t.sb("X", [P, TT, D])
        k.N = t.sb("N", [P, TT, D])
        k.NT = t.sb("NT", [P, KC, T])
        k.ident = t.sb("ident", [P, P])
        k.onesb = t.sb("ones_bf16", [P, P], BF16)
        k.ones = t.sb("ones_f32", [P, P])
        k.iota = t.sb("iota16", [P, NH])
        k.twos = t.sb("twos", [P, 1])
        with stage(nc, "x_load", "unused") as (block, load, _unused):
            @block.sync
            def _(sp):
                sp.dma_start(k.X[:, :, :], d["x"]).then_inc(load, 16)
                sp.dma_start(k.ident[:, :], d["ident"]).then_inc(load, 16)
                sp.dma_start(k.iota[:, :], d["iota16"]).then_inc(load, 16)
                sp.dma_start(k.twos[:, :], d["twos"]).then_inc(load, 16)
                sp.wait_ge(load, 64)

            @block.gpsimd
            def _(pool):
                nc.gpsimd.memset(k.onesb[:, :], 1.0)
                nc.gpsimd.memset(k.ones[:, :], 1.0)

        for layer in (layer0_cross, layer0_self, layer0_ff, layer1_cross, layer1_self, layer1_ff,
                      layer2_cross, layer2_self, layer2_ff, layer3_cross, layer3_self, layer3_ff):
            layer(nc, k, d)

        with stage(nc, "stored", "unused2") as (block, stored, _unused):
            @block.sync
            def _(sp):
                sp.dma_start(out.rearrange("b (i p) f -> p (b i) f", p=P), k.X[:, :, :]).then_inc(stored, 16)
                sp.wait_ge(stored, 16)


def layouts(inp):
    def rows(w):
        return np.ascontiguousarray(np.asarray(w).reshape(-1, P, np.asarray(w).shape[-1]).transpose(1, 0, 2))

    def cols(v):
        return np.ascontiguousarray(np.asarray(v).reshape(-1, P).T)

    def spread(v):
        return np.ascontiguousarray(np.broadcast_to(np.asarray(v).reshape(1, -1), (P, np.asarray(v).size)))

    i = {n: np.asarray(a) for n, a in inp.items()}
    a = {}
    a["x"] = rows(i["x"].reshape(T, D))
    ctx = i["ctx_1024"]
    a["ctxT"] = np.stack([rows(np.ascontiguousarray(ctx[b].T)) for b in range(B)])
    a["ctx_rows"] = np.stack([rows(ctx[b]) for b in range(B)])
    a["ident"] = np.eye(P, dtype=np.float32)
    a["iota16"] = np.ascontiguousarray(np.broadcast_to(np.arange(NH, dtype=np.float32), (P, NH)))
    a["L0x_wqT"], a["L0x_wk"] = rows(i["L0_xattn_Wq"].T), rows(i["L0_xattn_Wk"])
    a["L0x_bq"] = cols(i["L0_xattn_bq"])
    a["L0x_wvT"], a["L0x_bv"] = rows(i["L0_xattn_Wv"].T), cols(i["L0_xattn_bv"])
    a["L0x_woT"], a["L0x_bo"] = rows(i["L0_xattn_Wo"].T), spread(i["L0_xattn_bo"])
    for more in (cross_layouts, cross64_layouts, expert_layouts, self_layouts, scan_layouts):
        more(a, i, rows, cols, spread)
    return a


def kernel(**inputs):
    import concourse.bacc as bacc
    from concourse.bass_utils import run_bass_kernel_spmd

    nc = bacc.Bacc("TRN2", target_bir_lowering=False, num_devices=1)
    arrays = {"in_" + n: a for n, a in layouts(inputs).items()}
    d = {n[3:]: nc.dram_tensor(n, a.shape, mybir.dt.from_np(a.dtype), kind="ExternalInput").ap() for n, a in arrays.items()}
    out = nc.dram_tensor("out", (B, S, D), F32, kind="ExternalOutput").ap()
    program(nc, d, out)
    r = run_bass_kernel_spmd(nc, [arrays], core_ids=[0])
    return r.results[0]["out"]
```
